# Optimizing a Trainium2 kernel written in Bass

```python
import numpy as np
import jax
import jax.numpy as jnp

def _softmax(x, axis=-1):
    return jax.nn.softmax(x, axis=axis)

def _gelu(x):
    return jax.nn.gelu(x, approximate=True)

def _silu(x):
    return jax.nn.silu(x)

def _sigmoid(x):
    return jax.nn.sigmoid(x)

def _layernorm(x, axis=-1, eps=1e-05):
    m = jnp.mean(x, axis=axis, keepdims=True)
    v = jnp.var(x, axis=axis, keepdims=True)
    return (x - m) / jnp.sqrt(v + eps)

def _scatter_add(tgt, idx, src, axis=0):
    return tgt.at[idx].add(src)

def _segment_sum(src, seg, n):
    return jax.ops.segment_sum(src, seg, n)
kernel_name = 'mk_vit_tower_d4_tok_img1024_r4_ab5dcf'

def setup_inputs(seed: int=0):
    np.random.seed(seed)
    _w = jnp.asarray

    def _rec_inputs():
        import jax
        import jax.numpy as jnp
        _rk = jax.random.key(seed)
        x = -0.00016672 + 0.999947 * jax.random.normal(jax.random.fold_in(_rk, 1), (32, 3, 96, 96), jnp.float32)
        return x
    x = _rec_inputs()

    def _L0_tok_setup():
        import jax, jax.numpy as jnp
        import numpy as np
        IMG = 96
        PATCH = 16
        C_IN = 3
        EMBED = 256
        NPH = IMG // PATCH
        NUM_PATCHES = NPH * NPH
        PATCH_DIM = PATCH * PATCH * C_IN
        key = jax.random.key(seed)
        k_x, k_w, k_b, k_cls, k_pos = jax.random.split(key, 5)
        x = jax.random.normal(k_x, (64, C_IN, IMG, IMG), dtype=jnp.float32)
        W = jax.random.normal(k_w, (EMBED, PATCH_DIM), dtype=jnp.float32) * (1.0 / np.sqrt(PATCH_DIM))
        b = jax.random.normal(k_b, (EMBED,), dtype=jnp.float32) * 0.01
        cls_token = jax.random.normal(k_cls, (1, 1, EMBED), dtype=jnp.float32) * 0.02
        pos_embed = jax.random.normal(k_pos, (1, NUM_PATCHES + 1, EMBED), dtype=jnp.float32) * 0.02
        return {'x': x, 'W': W, 'b': b, 'cls_token': cls_token, 'pos_embed': pos_embed}
    _L0_tok_all = _L0_tok_setup()
    _L0_tok_in = {k: v for k, v in _L0_tok_all.items() if k in ('W', 'b', 'cls_token', 'pos_embed')}
    del _L0_tok_all

    def _L0_attn_setup():
        import jax, jax.numpy as jnp
        import numpy as np
        DIM = 256
        H = 16
        D = DIM // H
        HID = H * D
        N, T = (2, 256)
        key = jax.random.key(seed)
        ks = jax.random.split(key, 6)
        x = jax.random.normal(ks[0], (N, T, DIM), dtype=jnp.float32)
        key_w = jax.random.normal(ks[1], (HID, DIM), dtype=jnp.float32) * DIM ** (-0.5)
        key_b = jax.random.uniform(ks[2], (HID,), minval=-4.0, maxval=4.0, dtype=jnp.float32)
        vq_w = jax.random.normal(ks[3], (2 * HID, DIM), dtype=jnp.float32) * DIM ** (-0.5)
        out_w = jax.random.normal(ks[4], (DIM, HID), dtype=jnp.float32) * HID ** (-0.5)
        out_b = jax.random.normal(ks[5], (DIM,), dtype=jnp.float32) * 0.02
        return {'x': x, 'key_w': key_w, 'key_b': key_b, 'vq_w': vq_w, 'out_w': out_w, 'out_b': out_b}
    _L0_attn_all = _L0_attn_setup()
    _L0_attn_in = {k: v for k, v in _L0_attn_all.items() if k in ('key_w', 'key_b', 'vq_w', 'out_w', 'out_b')}
    del _L0_attn_all

    def _L0_ffn_setup():
        import jax, jax.numpy as jnp
        import numpy as np
        E = 8
        K = 2
        B, S, H = (4, 512, 256)
        key = jax.random.key(seed)
        k1, k2, k3 = jax.random.split(key, 3)
        hidden_states = jax.random.normal(k1, (B, S, H), dtype=jnp.float32)
        weight = jax.random.normal(k2, (E, H, H), dtype=jnp.float32) * 0.02
        bias = jnp.zeros((E, H), dtype=jnp.float32)
        router_weight = jax.random.normal(k3, (E, H), dtype=jnp.float32) * 0.01
        router_bias = jnp.zeros((E,), dtype=jnp.float32)
        return {'hidden_states': hidden_states, 'weight': weight, 'bias': bias, 'router_weight': router_weight, 'router_bias': router_bias}
    _L0_ffn_all = _L0_ffn_setup()
    _L0_ffn_in = {k: v for k, v in _L0_ffn_all.items() if k in ('weight', 'bias', 'router_weight', 'router_bias')}
    del _L0_ffn_all

    def _L1_attn_setup():
        import jax, jax.numpy as jnp
        import numpy as np
        import math
        D_MODEL, N_HEADS, D_K, D_C, D_HR = (256, 8, 128, 32, 32)
        B, S = (4, 512)
        key = jax.random.key(seed)
        ks = jax.random.split(key, 17)

        def lin(k, fan_in, fan_out):
            lim = 1.0 / math.sqrt(fan_in)
            kw, kb = jax.random.split(k)
            W = jax.random.uniform(kw, (fan_in, fan_out), jnp.float32, -lim, lim)
            b = jax.random.uniform(kb, (fan_out,), jnp.float32, -lim, lim)
            return (W, b)
        W_DQ, b_DQ = lin(ks[0], D_MODEL, D_C)
        W_UQ, b_UQ = lin(ks[1], D_C, N_HEADS * D_K)
        W_DKV, b_DKV = lin(ks[2], D_MODEL, D_C)
        W_UK, b_UK = lin(ks[3], D_C, N_HEADS * D_K)
        W_UV, b_UV = lin(ks[4], D_C, N_HEADS * D_K)
        W_QR, b_QR = lin(ks[5], D_C, N_HEADS * D_HR)
        W_KR, b_KR = lin(ks[6], D_MODEL, D_HR)
        W_O, b_O = lin(ks[7], N_HEADS * D_K, D_MODEL)
        h_t = jax.random.normal(ks[8], (B, S, D_MODEL), jnp.float32)
        return {'h_t': h_t, 'W_DQ': W_DQ, 'b_DQ': b_DQ, 'W_UQ': W_UQ, 'b_UQ': b_UQ, 'W_DKV': W_DKV, 'b_DKV': b_DKV, 'W_UK': W_UK, 'b_UK': b_UK, 'W_UV': W_UV, 'b_UV': b_UV, 'W_QR': W_QR, 'b_QR': b_QR, 'W_KR': W_KR, 'b_KR': b_KR, 'W_O': W_O, 'b_O': b_O}
    _L1_attn_all = _L1_attn_setup()
    _L1_attn_in = {k: v for k, v in _L1_attn_all.items() if k in ('W_DQ', 'b_DQ', 'W_UQ', 'b_UQ', 'W_DKV', 'b_DKV', 'W_UK', 'b_UK', 'W_UV', 'b_UV', 'W_QR', 'b_QR', 'W_KR', 'b_KR', 'W_O', 'b_O')}
    del _L1_attn_all

    def _L1_ffn_setup():
        import jax, jax.numpy as jnp
        import numpy as np
        NUM_TRUE = 8
        NUM_NULL = 2
        NUM_EXPERTS = NUM_TRUE + NUM_NULL
        TOP_K = 2
        key = jax.random.key(seed)
        k0, k1, k2 = jax.random.split(key, 3)
        B, S, D = (4, 512, 256)
        inputs = jax.random.normal(k0, (B, S, D), dtype=jnp.float32)
        gate_w = jax.random.normal(k1, (NUM_EXPERTS, D), dtype=jnp.float32) * 0.02
        gate_b = jnp.zeros((NUM_EXPERTS,), dtype=jnp.float32)
        expert_w = jax.random.normal(k2, (NUM_TRUE, D, D), dtype=jnp.float32) * 0.02
        expert_b = jnp.zeros((NUM_TRUE, D), dtype=jnp.float32)
        return {'inputs': inputs, 'gate_w': gate_w, 'gate_b': gate_b, 'expert_w': expert_w, 'expert_b': expert_b}
    _L1_ffn_all = _L1_ffn_setup()
    _L1_ffn_in = {k: v for k, v in _L1_ffn_all.items() if k in ('gate_w', 'gate_b', 'expert_w', 'expert_b')}
    del _L1_ffn_all

    def _L2_attn_setup():
        import jax, jax.numpy as jnp
        import numpy as np
        DIM = 256
        D_STATE = 64
        D_CONV = 4
        EXPAND = 2
        N_HEADS = 8
        D_INNER = DIM * EXPAND
        HEAD_DIM = D_INNER // N_HEADS
        D_IN_PROJ = D_INNER + D_INNER + N_HEADS + D_STATE + D_STATE
        BATCH, SEQ = (2, 256)
        EPS = 1e-06

        def _rms_norm(y, w):
            rms = jnp.sqrt(jnp.mean(y * y, axis=-1, keepdims=True) + EPS)
            return y / rms * w

        def _depthwise_causal_conv(u, w, b):
            L = u.shape[1]
            up = jnp.pad(u, ((0, 0), (D_CONV - 1, 0), (0, 0)))
            out = b[None, None, :]
            for k in range(D_CONV):
                out = out + up[:, k:k + L, :] * w[None, None, :, k]
            return out

        def _mamba2_forward(x, in_proj_w, conv_w, conv_b, A_log, D_param, dt_bias, norm_w, out_proj_w):
            B_sz, L, _ = x.shape
            zxBCdt = x @ in_proj_w.T
            z, xc, Bm, Cm, dt = jnp.split(zxBCdt, [D_INNER, 2 * D_INNER, 2 * D_INNER + N_HEADS, 2 * D_INNER + N_HEADS + D_STATE], axis=-1)
            xc = _depthwise_causal_conv(xc, conv_w, conv_b)
            xc = jax.nn.silu(xc)
            xh = xc.reshape(B_sz, L, N_HEADS, HEAD_DIM)
            A = -jnp.exp(A_log)
            dt = jax.nn.softplus(Bm + dt_bias)
            a_bar = jnp.exp(dt * A[None, None, :])

            def step(h, t):
                a_t, b_t, c_t, x_t = t
                h = a_t[:, :, None, None] * h + b_t[:, None, None, :] * x_t[..., None]
                y_t = jnp.einsum('bhdn,bn->bhd', h, c_t)
                return (h, y_t)
            h0 = jnp.zeros((B_sz, N_HEADS, HEAD_DIM, D_STATE), dtype=x.dtype)
            xs = (jnp.moveaxis(a_bar, 1, 0), jnp.moveaxis(Cm, 1, 0) * 0 + jnp.moveaxis(Cm, 1, 0), jnp.moveaxis(dt, 1, 0) * 0, jnp.moveaxis(xh, 1, 0))
            B_proj, C_proj = (Cm, dt if False else (Cm, None))
            raise NotImplementedError
        key = jax.random.key(seed)
        ks = jax.random.split(key, 9)
        x = jax.random.normal(ks[0], (BATCH, SEQ, DIM), dtype=jnp.float32)
        in_proj_w = jax.random.normal(ks[1], (D_IN_PROJ, DIM), dtype=jnp.float32) * 0.02
        conv_w = jax.random.normal(ks[2], (D_INNER, D_CONV), dtype=jnp.float32) * 0.2
        conv_b = jax.random.normal(ks[3], (D_INNER,), dtype=jnp.float32) * 0.02
        A_log = jax.random.normal(ks[4], (N_HEADS,), dtype=jnp.float32) * 0.5
        D_param = jnp.ones((N_HEADS,), dtype=jnp.float32) + 0.1 * jax.random.normal(ks[5], (N_HEADS,), dtype=jnp.float32)
        dt_bias = jax.random.normal(ks[6], (N_HEADS,), dtype=jnp.float32) * 0.5
        norm_w = jnp.ones((D_INNER,), dtype=jnp.float32)
        out_proj_w = jax.random.normal(ks[7], (DIM, D_INNER), dtype=jnp.float32) * 0.02
        return {'x': x, 'in_proj_w': in_proj_w, 'conv_w': conv_w, 'conv_b': conv_b, 'A_log': A_log, 'D_param': D_param, 'dt_bias': dt_bias, 'norm_w': norm_w, 'out_proj_w': out_proj_w}
    _L2_attn_all = _L2_attn_setup()
    _L2_attn_in = {k: v for k, v in _L2_attn_all.items() if k in ('in_proj_w', 'conv_w', 'conv_b', 'A_log', 'D_param', 'dt_bias', 'norm_w', 'out_proj_w')}
    del _L2_attn_all

    def _L2_ffn_setup():
        import jax, jax.numpy as jnp
        import numpy as np
        B, S, D, H, E, F, K = (2, 256, 256, 16, 8, 1024, 2)
        EPS = 1e-05

        def _layernorm(x, g, b):
            mu = jnp.mean(x, axis=-1, keepdims=True)
            var = jnp.mean(jnp.square(x - mu), axis=-1, keepdims=True)
            return (x - mu) * jax.lax.rsqrt(var + EPS) * g + b
        key = jax.random.key(seed)
        ks = jax.random.split(key, 12)
        w = lambda k, shape: jax.random.normal(k, shape, dtype=jnp.float32) * 0.02
        return {'x': jax.random.normal(ks[0], (B, S, D), dtype=jnp.float32), 'ln1_g': jnp.ones((D,), jnp.float32), 'ln1_b': jnp.zeros((D,), jnp.float32), 'ln2_g': jnp.ones((D,), jnp.float32), 'ln2_b': jnp.zeros((D,), jnp.float32), 'Wq': w(ks[1], (D, D)), 'Wk': w(ks[2], (D, D)), 'Wv': w(ks[3], (D, D)), 'Wo': w(ks[4], (D, D)), 'Wg': w(ks[5], (D, E)), 'W1': w(ks[6], (E, D, F)), 'b1': jnp.zeros((E, F), jnp.float32), 'W2': w(ks[7], (E, F, D)), 'b2': jnp.zeros((E, D), jnp.float32)}
    _L2_ffn_all = _L2_ffn_setup()
    _L2_ffn_in = {k: v for k, v in _L2_ffn_all.items() if k in ('ln1_g', 'ln1_b', 'ln2_g', 'ln2_b', 'Wq', 'Wk', 'Wv', 'Wo', 'Wg', 'W1', 'b1', 'W2', 'b2')}
    del _L2_ffn_all

    def _L3_attn_setup():
        import jax, jax.numpy as jnp
        import numpy as np
        HID = 256
        NH = 16
        HD = HID // NH
        RANK = 16
        B, L = (2, 512)
        key = jax.random.key(seed)
        ks = jax.random.split(key, 9)
        s = 0.02
        return {'x': jax.random.normal(ks[0], (B, L, HID), dtype=jnp.float32), 'Wq': jax.random.normal(ks[1], (HID, HID), dtype=jnp.float32) * s, 'Wk': jax.random.normal(ks[2], (HID, HID), dtype=jnp.float32) * s, 'Wv': jax.random.normal(ks[3], (HID, HID), dtype=jnp.float32) * s, 'Wg': jax.random.normal(ks[4], (HID, HID), dtype=jnp.float32) * s, 'Wgk1': jax.random.normal(ks[5], (HID, RANK), dtype=jnp.float32) * s, 'Wgk2': jax.random.normal(ks[6], (RANK, HID), dtype=jnp.float32) * s, 'bgk2': jnp.zeros((HID,), dtype=jnp.float32), 'gamma': jnp.ones((HID,), dtype=jnp.float32), 'beta': jnp.zeros((HID,), dtype=jnp.float32), 'Wout': jax.random.normal(ks[7], (HID, HID), dtype=jnp.float32) * s}
    _L3_attn_all = _L3_attn_setup()
    _L3_attn_in = {k: v for k, v in _L3_attn_all.items() if k in ('Wq', 'Wk', 'Wv', 'Wg', 'Wgk1', 'Wgk2', 'bgk2', 'gamma', 'beta', 'Wout')}
    del _L3_attn_all

    def _L3_ffn_setup():
        import jax, jax.numpy as jnp
        import numpy as np
        B, SEQ, DIM = (2, 1024, 256)
        E, S = (8, 128)
        HID = 4 * DIM
        SCALE = DIM ** 0.5

        def rmsnorm(x, gamma):
            n = jnp.linalg.norm(x, axis=-1, keepdims=True)
            return x / jnp.maximum(n, 1e-12) * SCALE * gamma
        key = jax.random.key(seed)
        ks = jax.random.split(key, 4)
        w_init = lambda k, shape: jax.random.normal(k, shape, dtype=jnp.float32) * 0.02
        return {'x': jax.random.normal(ks[0], (B, SEQ, DIM), dtype=jnp.float32), 'norm_gamma': jnp.ones((DIM,), jnp.float32), 'slot_norm_gamma': jnp.ones((DIM,), jnp.float32), 'slot_embeds': jax.random.normal(ks[1], (E, S, DIM), dtype=jnp.float32), 'w1': w_init(ks[2], (E, DIM, HID)), 'b1': jnp.zeros((E, HID), jnp.float32), 'w2': w_init(ks[3], (E, HID, DIM)), 'b2': jnp.zeros((E, DIM), jnp.float32)}
    _L3_ffn_all = _L3_ffn_setup()
    _L3_ffn_in = {k: v for k, v in _L3_ffn_all.items() if k in ('norm_gamma', 'slot_norm_gamma', 'slot_embeds', 'w1', 'b1', 'w2', 'b2')}
    del _L3_ffn_all
    return {'x': x, 'L0_tok_W': _L0_tok_in['W'], 'L0_tok_b': _L0_tok_in['b'], 'L0_tok_cls_token': _L0_tok_in['cls_token'], 'L0_tok_pos_embed': _L0_tok_in['pos_embed'], 'L0_attn_key_w': _L0_attn_in['key_w'], 'L0_attn_key_b': _L0_attn_in['key_b'], 'L0_attn_vq_w': _L0_attn_in['vq_w'], 'L0_attn_out_w': _L0_attn_in['out_w'], 'L0_attn_out_b': _L0_attn_in['out_b'], 'L0_ffn_weight': _L0_ffn_in['weight'], 'L0_ffn_bias': _L0_ffn_in['bias'], 'L0_ffn_router_weight': _L0_ffn_in['router_weight'], 'L0_ffn_router_bias': _L0_ffn_in['router_bias'], 'L1_attn_W_DQ': _L1_attn_in['W_DQ'], 'L1_attn_b_DQ': _L1_attn_in['b_DQ'], 'L1_attn_W_UQ': _L1_attn_in['W_UQ'], 'L1_attn_b_UQ': _L1_attn_in['b_UQ'], 'L1_attn_W_DKV': _L1_attn_in['W_DKV'], 'L1_attn_b_DKV': _L1_attn_in['b_DKV'], 'L1_attn_W_UK': _L1_attn_in['W_UK'], 'L1_attn_b_UK': _L1_attn_in['b_UK'], 'L1_attn_W_UV': _L1_attn_in['W_UV'], 'L1_attn_b_UV': _L1_attn_in['b_UV'], 'L1_attn_W_QR': _L1_attn_in['W_QR'], 'L1_attn_b_QR': _L1_attn_in['b_QR'], 'L1_attn_W_KR': _L1_attn_in['W_KR'], 'L1_attn_b_KR': _L1_attn_in['b_KR'], 'L1_attn_W_O': _L1_attn_in['W_O'], 'L1_attn_b_O': _L1_attn_in['b_O'], 'L1_ffn_gate_w': _L1_ffn_in['gate_w'], 'L1_ffn_gate_b': _L1_ffn_in['gate_b'], 'L1_ffn_expert_w': _L1_ffn_in['expert_w'], 'L1_ffn_expert_b': _L1_ffn_in['expert_b'], 'L2_attn_in_proj_w': _L2_attn_in['in_proj_w'], 'L2_attn_conv_w': _L2_attn_in['conv_w'], 'L2_attn_conv_b': _L2_attn_in['conv_b'], 'L2_attn_A_log': _L2_attn_in['A_log'], 'L2_attn_D_param': _L2_attn_in['D_param'], 'L2_attn_dt_bias': _L2_attn_in['dt_bias'], 'L2_attn_norm_w': _L2_attn_in['norm_w'], 'L2_attn_out_proj_w': _L2_attn_in['out_proj_w'], 'L2_ffn_ln1_g': _L2_ffn_in['ln1_g'], 'L2_ffn_ln1_b': _L2_ffn_in['ln1_b'], 'L2_ffn_ln2_g': _L2_ffn_in['ln2_g'], 'L2_ffn_ln2_b': _L2_ffn_in['ln2_b'], 'L2_ffn_Wq': _L2_ffn_in['Wq'], 'L2_ffn_Wk': _L2_ffn_in['Wk'], 'L2_ffn_Wv': _L2_ffn_in['Wv'], 'L2_ffn_Wo': _L2_ffn_in['Wo'], 'L2_ffn_Wg': _L2_ffn_in['Wg'], 'L2_ffn_W1': _L2_ffn_in['W1'], 'L2_ffn_b1': _L2_ffn_in['b1'], 'L2_ffn_W2': _L2_ffn_in['W2'], 'L2_ffn_b2': _L2_ffn_in['b2'], 'L3_attn_Wq': _L3_attn_in['Wq'], 'L3_attn_Wk': _L3_attn_in['Wk'], 'L3_attn_Wv': _L3_attn_in['Wv'], 'L3_attn_Wg': _L3_attn_in['Wg'], 'L3_attn_Wgk1': _L3_attn_in['Wgk1'], 'L3_attn_Wgk2': _L3_attn_in['Wgk2'], 'L3_attn_bgk2': _L3_attn_in['bgk2'], 'L3_attn_gamma': _L3_attn_in['gamma'], 'L3_attn_beta': _L3_attn_in['beta'], 'L3_attn_Wout': _L3_attn_in['Wout'], 'L3_ffn_norm_gamma': _L3_ffn_in['norm_gamma'], 'L3_ffn_slot_norm_gamma': _L3_ffn_in['slot_norm_gamma'], 'L3_ffn_slot_embeds': _L3_ffn_in['slot_embeds'], 'L3_ffn_w1': _L3_ffn_in['w1'], 'L3_ffn_b1': _L3_ffn_in['b1'], 'L3_ffn_w2': _L3_ffn_in['w2'], 'L3_ffn_b2': _L3_ffn_in['b2']}

def reference(x, L0_tok_W, L0_tok_b, L0_tok_cls_token, L0_tok_pos_embed, L0_attn_key_w, L0_attn_key_b, L0_attn_vq_w, L0_attn_out_w, L0_attn_out_b, L0_ffn_weight, L0_ffn_bias, L0_ffn_router_weight, L0_ffn_router_bias, L1_attn_W_DQ, L1_attn_b_DQ, L1_attn_W_UQ, L1_attn_b_UQ, L1_attn_W_DKV, L1_attn_b_DKV, L1_attn_W_UK, L1_attn_b_UK, L1_attn_W_UV, L1_attn_b_UV, L1_attn_W_QR, L1_attn_b_QR, L1_attn_W_KR, L1_attn_b_KR, L1_attn_W_O, L1_attn_b_O, L1_ffn_gate_w, L1_ffn_gate_b, L1_ffn_expert_w, L1_ffn_expert_b, L2_attn_in_proj_w, L2_attn_conv_w, L2_attn_conv_b, L2_attn_A_log, L2_attn_D_param, L2_attn_dt_bias, L2_attn_norm_w, L2_attn_out_proj_w, L2_ffn_ln1_g, L2_ffn_ln1_b, L2_ffn_ln2_g, L2_ffn_ln2_b, L2_ffn_Wq, L2_ffn_Wk, L2_ffn_Wv, L2_ffn_Wo, L2_ffn_Wg, L2_ffn_W1, L2_ffn_b1, L2_ffn_W2, L2_ffn_b2, L3_attn_Wq, L3_attn_Wk, L3_attn_Wv, L3_attn_Wg, L3_attn_Wgk1, L3_attn_Wgk2, L3_attn_bgk2, L3_attn_gamma, L3_attn_beta, L3_attn_Wout, L3_ffn_norm_gamma, L3_ffn_slot_norm_gamma, L3_ffn_slot_embeds, L3_ffn_w1, L3_ffn_b1, L3_ffn_w2, L3_ffn_b2):
    import jax
    import jax.numpy as jnp

    def _L0_tok_ref(x, W, b, cls_token, pos_embed):
        import jax, jax.numpy as jnp
        import numpy as np
        IMG = 96
        PATCH = 16
        C_IN = 3
        EMBED = 256
        NPH = IMG // PATCH
        NUM_PATCHES = NPH * NPH
        PATCH_DIM = PATCH * PATCH * C_IN
        B, C, H, Wd = x.shape
        nph, npw = (H // PATCH, Wd // PATCH)
        patches = x.reshape(B, C, nph, PATCH, npw, PATCH)
        patches = patches.transpose(0, 2, 4, 1, 3, 5)
        patches = patches.reshape(B, nph * npw, C * PATCH * PATCH)
        proj = jnp.einsum('bnd,ed->bne', patches, W) + b
        cls = jnp.broadcast_to(cls_token, (B, 1, cls_token.shape[-1]))
        out = jnp.concatenate([cls, proj], axis=1) + pos_embed
        return out

    def _L0_attn_ref(x, key_w, key_b, vq_w, out_w, out_b):
        import jax, jax.numpy as jnp
        import numpy as np
        DIM = 256
        H = 16
        D = DIM // H
        HID = H * D
        N, T = (2, 256)
        n, t, dim = x.shape
        vq = x @ vq_w.T
        v, q = jnp.split(vq, 2, axis=-1)
        k = jax.nn.sigmoid(x @ key_w.T + key_b)
        k = k.reshape(n, t, H, D)
        v = v.reshape(n, t, H, D)
        upd = (1.0 - k)[..., :, None] * v[..., None, :]
        decay = k[..., :, None]

        def combine(c1, c2):
            a1, b1 = c1
            a2, b2 = c2
            return (a1 * a2, b1 * a2 + b2)
        _, kv = jax.lax.associative_scan(combine, (decay, upd), axis=1)
        qh = q.reshape(n, t, H, D)
        h = jnp.einsum('nthd,nthde->nthe', qh, kv).reshape(n, t, HID)
        return h @ out_w.T + out_b

    def _L0_ffn_ref(hidden_states, weight, bias, router_weight, router_bias):
        import jax, jax.numpy as jnp
        import numpy as np
        E = 8
        K = 2
        B, S, H = (4, 512, 256)
        b, s, h = hidden_states.shape
        flat = hidden_states.reshape(b * s, h)
        logits = flat @ router_weight.T + router_bias
        scores = jax.nn.softmax(logits, axis=-1)
        _, topk_idx = jax.lax.top_k(scores, K)
        y = jnp.einsum('th,ehk->tek', flat, weight) + bias[None]
        sel = jnp.take_along_axis(y, topk_idx[:, :, None], axis=1)
        out = sel.sum(axis=1).reshape(b, s, h)
        return out

    def _L1_attn_ref(h_t, W_DQ, b_DQ, W_UQ, b_UQ, W_DKV, b_DKV, W_UK, b_UK, W_UV, b_UV, W_QR, b_QR, W_KR, b_KR, W_O, b_O):
        import jax, jax.numpy as jnp
        import numpy as np
        import math
        D_MODEL, N_HEADS, D_K, D_C, D_HR = (256, 8, 128, 32, 32)
        B, S = (4, 512)
        b, s, _ = h_t.shape
        c_q = h_t @ W_DQ + b_DQ
        c_kv = h_t @ W_DKV + b_DKV
        q_c = (c_q @ W_UQ + b_UQ).reshape(b, s, N_HEADS, D_K).transpose(0, 2, 1, 3)
        k_c = (c_kv @ W_UK + b_UK).reshape(b, s, N_HEADS, D_K).transpose(0, 2, 1, 3)
        v_c = (c_kv @ W_UV + b_UV).reshape(b, s, N_HEADS, D_K).transpose(0, 2, 1, 3)
        q_r = (c_q @ W_QR + b_QR).reshape(b, s, N_HEADS, D_HR).transpose(0, 2, 1, 3)
        k_r = (h_t @ W_KR + b_KR)[:, None, :, :]
        k_r = jnp.broadcast_to(k_r, (b, N_HEADS, s, D_HR))
        q = jnp.concatenate([q_c, q_r], axis=-1)
        k = jnp.concatenate([k_c, k_r], axis=-1)
        scale = 1.0 / math.sqrt(D_K + D_HR)
        scores = jnp.einsum('bhsd,bhtd->bhst', q, k) * scale
        attn = jax.nn.softmax(scores, axis=-1)
        o = jnp.einsum('bhst,bhtd->bhsd', attn, v_c)
        o = o.transpose(0, 2, 1, 3).reshape(b, s, N_HEADS * D_K)
        return o @ W_O + b_O

    def _L1_ffn_ref(inputs, gate_w, gate_b, expert_w, expert_b):
        import jax, jax.numpy as jnp
        import numpy as np
        NUM_TRUE = 8
        NUM_NULL = 2
        NUM_EXPERTS = NUM_TRUE + NUM_NULL
        TOP_K = 2
        D = inputs.shape[-1]
        x = inputs.reshape(-1, D)
        gate_logits = x @ gate_w.T + gate_b
        gate_probs = jax.nn.softmax(gate_logits, axis=-1)
        weights, selected = jax.lax.top_k(gate_probs, TOP_K)
        true_mask = selected < NUM_TRUE
        true_weights = weights * true_mask
        denom = true_weights.sum(axis=-1, keepdims=True)
        denom = jnp.where(denom > 0, denom, jnp.ones_like(denom))
        norm_w = (true_weights / denom).astype(x.dtype)
        one_hot = jax.nn.one_hot(selected, NUM_EXPERTS, dtype=norm_w.dtype)
        combine_w = jnp.einsum('tk,tke->te', norm_w, one_hot)[:, :NUM_TRUE]
        expert_out = jnp.einsum('td,edh->teh', x, expert_w) + expert_b[None, :, :]
        out = jnp.einsum('te,teh->th', combine_w, expert_out)
        return out.reshape(inputs.shape[:-1] + (out.shape[-1],))

    def _L2_attn_ref(x, in_proj_w, conv_w, conv_b, A_log, D_param, dt_bias, norm_w, out_proj_w):
        import jax, jax.numpy as jnp
        import numpy as np
        DIM = 256
        D_STATE = 64
        D_CONV = 4
        EXPAND = 2
        N_HEADS = 8
        D_INNER = DIM * EXPAND
        HEAD_DIM = D_INNER // N_HEADS
        D_IN_PROJ = D_INNER + D_INNER + N_HEADS + D_STATE + D_STATE
        BATCH, SEQ = (2, 256)
        EPS = 1e-06

        def _rms_norm(y, w):
            rms = jnp.sqrt(jnp.mean(y * y, axis=-1, keepdims=True) + EPS)
            return y / rms * w

        def _depthwise_causal_conv(u, w, b):
            L = u.shape[1]
            up = jnp.pad(u, ((0, 0), (D_CONV - 1, 0), (0, 0)))
            out = b[None, None, :]
            for k in range(D_CONV):
                out = out + up[:, k:k + L, :] * w[None, None, :, k]
            return out

        def _mamba2_forward(x, in_proj_w, conv_w, conv_b, A_log, D_param, dt_bias, norm_w, out_proj_w):
            B_sz, L, _ = x.shape
            zxBCdt = x @ in_proj_w.T
            z, xc, Bm, Cm, dt = jnp.split(zxBCdt, [D_INNER, 2 * D_INNER, 2 * D_INNER + N_HEADS, 2 * D_INNER + N_HEADS + D_STATE], axis=-1)
            xc = _depthwise_causal_conv(xc, conv_w, conv_b)
            xc = jax.nn.silu(xc)
            xh = xc.reshape(B_sz, L, N_HEADS, HEAD_DIM)
            A = -jnp.exp(A_log)
            dt = jax.nn.softplus(Bm + dt_bias)
            a_bar = jnp.exp(dt * A[None, None, :])

            def step(h, t):
                a_t, b_t, c_t, x_t = t
                h = a_t[:, :, None, None] * h + b_t[:, None, None, :] * x_t[..., None]
                y_t = jnp.einsum('bhdn,bn->bhd', h, c_t)
                return (h, y_t)
            h0 = jnp.zeros((B_sz, N_HEADS, HEAD_DIM, D_STATE), dtype=x.dtype)
            xs = (jnp.moveaxis(a_bar, 1, 0), jnp.moveaxis(Cm, 1, 0) * 0 + jnp.moveaxis(Cm, 1, 0), jnp.moveaxis(dt, 1, 0) * 0, jnp.moveaxis(xh, 1, 0))
            B_proj, C_proj = (Cm, dt if False else (Cm, None))
            raise NotImplementedError
        B_sz, L, _ = x.shape
        zxBCdt = x @ in_proj_w.T
        z = zxBCdt[..., :D_INNER]
        xc = zxBCdt[..., D_INNER:2 * D_INNER]
        Bp = zxBCdt[..., 2 * D_INNER:2 * D_INNER + N_HEADS]
        Bm = zxBCdt[..., 2 * D_INNER:2 * D_INNER + N_HEADS]
        Cm = zxBCdt[..., 2 * D_INNER + N_HEADS:2 * D_INNER + N_HEADS + D_STATE]
        dtm = zxBCdt[..., 2 * D_INNER + N_HEADS + D_STATE:]
        dt = jax.nn.softplus(Bm + dt_bias)
        B_proj, C_proj = (Cm, dtm)
        xc = _depthwise_causal_conv(xc, conv_w, conv_b)
        xc = jax.nn.silu(xc)
        xh = xc.reshape(B_sz, L, N_HEADS, HEAD_DIM)
        A = -jnp.exp(A_log)
        a_bar = jnp.exp(dt * A[None, None, :])

        def step(h, t):
            a_t, b_t, c_t, x_t = t
            h = a_t[:, :, None, None] * h + b_t[:, None, None, :] * x_t[..., None]
            y_t = jnp.einsum('bhdn,bn->bhd', h, c_t)
            return (h, y_t)
        h0 = jnp.zeros((B_sz, N_HEADS, HEAD_DIM, D_STATE), dtype=x.dtype)
        ts = (jnp.moveaxis(a_bar, 1, 0), jnp.moveaxis(B_proj, 1, 0), jnp.moveaxis(C_proj, 1, 0), jnp.moveaxis(xh, 1, 0))
        _, ys = jax.lax.scan(step, h0, ts)
        y = jnp.moveaxis(ys, 0, 1)
        y = y + xh * D_param[None, None, :, None]
        y = y.reshape(B_sz, L, D_INNER)
        y = y * jax.nn.silu(z)
        y = _rms_norm(y, norm_w)
        return y @ out_proj_w.T

    def _L2_ffn_ref(x, ln1_g, ln1_b, ln2_g, ln2_b, Wq, Wk, Wv, Wo, Wg, W1, b1, W2, b2):
        import jax, jax.numpy as jnp
        import numpy as np
        B, S, D, H, E, F, K = (2, 256, 256, 16, 8, 1024, 2)
        EPS = 1e-05

        def _layernorm(x, g, b):
            mu = jnp.mean(x, axis=-1, keepdims=True)
            var = jnp.mean(jnp.square(x - mu), axis=-1, keepdims=True)
            return (x - mu) * jax.lax.rsqrt(var + EPS) * g + b
        Bb, Ss, Dd = x.shape
        Dh = Dd // H
        h = _layernorm(x, ln1_g, ln1_b)
        q = (h @ Wq).reshape(Bb, Ss, H, Dh)
        k = (h @ Wk).reshape(Bb, Ss, H, Dh)
        v = (h @ Wv).reshape(Bb, Ss, H, Dh)
        scores = jnp.einsum('bqhd,bkhd->bhqk', q, k) / jnp.sqrt(jnp.float32(Dh))
        attn = jax.nn.softmax(scores, axis=-1)
        ctx = jnp.einsum('bhqk,bkhd->bqhd', attn, v).reshape(Bb, Ss, Dd)
        x = x + ctx @ Wo
        m = _layernorm(x, ln2_g, ln2_b)
        xt = m.reshape(-1, Dd)
        T = xt.shape[0]
        probs = jax.nn.softmax(xt @ Wg, axis=-1)
        wts, idx = jax.lax.top_k(probs, K)
        wts = wts / jnp.sum(wts, axis=-1, keepdims=True)
        h1 = jax.nn.gelu(jnp.einsum('td,edf->etf', xt, W1) + b1[:, None, :])
        ye = jnp.einsum('etf,efd->etd', h1, W2) + b2[:, None, :]
        sel = ye[idx, jnp.arange(T)[:, None], :]
        moe_out = jnp.sum(wts[..., None] * sel, axis=1).reshape(Bb, Ss, Dd)
        return x + moe_out

    def _L3_attn_ref(x, Wq, Wk, Wv, Wg, Wgk1, Wgk2, bgk2, gamma, beta, Wout):
        import jax, jax.numpy as jnp
        import numpy as np
        HID = 256
        NH = 16
        HD = HID // NH
        RANK = 16
        B, L = (2, 512)
        Bb, Ll, Hid = x.shape
        H, Dh = (NH, HD)
        q = (x @ Wq).reshape(Bb, Ll, H, Dh)
        k = (x @ Wk).reshape(Bb, Ll, H, Dh)
        v = (x @ Wv).reshape(Bb, Ll, H, Dh)
        gk = (jax.nn.log_sigmoid(x @ Wgk1 @ Wgk2 + bgk2) / 16.0).reshape(Bb, Ll, H, Dh)
        qT = jnp.transpose(q, (1, 0, 2, 3))
        kT = jnp.transpose(k, (1, 0, 2, 3))
        vT = jnp.transpose(v, (1, 0, 2, 3))
        gT = jnp.transpose(gk, (1, 0, 2, 3))

        def step(state, inp):
            qt, kt, vt, gt = inp
            gate = jnp.exp(gt)
            state = state * gate[..., None] + vt[..., None] * kt[..., None, :]
            out_t = jnp.einsum('bhvk,bhk->bhv', state, qt)
            return (state, out_t)
        state0 = jnp.zeros((Bb, H, Dh, Dh), dtype=x.dtype)
        _, outs = jax.lax.scan(step, state0, (qT, kT, vT, gT))
        out = jnp.transpose(outs, (1, 0, 2, 3)).reshape(Bb, Ll, Hid)
        mu = out.mean(-1, keepdims=True)
        var = out.var(-1, keepdims=True)
        out = (out - mu) / jnp.sqrt(var + 1e-05) * gamma + beta
        out = out * jax.nn.silu(x @ Wg)
        return out @ Wout

    def _L3_ffn_ref(x, norm_gamma, slot_norm_gamma, slot_embeds, w1, b1, w2, b2):
        import jax, jax.numpy as jnp
        import numpy as np
        B, SEQ, DIM = (2, 1024, 256)
        E, S = (8, 128)
        HID = 4 * DIM
        SCALE = DIM ** 0.5

        def rmsnorm(x, gamma):
            n = jnp.linalg.norm(x, axis=-1, keepdims=True)
            return x / jnp.maximum(n, 1e-12) * SCALE * gamma
        xn = rmsnorm(x, norm_gamma)
        sn = rmsnorm(slot_embeds, slot_norm_gamma)
        logits = jnp.einsum('bnd,esd->bnes', xn, sn)
        dispatch = jax.nn.softmax(logits, axis=1)
        b, n, e, s = logits.shape
        combine = jax.nn.softmax(logits.reshape(b, n, e * s), axis=-1)
        slots = jnp.einsum('bnd,bnes->besd', xn, dispatch)
        h = jnp.einsum('besd,edh->besh', slots, w1) + b1[None, :, None, :]
        h = jax.nn.gelu(h, approximate=False)
        eo = jnp.einsum('besh,ehd->besd', h, w2) + b2[None, :, None, :]
        eo = eo.reshape(b, e * s, DIM)
        out = jnp.einsum('bmd,bnm->bnd', eo, combine)
        return out
    h = _L0_tok_ref(x, L0_tok_W, L0_tok_b, L0_tok_cls_token, L0_tok_pos_embed)
    h = h + _L0_attn_ref(_layernorm(h, axis=-1), L0_attn_key_w, L0_attn_key_b, L0_attn_vq_w, L0_attn_out_w, L0_attn_out_b)
    h = h + _L0_ffn_ref(_layernorm(h, axis=-1), L0_ffn_weight, L0_ffn_bias, L0_ffn_router_weight, L0_ffn_router_bias)
    h = h + _L1_attn_ref(_layernorm(h, axis=-1), L1_attn_W_DQ, L1_attn_b_DQ, L1_attn_W_UQ, L1_attn_b_UQ, L1_attn_W_DKV, L1_attn_b_DKV, L1_attn_W_UK, L1_attn_b_UK, L1_attn_W_UV, L1_attn_b_UV, L1_attn_W_QR, L1_attn_b_QR, L1_attn_W_KR, L1_attn_b_KR, L1_attn_W_O, L1_attn_b_O)
    h = h + _L1_ffn_ref(_layernorm(h, axis=-1), L1_ffn_gate_w, L1_ffn_gate_b, L1_ffn_expert_w, L1_ffn_expert_b)
    h = h + _L2_attn_ref(_layernorm(h, axis=-1), L2_attn_in_proj_w, L2_attn_conv_w, L2_attn_conv_b, L2_attn_A_log, L2_attn_D_param, L2_attn_dt_bias, L2_attn_norm_w, L2_attn_out_proj_w)
    h = h + _L2_ffn_ref(_layernorm(h, axis=-1), L2_ffn_ln1_g, L2_ffn_ln1_b, L2_ffn_ln2_g, L2_ffn_ln2_b, L2_ffn_Wq, L2_ffn_Wk, L2_ffn_Wv, L2_ffn_Wo, L2_ffn_Wg, L2_ffn_W1, L2_ffn_b1, L2_ffn_W2, L2_ffn_b2)
    h = h + _L3_attn_ref(_layernorm(h, axis=-1), L3_attn_Wq, L3_attn_Wk, L3_attn_Wv, L3_attn_Wg, L3_attn_Wgk1, L3_attn_Wgk2, L3_attn_bgk2, L3_attn_gamma, L3_attn_beta, L3_attn_Wout)
    h = h + _L3_ffn_ref(_layernorm(h, axis=-1), L3_ffn_norm_gamma, L3_ffn_slot_norm_gamma, L3_ffn_slot_embeds, L3_ffn_w1, L3_ffn_b1, L3_ffn_w2, L3_ffn_b2)
    return h

_drawn_inputs = setup_inputs


def setup_inputs(seed=0):
    import zlib

    import numpy as np

    out = dict(_drawn_inputs(seed))
    spreads = {'L0_ffn_bias': (0.0, 0.1),
     'L0_ffn_router_bias': (0.0, 0.1),
     'L1_ffn_gate_b': (0.0, 0.1),
     'L1_ffn_expert_b': (0.0, 0.1),
     'L2_attn_norm_w': (1.0, 0.2),
     'L2_ffn_ln1_g': (1.0, 0.6),
     'L2_ffn_ln1_b': (0.0, 0.8),
     'L2_ffn_ln2_g': (1.0, 0.6),
     'L2_ffn_ln2_b': (0.0, 2.0),
     'L2_ffn_b1': (0.0, 2.0),
     'L2_ffn_b2': (0.0, 1.209),
     'L3_attn_bgk2': (0.0, 2.0),
     'L3_attn_gamma': (1.0, 0.6),
     'L3_attn_beta': (0.0, 0.8),
     'L3_ffn_norm_gamma': (1.0, 0.6),
     'L3_ffn_slot_norm_gamma': (1.0, 0.6),
     'L3_ffn_b1': (0.0, 2.0),
     'L3_ffn_b2': (0.0, 0.979)}
    factors = {'L1_attn_W_DQ': 8.0,
     'L1_attn_b_DQ': 8.0,
     'L1_attn_W_UQ': 8.0,
     'L1_attn_b_UQ': 8.0,
     'L1_attn_W_DKV': 3.451,
     'L1_attn_b_DKV': 7.638,
     'L1_attn_W_UK': 8.0,
     'L1_attn_b_UK': 64.0,
     'L1_attn_W_UV': 3.35,
     'L1_attn_W_QR': 8.0,
     'L1_attn_b_QR': 8.0,
     'L1_attn_W_KR': 8.0,
     'L1_attn_b_KR': 64.0,
     'L1_attn_b_O': 5.421,
     'L2_ffn_Wq': 8.0,
     'L2_ffn_Wk': 8.0,
     'L2_ffn_Wv': 8.0,
     'L2_ffn_Wo': 8.0,
     'L3_attn_Wq': 2.864,
     'L3_attn_Wk': 2.87,
     'L3_attn_Wv': 2.805,
     'L3_attn_Wg': 3.256,
     'L3_attn_Wgk1': 35.664,
     'L3_attn_Wgk2': 34.345,
     'L3_attn_Wout': 2.814,
     'L2_ffn_W1': 4.213,
     'L3_ffn_w1': 3.568}
    for name, (base, spread) in spreads.items():
        noise = np.random.default_rng([zlib.crc32(name.encode()), seed]).standard_normal(out[name].shape)
        drawn = base * np.exp(spread * noise) if base else spread * noise
        out[name] = jnp.asarray(drawn.astype(out[name].dtype))
    for name, factor in factors.items():
        out[name] = (out[name] * factor).astype(out[name].dtype)
    return out
```

```python
from contextlib import ExitStack

import concourse.bass as bass
from concourse import mybir

F32 = mybir.dt.float32
ACT = mybir.ActivationFunctionType
ALU = mybir.AluOpType
AX = mybir.AxisListType

T = 37
SEQ = 3
ROWS = SEQ * T
TILES = 11
COLS = ROWS * TILES
NSEQ = COLS // T
THIRD = COLS // 3
D = 256
KD = D // 128
GROUPS = [(0, 4), (4, 4), (8, 3)]
LN_EPS = 1e-5


class Memory:

    def __init__(self, nc, ctx):
        self.nc, self.ctx, self.sems = nc, ctx, []
        self.h = self.sbuf(ctx, "h", [ROWS, TILES, D])
        self.xn = self.sbuf(ctx, "xn", [ROWS, TILES, D])
        self.xT = self.sbuf(ctx, "xT", [128, KD, COLS])
        self.ident = self.sbuf(ctx, "ident", [128, 128])
        self.ones = self.sbuf(ctx, "ones", [1, 128])
        self.ps = ctx.enter_context(nc.psum_tensor("ps", [128, 8, 512], F32))

    def sbuf(self, ctx, name, shape):
        return ctx.enter_context(self.nc.sbuf_tensor(name, shape, F32))

    def sem(self, name):
        self.sems.append(self.nc.alloc_semaphore(name))
        return self.sems[-1]

    def end_stage(self):
        self.nc.clear_and_free_semaphores(self.sems)
        self.nc.all_engine_barrier()
        self.sems = []


def tile_cols(t):
    return slice(t * ROWS, (t + 1) * ROWS)


def third(c):
    return slice(c * THIRD, (c + 1) * THIRD)


def constants(nc, m, dram):
    loaded = m.sem("const_loaded")
    ones_set = m.sem("const_ones")
    with nc.Block() as block:
        @block.sync
        def _(sp):
            sp.dma_start(m.ident[:, :], dram["c_ident"]).then_inc(loaded, 16)
            sp.wait_ge(loaded, 16)

        @block.vector
        def _(dve):
            nc.vector.memset(m.ones[:, :], 1.0).then_inc(ones_set, 1)
            dve.wait_ge(ones_set, 1)


def tokens(nc, m, dram):
    K = 6
    with ExitStack() as ctx:
        patches = m.sbuf(ctx, "tok_patches", [128, K, COLS])
        w = m.sbuf(ctx, "tok_w", [128, K, D])
        base = m.sbuf(ctx, "tok_base", [ROWS, D])
        pos = m.sbuf(ctx, "tok_pos", [ROWS, D])
        loaded = [m.sem(f"tok_loaded{k}") for k in range(K)]
        base_loaded = m.sem("tok_base_loaded")
        base_summed = m.sem("tok_base_summed")
        projected = m.sem("tok_projected")
        stored = m.sem("tok_stored")
        with nc.Block() as block:
            @block.sync
            def _(sp):
                for k in range(K):
                    sp.dma_start(patches[:, k, :], dram["patchesT"][k * 128:(k + 1) * 128, :]).then_inc(loaded[k], 16)
                    sp.dma_start(w[:, k, :], dram["tok_wT"][k * 128:(k + 1) * 128, :]).then_inc(loaded[k], 16)
                sp.dma_start(base[:, :], dram["tok_base"]).then_inc(base_loaded, 16)
                sp.dma_start(pos[:, :], dram["tok_pos"]).then_inc(base_loaded, 16)

            @block.tensor
            def _(pe):
                for t in range(TILES):
                    if t >= 4:
                        pe.wait_ge(stored, t - 3)
                    for k in range(K):
                        if t == 0:
                            pe.wait_ge(loaded[k], 32)
                        mm = nc.tensor.matmul(m.ps[:ROWS, t % 4, :D], patches[:, k, tile_cols(t)], w[:, k, :],
                                              start=(k == 0), stop=(k == K - 1))
                    mm.then_inc(projected, 1)

            @block.vector
            def _(dve):
                dve.wait_ge(base_loaded, 32)
                nc.vector.tensor_tensor(base[:, :], base[:, :], pos[:, :], ALU.add).then_inc(base_summed, 1)
                dve.wait_ge(base_summed, 1)
                for t in range(TILES):
                    dve.wait_ge(projected, t + 1)
                    nc.vector.tensor_tensor(m.h[:, t, :], m.ps[:ROWS, t % 4, :D], base[:, :],
                                            ALU.add).then_inc(stored, 1)


def normalise(nc, m, name, src, tok=None, dstT=None, eps=LN_EPS, affine=None, turn=True):
    tok = m.xn if tok is None else tok
    dstT = m.xT if dstT is None else dstT
    with ExitStack() as ctx:
        stats = m.sbuf(ctx, name + "_stats", [ROWS, TILES, 6])
        mv = m.sbuf(ctx, name + "_mv", [ROWS, TILES, 2])
        std = m.sbuf(ctx, name + "_std", [ROWS, TILES])
        rstd = m.sbuf(ctx, name + "_rstd", [ROWS, TILES])
        gb = m.sbuf(ctx, name + "_gb", [128, 2, KD])
        counted = m.sem(name + "_counted")
        varred = m.sem(name + "_var")
        rooted = m.sem(name + "_rooted")
        inverted = m.sem(name + "_inverted")
        centred = m.sem(name + "_centred")
        turned = m.sem(name + "_turned")
        kept = m.sem(name + "_kept")
        gb_loaded = m.sem(name + "_gb_loaded")
        with nc.Block() as block:
            @block.sync
            def _(sp):
                if affine is not None:
                    sp.dma_start(gb[:, :, :], affine).then_inc(gb_loaded, 16)

            @block.vector
            def _(dve):
                for t in range(TILES):
                    nc.vector.bn_stats(stats[:, t, :], src[:, t, :]).then_inc(counted, 1)
                for t in range(TILES):
                    dve.wait_ge(counted, t + 1)
                    nc.vector.bn_aggr(mv[:, t, :], stats[:, t, :]).then_inc(varred, 1)
                dve.wait_ge(varred, TILES)
                nc.vector.tensor_scalar(std[:, :], mv[:, :, 1], eps, None, ALU.add).then_inc(varred, 1)
                dve.wait_ge(rooted, 1)
                nc.vector.reciprocal(rstd[:, :], std[:, :]).then_inc(inverted, 1)
                dve.wait_ge(inverted, 1)
                for t in range(TILES):
                    nc.vector.tensor_scalar(tok[:, t, :], src[:, t, :], mv[:, t, 0:1], rstd[:, t:t + 1],
                                            ALU.subtract, ALU.mult).then_inc(centred, 1)

            @block.scalar
            def _(act):
                act.wait_ge(varred, TILES + 1)
                nc.scalar.activation(std[:, :], std[:, :], ACT.Sqrt).then_inc(rooted, 1)
                if affine is not None:
                    act.wait_ge(gb_loaded, 16)
                for g, (t0, n) in enumerate(GROUPS if turn else []):
                    for k in range(KD):
                        i = g * KD + k
                        act.wait_ge(turned, i + 1)
                        out = dstT[:, k, t0 * ROWS:(t0 + n) * ROWS]
                        if affine is None:
                            nc.scalar.activation(out, m.ps[:, i, :n * ROWS], ACT.Copy).then_inc(kept, 1)
                        else:
                            nc.scalar.activation(out, m.ps[:, i, :n * ROWS], ACT.Identity, scale=gb[:, 0, k:k + 1],
                                                 bias=gb[:, 1, k:k + 1]).then_inc(kept, 1)

            @block.tensor
            def _(pe):
                for g, (t0, n) in enumerate(GROUPS if turn else []):
                    pe.wait_ge(centred, t0 + n)
                    for k in range(KD):
                        for j in range(n):
                            mm = nc.tensor.transpose(m.ps[:, g * KD + k, j * ROWS:(j + 1) * ROWS],
                                                     tok[:, t0 + j, k * 128:(k + 1) * 128], m.ident[:ROWS, :ROWS])
                        mm.then_inc(turned, 1)


def decayed_sums(nc, m, dram):
    H, DH = 16, 16
    with ExitStack() as ctx:
        wk = m.sbuf(ctx, "l0a_wk", [128, KD, D])
        wv = m.sbuf(ctx, "l0a_wv", [128, KD, 2 * D])
        wo = m.sbuf(ctx, "l0a_wo", [128, KD, D])
        kb = m.sbuf(ctx, "l0a_kb", [128, KD])
        ob = m.sbuf(ctx, "l0a_ob", [1, D])
        spread = m.sbuf(ctx, "l0a_spread", [128, DH, 128])
        gather = m.sbuf(ctx, "l0a_gather", [128, DH, 128])
        kT = m.sbuf(ctx, "l0a_kT", [128, KD, COLS])
        omk = m.sbuf(ctx, "l0a_omk", [128, KD, COLS])
        vT = m.sbuf(ctx, "l0a_vT", [128, KD, COLS])
        qT = m.sbuf(ctx, "l0a_qT", [128, KD, COLS])
        upd = m.sbuf(ctx, "l0a_upd", [128, 2, COLS])
        state = m.sbuf(ctx, "l0a_state", [128, 2, COLS])
        read = m.sbuf(ctx, "l0a_read", [128, 2, COLS])
        oT = m.sbuf(ctx, "l0a_oT", [128, KD, COLS])
        w_loaded = m.sem("l0a_w_loaded")
        c_loaded = m.sem("l0a_c_loaded")
        projected = m.sem("l0a_projected")
        kept = m.sem("l0a_kept")
        complemented = m.sem("l0a_complemented")
        cut = m.sem("l0a_cut")
        spread_done = m.sem("l0a_spread_done")
        updated = m.sem("l0a_updated")
        scanned = m.sem("l0a_scanned")
        was_read = m.sem("l0a_was_read")
        gathered = m.sem("l0a_gathered")
        o_kept = m.sem("l0a_o_kept")
        out_done = m.sem("l0a_out_done")
        added = m.sem("l0a_added")
        jobs = [(wk, 0, kT, 0), (wk, 128, kT, 1), (wv, 0, vT, 0), (wv, 128, vT, 1), (wv, 256, qT, 0), (wv, 384, qT, 1)]
        STEPS = KD * DH
        with nc.Block() as block:
            @block.sync
            def _(sp):
                sp.dma_start(wk[:, :, :], dram["l0a_kwT"].rearrange("(k p) n -> p k n", p=128)).then_inc(w_loaded, 16)
                sp.dma_start(wv[:, :, :], dram["l0a_vqT"].rearrange("(k p) n -> p k n", p=128)).then_inc(w_loaded, 16)
                sp.dma_start(kb[:, :], dram["l0a_kb"]).then_inc(w_loaded, 16)
                sp.dma_start(spread[:, :, :], dram["c_spread"]).then_inc(c_loaded, 16)
                sp.dma_start(gather[:, :, :], dram["c_gather"]).then_inc(c_loaded, 16)
                sp.dma_start(wo[:, :, :], dram["l0a_owT"].rearrange("(k p) n -> p k n", p=128)).then_inc(c_loaded, 16)
                sp.dma_start(ob[:, :], dram["l0a_ob"]).then_inc(c_loaded, 16)

            @block.tensor
            def _(pe):
                pe.wait_ge(w_loaded, 48)
                for j, (w, col, _, _) in enumerate(jobs):
                    if j >= 2:
                        pe.wait_ge(kept, j - 1)
                    for c in range(3):
                        for k in range(KD):
                            mm = nc.tensor.matmul(m.ps[:, 3 * (j % 2) + c, :THIRD], w[:, k, col:col + 128],
                                                  m.xT[:, k, third(c)], start=(k == 0), stop=(k == KD - 1))
                    mm.then_inc(projected, 1)
                pe.wait_ge(kept, len(jobs))
                pe.wait_ge(c_loaded, 64)

                def sum_up(i):
                    pe.wait_ge(was_read, i + 1)
                    if i == DH:
                        pe.wait_ge(o_kept, 3)
                    for c in range(3):
                        mm = nc.tensor.matmul(m.ps[:, 5 + c, :THIRD], gather[:, i % DH, :], read[:, i % 2, third(c)],
                                              start=(i % DH == 0), stop=(i % DH == DH - 1), skip_group_check=True)
                    mm.then_inc(gathered, 1)

                for i in range(STEPS):
                    for c in range(3):
                        n = 3 * i + c
                        if n >= 5:
                            pe.wait_ge(updated, n - 4)
                        nc.tensor.matmul(m.ps[:, n % 5, :THIRD], spread[:, i % DH, :], vT[:, i // DH, third(c)],
                                         start=True, stop=True).then_inc(spread_done, 1)
                    if i >= 1:
                        sum_up(i - 1)
                sum_up(STEPS - 1)
                pe.wait_ge(o_kept, 6)
                for t in range(TILES):
                    if t >= 4:
                        pe.wait_ge(added, t - 3)
                    for k in range(KD):
                        nc.tensor.matmul(m.ps[:ROWS, t % 4, :D], oT[:, k, tile_cols(t)], wo[:, k, :],
                                         start=(k == 0), stop=False)
                    nc.tensor.matmul(m.ps[:ROWS, t % 4, :D], m.ones[:, :ROWS], ob[:, :],
                                     start=False, stop=True).then_inc(out_done, 1)

            @block.scalar
            def _(act):
                for j, (_, _, dst, k) in enumerate(jobs):
                    act.wait_ge(projected, j + 1)
                    src = m.ps[:, 3 * (j % 2):3 * (j % 2) + 3, :THIRD]
                    out = dst[:, k, :].rearrange("p (c n) -> p c n", c=3)
                    if dst is kT:
                        nc.scalar.activation(out, src, ACT.Sigmoid, bias=kb[:, k:k + 1]).then_inc(kept, 1)
                    else:
                        nc.scalar.activation(out, src, ACT.Copy).then_inc(kept, 1)
                for k in range(KD):
                    act.wait_ge(gathered, DH * (k + 1))
                    for c in range(3):
                        nc.scalar.activation(oT[:, k, third(c)], m.ps[:, 5 + c, :THIRD], ACT.Copy).then_inc(o_kept, 1)

            @block.vector
            def _(dve):
                for k in range(KD):
                    dve.wait_ge(kept, k + 1)
                    nc.vector.tensor_scalar(omk[:, k, :], kT[:, k, :], -1.0, 1.0, ALU.mult,
                                            ALU.add).then_inc(complemented, 1)
                    dve.wait_ge(complemented, k + 1)
                    nc.vector.memset(kT[:, k, 0:COLS:T], 0.0).then_inc(cut, 1)
                dve.wait_ge(cut, 2)
                for i in range(STEPS):
                    if i >= 2:
                        dve.wait_ge(scanned, i - 1)
                    for c in range(3):
                        dve.wait_ge(spread_done, 3 * i + c + 1)
                        nc.vector.tensor_tensor(upd[:, i % 2, third(c)], m.ps[:, (3 * i + c) % 5, :THIRD],
                                                omk[:, i // DH, third(c)], ALU.mult).then_inc(updated, 1)
                    dve.wait_ge(updated, 3 * i + 3)
                    if i >= 2:
                        dve.wait_ge(was_read, i - 1)
                    nc.vector.tensor_tensor_scan(state[:, i % 2, :], kT[:, i // DH, :], upd[:, i % 2, :], 0.0,
                                                 ALU.mult, ALU.add).then_inc(scanned, 1)
                for t in range(TILES):
                    dve.wait_ge(out_done, t + 1)
                    nc.vector.tensor_tensor(m.h[:, t, :], m.ps[:ROWS, t % 4, :D], m.h[:, t, :],
                                            ALU.add).then_inc(added, 1)

            @block.gpsimd
            def _(pool):
                pool.wait_ge(kept, 6)
                for i in range(STEPS):
                    pool.wait_ge(scanned, i + 1)
                    if i >= 2:
                        pool.wait_ge(gathered, i - 1)
                    nc.gpsimd.tensor_tensor(read[:, i % 2, :], state[:, i % 2, :], qT[:, i // DH, :],
                                            ALU.mult).then_inc(was_read, 1)


def gate(nc, m, name, gw, gb, E, wts, wtsT, weighted):
    PAD = 6
    with ExitStack() as ctx:
        w = m.sbuf(ctx, name + "_gw", [128, KD, E])
        b = m.sbuf(ctx, name + "_gb", [1, E])
        mx = m.sbuf(ctx, name + "_mx", [ROWS, TILES])
        ex = m.sbuf(ctx, name + "_ex", [ROWS, TILES, E])
        den = m.sbuf(ctx, name + "_den", [ROWS, TILES])
        pr = m.sbuf(ctx, name + "_pr", [ROWS, TILES, E + PAD])
        rest = m.sbuf(ctx, name + "_rest", [ROWS, TILES, E + PAD])
        top = m.sbuf(ctx, name + "_top", [ROWS, TILES, 8])
        loaded = m.sem(name + "_loaded")
        scored = m.sem(name + "_scored")
        step = m.sem(name + "_dve_step")
        shifted = m.sem(name + "_shifted")
        expd = m.sem(name + "_expd")
        weighed = m.sem(name + "_weighed")
        turned = m.sem(name + "_turned")
        kept = m.sem(name + "_kept")
        logits = m.ps[:ROWS, 0, :TILES * E].rearrange("p (t e) -> p t e", e=E)

        def over_e(x, n):
            return x[:, :].rearrange("p (t o) -> p t o", o=1).broadcast_to([ROWS, TILES, n])

        with nc.Block() as block:
            @block.sync
            def _(sp):
                sp.dma_start(w[:, :, :], gw.rearrange("(k p) n -> p k n", p=128)).then_inc(loaded, 16)
                sp.dma_start(b[:, :], gb).then_inc(loaded, 16)

            @block.tensor
            def _(pe):
                pe.wait_ge(loaded, 32)
                for t in range(TILES):
                    for k in range(KD):
                        nc.tensor.matmul(logits[:, t, :], m.xT[:, k, tile_cols(t)], w[:, k, :],
                                         start=(k == 0), stop=False)
                    mm = nc.tensor.matmul(logits[:, t, :], m.ones[:, :ROWS], b[:, :], start=False, stop=True)
                mm.then_inc(scored, 1)
                pe.wait_ge(weighed, 1)
                for g, (t0, n) in enumerate(GROUPS):
                    for j in range(n):
                        mm = nc.tensor.transpose(m.ps[:8, 1 + g, j * ROWS:(j + 1) * ROWS], wts[:, t0 + j, :],
                                                 m.ident[:ROWS, :ROWS])
                    mm.then_inc(turned, 1)

            @block.scalar
            def _(act):
                act.wait_ge(shifted, 1)
                nc.scalar.activation(ex[:, :, :], ex[:, :, :], ACT.Exp).then_inc(expd, 1)
                for g, (t0, n) in enumerate(GROUPS):
                    act.wait_ge(turned, g + 1)
                    nc.scalar.activation(wtsT[:, t0 * ROWS:(t0 + n) * ROWS], m.ps[:8, 1 + g, :n * ROWS],
                                         ACT.Copy).then_inc(kept, 1)

            @block.vector
            def _(dve):
                done = [0]

                def link(ins):
                    done[0] += 1
                    ins.then_inc(step, 1)
                    dve.wait_ge(step, done[0])

                dve.wait_ge(scored, 1)
                nc.vector.memset(pr[:, :, E:], -1.0).then_inc(step, 1)
                done[0] += 1
                link(nc.vector.tensor_reduce(mx[:, :], logits, AX.X, ALU.max))
                nc.vector.tensor_tensor(ex[:, :, :], logits, over_e(mx, E), ALU.subtract).then_inc(shifted, 1)
                dve.wait_ge(expd, 1)
                link(nc.vector.tensor_reduce(den[:, :], ex[:, :, :], AX.X, ALU.add))
                link(nc.vector.reciprocal(den[:, :], den[:, :]))
                link(nc.vector.tensor_tensor(pr[:, :, :E], ex[:, :, :], over_e(den, E), ALU.mult))
                for t in range(TILES):
                    ins = nc.vector.max(top[:, t, :], pr[:, t, :E])
                link(ins)
                link(nc.vector.memset(top[:, :, 2:], -1.0))
                for t in range(TILES):
                    ins = nc.vector.match_replace(rest[:, t, :], top[:, t, :], pr[:, t, :], -2.0)
                link(ins)
                if not weighted:
                    nc.vector.tensor_tensor(wts[:, :, :], pr[:, :, :8], rest[:, :, :8], ALU.is_gt).then_inc(weighed, 1)
                    return
                link(nc.vector.tensor_tensor(ex[:, :, :8], pr[:, :, :8], rest[:, :, :8], ALU.is_gt))
                link(nc.vector.tensor_tensor(ex[:, :, :8], ex[:, :, :8], pr[:, :, :8], ALU.mult))
                link(nc.vector.tensor_reduce(den[:, :], ex[:, :, :8], AX.X, ALU.add))
                link(nc.vector.scalar_tensor_tensor(mx[:, :], den[:, :], 0.0, den[:, :], ALU.is_le, ALU.add))
                link(nc.vector.reciprocal(den[:, :], mx[:, :]))
                nc.vector.tensor_tensor(wts[:, :, :], ex[:, :, :8], over_e(den, 8), ALU.mult).then_inc(weighed, 1)


def small_experts(nc, m, name, ew, eb, wts, wtsT):
    E = 8
    with ExitStack() as ctx:
        w = m.sbuf(ctx, name + "_w", [128, KD, E, D])
        b = m.sbuf(ctx, name + "_b", [E, D])
        loaded = m.sem(name + "_loaded")
        multiplied = m.sem(name + "_multiplied")
        biased = m.sem(name + "_biased")
        added = m.sem(name + "_added")
        with nc.Block() as block:
            @block.sync
            def _(sp):
                for e in range(E):
                    sp.dma_start(w[:, :, e, :], ew[e].rearrange("(k p) n -> p k n", p=128)).then_inc(loaded, 16)
                sp.dma_start(b[:, :], eb).then_inc(loaded, 16)

            @block.tensor
            def _(pe):
                pe.wait_ge(loaded, 16 * (E + 1))
                for t in range(TILES):
                    if t >= 2:
                        pe.wait_ge(added, 9 * (t - 1) - 8)
                    nc.tensor.matmul(m.ps[:ROWS, 6 + t % 2, :D], wtsT[:, tile_cols(t)], b[:, :],
                                     start=True, stop=True).then_inc(biased, 1)
                    for p in range(E // 2):
                        i = t * (E // 2) + p
                        if i >= 6:
                            j = i - 6
                            pe.wait_ge(added, 9 * (j // 4) + 1 + 2 * (j % 4 + 1))
                        for k in range(KD):
                            mm = nc.tensor.matmul(m.ps[:ROWS, i % 6, :], m.xT[:, k, tile_cols(t)],
                                                  w[:, k, 2 * p:2 * p + 2, :], start=(k == 0), stop=(k == KD - 1))
                        mm.then_inc(multiplied, 1)

            @block.vector
            def _(dve):
                for t in range(TILES):
                    dve.wait_ge(biased, t + 1)
                    nc.vector.tensor_tensor(m.h[:, t, :], m.ps[:ROWS, 6 + t % 2, :D], m.h[:, t, :],
                                            ALU.add).then_inc(added, 1)
                    for e in range(E):
                        i = t * (E // 2) + e // 2
                        if e % 2 == 0:
                            dve.wait_ge(multiplied, i + 1)
                        dve.wait_ge(added, 9 * t + e + 1)
                        nc.vector.scalar_tensor_tensor(m.h[:, t, :], m.ps[:ROWS, i % 6, (e % 2) * D:(e % 2 + 1) * D],
                                                       wts[:, t, e:e + 1], m.h[:, t, :], ALU.mult,
                                                       ALU.add).then_inc(added, 1)


def selecting_experts(nc, m, dram, name, E, weighted):
    with ExitStack() as ctx:
        wts = m.sbuf(ctx, name + "_wts", [ROWS, TILES, 8])
        wtsT = m.sbuf(ctx, name + "_wtsT", [8, COLS])
        gate(nc, m, name + "g", dram[name + "_gwT"], dram[name + "_gb"], E, wts, wtsT, weighted)
        small_experts(nc, m, name + "e", dram[name + "_ew"], dram[name + "_eb"], wts, wtsT)


STAGE = {
    0: tokens,
    1: lambda nc, m, dram: (normalise(nc, m, "l0a_ln", m.h), decayed_sums(nc, m, dram)),
    2: lambda nc, m, dram: (normalise(nc, m, "l0f_ln", m.h), selecting_experts(nc, m, dram, "l0f", 8, False)),
    4: lambda nc, m, dram: (normalise(nc, m, "l1f_ln", m.h), selecting_experts(nc, m, dram, "l1f", 10, True)),
}
class MaskedSoftmax:

    N = 4 * ROWS

    def __init__(self, nc, m, name, ctx, mask_dram, scale):
        self.nc, self.m, self.scale, self.mask_dram = nc, m, scale, mask_dram
        self.mask = m.sbuf(ctx, name + "_mask", [ROWS, self.N])
        self.scores = m.sbuf(ctx, name + "_scores", [ROWS, 3, self.N])
        self.turnedP = m.sbuf(ctx, name + "_turnedP", [ROWS, 2, self.N])
        self.mx = m.sbuf(ctx, name + "_mx", [ROWS, 3, 4])
        self.den = m.sbuf(ctx, name + "_den", [ROWS, 3, 4])
        self.mask_loaded = m.sem(name + "_mask_loaded")
        self.scored = m.sem(name + "_scored")
        self.masked = m.sem(name + "_masked")
        self.max_found = m.sem(name + "_max_found")
        self.shifted = m.sem(name + "_shifted")
        self.expd = m.sem(name + "_expd")
        self.summed = m.sem(name + "_summed")
        self.inverted = m.sem(name + "_inverted")
        self.normed = m.sem(name + "_normed")
        self.turned = m.sem(name + "_turned")
        self.kept = m.sem(name + "_kept")
        self.used = m.sem(name + "_used")

    def by_head(self, x):
        return x.rearrange("p (g n) -> p g n", g=4)

    def spread(self, x):
        return x.rearrange("p (g o) -> p g o", o=1).broadcast_to([ROWS, 4, ROWS])

    def load_mask(self, sp):
        sp.dma_start(self.mask[:, :], self.mask_dram).then_inc(self.mask_loaded, 16)

    def vector_mask(self, dve, i):
        dve.wait_ge(self.scored, i + 1)
        if i >= 3:
            dve.wait_ge(self.turned, i - 2)
        self.nc.vector.scalar_tensor_tensor(self.scores[:, i % 3, :], self.m.ps[:ROWS, i % 2, :self.N], self.scale,
                                            self.mask[:, :], ALU.mult, ALU.add).then_inc(self.masked, 1)
        dve.wait_ge(self.masked, i + 1)
        if i >= 3:
            dve.wait_ge(self.shifted, i - 2)
        self.nc.vector.tensor_reduce(self.mx[:, i % 3, :], self.by_head(self.scores[:, i % 3, :]), AX.X,
                                     ALU.max).then_inc(self.max_found, 1)

    def vector_sum(self, dve, i):
        x = self.by_head(self.scores[:, i % 3, :])
        dve.wait_ge(self.expd, i + 1)
        if i >= 3:
            dve.wait_ge(self.normed, i - 2)
        self.nc.vector.tensor_reduce(self.den[:, i % 3, :], x, AX.X, ALU.add).then_inc(self.summed, 1)
        dve.wait_ge(self.summed, i + 1)
        self.nc.vector.reciprocal(self.den[:, i % 3, :], self.den[:, i % 3, :]).then_inc(self.inverted, 1)
        dve.wait_ge(self.inverted, i + 1)
        self.nc.vector.tensor_tensor(x, x, self.spread(self.den[:, i % 3, :]), ALU.mult).then_inc(self.normed, 1)

    def scalar_exp(self, act, i):
        act.wait_ge(self.shifted, i + 1)
        self.nc.scalar.activation(self.scores[:, i % 3, :], self.scores[:, i % 3, :], ACT.Exp).then_inc(self.expd, 1)

    def scalar_keep(self, act, i, used):
        act.wait_ge(self.turned, i + 1)
        if i >= 2:
            act.wait_ge(used, i - 1)
        self.nc.scalar.activation(self.turnedP[:, i % 2, :], self.m.ps[:ROWS, 2 + i % 2, :self.N],
                                  ACT.Copy).then_inc(self.kept, 1)

    def pool_shift(self, pool, i):
        x = self.by_head(self.scores[:, i % 3, :])
        pool.wait_ge(self.max_found, i + 1)
        self.nc.gpsimd.tensor_tensor(x, x, self.spread(self.mx[:, i % 3, :]), ALU.subtract).then_inc(self.shifted, 1)

    def tensor_turn(self, pe, i):
        pe.wait_ge(self.normed, i + 1)
        if i >= 2:
            pe.wait_ge(self.kept, i - 1)
        for j in range(4):
            own = slice(j * ROWS, (j + 1) * ROWS)
            mm = self.nc.tensor.transpose(self.m.ps[:ROWS, 2 + i % 2, own], self.scores[:, i % 3, own],
                                          self.m.ident[:ROWS, :ROWS])
        mm.then_inc(self.turned, 1)


def latent_attention(nc, m, dram):
    H, DK, DC = 8, 128, 32
    scale = float((DK + DC) ** -0.5)
    names = ("DQ", "DKV", "KR")
    with ExitStack() as ctx:
        wd = [m.sbuf(ctx, "l1a_wd" + n, [128, KD, DC]) for n in names]
        bd = [m.sbuf(ctx, "l1a_bd" + n, [DC, 1]) for n in names]
        latent = [m.sbuf(ctx, "l1a_latent" + n, [DC, COLS]) for n in names]
        wuq = m.sbuf(ctx, "l1a_wuq", [DC, H * DK])
        wuk = m.sbuf(ctx, "l1a_wuk", [DC, H * DK])
        wuv = m.sbuf(ctx, "l1a_wuv", [DC, H * DK])
        wqr = m.sbuf(ctx, "l1a_wqr", [DC, H * DC])
        buq = m.sbuf(ctx, "l1a_buq", [128, H])
        buk = m.sbuf(ctx, "l1a_buk", [128, H])
        buv = m.sbuf(ctx, "l1a_buv", [1, H * DK])
        bqr = m.sbuf(ctx, "l1a_bqr", [DC, H])
        wo = m.sbuf(ctx, "l1a_wo", [128, H, D])
        bo = m.sbuf(ctx, "l1a_bo", [1, D])
        q = m.sbuf(ctx, "l1a_q", [128, H, 2, 4 * ROWS])
        k = m.sbuf(ctx, "l1a_k", [128, H, 2, 4 * ROWS])
        qr = m.sbuf(ctx, "l1a_qr", [DC, H, 2, 4 * ROWS])
        v = m.sbuf(ctx, "l1a_v", [ROWS, 2, H * DK])
        oT = m.sbuf(ctx, "l1a_oT", [128, 2, H, ROWS])
        sm = MaskedSoftmax(nc, m, "l1a_sm", ctx, dram["c_mask"], scale)
        loaded = m.sem("l1a_loaded")
        o_loaded = m.sem("l1a_o_loaded")
        compressed = m.sem("l1a_compressed")
        latent_kept = m.sem("l1a_latent_kept")
        expanded = m.sem("l1a_expanded")
        kept = m.sem("l1a_kept")
        v_made = m.sem("l1a_v_made")
        v_kept = m.sem("l1a_v_kept")
        mixed = m.sem("l1a_mixed")
        mix_kept = m.sem("l1a_mix_kept")
        out_done = m.sem("l1a_out_done")
        added = m.sem("l1a_added")
        ITEMS = TILES * 2
        EXP = 3 * H

        with nc.Block() as block:
            @block.sync
            def _(sp):
                for i, n in enumerate(names):
                    sp.dma_start(wd[i][:, :, :], dram["l1a_w" + n].rearrange("(k p) n -> p k n", p=128)).then_inc(loaded, 16)
                    sp.dma_start(bd[i][:, :], dram["l1a_b" + n]).then_inc(loaded, 16)
                for t, n in ((wuq, "wUQ"), (wuk, "wUK"), (wuv, "wUV"), (wqr, "wQR"), (buq, "bUQ"), (buk, "bUK"),
                             (buv, "bUV"), (bqr, "bQR")):
                    sp.dma_start(t[:, :], dram["l1a_" + n]).then_inc(loaded, 16)
                sm.load_mask(sp)
                sp.dma_start(wo[:, :, :], dram["l1a_wO"].rearrange("(k p) n -> p k n", p=128)).then_inc(o_loaded, 16)
                sp.dma_start(bo[:, :], dram["l1a_bO"]).then_inc(o_loaded, 16)

            @block.tensor
            def _(pe):
                pe.wait_ge(loaded, 16 * 14)
                for i in range(3):
                    for c in range(3):
                        n = 3 * i + c
                        if n >= 8:
                            pe.wait_ge(latent_kept, n - 7)
                        for kk in range(KD):
                            mm = nc.tensor.matmul(m.ps[:DC, n % 8, :THIRD], wd[i][:, kk, :], m.xT[:, kk, third(c)],
                                                  start=(kk == 0), stop=(kk == KD - 1))
                        mm.then_inc(compressed, 1)
                pe.wait_ge(latent_kept, 9)

                def expand(g):
                    t0, n = GROUPS[g]
                    cols = slice(t0 * ROWS, (t0 + n) * ROWS)
                    for h in range(H):
                        for j, (w, src, M) in enumerate(((wuq, 0, DK), (wuk, 1, DK), (wqr, 0, DC))):
                            i = g * EXP + 3 * h + j
                            if i >= 2:
                                pe.wait_ge(kept, i - 1)
                            nc.tensor.matmul(m.ps[:M, 4 + i % 2, :n * ROWS], w[:, h * M:(h + 1) * M],
                                             latent[src][:, cols], start=True, stop=True).then_inc(expanded, 1)

                def values(t):
                    for j in range(2):
                        i = 2 * t + j
                        if i >= 2:
                            pe.wait_ge(v_kept, i - 1)
                        if t >= 1:
                            pe.wait_ge(mix_kept, 2 * t)
                            pe.wait_ge(added, t)
                        nc.tensor.matmul(m.ps[:ROWS, 6 + j, :], latent[1][:, tile_cols(t)],
                                         wuv[:, j * 512:(j + 1) * 512], start=True, stop=False)
                        nc.tensor.matmul(m.ps[:ROWS, 6 + j, :], m.ones[:, :ROWS], buv[:, j * 512:(j + 1) * 512],
                                         start=False, stop=True).then_inc(v_made, 1)

                def scores(i):
                    t, half = i // 2, i % 2
                    g, r = t // 4, t % 4
                    if i >= 2:
                        pe.wait_ge(sm.masked, i - 1)
                    pe.wait_ge(kept, (g + 1) * EXP)
                    own = slice(r * ROWS, (r + 1) * ROWS)
                    for j in range(4):
                        h = half * 4 + j
                        out = m.ps[:ROWS, i % 2, j * ROWS:(j + 1) * ROWS]
                        nc.tensor.matmul(out, q[:, h, g % 2, own], k[:, h, g % 2, own], start=True, stop=False)
                        mm = nc.tensor.matmul(out, qr[:, h, g % 2, own], latent[2][:, tile_cols(t)],
                                              start=False, stop=True)
                    mm.then_inc(sm.scored, 1)

                def mix(i):
                    t, half = i // 2, i % 2
                    pe.wait_ge(sm.kept, i + 1)
                    pe.wait_ge(v_kept, 2 * t + 2)
                    if half == 0 and t >= 1:
                        pe.wait_ge(mix_kept, 2 * t)
                    for j in range(4):
                        h = half * 4 + j
                        mm = nc.tensor.matmul(m.ps[:, 6, j * ROWS:(j + 1) * ROWS] if half == 0 else
                                              m.ps[:, 7, j * ROWS:(j + 1) * ROWS],
                                              v[:, t % 2, h * DK:(h + 1) * DK], sm.turnedP[:, i % 2, j * ROWS:(j + 1) * ROWS],
                                              start=True, stop=True)
                    mm.then_inc(mixed, 1)

                def output(t):
                    pe.wait_ge(mix_kept, 2 * t + 2)
                    if t == 0:
                        pe.wait_ge(o_loaded, 32)
                    for h in range(H):
                        nc.tensor.matmul(m.ps[:ROWS, 6, :D], oT[:, t % 2, h, :], wo[:, h, :], start=(h == 0), stop=False)
                    nc.tensor.matmul(m.ps[:ROWS, 6, :D], m.ones[:, :ROWS], bo[:, :], start=False,
                                     stop=True).then_inc(out_done, 1)

                expand(0)
                for i in range(ITEMS + 2):
                    if i < ITEMS:
                        if i % 8 == 2 and i // 8 + 1 < len(GROUPS):
                            expand(i // 8 + 1)
                        scores(i)
                    if 1 <= i <= ITEMS:
                        sm.tensor_turn(pe, i - 1)
                    if i >= 2:
                        if i % 2 == 0:
                            values(i // 2 - 1)
                        mix(i - 2)
                        if i % 2 == 1:
                            output((i - 3) // 2)

            @block.scalar
            def _(act):
                for i in range(3):
                    for c in range(3):
                        n = 3 * i + c
                        act.wait_ge(compressed, n + 1)
                        nc.scalar.activation(latent[i][:, third(c)], m.ps[:DC, n % 8, :THIRD], ACT.Identity,
                                             bias=bd[i][:, 0:1]).then_inc(latent_kept, 1)

                def keep(g):
                    t0, n = GROUPS[g]
                    if g >= 2:
                        act.wait_ge(sm.scored, 2 * 4 * (g - 1))
                    for h in range(H):
                        for j, (dst, b, M) in enumerate(((q, buq, DK), (k, buk, DK), (qr, bqr, DC))):
                            i = g * EXP + 3 * h + j
                            act.wait_ge(expanded, i + 1)
                            nc.scalar.activation(dst[:, h, g % 2, :n * ROWS], m.ps[:M, 4 + i % 2, :n * ROWS],
                                                 ACT.Identity, bias=b[:, h:h + 1]).then_inc(kept, 1)

                keep(0)
                for i in range(ITEMS + 2):
                    if i < ITEMS:
                        if i % 8 == 2 and i // 8 + 1 < len(GROUPS):
                            keep(i // 8 + 1)
                        sm.scalar_exp(act, i)
                    if 1 <= i <= ITEMS:
                        sm.scalar_keep(act, i - 1, mixed)
                    if i >= 2:
                        t, half = (i - 2) // 2, i % 2
                        if half == 0:
                            for j in range(2):
                                act.wait_ge(v_made, 2 * t + j + 1)
                                if t >= 2:
                                    act.wait_ge(mixed, 2 * (t - 1))
                                nc.scalar.activation(v[:, t % 2, j * 512:(j + 1) * 512], m.ps[:ROWS, 6 + j, :],
                                                     ACT.Copy).then_inc(v_kept, 1)
                        act.wait_ge(mixed, i - 1)
                        if t >= 2:
                            act.wait_ge(out_done, t - 1)
                        nc.scalar.activation(oT[:, t % 2, 4 * half:4 * half + 4, :],
                                             m.ps[:, 6 + half, :4 * ROWS].rearrange("p (g n) -> p g n", g=4),
                                             ACT.Copy).then_inc(mix_kept, 1)

            @block.vector
            def _(dve):
                dve.wait_ge(sm.mask_loaded, 16)
                for i in range(ITEMS + 2):
                    if i < ITEMS:
                        sm.vector_mask(dve, i)
                    if 1 <= i <= ITEMS:
                        sm.vector_sum(dve, i - 1)
                    if i >= 3 and i % 2 == 1:
                        t = (i - 3) // 2
                        dve.wait_ge(out_done, t + 1)
                        nc.vector.tensor_tensor(m.h[:, t, :], m.ps[:ROWS, 6, :D], m.h[:, t, :],
                                                ALU.add).then_inc(added, 1)

            @block.gpsimd
            def _(pool):
                for i in range(ITEMS):
                    sm.pool_shift(pool, i)


STAGE[3] = lambda nc, m, dram: (normalise(nc, m, "l1a_ln", m.h), latent_attention(nc, m, dram))
def state_space(nc, m, dram):
    H, NS, DI = 8, 64, 512
    KI = DI // 128
    TAPS = 4
    with ExitStack() as ctx:
        wz = m.sbuf(ctx, "l2a_wz", [128, KD, DI])
        wx = m.sbuf(ctx, "l2a_wx", [128, KD, DI])
        wdt = m.sbuf(ctx, "l2a_wdt", [128, KD, H])
        wB = m.sbuf(ctx, "l2a_wB", [128, KD, NS])
        wC = m.sbuf(ctx, "l2a_wC", [128, KD, NS])
        conv_w = m.sbuf(ctx, "l2a_conv_w", [128, KI, TAPS])
        conv_b = m.sbuf(ctx, "l2a_conv_b", [128, KI])
        a_log = m.sbuf(ctx, "l2a_A_log", [H, 1])
        dt_bias = m.sbuf(ctx, "l2a_dt_bias", [H, 1])
        skip = m.sbuf(ctx, "l2a_skip", [ROWS, DI])
        norm_w = m.sbuf(ctx, "l2a_norm_w", [128, KI])
        wo = m.sbuf(ctx, "l2a_wo", [128, KI, D])
        causal = m.sbuf(ctx, "l2a_causal", [ROWS, 4 * ROWS])
        rows8 = m.sbuf(ctx, "l2a_rows8", [8, 8, 128])
        xc = m.sbuf(ctx, "l2a_xc", [128, KI, COLS])
        conv = m.sbuf(ctx, "l2a_conv", [128, KI, COLS])
        BT = m.sbuf(ctx, "l2a_BT", [NS, COLS])
        CT = m.sbuf(ctx, "l2a_CT", [NS, COLS])
        dt = m.sbuf(ctx, "l2a_dt", [H, COLS])
        mag = m.sbuf(ctx, "l2a_mag", [H, COLS])
        ones = m.sbuf(ctx, "l2a_ones", [H, COLS])
        logs = m.sbuf(ctx, "l2a_logs", [H, COLS])
        negL = m.sbuf(ctx, "l2a_negL", [ROWS, TILES, H])
        x_tok = m.sbuf(ctx, "l2a_x_tok", [ROWS, 2, DI])
        z_tok = m.sbuf(ctx, "l2a_z_tok", [ROWS, TILES, DI])
        G = m.sbuf(ctx, "l2a_G", [ROWS, 2, ROWS])
        W = m.sbuf(ctx, "l2a_W", [ROWS, 2, H, ROWS])
        y = m.sbuf(ctx, "l2a_y", [ROWS, 2, DI])
        sq = m.sbuf(ctx, "l2a_sq", [ROWS, DI])
        ss = m.sbuf(ctx, "l2a_ss", [ROWS, TILES])
        rms = m.sbuf(ctx, "l2a_rms", [ROWS, TILES])
        half = m.sbuf(ctx, "l2a_half", [ROWS, 1])
        yT = m.sbuf(ctx, "l2a_yT", [128, 2, KI, ROWS])
        S = {n: m.sem("l2a_" + n) for n in (
            "loaded", "late_loaded", "ones_set", "made", "kept", "convolved", "x_ready", "exp_a", "mag_ready", "logs_ready",
            "sp1", "lturn", "l_kept", "z_made", "z_kept", "lt_made", "e_made", "g_made", "g_kept", "w_made", "x_turned",
            "x_kept", "y_made", "y_step", "y_ready", "rooted", "scaled", "y_turned", "yt_kept", "out_done", "added")}
        jobs = [(wx, 128 * k, 128, xc[:, k, :]) for k in range(KI)] + [(wB, 0, NS, BT), (wC, 0, NS, CT), (wdt, 0, H, dt)]
        with nc.Block() as block:
            @block.sync
            def _(sp):
                for t, n in ((wx, "wx"), (wB, "wB"), (wC, "wC"), (wdt, "wdt"), (wz, "wz")):
                    sp.dma_start(t[:, :, :], dram["l2a_" + n].rearrange("(k p) n -> p k n", p=128)).then_inc(S["loaded"], 16)
                sp.dma_start(conv_w[:, :, :], dram["l2a_conv_w"]).then_inc(S["loaded"], 16)
                sp.dma_start(conv_b[:, :], dram["l2a_conv_b"]).then_inc(S["loaded"], 16)
                sp.dma_start(a_log[:, :], dram["l2a_A_log"]).then_inc(S["loaded"], 16)
                sp.dma_start(dt_bias[:, :], dram["l2a_dt_bias"]).then_inc(S["loaded"], 16)
                sp.dma_start(skip[:, :], dram["l2a_D"]).then_inc(S["late_loaded"], 16)
                sp.dma_start(norm_w[:, :], dram["l2a_norm_w"]).then_inc(S["late_loaded"], 16)
                sp.dma_start(wo[:, :, :], dram["l2a_owT"].rearrange("(k p) n -> p k n", p=128)).then_inc(S["late_loaded"], 16)
                sp.dma_start(causal[:, :], dram["c_causal"]).then_inc(S["late_loaded"], 16)
                sp.dma_start(rows8[:, :, :], dram["c_rows8"]).then_inc(S["late_loaded"], 16)

            @block.tensor
            def _(pe):
                pe.wait_ge(S["loaded"], 16 * 9)
                for j, (w, col, M, _) in enumerate(jobs):
                    for c in range(3):
                        n = 3 * j + c
                        if n >= 8:
                            pe.wait_ge(S["kept"], n - 7)
                        for k in range(KD):
                            mm = nc.tensor.matmul(m.ps[:M, n % 8, :THIRD], w[:, k, col:col + M], m.xT[:, k, third(c)],
                                                  start=(k == 0), stop=(k == KD - 1))
                        mm.then_inc(S["made"], 1)
                for t in range(TILES):
                    if t == 0:
                        pe.wait_ge(S["kept"], 3 * len(jobs))
                    if t >= 4:
                        pe.wait_ge(S["z_kept"], t - 3)
                    for k in range(KD):
                        mm = nc.tensor.matmul(m.ps[:ROWS, t % 4, :], m.xT[:, k, tile_cols(t)], wz[:, k, :],
                                              start=(k == 0), stop=(k == KD - 1))
                    mm.then_inc(S["z_made"], 1)
                pe.wait_ge(S["logs_ready"], 1)
                for t in range(TILES):
                    mm = nc.tensor.transpose(m.ps[:ROWS, 4, t * H:(t + 1) * H], logs[:, tile_cols(t)], m.ident[:H, :H])
                mm.then_inc(S["lturn"], 1)
                pe.wait_ge(S["late_loaded"], 16 * 5)
                pe.wait_ge(S["z_kept"], TILES)
                pe.wait_ge(S["l_kept"], 1)

                def decays(t):
                    if t >= 1:
                        pe.wait_ge(S["e_made"], 8 * t)
                    for b in range(2):
                        nc.tensor.matmul(m.ps[:ROWS, b, :4 * ROWS], m.ident[:ROWS, :ROWS], causal[:, :],
                                         start=True, stop=False, skip_group_check=True)
                        for j in range(4):
                            mm = nc.tensor.matmul(m.ps[:ROWS, b, j * ROWS:(j + 1) * ROWS], rows8[:, 4 * b + j, :ROWS],
                                                  logs[:, tile_cols(t)], start=False, stop=(j == 3), skip_group_check=True)
                    mm.then_inc(S["lt_made"], 1)
                    if t >= 1:
                        pe.wait_ge(S["g_kept"], t)
                    nc.tensor.matmul(m.ps[:ROWS, 2, :ROWS], BT[:, tile_cols(t)], CT[:, tile_cols(t)],
                                     start=True, stop=True).then_inc(S["g_made"], 1)
                    if t >= 1:
                        pe.wait_ge(S["x_kept"], t)
                    for k in range(KI):
                        mm = nc.tensor.transpose(m.ps[:ROWS, 3, k * 128:(k + 1) * 128], xc[:, k, tile_cols(t)],
                                                 m.ident[:, :])
                    mm.then_inc(S["x_turned"], 1)

                def weigh(t):
                    pe.wait_ge(S["w_made"], 2 * t + 2)
                    pe.wait_ge(S["x_kept"], t + 1)
                    if t >= 2:
                        pe.wait_ge(S["y_step"], 2 * (t - 1) - 1)
                    for h in range(H):
                        mm = nc.tensor.matmul(m.ps[:ROWS, 4 + t % 2, h * 64:(h + 1) * 64], W[:, t % 2, h, :],
                                              x_tok[:, t % 2, h * 64:(h + 1) * 64], start=True, stop=True)
                    mm.then_inc(S["y_made"], 1)

                def output(t):
                    pe.wait_ge(S["scaled"], t + 1)
                    if t >= 1:
                        pe.wait_ge(S["yt_kept"], KI * t)
                    for k in range(KI):
                        mm = nc.tensor.transpose(m.ps[:, 6, k * ROWS:(k + 1) * ROWS], y[:, t % 2, k * 128:(k + 1) * 128],
                                                 m.ident[:ROWS, :ROWS])
                    mm.then_inc(S["y_turned"], 1)
                    pe.wait_ge(S["yt_kept"], KI * (t + 1))
                    if t >= 1:
                        pe.wait_ge(S["added"], t)
                    for k in range(KI):
                        mm = nc.tensor.matmul(m.ps[:ROWS, 7, :D], yT[:, t % 2, k, :], wo[:, k, :],
                                              start=(k == 0), stop=(k == KI - 1))
                    mm.then_inc(S["out_done"], 1)

                pe.wait_ge(S["x_ready"], KI)
                for t in range(TILES + 2):
                    if t < TILES:
                        decays(t)
                    if 1 <= t <= TILES:
                        weigh(t - 1)
                    if t >= 2:
                        output(t - 2)

            @block.scalar
            def _(act):
                act.wait_ge(S["loaded"], 16 * 9)
                nc.scalar.activation(a_log[:, :], a_log[:, :], ACT.Exp).then_inc(S["exp_a"], 1)
                for j, (_, _, M, dst) in enumerate(jobs):
                    for c in range(3):
                        n = 3 * j + c
                        act.wait_ge(S["made"], n + 1)
                        src = m.ps[:M, n % 8, :THIRD]
                        if dst is dt:
                            nc.scalar.activation(dst[:, third(c)], src, ACT.Identity, bias=dt_bias[:, 0:1]).then_inc(S["kept"], 1)
                        else:
                            nc.scalar.activation(dst[:, third(c)], src, ACT.Copy).then_inc(S["kept"], 1)
                act.wait_ge(S["kept"], 3 * len(jobs))
                nc.scalar.activation(mag[:, :], dt[:, :], ACT.Abs).then_inc(S["sp1"], 1)
                act.wait_ge(S["sp1"], 1)
                nc.scalar.activation(mag[:, :], mag[:, :], ACT.Exp, scale=-1.0).then_inc(S["sp1"], 1)
                act.wait_ge(S["sp1"], 2)
                nc.scalar.activation(mag[:, :], mag[:, :], ACT.Ln, bias=1.0).then_inc(S["mag_ready"], 1)
                for k in range(KI):
                    act.wait_ge(S["convolved"], TAPS * (k + 1))
                    nc.scalar.activation(xc[:, k, :], conv[:, k, :], ACT.Silu).then_inc(S["x_ready"], 1)
                for t in range(TILES):
                    act.wait_ge(S["z_made"], t + 1)
                    nc.scalar.activation(z_tok[:, t, :], m.ps[:ROWS, t % 4, :], ACT.Silu).then_inc(S["z_kept"], 1)

                def kept_out(act, t):
                    act.wait_ge(S["y_turned"], t + 1)
                    if t >= 2:
                        act.wait_ge(S["out_done"], t - 1)
                    for k in range(KI):
                        nc.scalar.activation(yT[:, t % 2, k, :], m.ps[:, 6, k * ROWS:(k + 1) * ROWS], ACT.Copy,
                                             scale=norm_w[:, k:k + 1]).then_inc(S["yt_kept"], 1)

                def copies(t):
                    act.wait_ge(S["g_made"], t + 1)
                    if t >= 2:
                        act.wait_ge(S["w_made"], 2 * (t - 1))
                    nc.scalar.activation(G[:, t % 2, :], m.ps[:ROWS, 2, :ROWS], ACT.Copy).then_inc(S["g_kept"], 1)
                    act.wait_ge(S["x_turned"], t + 1)
                    if t >= 2:
                        act.wait_ge(S["y_made"], t - 1)
                        act.wait_ge(S["y_step"], 2 * (t - 1) - 1)
                    nc.scalar.activation(x_tok[:, t % 2, :], m.ps[:ROWS, 3, :], ACT.Copy).then_inc(S["x_kept"], 1)

                act.wait_ge(S["l_kept"], 1)
                for t in range(TILES):
                    act.wait_ge(S["lt_made"], t + 1)
                    if t >= 2:
                        act.wait_ge(S["y_made"], t - 1)
                    for h in range(H):
                        nc.scalar.activation(W[:, t % 2, h, :], m.ps[:ROWS, h // 4, (h % 4) * ROWS:(h % 4 + 1) * ROWS],
                                             ACT.Exp, bias=negL[:, t, h:h + 1]).then_inc(S["e_made"], 1)
                    copies(t)
                    if t >= 1:
                        kept_out(act, t - 1)
                kept_out(act, TILES - 1)

            @block.vector
            def _(dve):
                def seqs(x, k):
                    return x[:, k, :].rearrange("p (s t) -> p s t", t=T)

                nc.vector.memset(ones[:, :], 1.0).then_inc(S["ones_set"], 1)
                dve.wait_ge(S["ones_set"], 1)
                nc.vector.memset(ones[:, 0:COLS:T], 0.0).then_inc(S["exp_a"], 1)
                for k in range(KI):
                    dve.wait_ge(S["kept"], 3 * (k + 1))
                    nc.vector.tensor_scalar(conv[:, k, :], xc[:, k, :], conv_w[:, k, 3:4], conv_b[:, k:k + 1], ALU.mult,
                                            ALU.add).then_inc(S["convolved"], 1)
                    for shift in range(1, TAPS):
                        dve.wait_ge(S["convolved"], TAPS * k + shift)
                        nc.vector.scalar_tensor_tensor(seqs(conv, k)[:, :, shift:], seqs(xc, k)[:, :, :T - shift],
                                                       conv_w[:, k, 3 - shift:4 - shift], seqs(conv, k)[:, :, shift:],
                                                       ALU.mult, ALU.add).then_inc(S["convolved"], 1)
                dve.wait_ge(S["mag_ready"], 1)
                dve.wait_ge(S["exp_a"], 2)
                step = S["y_ready"]
                nc.vector.scalar_tensor_tensor(dt[:, :], dt[:, :], 0.0, mag[:, :], ALU.max, ALU.add).then_inc(step, 1)
                dve.wait_ge(step, 1)
                nc.vector.tensor_scalar(dt[:, :], dt[:, :], a_log[:, 0:1], -1.0, ALU.mult, ALU.mult).then_inc(step, 1)
                dve.wait_ge(step, 2)
                nc.vector.tensor_tensor_scan(logs[:, :], ones[:, :], dt[:, :], 0.0, ALU.mult,
                                             ALU.add).then_inc(S["logs_ready"], 1)
                dve.wait_ge(S["lturn"], 1)
                nc.vector.tensor_scalar(negL[:, :, :], m.ps[:ROWS, 4, :TILES * H].rearrange("p (t h) -> p t h", h=H),
                                        -1.0, None, ALU.mult).then_inc(S["l_kept"], 1)
                dve.wait_ge(S["late_loaded"], 16 * 5)

                def finish(t):
                    yy = y[:, t % 2, :]
                    dve.wait_ge(S["y_made"], t + 1)
                    if t >= 2:
                        dve.wait_ge(S["y_turned"], t - 1)
                    n = 2 + 4 * t
                    nc.vector.tensor_tensor(sq[:, :], x_tok[:, t % 2, :], skip[:, :], ALU.mult).then_inc(step, 1)
                    dve.wait_ge(step, n + 1)
                    nc.vector.tensor_tensor(yy, m.ps[:ROWS, 4 + t % 2, :], sq[:, :], ALU.add).then_inc(S["y_step"], 1)
                    dve.wait_ge(S["y_step"], 2 * t + 1)
                    nc.vector.tensor_tensor(yy, yy, z_tok[:, t, :], ALU.mult).then_inc(S["y_step"], 1)
                    dve.wait_ge(S["y_step"], 2 * t + 2)
                    nc.vector.tensor_tensor(sq[:, :], yy, yy, ALU.mult).then_inc(step, 1)
                    dve.wait_ge(step, n + 2)
                    nc.vector.tensor_reduce(ss[:, t:t + 1], sq[:, :], AX.X, ALU.add).then_inc(step, 1)
                    dve.wait_ge(step, n + 3)
                    nc.vector.tensor_scalar(ss[:, t:t + 1], ss[:, t:t + 1], 1.0 / DI, 1e-6, ALU.mult,
                                            ALU.add).then_inc(step, 1)
                    dve.wait_ge(S["rooted"], t + 2)
                    nc.vector.tensor_scalar(yy, yy, rms[:, t:t + 1], None, ALU.mult).then_inc(S["scaled"], 1)

                for t in range(TILES + 2):
                    if t < TILES:
                        dve.wait_ge(S["g_kept"], t + 1)
                        for b in range(2):
                            dve.wait_ge(S["e_made"], 8 * t + 4 * b + 4)
                            w4 = W[:, t % 2, 4 * b:4 * b + 4, :]
                            g4 = G[:, t % 2, :].rearrange("p (o n) -> p o n", o=1).broadcast_to([ROWS, 4, ROWS])
                            nc.vector.tensor_tensor(w4, w4, g4, ALU.mult).then_inc(S["w_made"], 1)
                    if 1 <= t <= TILES:
                        finish(t - 1)
                    if t >= 2:
                        dve.wait_ge(S["out_done"], t - 1)
                        nc.vector.tensor_tensor(m.h[:, t - 2, :], m.ps[:ROWS, 7, :D], m.h[:, t - 2, :],
                                                ALU.add).then_inc(S["added"], 1)

            @block.gpsimd
            def _(pool):
                nc.gpsimd.memset(half[:, :], -0.5).then_inc(S["rooted"], 1)
                pool.wait_ge(S["rooted"], 1)
                for t in range(TILES):
                    pool.wait_ge(S["y_ready"], 2 + 4 * t + 4)
                    nc.gpsimd.tensor_tensor(rms[:, t:t + 1], ss[:, t:t + 1], half[:, :], ALU.pow).then_inc(S["rooted"], 1)


STAGE[5] = lambda nc, m, dram: (normalise(nc, m, "l2a_ln", m.h), state_space(nc, m, dram))


def small_head_attention(nc, m, dram):
    H, DH = 16, 16
    HALF = H // KD
    ITEMS = TILES * 4
    scale = float(DH ** -0.5)
    with ExitStack() as ctx:
        wq = m.sbuf(ctx, "l2f_wq", [128, KD, D])
        wk = m.sbuf(ctx, "l2f_wk", [128, KD, D])
        wv = m.sbuf(ctx, "l2f_wv", [128, KD, D])
        wo = m.sbuf(ctx, "l2f_wo", [128, KD, D])
        heads = m.sbuf(ctx, "l2f_heads", [128, HALF])
        qT = m.sbuf(ctx, "l2f_qT", [128, KD, COLS])
        kT = m.sbuf(ctx, "l2f_kT", [128, KD, COLS])
        own = m.sbuf(ctx, "l2f_own", [128, 2, HALF, ROWS])
        v = m.sbuf(ctx, "l2f_v", [ROWS, TILES, D])
        mix = m.sbuf(ctx, "l2f_mix", [ROWS, 2, D])
        mixT = m.sbuf(ctx, "l2f_mixT", [128, 2, KD, ROWS])
        sm = MaskedSoftmax(nc, m, "l2f_sm", ctx, dram["c_mask"], scale)
        S = {n: m.sem("l2f_" + n) for n in (
            "loaded", "made", "kept", "v_made", "v_kept", "owned", "mixed", "mix_kept", "mix_turned", "mixT_kept",
            "out_done", "added")}
        jobs = [(wq, k, qT) for k in range(KD)] + [(wk, k, kT) for k in range(KD)]
        with nc.Block() as block:
            @block.sync
            def _(sp):
                for t, n in ((wq, "Wq"), (wk, "Wk"), (wv, "Wv"), (wo, "Wo")):
                    sp.dma_start(t[:, :, :], dram["l2f_" + n].rearrange("(k p) n -> p k n", p=128)).then_inc(S["loaded"], 16)
                sp.dma_start(heads[:, :], dram["c_heads"]).then_inc(S["loaded"], 16)
                sm.load_mask(sp)

            @block.tensor
            def _(pe):
                pe.wait_ge(S["loaded"], 16 * 5)
                for j, (w, mk, _) in enumerate(jobs):
                    for c in range(3):
                        n = 3 * j + c
                        if n >= 4:
                            pe.wait_ge(S["kept"], n - 3)
                        for k in range(KD):
                            mm = nc.tensor.matmul(m.ps[:, n % 4, :THIRD], w[:, k, mk * 128:(mk + 1) * 128],
                                                  m.xT[:, k, third(c)], start=(k == 0), stop=(k == KD - 1))
                        mm.then_inc(S["made"], 1)
                for t in range(TILES):
                    if t >= 4:
                        pe.wait_ge(S["v_kept"], t - 3)
                    for k in range(KD):
                        mm = nc.tensor.matmul(m.ps[:ROWS, 4 + t % 4, :D], m.xT[:, k, tile_cols(t)], wv[:, k, :],
                                              start=(k == 0), stop=(k == KD - 1))
                    mm.then_inc(S["v_made"], 1)
                pe.wait_ge(S["kept"], 3 * len(jobs))
                pe.wait_ge(S["v_kept"], TILES)

                def scores(i):
                    t, q4 = i // 4, i % 4
                    u = i // 2
                    pe.wait_ge(S["owned"], u + 1)
                    if i >= 2:
                        pe.wait_ge(sm.masked, i - 1)
                    nc.tensor.matmul(m.ps[:ROWS, i % 2, :4 * ROWS], qT[:, q4 // 2, tile_cols(t)],
                                     own[:, u % 2, 4 * (q4 % 2):4 * (q4 % 2) + 4, :], start=True,
                                     stop=True).then_inc(sm.scored, 1)

                def weigh(i):
                    t, q4 = i // 4, i % 4
                    pe.wait_ge(sm.kept, i + 1)
                    if q4 == 0 and t >= 2:
                        pe.wait_ge(S["mix_kept"], t - 1)
                    for j in range(4):
                        h = 4 * q4 + j
                        mm = nc.tensor.matmul(m.ps[:ROWS, 4 + t % 2, h * DH:(h + 1) * DH],
                                              sm.turnedP[:, i % 2, j * ROWS:(j + 1) * ROWS],
                                              v[:, t, h * DH:(h + 1) * DH], start=True, stop=True)
                    mm.then_inc(sm.used, 1)

                def turn_mix(t):
                    pe.wait_ge(S["mix_kept"], t + 1)
                    if t >= 1:
                        pe.wait_ge(S["mixT_kept"], t)
                    for k in range(KD):
                        mm = nc.tensor.transpose(m.ps[:, 6, k * ROWS:(k + 1) * ROWS], mix[:, t % 2, k * 128:(k + 1) * 128],
                                                 m.ident[:ROWS, :ROWS])
                    mm.then_inc(S["mix_turned"], 1)

                def output(t):
                    pe.wait_ge(S["mixT_kept"], t + 1)
                    if t >= 1:
                        pe.wait_ge(S["added"], t)
                    for k in range(KD):
                        mm = nc.tensor.matmul(m.ps[:ROWS, 7, :D], mixT[:, t % 2, k, :], wo[:, k, :],
                                              start=(k == 0), stop=(k == KD - 1))
                    mm.then_inc(S["out_done"], 1)

                for i in range(ITEMS + 5):
                    if i < ITEMS:
                        scores(i)
                    if 1 <= i <= ITEMS:
                        sm.tensor_turn(pe, i - 1)
                    if 2 <= i < ITEMS + 2:
                        weigh(i - 2)
                    if i >= 6 and (i - 6) % 4 == 0:
                        turn_mix((i - 6) // 4)
                    if i >= 7 and (i - 7) % 4 == 0:
                        output((i - 7) // 4)

            @block.scalar
            def _(act):
                for j, (_, mk, dst) in enumerate(jobs):
                    for c in range(3):
                        n = 3 * j + c
                        act.wait_ge(S["made"], n + 1)
                        nc.scalar.activation(dst[:, mk, third(c)], m.ps[:, n % 4, :THIRD], ACT.Copy).then_inc(S["kept"], 1)
                for t in range(TILES):
                    act.wait_ge(S["v_made"], t + 1)
                    nc.scalar.activation(v[:, t, :], m.ps[:ROWS, 4 + t % 4, :D], ACT.Copy).then_inc(S["v_kept"], 1)

                def keep_mix(t):
                    act.wait_ge(sm.used, 4 * (t + 1))
                    if t >= 2:
                        act.wait_ge(S["mix_turned"], t - 1)
                    nc.scalar.activation(mix[:, t % 2, :], m.ps[:ROWS, 4 + t % 2, :D], ACT.Copy).then_inc(S["mix_kept"], 1)

                def keep_mixT(t):
                    act.wait_ge(S["mix_turned"], t + 1)
                    if t >= 2:
                        act.wait_ge(S["out_done"], t - 1)
                    nc.scalar.activation(mixT[:, t % 2, :, :].rearrange("p k n -> p (k n)"), m.ps[:, 6, :KD * ROWS],
                                         ACT.Copy).then_inc(S["mixT_kept"], 1)

                for i in range(ITEMS + 5):
                    if i < ITEMS:
                        sm.scalar_exp(act, i)
                    if 1 <= i <= ITEMS:
                        sm.scalar_keep(act, i - 1, sm.used)
                    if i >= 6 and (i - 6) % 4 == 0:
                        keep_mix((i - 6) // 4)
                    if i >= 7 and (i - 7) % 4 == 0:
                        keep_mixT((i - 7) // 4)

            @block.vector
            def _(dve):
                dve.wait_ge(sm.mask_loaded, 16)

                def add(t):
                    dve.wait_ge(S["out_done"], t + 1)
                    nc.vector.tensor_tensor(m.xn[:, t, :], m.ps[:ROWS, 7, :D], m.xn[:, t, :],
                                            ALU.add).then_inc(S["added"], 1)

                for i in range(ITEMS + 5):
                    if i < ITEMS:
                        sm.vector_mask(dve, i)
                    if 1 <= i <= ITEMS:
                        sm.vector_sum(dve, i - 1)
                    if i >= 8 and (i - 8) % 4 == 0:
                        add((i - 8) // 4)

            @block.gpsimd
            def _(pool):
                pool.wait_ge(S["loaded"], 16 * 5)
                pool.wait_ge(S["kept"], 3 * len(jobs))

                def own_keys(u):
                    t, k = u // 2, u % 2
                    if u >= 2:
                        pool.wait_ge(sm.scored, 2 * (u - 1))
                    keys = kT[:, k, tile_cols(t)].rearrange("p (o n) -> p o n", o=1).broadcast_to([128, HALF, ROWS])
                    mine = heads[:, :].rearrange("p (h o) -> p h o", o=1).broadcast_to([128, HALF, ROWS])
                    nc.gpsimd.tensor_tensor(own[:, u % 2, :, :], keys, mine, ALU.mult).then_inc(S["owned"], 1)

                own_keys(0)
                own_keys(1)
                for i in range(ITEMS):
                    if i % 2 == 0 and 2 <= i and i // 2 + 1 < 2 * TILES:
                        own_keys(i // 2 + 1)
                    sm.pool_shift(pool, i)


def ds(i):
    return bass.ds(i, 1)


def experts_mlp(nc, m, dram, wts, wtsT):
    E, F = 8, 1024
    KF = F // 128
    NG = len(GROUPS)
    with ExitStack() as ctx:
        w1 = [m.sbuf(ctx, f"l2m_w1_{p}", [128, KD, F]) for p in range(2)]
        w2 = [m.sbuf(ctx, f"l2m_w2_{p}", [128, KF, D]) for p in range(2)]
        b1 = [m.sbuf(ctx, f"l2m_b1_{p}", [128, KF]) for p in range(2)]
        b2 = m.sbuf(ctx, "l2m_b2", [E, D])
        hid = m.sbuf(ctx, "l2m_hid", [128, 2, KF, 4 * ROWS])
        w_loaded = [m.sem(f"l2m_w_loaded{p}") for p in range(2)]
        b_loaded = m.sem("l2m_b_loaded")
        raised = m.sem("l2m_raised")
        gelued = m.sem("l2m_gelued")
        lowered = m.sem("l2m_lowered")
        summed = m.sem("l2m_summed")
        biased = m.sem("l2m_biased")
        bias_added = m.sem("l2m_bias_added")
        UP, DOWN = 2 * NG * KF, 2 * TILES

        def steps(p):
            return [(g, p * NG + g, t0, n, p * TILES + t0) for g, (t0, n) in enumerate(GROUPS)]

        with nc.Block() as block:
            @block.sync
            def _(sp):
                sp.dma_start(b2[:, :], dram["l2m_b2"]).then_inc(b_loaded, 16)
                with sp.Fori(0, E // 2) as i:
                    for p in range(2):
                        sp.wait_ge(lowered, i * DOWN + (p + 1) * TILES)
                        sp.dma_start(w1[p][:, :, :], dram["l2m_w1"][ds(2 * i + p)].rearrange("o (k p) n -> p (o k) n", p=128)).then_inc(w_loaded[p], 16)
                        sp.dma_start(w2[p][:, :, :], dram["l2m_w2"][ds(2 * i + p)].rearrange("o (k p) n -> p (o k) n", p=128)).then_inc(w_loaded[p], 16)
                        sp.dma_start(b1[p][:, :], dram["l2m_b1"][ds(2 * i + p)].rearrange("o p f -> (o p) f")).then_inc(w_loaded[p], 16)

            @block.tensor
            def _(pe):
                pe.sem_inc(lowered, DOWN)
                pe.wait_ge(b_loaded, 16)
                for t in range(TILES):
                    if t >= 4:
                        pe.wait_ge(bias_added, t - 3)
                    nc.tensor.matmul(m.ps[:ROWS, t % 4, :D], wtsT[:, tile_cols(t)], b2[:, :], start=True,
                                     stop=True).then_inc(biased, 1)
                pe.wait_ge(bias_added, TILES)
                with pe.Fori(0, E // 2) as i:
                    def lower(p, u, t0, n, before):
                        pe.wait_ge(gelued, i * UP + UP + (u + 1) * KF)
                        for r in range(n):
                            c = before + r
                            pe.wait_ge(summed, i * DOWN + DOWN + c - 1)
                            for f in range(KF):
                                mm = nc.tensor.matmul(m.ps[:ROWS, 6 + c % 2, :D], hid[:, u % 2, f, r * ROWS:(r + 1) * ROWS],
                                                      w2[p][:, f, :], start=(f == 0), stop=(f == KF - 1))
                            mm.then_inc(lowered, 1)

                    waiting = None
                    for p in range(2):
                        pe.wait_ge(w_loaded[p], i * 48 + 48)
                        for g, u, t0, n, before in steps(p):
                            cols = slice(t0 * ROWS, (t0 + n) * ROWS)
                            for f in range(KF):
                                c = u * KF + f
                                pe.wait_ge(gelued, i * UP + UP + c - 5)
                                for k in range(KD):
                                    mm = nc.tensor.matmul(m.ps[:, c % 6, :n * ROWS], w1[p][:, k, f * 128:(f + 1) * 128],
                                                          m.xT[:, k, cols], start=(k == 0), stop=(k == KD - 1))
                                mm.then_inc(raised, 1)
                            if waiting is not None:
                                lower(*waiting)
                            waiting = (p, u, t0, n, before)
                    lower(*waiting)

            @block.scalar
            def _(act):
                act.sem_inc(gelued, UP)
                with act.Fori(0, E // 2) as i:
                    for p in range(2):
                        for g, u, t0, n, before in steps(p):
                            act.wait_ge(lowered, i * DOWN + DOWN + before - (GROUPS[g - 1][1]))
                            for f in range(KF):
                                c = u * KF + f
                                act.wait_ge(raised, i * UP + c + 1)
                                nc.scalar.activation(hid[:, u % 2, f, :n * ROWS], m.ps[:, c % 6, :n * ROWS],
                                                     ACT.Gelu_apprx_tanh,
                                                     bias=b1[p][:, f:f + 1]).then_inc(gelued, 1)

            @block.vector
            def _(dve):
                dve.sem_inc(summed, DOWN)
                for t in range(TILES):
                    dve.wait_ge(biased, t + 1)
                    nc.vector.tensor_tensor(m.xn[:, t, :], m.ps[:ROWS, t % 4, :D], m.xn[:, t, :],
                                            ALU.add).then_inc(bias_added, 1)
                with dve.Fori(0, E // 2) as i:
                    for p in range(2):
                        for t in range(TILES):
                            c = p * TILES + t
                            dve.wait_ge(lowered, i * DOWN + DOWN + c + 1)
                            dve.wait_ge(summed, i * DOWN + DOWN + c - TILES + 1)
                            nc.vector.scalar_tensor_tensor(m.xn[:, t, :], m.ps[:ROWS, 6 + c % 2, :D],
                                                           wts[:, t, ds(2 * i + p)], m.xn[:, t, :], ALU.mult,
                                                           ALU.add).then_inc(summed, 1)
                dve.wait_ge(summed, DOWN * (E // 2 + 1))
                nc.vector.tensor_tensor(m.h[:, :, :], m.h[:, :, :], m.xn[:, :, :], ALU.add).then_inc(bias_added, 1)
                dve.wait_ge(bias_added, TILES + 1)


def layer2_ffn(nc, m, dram):
    normalise(nc, m, "l2f_ln", m.h, turn=False)
    with ExitStack() as ctx:
        scratch = m.sbuf(ctx, "l2f_scratch", [ROWS, TILES, D])
        normalise(nc, m, "l2f_ln1", m.xn, tok=scratch, affine=dram["l2f_ln1"])
    small_head_attention(nc, m, dram)
    with ExitStack() as ctx:
        scratch = m.sbuf(ctx, "l2f_scratch2", [ROWS, TILES, D])
        normalise(nc, m, "l2f_ln2", m.xn, tok=scratch, affine=dram["l2f_ln2"])
    with ExitStack() as ctx:
        wts = m.sbuf(ctx, "l2m_wts", [ROWS, TILES, 8])
        wtsT = m.sbuf(ctx, "l2m_wtsT", [8, COLS])
        gate(nc, m, "l2g", dram["l2g_gw"], dram["l2g_gb"], 8, wts, wtsT, True)
        experts_mlp(nc, m, dram, wts, wtsT)


STAGE[6] = layer2_ffn


def gated_sums(nc, m, dram, gT):
    H, DH, RANK = 16, 16, 16
    with ExitStack() as ctx:
        w = {n: m.sbuf(ctx, "l3a_" + n, [128, KD, D]) for n in ("Wq", "Wk", "Wv", "Wg")}
        w1 = m.sbuf(ctx, "l3a_Wgk1", [128, KD, RANK])
        w2 = m.sbuf(ctx, "l3a_Wgk2", [RANK, D])
        b2 = m.sbuf(ctx, "l3a_bgk2", [128, KD])
        spread = m.sbuf(ctx, "l3a_spread", [128, DH, 128])
        low = m.sbuf(ctx, "l3a_low", [RANK, COLS])
        kT = m.sbuf(ctx, "l3a_kT", [128, KD, COLS])
        vT = m.sbuf(ctx, "l3a_vT", [128, KD, COLS])
        qT = m.sbuf(ctx, "l3a_qT", [128, KD, COLS])
        gates = m.sbuf(ctx, "l3a_gates", [128, KD, COLS])
        mag = m.sbuf(ctx, "l3a_mag", [128, KD, COLS])
        upd = m.sbuf(ctx, "l3a_upd", [128, 2, COLS])
        state = m.sbuf(ctx, "l3a_state", [128, 2, COLS])
        qs = m.sbuf(ctx, "l3a_qs", [128, 2, COLS])
        read = m.sbuf(ctx, "l3a_read", [128, 2, COLS])
        S = {n: m.sem("l3a_" + n) for n in (
            "loaded", "c_loaded", "low_made", "low_kept", "made", "kept", "soft", "log_ready", "gated", "cut", "k_spread",
            "q_spread", "updated", "q_kept", "scanned", "was_read", "gathered", "o_kept", "turned", "stored")}
        jobs = [(w["Wk"], k, kT) for k in range(KD)] + [(w["Wv"], k, vT) for k in range(KD)]
        jobs += [(w["Wq"], k, qT) for k in range(KD)] + [(w["Wg"], k, gT) for k in range(KD)]
        STEPS = KD * DH
        with nc.Block() as block:
            @block.sync
            def _(sp):
                sp.dma_start(w1[:, :, :], dram["l3a_Wgk1"].rearrange("(k p) n -> p k n", p=128)).then_inc(S["loaded"], 16)
                sp.dma_start(w2[:, :], dram["l3a_Wgk2"]).then_inc(S["loaded"], 16)
                sp.dma_start(b2[:, :], dram["l3a_bgk2"]).then_inc(S["loaded"], 16)
                for n in ("Wk", "Wv", "Wq", "Wg"):
                    sp.dma_start(w[n][:, :, :], dram["l3a_" + n].rearrange("(k p) n -> p k n", p=128)).then_inc(S["loaded"], 16)
                sp.dma_start(spread[:, :, :], dram["c_spread"]).then_inc(S["c_loaded"], 16)

            @block.tensor
            def _(pe):
                pe.wait_ge(S["loaded"], 16 * 7)
                for c in range(3):
                    for k in range(KD):
                        mm = nc.tensor.matmul(m.ps[:RANK, 6, :THIRD] if c == 0 else m.ps[:RANK, 6 + (c % 2), :THIRD],
                                              w1[:, k, :], m.xT[:, k, third(c)], start=(k == 0), stop=(k == KD - 1))
                    mm.then_inc(S["low_made"], 1)
                    pe.wait_ge(S["low_kept"], c + 1)
                for j in range(KD + len(jobs)):
                    for c in range(3):
                        n = 3 * j + c
                        if n >= 6:
                            pe.wait_ge(S["kept"], n - 5)
                        out = m.ps[:, n % 6, :THIRD]
                        if j < KD:
                            mm = nc.tensor.matmul(out, w2[:, j * 128:(j + 1) * 128], low[:, third(c)], start=True, stop=True)
                        else:
                            ww, mk, _ = jobs[j - KD]
                            for k in range(KD):
                                mm = nc.tensor.matmul(out, ww[:, k, mk * 128:(mk + 1) * 128], m.xT[:, k, third(c)],
                                                      start=(k == 0), stop=(k == KD - 1))
                        mm.then_inc(S["made"], 1)
                pe.wait_ge(S["kept"], 3 * (KD + len(jobs)))
                pe.wait_ge(S["c_loaded"], 16)

                def sum_up(i):
                    pe.wait_ge(S["was_read"], i + 1)
                    if i == DH:
                        pe.wait_ge(S["o_kept"], 3)
                    for c in range(3):
                        mm = nc.tensor.matmul(m.ps[:, 5 + c, :THIRD], m.ident[:, :], read[:, i % 2, third(c)],
                                              start=(i % DH == 0), stop=(i % DH == DH - 1), skip_group_check=True)
                    mm.then_inc(S["gathered"], 1)

                for i in range(STEPS):
                    for c in range(3):
                        n = 3 * i + c
                        if n >= 3:
                            pe.wait_ge(S["updated"], n - 2)
                        nc.tensor.matmul(m.ps[:, n % 3, :THIRD], spread[:, i % DH, :], kT[:, i // DH, third(c)],
                                         start=True, stop=True).then_inc(S["k_spread"], 1)
                        if n >= 2:
                            pe.wait_ge(S["q_kept"], n - 1)
                        nc.tensor.matmul(m.ps[:, 3 + n % 2, :THIRD], spread[:, i % DH, :], qT[:, i // DH, third(c)],
                                         start=True, stop=True).then_inc(S["q_spread"], 1)
                    if i >= 1:
                        sum_up(i - 1)
                sum_up(STEPS - 1)
                pe.wait_ge(S["o_kept"], 6)
                for t in range(TILES):
                    if t >= 4:
                        pe.wait_ge(S["stored"], t - 3)
                    for k in range(KD):
                        mm = nc.tensor.transpose(m.ps[:ROWS, t % 4, k * 128:(k + 1) * 128], mag[:, k, tile_cols(t)],
                                                 m.ident[:, :])
                    mm.then_inc(S["turned"], 1)

            @block.scalar
            def _(act):
                for c in range(3):
                    act.wait_ge(S["low_made"], c + 1)
                    nc.scalar.activation(low[:, third(c)], m.ps[:RANK, 6 + (c % 2), :THIRD], ACT.Copy).then_inc(S["low_kept"], 1)
                for j in range(KD):
                    for c in range(3):
                        n = 3 * j + c
                        act.wait_ge(S["made"], n + 1)
                        nc.scalar.activation(gates[:, j, third(c)], m.ps[:, n % 6, :THIRD], ACT.Identity,
                                             bias=b2[:, j:j + 1]).then_inc(S["kept"], 1)
                for j, (_, mk, dst) in enumerate(jobs[:6]):
                    for c in range(3):
                        n = 3 * (j + KD) + c
                        act.wait_ge(S["made"], n + 1)
                        nc.scalar.activation(dst[:, mk, third(c)], m.ps[:, n % 6, :THIRD], ACT.Copy).then_inc(S["kept"], 1)
                nc.scalar.activation(mag[:, :, :], gates[:, :, :], ACT.Abs).then_inc(S["soft"], 1)
                act.wait_ge(S["soft"], 1)
                nc.scalar.activation(mag[:, :, :], mag[:, :, :], ACT.Exp, scale=-1.0).then_inc(S["soft"], 1)
                act.wait_ge(S["soft"], 2)
                nc.scalar.activation(mag[:, :, :], mag[:, :, :], ACT.Ln, bias=1.0).then_inc(S["soft"], 1)
                act.wait_ge(S["log_ready"], 1)
                nc.scalar.activation(gates[:, :, :], gates[:, :, :], ACT.Exp, scale=1.0 / 16.0).then_inc(S["gated"], 1)
                for j, (_, mk, dst) in enumerate(jobs[6:]):
                    for c in range(3):
                        n = 3 * (j + 6 + KD) + c
                        act.wait_ge(S["made"], n + 1)
                        nc.scalar.activation(dst[:, mk, third(c)], m.ps[:, n % 6, :THIRD], ACT.Silu).then_inc(S["kept"], 1)
                def sums(act, k):
                    act.wait_ge(S["gathered"], DH * (k + 1))
                    for c in range(3):
                        nc.scalar.activation(mag[:, k, third(c)], m.ps[:, 5 + c, :THIRD], ACT.Copy).then_inc(S["o_kept"], 1)

                for i in range(STEPS):
                    if i >= 2:
                        act.wait_ge(S["was_read"], i - 1)
                    for c in range(3):
                        n = 3 * i + c
                        act.wait_ge(S["q_spread"], n + 1)
                        nc.scalar.activation(qs[:, i % 2, third(c)], m.ps[:, 3 + n % 2, :THIRD], ACT.Copy).then_inc(S["q_kept"], 1)
                    if i == DH + 1:
                        sums(act, 0)
                sums(act, 1)

            @block.vector
            def _(dve):
                dve.wait_ge(S["soft"], 3)
                nc.vector.scalar_tensor_tensor(gates[:, :, :], gates[:, :, :], 0.0, mag[:, :, :], ALU.min,
                                               ALU.subtract).then_inc(S["log_ready"], 1)
                dve.wait_ge(S["gated"], 1)
                nc.vector.memset(gates[:, 0, 0:COLS:T], 0.0).then_inc(S["cut"], 1)
                nc.vector.memset(gates[:, 1, 0:COLS:T], 0.0).then_inc(S["cut"], 1)
                dve.wait_ge(S["cut"], 2)
                dve.wait_ge(S["kept"], 3 * (KD + len(jobs)))
                for i in range(STEPS):
                    if i >= 2:
                        dve.wait_ge(S["scanned"], i - 1)
                    for c in range(3):
                        dve.wait_ge(S["k_spread"], 3 * i + c + 1)
                        nc.vector.tensor_tensor(upd[:, i % 2, third(c)], m.ps[:, (3 * i + c) % 3, :THIRD],
                                                vT[:, i // DH, third(c)], ALU.mult).then_inc(S["updated"], 1)
                    dve.wait_ge(S["updated"], 3 * i + 3)
                    if i >= 2:
                        dve.wait_ge(S["was_read"], i - 1)
                    nc.vector.tensor_tensor_scan(state[:, i % 2, :], gates[:, i // DH, :], upd[:, i % 2, :], 0.0,
                                                 ALU.mult, ALU.add).then_inc(S["scanned"], 1)
                for t in range(TILES):
                    dve.wait_ge(S["turned"], t + 1)
                    nc.vector.tensor_copy(m.xn[:, t, :], m.ps[:ROWS, t % 4, :D]).then_inc(S["stored"], 1)

            @block.gpsimd
            def _(pool):
                for i in range(STEPS):
                    pool.wait_ge(S["scanned"], i + 1)
                    pool.wait_ge(S["q_kept"], 3 * i + 3)
                    if i >= 2:
                        pool.wait_ge(S["gathered"], i - 1)
                    nc.gpsimd.tensor_tensor(read[:, i % 2, :], state[:, i % 2, :], qs[:, i % 2, :],
                                            ALU.mult).then_inc(S["was_read"], 1)


def gated_output(nc, m, dram, gT):
    with ExitStack() as ctx:
        wo = m.sbuf(ctx, "l3o_Wout", [128, KD, D])
        loaded = m.sem("l3o_loaded")
        gated = m.sem("l3o_gated")
        out_done = m.sem("l3o_out_done")
        added = m.sem("l3o_added")
        with nc.Block() as block:
            @block.sync
            def _(sp):
                sp.dma_start(wo[:, :, :], dram["l3a_Wout"].rearrange("(k p) n -> p k n", p=128)).then_inc(loaded, 16)

            @block.tensor
            def _(pe):
                pe.wait_ge(loaded, 16)
                for t in range(TILES):
                    pe.wait_ge(gated, t + 1)
                    if t >= 4:
                        pe.wait_ge(added, t - 3)
                    for k in range(KD):
                        mm = nc.tensor.matmul(m.ps[:ROWS, t % 4, :D], m.xT[:, k, tile_cols(t)], wo[:, k, :],
                                              start=(k == 0), stop=(k == KD - 1))
                    mm.then_inc(out_done, 1)

            @block.gpsimd
            def _(pool):
                for t in range(TILES):
                    x = m.xT[:, :, tile_cols(t)]
                    nc.gpsimd.tensor_tensor(x, x, gT[:, :, tile_cols(t)], ALU.mult).then_inc(gated, 1)

            @block.vector
            def _(dve):
                for t in range(TILES):
                    dve.wait_ge(out_done, t + 1)
                    nc.vector.tensor_tensor(m.h[:, t, :], m.ps[:ROWS, t % 4, :D], m.h[:, t, :],
                                            ALU.add).then_inc(added, 1)


def layer3_attention(nc, m, dram):
    normalise(nc, m, "l3a_ln", m.h)
    with ExitStack() as ctx:
        gT = m.sbuf(ctx, "l3a_gT", [128, KD, COLS])
        gated_sums(nc, m, dram, gT)
        scratch = m.sbuf(ctx, "l3a_scratch", [ROWS, TILES, D])
        normalise(nc, m, "l3a_on", m.xn, tok=scratch, affine=dram["l3a_norm"])
        gated_output(nc, m, dram, gT)


STAGE[7] = layer3_attention


def rms_turned(nc, m, name, src, rows, tiles, gamma, dstT, scratch):
    per = 512 // rows if rows < 128 else 4
    groups = [(g, min(per, tiles - g)) for g in range(0, tiles, per)]
    with ExitStack() as ctx:
        g = m.sbuf(ctx, name + "_gamma", [128, KD])
        ss = m.sbuf(ctx, name + "_ss", [rows, tiles])
        S = {n: m.sem(f"{name}_{n}") for n in ("loaded", "squared", "summed", "rooted", "step", "scaled", "turned", "kept")}
        with nc.Block() as block:
            @block.sync
            def _(sp):
                sp.dma_start(g[:, :], gamma).then_inc(S["loaded"], 16)

            @block.vector
            def _(dve):
                nc.vector.tensor_tensor(scratch[:, :, :], src[:, :, :], src[:, :, :], ALU.mult).then_inc(S["squared"], 1)
                dve.wait_ge(S["squared"], 1)
                nc.vector.tensor_reduce(ss[:, :], scratch[:, :, :], AX.X, ALU.add).then_inc(S["summed"], 1)
                dve.wait_ge(S["rooted"], 1)
                nc.vector.tensor_scalar(ss[:, :], ss[:, :], 1e-12, None, ALU.max).then_inc(S["step"], 1)
                dve.wait_ge(S["step"], 1)
                nc.vector.reciprocal(ss[:, :], ss[:, :]).then_inc(S["step"], 1)
                dve.wait_ge(S["step"], 2)
                for t in range(tiles):
                    nc.vector.tensor_scalar(scratch[:, t, :], src[:, t, :], ss[:, t:t + 1], float(D) ** 0.5, ALU.mult,
                                            ALU.mult).then_inc(S["scaled"], 1)

            @block.scalar
            def _(act):
                act.wait_ge(S["summed"], 1)
                nc.scalar.activation(ss[:, :], ss[:, :], ACT.Sqrt).then_inc(S["rooted"], 1)
                act.wait_ge(S["loaded"], 16)
                for i, (t0, n) in enumerate(groups):
                    for k in range(KD):
                        act.wait_ge(S["turned"], KD * i + k + 1)
                        nc.scalar.activation(dstT[:, k, t0 * rows:(t0 + n) * rows], m.ps[:, (KD * i + k) % 8, :n * rows],
                                             ACT.Copy, scale=g[:, k:k + 1]).then_inc(S["kept"], 1)

            @block.tensor
            def _(pe):
                for i, (t0, n) in enumerate(groups):
                    pe.wait_ge(S["scaled"], t0 + n)
                    for k in range(KD):
                        b = KD * i + k
                        if b >= 8:
                            pe.wait_ge(S["kept"], b - 7)
                        for j in range(n):
                            mm = nc.tensor.transpose(m.ps[:, b % 8, j * rows:(j + 1) * rows],
                                                     scratch[:, t0 + j, k * 128:(k + 1) * 128], m.ident[:rows, :rows])
                        mm.then_inc(S["turned"], 1)


def combine_weights(nc, m, dram, slotsT, combT, csumT):
    E, SL = 8, 128
    with ExitStack() as ctx:
        b2 = m.sbuf(ctx, "l3c_b2", [E, D])
        p = m.sbuf(ctx, "l3c_p", [ROWS, 2, E, SL])
        mx = m.sbuf(ctx, "l3c_mx", [ROWS, TILES])
        den = m.sbuf(ctx, "l3c_den", [ROWS, TILES])
        csum = m.sbuf(ctx, "l3c_csum", [ROWS, TILES, E])
        S = {n: m.sem("l3c_" + n) for n in ("loaded", "scored", "max_found", "expd", "inverted", "normed", "csummed",
                                            "turned", "kept", "c_turned", "c_kept", "biased", "added")}
        with nc.Block() as block:
            @block.sync
            def _(sp):
                sp.dma_start(b2[:, :], dram["l3f_b2"]).then_inc(S["loaded"], 16)

            @block.tensor
            def _(pe):
                def score(t):
                    if t >= 2:
                        pe.wait_ge(S["expd"], t - 1)
                    for j in range(2):
                        for k in range(KD):
                            mm = nc.tensor.matmul(m.ps[:ROWS, 2 * (t % 2) + j, :], m.xT[:, k, tile_cols(t)],
                                                  slotsT[:, k, j * 512:(j + 1) * 512], start=(k == 0), stop=(k == KD - 1))
                    mm.then_inc(S["scored"], 1)

                def turn(t):
                    pe.wait_ge(S["normed"], t + 1)
                    if t >= 1:
                        pe.wait_ge(S["kept"], 2 * t)
                    for j in range(2):
                        for e in range(4):
                            mm = nc.tensor.transpose(m.ps[:, 4 + j, e * ROWS:(e + 1) * ROWS], p[:, t % 2, 4 * j + e, :],
                                                     m.ident[:ROWS, :ROWS])
                        mm.then_inc(S["turned"], 1)

                for t in range(TILES + 1):
                    if t < TILES:
                        score(t)
                    if t >= 1:
                        turn(t - 1)
                pe.wait_ge(S["csummed"], TILES)
                for g, (t0, n) in enumerate(GROUPS):
                    for j in range(n):
                        mm = nc.tensor.transpose(m.ps[:E, 6, j * ROWS:(j + 1) * ROWS], csum[:, t0 + j, :],
                                                 m.ident[:ROWS, :ROWS])
                    mm.then_inc(S["c_turned"], 1)
                    pe.wait_ge(S["c_kept"], g + 1)
                pe.wait_ge(S["loaded"], 16)
                for t in range(TILES):
                    if t >= 4:
                        pe.wait_ge(S["added"], t - 3)
                    nc.tensor.matmul(m.ps[:ROWS, t % 4, :D], csumT[:, tile_cols(t)], b2[:, :], start=True,
                                     stop=True).then_inc(S["biased"], 1)

            @block.scalar
            def _(act):
                def keep(t):
                    for j in range(2):
                        act.wait_ge(S["turned"], 2 * t + j + 1)
                        nc.scalar.activation(combT[:, 4 * j:4 * j + 4, tile_cols(t)],
                                             m.ps[:, 4 + j, :4 * ROWS].rearrange("p (e n) -> p e n", e=4),
                                             ACT.Copy).then_inc(S["kept"], 1)

                for t in range(TILES + 1):
                    if t < TILES:
                        act.wait_ge(S["max_found"], t + 1)
                        if t >= 2:
                            act.wait_ge(S["turned"], 2 * (t - 1))
                            act.wait_ge(S["csummed"], t - 1)
                        nc.scalar.activation(p[:, t % 2, :, :].rearrange("p e s -> p (e s)"),
                                             m.ps[:ROWS, 2 * (t % 2):2 * (t % 2) + 2, :].rearrange("p b s -> p (b s)"),
                                             ACT.Exp, bias=mx[:, t:t + 1],
                                             accum_out=den[:, t:t + 1]).then_inc(S["expd"], 1)
                    if t >= 1:
                        keep(t - 1)
                for g, (t0, n) in enumerate(GROUPS):
                    act.wait_ge(S["c_turned"], g + 1)
                    nc.scalar.activation(csumT[:, t0 * ROWS:(t0 + n) * ROWS], m.ps[:E, 6, :n * ROWS],
                                         ACT.Copy).then_inc(S["c_kept"], 1)

            @block.vector
            def _(dve):
                def norm(t):
                    dve.wait_ge(S["expd"], t + 1)
                    nc.vector.reciprocal(den[:, t:t + 1], den[:, t:t + 1]).then_inc(S["inverted"], 1)
                    dve.wait_ge(S["inverted"], t + 1)
                    nc.vector.tensor_scalar(p[:, t % 2, :, :], p[:, t % 2, :, :], den[:, t:t + 1], None,
                                            ALU.mult).then_inc(S["normed"], 1)
                    dve.wait_ge(S["normed"], t + 1)
                    nc.vector.tensor_reduce(csum[:, t, :], p[:, t % 2, :, :], AX.X, ALU.add).then_inc(S["csummed"], 1)

                for t in range(TILES + 1):
                    if t < TILES:
                        dve.wait_ge(S["scored"], t + 1)
                        nc.vector.tensor_reduce(mx[:, t:t + 1], m.ps[:ROWS, 2 * (t % 2):2 * (t % 2) + 2, :], AX.XY, ALU.max,
                                                negate=True).then_inc(S["max_found"], 1)
                    if t >= 1:
                        norm(t - 1)
                for t in range(TILES):
                    dve.wait_ge(S["biased"], t + 1)
                    nc.vector.tensor_tensor(m.h[:, t, :], m.ps[:ROWS, t % 4, :D], m.h[:, t, :],
                                            ALU.add).then_inc(S["added"], 1)


def dispatch_weights(nc, m, slotsT, disp):
    E = 8
    SEQS3 = NSEQ // 3
    with ExitStack() as ctx:
        mx = m.sbuf(ctx, "l3d_mx", [128, 3, NSEQ])
        den = m.sbuf(ctx, "l3d_den", [128, 3, NSEQ])
        S = {n: m.sem("l3d_" + n) for n in ("scored", "max_found", "shifted", "expd", "summed", "inverted", "normed")}

        def bank(x, c):
            return x[:, c * THIRD:(c + 1) * THIRD].rearrange("p (s t) -> p s t", t=T)

        def over_t(x, c=None):
            n = NSEQ if c is None else SEQS3
            x = x if c is None else x[:, c * SEQS3:(c + 1) * SEQS3]
            return x.rearrange("p (s o) -> p s o", o=1).broadcast_to([128, n, T])

        with nc.Block() as block:
            @block.tensor
            def _(pe):
                for e in range(E):
                    if e >= 2:
                        pe.wait_ge(S["shifted"], 3 * (e - 1))
                    for c in range(3):
                        for k in range(KD):
                            mm = nc.tensor.matmul(m.ps[:, 3 * (e % 2) + c, :THIRD], slotsT[:, k, e * 128:(e + 1) * 128],
                                                  m.xT[:, k, third(c)], start=(k == 0), stop=(k == KD - 1))
                    mm.then_inc(S["scored"], 1)

            @block.scalar
            def _(act):
                for e in range(E):
                    act.wait_ge(S["shifted"], 3 * (e + 1))
                    nc.scalar.activation(disp[:, e, :], disp[:, e, :], ACT.Exp).then_inc(S["expd"], 1)

            @block.vector
            def _(dve):
                def finish(e):
                    dve.wait_ge(S["expd"], e + 1)
                    nc.vector.tensor_reduce(den[:, e % 3, :], disp[:, e, :].rearrange("p (s t) -> p s t", t=T), AX.X,
                                            ALU.add).then_inc(S["summed"], 1)
                    dve.wait_ge(S["summed"], e + 1)
                    nc.vector.reciprocal(den[:, e % 3, :], den[:, e % 3, :]).then_inc(S["inverted"], 1)

                for e in range(E + 1):
                    if e < E:
                        dve.wait_ge(S["scored"], e + 1)
                        logits = m.ps[:, 3 * (e % 2):3 * (e % 2) + 3, :THIRD]
                        nc.vector.tensor_reduce(mx[:, e % 3, :], logits.rearrange("p c (s t) -> p c s t", t=T), AX.X,
                                                ALU.max).then_inc(S["max_found"], 1)
                        dve.wait_ge(S["max_found"], e + 1)
                        for c in range(3):
                            nc.vector.tensor_tensor(bank(disp[:, e, :], c),
                                                    m.ps[:, 3 * (e % 2) + c, :THIRD].rearrange("p (s t) -> p s t", t=T),
                                                    over_t(mx[:, e % 3, :], c), ALU.subtract).then_inc(S["shifted"], 1)
                    if e >= 1:
                        if e - 1 >= 3:
                            dve.wait_ge(S["normed"], e - 3)
                        finish(e - 1)

            @block.gpsimd
            def _(pool):
                for e in range(E):
                    pool.wait_ge(S["inverted"], e + 1)
                    x = disp[:, e, :].rearrange("p (s t) -> p s t", t=T)
                    nc.gpsimd.tensor_tensor(x, x, over_t(den[:, e % 3, :]), ALU.mult).then_inc(S["normed"], 1)


def soft_experts(nc, m, dram, combT, disp):
    E, F, SL = 8, 1024, 128
    KF = F // 128
    HALF = 512
    PAIR = 2 * TILES
    with ExitStack() as ctx:
        w1 = [m.sbuf(ctx, f"l3f_w1_{p}", [128, KD, F]) for p in range(2)]
        w2 = [m.sbuf(ctx, f"l3f_w2_{p}", [128, KF, D]) for p in range(2)]
        b1 = [m.sbuf(ctx, f"l3f_b1_{p}", [ROWS, F]) for p in range(2)]
        up = m.sbuf(ctx, "l3f_up", [ROWS, 2, F])
        diag = m.sbuf(ctx, "l3f_diag", [128, 2, SEQ * ROWS])
        to_slots = m.sbuf(ctx, "l3f_to_slots", [ROWS, 2, SEQ * SL])
        hid = m.sbuf(ctx, "l3f_hid", [128, 2, F])
        backT = m.sbuf(ctx, "l3f_backT", [128, 2, KF, ROWS])
        w_loaded = [m.sem(f"l3f_w_loaded{p}") for p in range(2)]
        cleared = m.sem("l3f_cleared")
        counts = {"up_made": 2 * PAIR, "up_kept": 2 * PAIR, "diag_set": PAIR, "d_turned": PAIR, "d_kept": PAIR,
                  "raised": 3 * PAIR, "gelued": 3 * PAIR, "drawn": 3 * PAIR, "back_kept": PAIR, "lowered": PAIR,
                  "added": PAIR}
        S = {n: m.sem("l3f_" + n) for n in counts}

        def wait(eng, i, name, n):
            eng.wait_ge(S[name], i * counts[name] + counts[name] + n)

        def start(eng, *names):
            for n in names:
                eng.sem_inc(S[n], counts[n])

        with nc.Block() as block:
            @block.sync
            def _(sp):
                with sp.Fori(0, E // 2) as i:
                    for p in range(2):
                        wait(sp, i, "lowered", (p + 1) * TILES - PAIR)
                        e = ds(2 * i + p)
                        sp.dma_start(w1[p][:, :, :], dram["l3f_w1"][e].rearrange("o (k p) n -> p (o k) n", p=128)).then_inc(w_loaded[p], 16)
                        sp.dma_start(w2[p][:, :, :], dram["l3f_w2"][e].rearrange("o (k p) n -> p (o k) n", p=128)).then_inc(w_loaded[p], 16)
                        sp.dma_start(b1[p][:, :], dram["l3f_b1"][e].broadcast_to([ROWS, F])).then_inc(w_loaded[p], 16)

            @block.tensor
            def _(pe):
                start(pe, "up_made", "d_turned", "raised", "drawn", "lowered")
                with pe.Fori(0, E // 2) as i:
                    def raise_tokens(c, half):
                        p, t = divmod(c, TILES)
                        if t == 0 and half == 0:
                            pe.wait_ge(w_loaded[p], i * 48 + 48)
                        wait(pe, i, "up_kept", 2 * c + half)
                        for k in range(KD):
                            mm = nc.tensor.matmul(m.ps[:ROWS, 6, :], m.xT[:, k, tile_cols(t)],
                                                  w1[p][:, k, half * HALF:(half + 1) * HALF], start=(k == 0),
                                                  stop=(k == KD - 1))
                        mm.then_inc(S["up_made"], 1)

                    def turn_disp(c):
                        wait(pe, i, "diag_set", c + 1)
                        wait(pe, i, "d_kept", c)
                        wait(pe, i, "added", max(c - 1, 0))
                        for b in range(SEQ):
                            mm = nc.tensor.transpose(m.ps[:ROWS, 7, b * SL:(b + 1) * SL],
                                                     diag[:, c % 2, b * ROWS:(b + 1) * ROWS], m.ident[:, :])
                        mm.then_inc(S["d_turned"], 1)

                    def raise_slots(n):
                        c, b = divmod(n, SEQ)
                        if b == 0:
                            wait(pe, i, "up_kept", 2 * c + 2)
                            wait(pe, i, "d_kept", c + 1)
                        wait(pe, i, "gelued", n - 1)
                        for half in range(2):
                            mm = nc.tensor.matmul(m.ps[:, 2 * (n % 2) + half, :], to_slots[:, c % 2, b * SL:(b + 1) * SL],
                                                  up[:, c % 2, half * HALF:(half + 1) * HALF], start=True, stop=True)
                        mm.then_inc(S["raised"], 1)

                    def draw(n):
                        c, b = divmod(n, SEQ)
                        p, t = divmod(c, TILES)
                        wait(pe, i, "gelued", n + 1)
                        if b == 0:
                            wait(pe, i, "back_kept", c)
                        own = slice(t * ROWS + b * T, t * ROWS + (b + 1) * T)
                        for f in range(KF):
                            col = (f % 4) * ROWS + b * T
                            mm = nc.tensor.matmul(m.ps[:, 4 + f // 4, col:col + T], hid[:, n % 2, f * 128:(f + 1) * 128],
                                                  combT[:, ds(2 * i + p), own], start=True, stop=True)
                        mm.then_inc(S["drawn"], 1)

                    def lower(c):
                        p = c // TILES
                        wait(pe, i, "back_kept", c + 1)
                        if c + 1 < PAIR:
                            wait(pe, i, "d_kept", c + 2)
                        else:
                            wait(pe, i, "added", c)
                        for f in range(KF):
                            mm = nc.tensor.matmul(m.ps[:ROWS, 7, :D], backT[:, c % 2, f, :], w2[p][:, f, :],
                                                  start=(f == 0), stop=(f == KF - 1))
                        mm.then_inc(S["lowered"], 1)

                    raise_tokens(0, 0)
                    turn_disp(0)
                    raise_tokens(0, 1)
                    for c in range(PAIR):
                        for b in range(SEQ):
                            n = SEQ * c + b
                            raise_slots(n)
                            if b == 0 and c + 1 < PAIR:
                                raise_tokens(c + 1, 0)
                            if b == 1 and c >= 1:
                                lower(c - 1)
                            if b == 2 and c + 1 < PAIR:
                                turn_disp(c + 1)
                                raise_tokens(c + 1, 1)
                            if n >= 1:
                                draw(n - 1)
                    draw(SEQ * PAIR - 1)
                    lower(PAIR - 1)

            @block.scalar
            def _(act):
                def keep_back(act, i, c):
                    wait(act, i, "drawn", SEQ * (c + 1))
                    wait(act, i, "lowered", c - 1)
                    nc.scalar.activation(backT[:, c % 2, :, :].rearrange("p (b f) n -> p b (f n)", b=2),
                                         m.ps[:, 4:6, :4 * ROWS], ACT.Copy).then_inc(S["back_kept"], 1)

                start(act, "gelued", "back_kept")
                with act.Fori(0, E // 2) as i:
                    for n in range(SEQ * PAIR):
                        wait(act, i, "raised", n + 1)
                        wait(act, i, "drawn", n - 1)
                        nc.scalar.activation(hid[:, n % 2, :],
                                             m.ps[:, 2 * (n % 2):2 * (n % 2) + 2, :].rearrange("p b s -> p (b s)"),
                                             ACT.Gelu).then_inc(S["gelued"], 1)
                        if n % SEQ == 0 and n >= SEQ:
                            keep_back(act, i, n // SEQ - 1)
                    keep_back(act, i, PAIR - 1)

            @block.vector
            def _(dve):
                start(dve, "up_kept", "diag_set", "d_kept", "added")
                nc.vector.memset(diag[:, :, :], 0.0).then_inc(cleared, 1)
                dve.wait_ge(cleared, 1)
                with dve.Fori(0, E // 2) as i:
                    def set_diag(c):
                        p, t = divmod(c, TILES)
                        wait(dve, i, "d_turned", c - 1)
                        out = diag[:, c % 2, :].rearrange("p (b s t) -> p b s t", b=SEQ, s=SEQ)
                        for b in range(SEQ):
                            own = slice(t * ROWS + b * T, t * ROWS + (b + 1) * T)
                            ins = nc.vector.tensor_scalar(out[:, b, b, :], disp[:, ds(2 * i + p), own], 1.0, None, ALU.mult)
                        ins.then_inc(S["diag_set"], 1)

                    def keep_up(c, half):
                        p = c // TILES
                        if half == 0:
                            wait(dve, i, "raised", SEQ * (c - 1))
                        wait(dve, i, "up_made", 2 * c + half + 1)
                        cols = slice(half * HALF, (half + 1) * HALF)
                        nc.vector.tensor_tensor(up[:, c % 2, cols], m.ps[:ROWS, 6, :], b1[p][:, cols],
                                                ALU.add).then_inc(S["up_kept"], 1)

                    def keep_disp(c):
                        wait(dve, i, "d_turned", c + 1)
                        wait(dve, i, "raised", SEQ * (c - 1))
                        nc.vector.tensor_copy(to_slots[:, c % 2, :], m.ps[:ROWS, 7, :SEQ * SL]).then_inc(S["d_kept"], 1)

                    def add(c):
                        t = c % TILES
                        wait(dve, i, "lowered", c + 1)
                        wait(dve, i, "added", c)
                        nc.vector.tensor_tensor(m.h[:, t, :], m.ps[:ROWS, 7, :D], m.h[:, t, :],
                                                ALU.add).then_inc(S["added"], 1)

                    set_diag(0)
                    keep_up(0, 0)
                    keep_disp(0)
                    keep_up(0, 1)
                    for c in range(PAIR):
                        if c + 1 < PAIR:
                            set_diag(c + 1)
                            keep_up(c + 1, 0)
                        if c >= 1:
                            add(c - 1)
                        if c + 1 < PAIR:
                            keep_disp(c + 1)
                            keep_up(c + 1, 1)
                    add(PAIR - 1)


def layer3_ffn(nc, m, dram):
    normalise(nc, m, "l3f_ln", m.h, turn=False)
    with ExitStack() as ctx:
        combT = m.sbuf(ctx, "l3f_combT", [128, 8, COLS])
        disp = m.sbuf(ctx, "l3f_disp", [128, 8, COLS])
        with ExitStack() as early:
            slots = m.sbuf(early, "l3f_slots", [128, 8, D])
            slotsT = m.sbuf(early, "l3f_slotsT", [128, KD, 8 * 128])
            csumT = m.sbuf(early, "l3f_csumT", [8, COLS])
            scratch = m.sbuf(early, "l3f_scratch", [ROWS, TILES, D])
            slot_scratch = m.sbuf(early, "l3f_slot_scratch", [128, 8, D])
            loaded = m.sem("l3f_slots_loaded")
            with nc.Block() as block:
                @block.sync
                def _(sp):
                    sp.dma_start(slots[:, :, :], dram["l3f_slots"].rearrange("e s d -> s e d")).then_inc(loaded, 16)
                    sp.wait_ge(loaded, 16)
            rms_turned(nc, m, "l3r", m.xn, ROWS, TILES, dram["l3f_gamma"], m.xT, scratch)
            rms_turned(nc, m, "l3s", slots, 128, 8, dram["l3f_slot_gamma"], slotsT, slot_scratch)
            combine_weights(nc, m, dram, slotsT, combT, csumT)
            dispatch_weights(nc, m, slotsT, disp)
        soft_experts(nc, m, dram, combT, disp)


STAGE[8] = layer3_ffn


def arranged(x):
    import numpy as np
    C = np.ascontiguousarray
    a = {k: np.asarray(v) for k, v in x.items()}
    out = {}
    B = a["x"].shape[0]
    p = a["x"].reshape(B, 3, 6, 16, 6, 16).transpose(1, 3, 5, 0, 2, 4).reshape(768, B, T - 1)
    patches = np.zeros((768, NSEQ, T), np.float32)
    patches[:, :B, 1:] = p
    out["patchesT"] = patches.reshape(768, COLS)
    out["tok_wT"] = C(a["L0_tok_W"].T)
    one = np.concatenate([a["L0_tok_cls_token"].reshape(1, D), np.repeat(a["L0_tok_b"].reshape(1, D), T - 1, axis=0)])
    out["tok_base"] = np.concatenate([one] * SEQ)
    out["tok_pos"] = np.concatenate([a["L0_tok_pos_embed"].reshape(T, D)] * SEQ)
    cols = lambda v: C(v.reshape(-1, 128).T)
    row = lambda v: v.reshape(1, -1)
    out["c_ident"] = np.eye(128, dtype=np.float32)
    DH = 16
    spread = np.zeros((128, DH, 128), np.float32)
    for j in range(128):
        for e in range(DH):
            spread[(j // DH) * DH + e, e, j] = 1.0
    out["c_spread"] = spread
    out["c_gather"] = C(spread.transpose(2, 1, 0))
    seq = np.arange(ROWS) // T
    out["c_mask"] = np.tile(np.where(seq[:, None] == seq[None, :], 0.0, -1e30).astype(np.float32), (1, 4))
    late = (seq[:, None] == seq[None, :]) & (np.arange(ROWS)[:, None] <= np.arange(ROWS)[None, :])
    out["c_causal"] = np.tile(np.where(late, 0.0, -1e30).astype(np.float32), (1, 4))
    rows8 = np.zeros((8, 8, 128), np.float32)
    for h in range(8):
        rows8[h, h, :] = 1.0
    out["c_rows8"] = rows8
    out["l0a_kwT"] = C(a["L0_attn_key_w"].T)
    out["l0a_vqT"] = C(a["L0_attn_vq_w"].T)
    out["l0a_owT"] = C(a["L0_attn_out_w"].T)
    out["l0a_kb"] = cols(a["L0_attn_key_b"])
    out["l0a_ob"] = row(a["L0_attn_out_b"])
    out["l0f_gwT"] = C(a["L0_ffn_router_weight"].T)
    out["l0f_gb"] = row(a["L0_ffn_router_bias"])
    out["l0f_ew"] = a["L0_ffn_weight"]
    out["l0f_eb"] = a["L0_ffn_bias"]
    for n in ("DQ", "DKV", "KR"):
        out["l1a_w" + n] = a["L1_attn_W_" + n]
        out["l1a_b" + n] = C(a["L1_attn_b_" + n].reshape(-1, 1))
    out["l1a_wUQ"] = a["L1_attn_W_UQ"]
    out["l1a_wUK"] = a["L1_attn_W_UK"]
    out["l1a_wUV"] = a["L1_attn_W_UV"]
    out["l1a_wQR"] = a["L1_attn_W_QR"]
    out["l1a_bUQ"] = cols(a["L1_attn_b_UQ"])
    out["l1a_bUK"] = cols(a["L1_attn_b_UK"])
    out["l1a_bUV"] = row(a["L1_attn_b_UV"])
    out["l1a_bQR"] = C(a["L1_attn_b_QR"].reshape(8, 32).T)
    out["l1a_wO"] = a["L1_attn_W_O"]
    out["l1a_bO"] = row(a["L1_attn_b_O"])
    out["l1f_gwT"] = C(a["L1_ffn_gate_w"].T)
    out["l1f_gb"] = row(a["L1_ffn_gate_b"])
    out["l1f_ew"] = a["L1_ffn_expert_w"]
    out["l1f_eb"] = a["L1_ffn_expert_b"]
    w = C(a["L2_attn_in_proj_w"].T)
    out["l2a_wz"], out["l2a_wx"] = C(w[:, :512]), C(w[:, 512:1024])
    out["l2a_wdt"], out["l2a_wB"], out["l2a_wC"] = C(w[:, 1024:1032]), C(w[:, 1032:1096]), C(w[:, 1096:1160])
    out["l2a_conv_w"] = C(a["L2_attn_conv_w"].reshape(4, 128, 4).transpose(1, 0, 2))
    out["l2a_conv_b"] = cols(a["L2_attn_conv_b"])
    out["l2a_A_log"] = C(a["L2_attn_A_log"].reshape(8, 1))
    out["l2a_dt_bias"] = C(a["L2_attn_dt_bias"].reshape(8, 1))
    out["l2a_D"] = C(np.broadcast_to(a["L2_attn_D_param"].reshape(1, 8, 1), (ROWS, 8, 64)).reshape(ROWS, 512))
    out["l2a_norm_w"] = cols(a["L2_attn_norm_w"])
    out["l2a_owT"] = C(a["L2_attn_out_proj_w"].T)
    for i in "12":
        out["l2f_ln" + i] = C(np.stack([a[f"L2_ffn_ln{i}_g"].reshape(2, 128), a[f"L2_ffn_ln{i}_b"].reshape(2, 128)]).transpose(2, 0, 1))
    for n in ("Wq", "Wk", "Wv", "Wo"):
        out["l2f_" + n] = a["L2_ffn_" + n]
    out["c_heads"] = np.repeat(np.eye(8, dtype=np.float32), 16, axis=0)
    out["l2g_gw"], out["l2g_gb"] = a["L2_ffn_Wg"], np.zeros((1, 8), np.float32)
    out["l2m_w1"], out["l2m_w2"] = a["L2_ffn_W1"], a["L2_ffn_W2"]
    out["l2m_b1"] = C(a["L2_ffn_b1"].reshape(8, 8, 128).transpose(0, 2, 1))
    out["l2m_b2"] = a["L2_ffn_b2"]
    for n in ("Wq", "Wk", "Wv", "Wg", "Wgk1", "Wgk2", "Wout"):
        out["l3a_" + n] = a["L3_attn_" + n]
    out["l3a_bgk2"] = cols(a["L3_attn_bgk2"])
    out["l3a_norm"] = C(np.stack([a["L3_attn_gamma"].reshape(2, 128), a["L3_attn_beta"].reshape(2, 128)]).transpose(2, 0, 1))
    out["l3f_gamma"] = cols(a["L3_ffn_norm_gamma"])
    out["l3f_slot_gamma"] = cols(a["L3_ffn_slot_norm_gamma"])
    out["l3f_slots"] = a["L3_ffn_slot_embeds"]
    out["l3f_w1"], out["l3f_w2"] = a["L3_ffn_w1"], a["L3_ffn_w2"]
    out["l3f_b1"] = a["L3_ffn_b1"]
    out["l3f_b2"] = a["L3_ffn_b2"]
    return {k: C(v) for k, v in out.items()}


def store(nc, m, out):
    whole = TILES - 1
    rows = out.rearrange("b t d -> (b t) d")
    left = rows.shape[0] - whole * ROWS
    stored = m.sem("stored")
    with nc.Block() as block:
        @block.sync
        def _(sp):
            sp.dma_start(rows[:whole * ROWS, :].rearrange("(t p) d -> p t d", p=ROWS), m.h[:, :whole, :]).then_inc(stored, 16)
            sp.dma_start(rows[whole * ROWS:, :], m.h[:left, whole, :]).then_inc(stored, 16)
            sp.wait_ge(stored, 32)


def vit_tower(nc, dram, out):
    with ExitStack() as ctx:
        m = Memory(nc, ctx)
        constants(nc, m, dram)
        for stage in sorted(STAGE):
            STAGE[stage](nc, m, dram)
            m.end_stage()
        store(nc, m, out)


def kernel(**inputs):
    import numpy as _np
    import concourse.bacc as _bacc
    from concourse import mybir as _mybir
    from concourse.bass_utils import run_bass_kernel_spmd as _run

    nc = _bacc.Bacc("TRN2", target_bir_lowering=False, num_devices=1)
    arrays, dram = {}, {}
    for name, a in arranged(inputs).items():
        arrays[f"in_{name}_dram"] = a
        dram[name] = nc.dram_tensor(f"in_{name}_dram", a.shape, _mybir.dt.from_np(a.dtype), kind="ExternalInput").ap()
    shape = (inputs["x"].shape[0], T, D)
    out = nc.dram_tensor("out_0_dram", shape, F32, kind="ExternalOutput").ap()
    vit_tower(nc, dram, out)
    r = _run(nc, [arrays], core_ids=[0])
    return r.results[0]["out_0_dram"]
```

```python
from contextlib import ExitStack

import concourse.bass as bass
from concourse import mybir

F32 = mybir.dt.float32
F32R = mybir.dt.float32r
PASSES = ((0, 0), (0, 1), (1, 0))
ACT = mybir.ActivationFunctionType
ALU = mybir.AluOpType
AX = mybir.AxisListType

T = 37
SEQ = 3
ROWS = SEQ * T
TILES = 11
COLS = ROWS * TILES
NSEQ = COLS // T
THIRD = COLS // 3
D = 256
KD = D // 128
GROUPS = [(0, 4), (4, 4), (8, 3)]
LN_EPS = 1e-5


class Memory:

    def __init__(self, nc, ctx):
        self.nc, self.ctx, self.sems = nc, ctx, []
        self.h = self.sbuf(ctx, "h", [ROWS, TILES, D])
        self.xn = self.sbuf(ctx, "xn", [ROWS, TILES, D])
        self.xT = self.sbuf(ctx, "xT", [128, KD, COLS])
        self.ident = self.sbuf(ctx, "ident", [128, 128])
        self.ones = self.sbuf(ctx, "ones", [1, 128])
        self.ps = ctx.enter_context(nc.psum_tensor("ps", [128, 8, 512], F32))

    def sbuf(self, ctx, name, shape, dtype=F32):
        return ctx.enter_context(self.nc.sbuf_tensor(name, shape, dtype))

    def pair(self, ctx, name, shape):
        return [self.sbuf(ctx, name + part, shape, F32R) for part in ("_hi", "_lo")]

    def sem(self, name):
        self.sems.append(self.nc.alloc_semaphore(name))
        return self.sems[-1]

    def end_stage(self):
        self.nc.clear_and_free_semaphores(self.sems)
        self.nc.all_engine_barrier()
        self.sems = []


def tile_cols(t):
    return slice(t * ROWS, (t + 1) * ROWS)


def third(c):
    return slice(c * THIRD, (c + 1) * THIRD)


EVEN = 2 * -(-COLS // 6)


def part(c):
    return slice(c * EVEN, min((c + 1) * EVEN, COLS))


def even_part(c):
    return slice(c * EVEN, min((c + 1) * EVEN, COLS + 1))


def width(cols):
    return cols.stop - cols.start


def constants(nc, m, dram):
    loaded = m.sem("const_loaded")
    ones_set = m.sem("const_ones")
    with nc.Block() as block:
        @block.sync
        def _(sp):
            sp.dma_start(m.ident[:, :], dram["c_ident"]).then_inc(loaded, 16)
            sp.wait_ge(loaded, 16)

        @block.vector
        def _(dve):
            nc.vector.memset(m.ones[:, :], 1.0).then_inc(ones_set, 1)
            dve.wait_ge(ones_set, 1)


def tokens(nc, m, dram):
    K = 6
    with ExitStack() as ctx:
        patches = m.sbuf(ctx, "tok_patches", [128, K, COLS])
        w = m.sbuf(ctx, "tok_w", [128, K, D])
        base = m.sbuf(ctx, "tok_base", [ROWS, D])
        pos = m.sbuf(ctx, "tok_pos", [ROWS, D])
        loaded = [m.sem(f"tok_loaded{k}") for k in range(K)]
        base_loaded = m.sem("tok_base_loaded")
        base_summed = m.sem("tok_base_summed")
        projected = m.sem("tok_projected")
        stored = m.sem("tok_stored")
        with nc.Block() as block:
            @block.sync
            def _(sp):
                for k in range(K):
                    sp.dma_start(patches[:, k, :], dram["patchesT"][k * 128:(k + 1) * 128, :]).then_inc(loaded[k], 16)
                    sp.dma_start(w[:, k, :], dram["tok_wT"][k * 128:(k + 1) * 128, :]).then_inc(loaded[k], 16)
                sp.dma_start(base[:, :], dram["tok_base"]).then_inc(base_loaded, 16)
                sp.dma_start(pos[:, :], dram["tok_pos"]).then_inc(base_loaded, 16)

            @block.tensor
            def _(pe):
                for t in range(TILES):
                    if t >= 4:
                        pe.wait_ge(stored, t - 3)
                    for k in range(K):
                        if t == 0:
                            pe.wait_ge(loaded[k], 32)
                        mm = nc.tensor.matmul(m.ps[:ROWS, t % 4, :D], patches[:, k, tile_cols(t)], w[:, k, :],
                                              start=(k == 0), stop=(k == K - 1))
                    mm.then_inc(projected, 1)

            @block.vector
            def _(dve):
                dve.wait_ge(base_loaded, 32)
                nc.vector.tensor_tensor(base[:, :], base[:, :], pos[:, :], ALU.add).then_inc(base_summed, 1)
                dve.wait_ge(base_summed, 1)
                for t in range(TILES):
                    dve.wait_ge(projected, t + 1)
                    nc.vector.tensor_tensor(m.h[:, t, :], m.ps[:ROWS, t % 4, :D], base[:, :],
                                            ALU.add).then_inc(stored, 1)


def normalise(nc, m, name, src, tok=None, dstT=None, eps=LN_EPS, affine=None, turn=True):
    tok = m.xn if tok is None else tok
    dstT = m.xT if dstT is None else dstT
    with ExitStack() as ctx:
        stats = m.sbuf(ctx, name + "_stats", [ROWS, TILES, 6])
        mv = m.sbuf(ctx, name + "_mv", [ROWS, TILES, 2])
        std = m.sbuf(ctx, name + "_std", [ROWS, TILES])
        rstd = m.sbuf(ctx, name + "_rstd", [ROWS, TILES])
        gb = m.sbuf(ctx, name + "_gb", [128, 2, KD])
        counted = m.sem(name + "_counted")
        varred = m.sem(name + "_var")
        rooted = m.sem(name + "_rooted")
        inverted = m.sem(name + "_inverted")
        centred = m.sem(name + "_centred")
        turned = m.sem(name + "_turned")
        kept = m.sem(name + "_kept")
        gb_loaded = m.sem(name + "_gb_loaded")
        with nc.Block() as block:
            @block.sync
            def _(sp):
                if affine is not None:
                    sp.dma_start(gb[:, :, :], affine).then_inc(gb_loaded, 16)

            @block.vector
            def _(dve):
                for t in range(TILES):
                    nc.vector.bn_stats(stats[:, t, :], src[:, t, :]).then_inc(counted, 1)
                for t in range(TILES):
                    dve.wait_ge(counted, t + 1)
                    nc.vector.bn_aggr(mv[:, t, :], stats[:, t, :]).then_inc(varred, 1)
                dve.wait_ge(varred, TILES)
                nc.vector.tensor_scalar(std[:, :], mv[:, :, 1], eps, None, ALU.add).then_inc(varred, 1)
                dve.wait_ge(rooted, 1)
                nc.vector.reciprocal(rstd[:, :], std[:, :]).then_inc(inverted, 1)
                dve.wait_ge(inverted, 1)
                for t in range(TILES):
                    nc.vector.tensor_scalar(tok[:, t, :], src[:, t, :], mv[:, t, 0:1], rstd[:, t:t + 1],
                                            ALU.subtract, ALU.mult).then_inc(centred, 1)

            @block.scalar
            def _(act):
                act.wait_ge(varred, TILES + 1)
                nc.scalar.activation(std[:, :], std[:, :], ACT.Sqrt).then_inc(rooted, 1)
                if affine is not None:
                    act.wait_ge(gb_loaded, 16)
                for g, (t0, n) in enumerate(GROUPS if turn else []):
                    for k in range(KD):
                        i = g * KD + k
                        act.wait_ge(turned, i + 1)
                        out = dstT[:, k, t0 * ROWS:(t0 + n) * ROWS]
                        if affine is None:
                            nc.scalar.activation(out, m.ps[:, i, :n * ROWS], ACT.Copy).then_inc(kept, 1)
                        else:
                            nc.scalar.activation(out, m.ps[:, i, :n * ROWS], ACT.Identity, scale=gb[:, 0, k:k + 1],
                                                 bias=gb[:, 1, k:k + 1]).then_inc(kept, 1)

            @block.tensor
            def _(pe):
                for g, (t0, n) in enumerate(GROUPS if turn else []):
                    pe.wait_ge(centred, t0 + n)
                    for k in range(KD):
                        for j in range(n):
                            mm = nc.tensor.transpose(m.ps[:, g * KD + k, j * ROWS:(j + 1) * ROWS],
                                                     tok[:, t0 + j, k * 128:(k + 1) * 128], m.ident[:ROWS, :ROWS])
                        mm.then_inc(turned, 1)


def decayed_sums(nc, m, dram):
    H, DH = 16, 16
    with ExitStack() as ctx:
        wk = m.sbuf(ctx, "l0a_wk", [128, KD, D])
        wv = m.sbuf(ctx, "l0a_wv", [128, KD, 2 * D])
        wo = m.sbuf(ctx, "l0a_wo", [128, KD, D])
        kb = m.sbuf(ctx, "l0a_kb", [128, KD])
        ob = m.sbuf(ctx, "l0a_ob", [1, D])
        spread_raw = m.sbuf(ctx, "l0a_spread_raw", [128, DH, 128])
        spread = m.sbuf(ctx, "l0a_spread", [128, DH, 128], F32R)
        gather = m.sbuf(ctx, "l0a_gather", [128, DH, 128])
        kT = m.sbuf(ctx, "l0a_kT", [128, KD, COLS])
        omk = m.sbuf(ctx, "l0a_omk", [128, KD, COLS])
        vT = m.pair(ctx, "l0a_vT", [128, KD, COLS + 1])
        qT = m.sbuf(ctx, "l0a_qT", [128, KD, COLS])
        upd = m.sbuf(ctx, "l0a_upd", [128, 2, COLS])
        state = m.sbuf(ctx, "l0a_state", [128, 2, COLS])
        read = m.sbuf(ctx, "l0a_read", [128, 2, COLS])
        oT = m.sbuf(ctx, "l0a_oT", [128, KD, COLS])
        w_loaded = m.sem("l0a_w_loaded")
        c_loaded = m.sem("l0a_c_loaded")
        projected = m.sem("l0a_projected")
        kept = m.sem("l0a_kept")
        padded = m.sem("l0a_padded")
        v_low = m.sem("l0a_v_low")
        spread_rounded = m.sem("l0a_spread_rounded")
        complemented = m.sem("l0a_complemented")
        cut = m.sem("l0a_cut")
        spread_done = m.sem("l0a_spread_done")
        updated = m.sem("l0a_updated")
        scanned = m.sem("l0a_scanned")
        was_read = m.sem("l0a_was_read")
        gathered = m.sem("l0a_gathered")
        o_kept = m.sem("l0a_o_kept")
        out_done = m.sem("l0a_out_done")
        added = m.sem("l0a_added")
        jobs = [(wk, 0, kT, 0), (wk, 128, kT, 1), (wv, 0, vT[0], 0), (wv, 128, vT[0], 1), (wv, 256, qT, 0), (wv, 384, qT, 1)]
        STEPS = KD * DH
        with nc.Block() as block:
            @block.sync
            def _(sp):
                sp.dma_start(wk[:, :, :], dram["l0a_kwT"].rearrange("(k p) n -> p k n", p=128)).then_inc(w_loaded, 16)
                sp.dma_start(wv[:, :, :], dram["l0a_vqT"].rearrange("(k p) n -> p k n", p=128)).then_inc(w_loaded, 16)
                sp.dma_start(kb[:, :], dram["l0a_kb"]).then_inc(w_loaded, 16)
                sp.dma_start(spread_raw[:, :, :], dram["c_spread"]).then_inc(c_loaded, 16)
                sp.dma_start(gather[:, :, :], dram["c_gather"]).then_inc(c_loaded, 16)
                sp.dma_start(wo[:, :, :], dram["l0a_owT"].rearrange("(k p) n -> p k n", p=128)).then_inc(c_loaded, 16)
                sp.dma_start(ob[:, :], dram["l0a_ob"]).then_inc(c_loaded, 16)

            @block.tensor
            def _(pe):
                pe.wait_ge(w_loaded, 48)
                for j, (w, col, _, _) in enumerate(jobs):
                    if j >= 2:
                        pe.wait_ge(kept, j - 1)
                    if j >= 4:
                        pe.wait_ge(v_low, j - 3)
                    for c in range(3):
                        for k in range(KD):
                            mm = nc.tensor.matmul(m.ps[:, 3 * (j % 2) + c, :THIRD], w[:, k, col:col + 128],
                                                  m.xT[:, k, third(c)], start=(k == 0), stop=(k == KD - 1))
                    mm.then_inc(projected, 1)
                pe.wait_ge(kept, len(jobs))
                pe.wait_ge(v_low, 2)
                pe.wait_ge(spread_rounded, 1)

                def sum_up(i):
                    pe.wait_ge(was_read, i + 1)
                    if i == DH:
                        pe.wait_ge(o_kept, 3)
                    for c in range(3):
                        mm = nc.tensor.matmul(m.ps[:, 5 + c, :THIRD], gather[:, i % DH, :], read[:, i % 2, third(c)],
                                              start=(i % DH == 0), stop=(i % DH == DH - 1), skip_group_check=True)
                    mm.then_inc(gathered, 1)

                for i in range(STEPS):
                    for c in range(3):
                        n = 3 * i + c
                        if n >= 5:
                            pe.wait_ge(updated, n - 4)
                        for high_low in range(2):
                            mm = nc.tensor.matmul(m.ps[:, n % 5, :width(even_part(c))], spread[:, i % DH, :],
                                                  vT[high_low][:, i // DH, even_part(c)], start=(high_low == 0),
                                                  stop=(high_low == 1))
                        mm.then_inc(spread_done, 1)
                    if i >= 1:
                        sum_up(i - 1)
                sum_up(STEPS - 1)
                pe.wait_ge(o_kept, 6)
                for t in range(TILES):
                    if t >= 4:
                        pe.wait_ge(added, t - 3)
                    for k in range(KD):
                        nc.tensor.matmul(m.ps[:ROWS, t % 4, :D], oT[:, k, tile_cols(t)], wo[:, k, :],
                                         start=(k == 0), stop=False)
                    nc.tensor.matmul(m.ps[:ROWS, t % 4, :D], m.ones[:, :ROWS], ob[:, :],
                                     start=False, stop=True).then_inc(out_done, 1)

            @block.scalar
            def _(act):
                for j, (_, _, dst, k) in enumerate(jobs):
                    act.wait_ge(projected, j + 1)
                    src = m.ps[:, 3 * (j % 2):3 * (j % 2) + 3, :THIRD]
                    out = dst[:, k, :COLS].rearrange("p (c n) -> p c n", c=3)
                    if dst is kT:
                        nc.scalar.activation(out, src, ACT.Sigmoid, bias=kb[:, k:k + 1]).then_inc(kept, 1)
                    else:
                        nc.scalar.activation(out, src, ACT.Copy).then_inc(kept, 1)
                act.wait_ge(c_loaded, 64)
                nc.scalar.activation(spread[:, :, :], spread_raw[:, :, :], ACT.Copy).then_inc(spread_rounded, 1)
                for k in range(KD):
                    act.wait_ge(gathered, DH * (k + 1))
                    for c in range(3):
                        nc.scalar.activation(oT[:, k, third(c)], m.ps[:, 5 + c, :THIRD], ACT.Copy).then_inc(o_kept, 1)

            @block.vector
            def _(dve):
                for half in vT:
                    nc.vector.tensor_copy(half[:, :, COLS:].rearrange("p k o -> p (k o)"), m.ident[:, :KD]).then_inc(padded, 1)
                dve.wait_ge(padded, 2)
                for k in range(KD):
                    dve.wait_ge(kept, k + 1)
                    nc.vector.tensor_scalar(omk[:, k, :], kT[:, k, :], -1.0, 1.0, ALU.mult,
                                            ALU.add).then_inc(complemented, 1)
                    dve.wait_ge(complemented, k + 1)
                    nc.vector.memset(kT[:, k, 0:COLS:T], 0.0).then_inc(cut, 1)
                for k in range(KD):
                    dve.wait_ge(kept, k + 3)
                    high, low = (half[:, k, :COLS].rearrange("p (c n) -> p c n", c=3) for half in vT)
                    nc.vector.tensor_tensor(low, m.ps[:, 3 * k:3 * k + 3, :THIRD], high, ALU.subtract).then_inc(v_low, 1)
                dve.wait_ge(cut, 2)
                for i in range(STEPS):
                    if i >= 2:
                        dve.wait_ge(scanned, i - 1)
                    for c in range(3):
                        dve.wait_ge(spread_done, 3 * i + c + 1)
                        nc.vector.tensor_tensor(upd[:, i % 2, part(c)], m.ps[:, (3 * i + c) % 5, :width(part(c))],
                                                omk[:, i // DH, part(c)], ALU.mult).then_inc(updated, 1)
                    dve.wait_ge(updated, 3 * i + 3)
                    if i >= 2:
                        dve.wait_ge(was_read, i - 1)
                    nc.vector.tensor_tensor_scan(state[:, i % 2, :], kT[:, i // DH, :], upd[:, i % 2, :], 0.0,
                                                 ALU.mult, ALU.add).then_inc(scanned, 1)
                for t in range(TILES):
                    dve.wait_ge(out_done, t + 1)
                    nc.vector.tensor_tensor(m.h[:, t, :], m.ps[:ROWS, t % 4, :D], m.h[:, t, :],
                                            ALU.add).then_inc(added, 1)

            @block.gpsimd
            def _(pool):
                pool.wait_ge(kept, 6)
                for i in range(STEPS):
                    pool.wait_ge(scanned, i + 1)
                    if i >= 2:
                        pool.wait_ge(gathered, i - 1)
                    nc.gpsimd.tensor_tensor(read[:, i % 2, :], state[:, i % 2, :], qT[:, i // DH, :],
                                            ALU.mult).then_inc(was_read, 1)


def gate(nc, m, name, gw, gb, E, wts, wtsT, weighted):
    PAD = 6
    with ExitStack() as ctx:
        w = m.sbuf(ctx, name + "_gw", [128, KD, E])
        b = m.sbuf(ctx, name + "_gb", [1, E])
        mx = m.sbuf(ctx, name + "_mx", [ROWS, TILES])
        ex = m.sbuf(ctx, name + "_ex", [ROWS, TILES, E])
        den = m.sbuf(ctx, name + "_den", [ROWS, TILES])
        pr = m.sbuf(ctx, name + "_pr", [ROWS, TILES, E + PAD])
        rest = m.sbuf(ctx, name + "_rest", [ROWS, TILES, E + PAD])
        top = m.sbuf(ctx, name + "_top", [ROWS, TILES, 8])
        loaded = m.sem(name + "_loaded")
        scored = m.sem(name + "_scored")
        step = m.sem(name + "_dve_step")
        shifted = m.sem(name + "_shifted")
        expd = m.sem(name + "_expd")
        weighed = m.sem(name + "_weighed")
        turned = m.sem(name + "_turned")
        kept = m.sem(name + "_kept")
        logits = m.ps[:ROWS, 0, :TILES * E].rearrange("p (t e) -> p t e", e=E)

        def over_e(x, n):
            return x[:, :].rearrange("p (t o) -> p t o", o=1).broadcast_to([ROWS, TILES, n])

        with nc.Block() as block:
            @block.sync
            def _(sp):
                sp.dma_start(w[:, :, :], gw.rearrange("(k p) n -> p k n", p=128)).then_inc(loaded, 16)
                sp.dma_start(b[:, :], gb).then_inc(loaded, 16)

            @block.tensor
            def _(pe):
                pe.wait_ge(loaded, 32)
                for t in range(TILES):
                    for k in range(KD):
                        nc.tensor.matmul(logits[:, t, :], m.xT[:, k, tile_cols(t)], w[:, k, :],
                                         start=(k == 0), stop=False)
                    mm = nc.tensor.matmul(logits[:, t, :], m.ones[:, :ROWS], b[:, :], start=False, stop=True)
                mm.then_inc(scored, 1)
                pe.wait_ge(weighed, 1)
                for g, (t0, n) in enumerate(GROUPS):
                    for j in range(n):
                        mm = nc.tensor.transpose(m.ps[:8, 1 + g, j * ROWS:(j + 1) * ROWS], wts[:, t0 + j, :],
                                                 m.ident[:ROWS, :ROWS])
                    mm.then_inc(turned, 1)

            @block.scalar
            def _(act):
                act.wait_ge(shifted, 1)
                nc.scalar.activation(ex[:, :, :], ex[:, :, :], ACT.Exp).then_inc(expd, 1)
                for g, (t0, n) in enumerate(GROUPS):
                    act.wait_ge(turned, g + 1)
                    nc.scalar.activation(wtsT[:, t0 * ROWS:(t0 + n) * ROWS], m.ps[:8, 1 + g, :n * ROWS],
                                         ACT.Copy).then_inc(kept, 1)

            @block.vector
            def _(dve):
                done = [0]

                def link(ins):
                    done[0] += 1
                    ins.then_inc(step, 1)
                    dve.wait_ge(step, done[0])

                dve.wait_ge(scored, 1)
                nc.vector.memset(pr[:, :, E:], -1.0).then_inc(step, 1)
                done[0] += 1
                link(nc.vector.tensor_reduce(mx[:, :], logits, AX.X, ALU.max))
                nc.vector.tensor_tensor(ex[:, :, :], logits, over_e(mx, E), ALU.subtract).then_inc(shifted, 1)
                dve.wait_ge(expd, 1)
                link(nc.vector.tensor_reduce(den[:, :], ex[:, :, :], AX.X, ALU.add))
                link(nc.vector.reciprocal(den[:, :], den[:, :]))
                link(nc.vector.tensor_tensor(pr[:, :, :E], ex[:, :, :], over_e(den, E), ALU.mult))
                for t in range(TILES):
                    ins = nc.vector.max(top[:, t, :], pr[:, t, :E])
                link(ins)
                link(nc.vector.memset(top[:, :, 2:], -1.0))
                for t in range(TILES):
                    ins = nc.vector.match_replace(rest[:, t, :], top[:, t, :], pr[:, t, :], -2.0)
                link(ins)
                if not weighted:
                    nc.vector.tensor_tensor(wts[:, :, :], pr[:, :, :8], rest[:, :, :8], ALU.is_gt).then_inc(weighed, 1)
                    return
                link(nc.vector.tensor_tensor(ex[:, :, :8], pr[:, :, :8], rest[:, :, :8], ALU.is_gt))
                link(nc.vector.tensor_tensor(ex[:, :, :8], ex[:, :, :8], pr[:, :, :8], ALU.mult))
                link(nc.vector.tensor_reduce(den[:, :], ex[:, :, :8], AX.X, ALU.add))
                link(nc.vector.scalar_tensor_tensor(mx[:, :], den[:, :], 0.0, den[:, :], ALU.is_le, ALU.add))
                link(nc.vector.reciprocal(den[:, :], mx[:, :]))
                nc.vector.tensor_tensor(wts[:, :, :], ex[:, :, :8], over_e(den, 8), ALU.mult).then_inc(weighed, 1)


def small_experts(nc, m, name, ew, eb, wts, wtsT):
    E = 8
    with ExitStack() as ctx:
        w = m.sbuf(ctx, name + "_w", [128, KD, E, D])
        b = m.sbuf(ctx, name + "_b", [E, D])
        loaded = m.sem(name + "_loaded")
        multiplied = m.sem(name + "_multiplied")
        biased = m.sem(name + "_biased")
        added = m.sem(name + "_added")
        with nc.Block() as block:
            @block.sync
            def _(sp):
                for e in range(E):
                    sp.dma_start(w[:, :, e, :], ew[e].rearrange("(k p) n -> p k n", p=128)).then_inc(loaded, 16)
                sp.dma_start(b[:, :], eb).then_inc(loaded, 16)

            @block.tensor
            def _(pe):
                pe.wait_ge(loaded, 16 * (E + 1))
                for t in range(TILES):
                    if t >= 2:
                        pe.wait_ge(added, 9 * (t - 1) - 8)
                    nc.tensor.matmul(m.ps[:ROWS, 6 + t % 2, :D], wtsT[:, tile_cols(t)], b[:, :],
                                     start=True, stop=True).then_inc(biased, 1)
                    for p in range(E // 2):
                        i = t * (E // 2) + p
                        if i >= 6:
                            j = i - 6
                            pe.wait_ge(added, 9 * (j // 4) + 1 + 2 * (j % 4 + 1))
                        for k in range(KD):
                            mm = nc.tensor.matmul(m.ps[:ROWS, i % 6, :], m.xT[:, k, tile_cols(t)],
                                                  w[:, k, 2 * p:2 * p + 2, :], start=(k == 0), stop=(k == KD - 1))
                        mm.then_inc(multiplied, 1)

            @block.vector
            def _(dve):
                for t in range(TILES):
                    dve.wait_ge(biased, t + 1)
                    nc.vector.tensor_tensor(m.h[:, t, :], m.ps[:ROWS, 6 + t % 2, :D], m.h[:, t, :],
                                            ALU.add).then_inc(added, 1)
                    for e in range(E):
                        i = t * (E // 2) + e // 2
                        if e % 2 == 0:
                            dve.wait_ge(multiplied, i + 1)
                        dve.wait_ge(added, 9 * t + e + 1)
                        nc.vector.scalar_tensor_tensor(m.h[:, t, :], m.ps[:ROWS, i % 6, (e % 2) * D:(e % 2 + 1) * D],
                                                       wts[:, t, e:e + 1], m.h[:, t, :], ALU.mult,
                                                       ALU.add).then_inc(added, 1)


def selecting_experts(nc, m, dram, name, E, weighted):
    with ExitStack() as ctx:
        wts = m.sbuf(ctx, name + "_wts", [ROWS, TILES, 8])
        wtsT = m.sbuf(ctx, name + "_wtsT", [8, COLS])
        gate(nc, m, name + "g", dram[name + "_gwT"], dram[name + "_gb"], E, wts, wtsT, weighted)
        small_experts(nc, m, name + "e", dram[name + "_ew"], dram[name + "_eb"], wts, wtsT)


STAGE = {
    0: tokens,
    1: lambda nc, m, dram: (normalise(nc, m, "l0a_ln", m.h), decayed_sums(nc, m, dram)),
    2: lambda nc, m, dram: (normalise(nc, m, "l0f_ln", m.h), selecting_experts(nc, m, dram, "l0f", 8, False)),
    4: lambda nc, m, dram: (normalise(nc, m, "l1f_ln", m.h), selecting_experts(nc, m, dram, "l1f", 10, True)),
}
class MaskedSoftmax:

    N = 4 * ROWS

    def __init__(self, nc, m, name, ctx, mask_dram, scale, items, room=None):
        self.nc, self.m, self.scale, self.mask_dram = nc, m, scale, mask_dram
        self.mask = m.sbuf(ctx, name + "_mask", [ROWS, self.N])
        if room is None:
            room = m.sbuf(ctx, name + "_room", [ROWS, 6 * self.N])
        self.scores = room[:, :4 * self.N].rearrange("p (i n) -> p i n", i=4)
        self.turnedP = room[:, 4 * self.N:6 * self.N].rearrange("p (i n) -> p i n", i=2)
        self.mx = m.sbuf(ctx, name + "_mx", [ROWS, 4, 4])
        self.den = m.sbuf(ctx, name + "_den", [ROWS, items, 4])
        self.mask_loaded = m.sem(name + "_mask_loaded")
        self.scored = m.sem(name + "_scored")
        self.masked = m.sem(name + "_masked")
        self.max_found = m.sem(name + "_max_found")
        self.expd = m.sem(name + "_expd")
        self.inverted = m.sem(name + "_inverted")
        self.normed = m.sem(name + "_normed")
        self.turned = m.sem(name + "_turned")
        self.kept = m.sem(name + "_kept")
        self.used = m.sem(name + "_used")

    def by_head(self, x):
        return x.rearrange("p (g n) -> p g n", g=4)

    def spread(self, x):
        return x.rearrange("p (g o) -> p g o", o=1).broadcast_to([ROWS, 4, ROWS])

    def load_mask(self, sp):
        sp.dma_start(self.mask[:, :], self.mask_dram).then_inc(self.mask_loaded, 16)

    def vector_mask(self, dve, i):
        dve.wait_ge(self.scored, i + 1)
        if i >= 4:
            dve.wait_ge(self.turned, i - 3)
        self.nc.vector.scalar_tensor_tensor(self.scores[:, i % 4, :], self.m.ps[:ROWS, i % 2, :self.N], self.scale,
                                            self.mask[:, :], ALU.mult, ALU.add).then_inc(self.masked, 1)
        dve.wait_ge(self.masked, i + 1)
        if i >= 4:
            dve.wait_ge(self.expd, i - 3)
        self.nc.vector.tensor_reduce(self.mx[:, i % 4, :], self.by_head(self.scores[:, i % 4, :]), AX.X,
                                     ALU.max, negate=True).then_inc(self.max_found, 1)

    def vector_norm(self, dve, i):
        x = self.by_head(self.scores[:, i % 4, :])
        dve.wait_ge(self.expd, i + 1)
        self.nc.vector.reciprocal(self.den[:, i, :], self.den[:, i, :]).then_inc(self.inverted, 1)
        dve.wait_ge(self.inverted, i + 1)
        self.nc.vector.tensor_tensor(x, x, self.spread(self.den[:, i, :]), ALU.mult).then_inc(self.normed, 1)

    def scalar_exp(self, act, i):
        act.wait_ge(self.max_found, i + 1)
        for j in range(4):
            x = self.scores[:, i % 4, j * ROWS:(j + 1) * ROWS]
            ins = self.nc.scalar.activation(x, x, ACT.Exp, bias=self.mx[:, i % 4, j:j + 1],
                                            accum_out=self.den[:, i, j:j + 1])
        ins.then_inc(self.expd, 1)

    def scalar_keep(self, act, i, used):
        act.wait_ge(self.turned, i + 1)
        if i >= 2:
            act.wait_ge(used, i - 1)
        self.nc.scalar.activation(self.turnedP[:, i % 2, :], self.m.ps[:ROWS, 2 + i % 2, :self.N],
                                  ACT.Copy).then_inc(self.kept, 1)

    def tensor_turn(self, pe, i, ready):
        pe.wait_ge(ready, i + 1)
        if i >= 2:
            pe.wait_ge(self.kept, i - 1)
        for j in range(4):
            own = slice(j * ROWS, (j + 1) * ROWS)
            mm = self.nc.tensor.transpose(self.m.ps[:ROWS, 2 + i % 2, own], self.scores[:, i % 4, own],
                                          self.m.ident[:ROWS, :ROWS])
        mm.then_inc(self.turned, 1)


def latent_attention(nc, m, dram):
    H, DK, DC = 8, 128, 32
    scale = float((DK + DC) ** -0.5)
    names = ("DQ", "DKV", "KR")
    with ExitStack() as ctx:
        wd = [m.sbuf(ctx, "l1a_wd" + n, [128, KD, DC]) for n in names]
        bd = [m.sbuf(ctx, "l1a_bd" + n, [DC, 1]) for n in names]
        latent = [m.sbuf(ctx, "l1a_latent" + n, [DC + (n == "DKV"), COLS]) for n in names]
        wuq = m.sbuf(ctx, "l1a_wuq", [DC, H * DK])
        wuk = m.sbuf(ctx, "l1a_wuk", [DC, H * DK])
        wuv = m.sbuf(ctx, "l1a_wuv", [DC + 1, H * DK])
        wqr = m.sbuf(ctx, "l1a_wqr", [DC, H * DC])
        buq = m.sbuf(ctx, "l1a_buq", [128, H])
        buk = m.sbuf(ctx, "l1a_buk", [128, H])
        bqr = m.sbuf(ctx, "l1a_bqr", [DC, H])
        wo = m.sbuf(ctx, "l1a_wo", [128, H, D])
        bo = m.sbuf(ctx, "l1a_bo", [1, D])
        q = m.sbuf(ctx, "l1a_q", [128, H, 2, 4 * ROWS])
        k = m.sbuf(ctx, "l1a_k", [128, H, 2, 4 * ROWS])
        qr = m.sbuf(ctx, "l1a_qr", [DC, H, 2, 4 * ROWS])
        v = m.sbuf(ctx, "l1a_v", [ROWS, TILES, H * DK])
        oT = m.sbuf(ctx, "l1a_oT", [128, 2, H, ROWS])
        room = m.xn[:, :, :].rearrange("p t d -> p (t d)")
        sm = MaskedSoftmax(nc, m, "l1a_sm", ctx, dram["c_mask"], scale, TILES * 2, room=room)
        loaded = m.sem("l1a_loaded")
        o_loaded = m.sem("l1a_o_loaded")
        compressed = m.sem("l1a_compressed")
        latent_kept = m.sem("l1a_latent_kept")
        ones_row_set = m.sem("l1a_ones_row_set")
        expanded = m.sem("l1a_expanded")
        kept = m.sem("l1a_kept")
        v_made = m.sem("l1a_v_made")
        v_kept = m.sem("l1a_v_kept")
        mixed = m.sem("l1a_mixed")
        mix_kept = m.sem("l1a_mix_kept")
        out_done = m.sem("l1a_out_done")
        added = m.sem("l1a_added")
        ITEMS = TILES * 2
        EXP = 3 * H

        with nc.Block() as block:
            @block.sync
            def _(sp):
                for i, n in enumerate(names):
                    sp.dma_start(wd[i][:, :, :], dram["l1a_w" + n].rearrange("(k p) n -> p k n", p=128)).then_inc(loaded, 16)
                    sp.dma_start(bd[i][:, :], dram["l1a_b" + n]).then_inc(loaded, 16)
                for t, n in ((wuq, "wUQ"), (wuk, "wUK"), (wuv, "wUV"), (wqr, "wQR"), (buq, "bUQ"), (buk, "bUK"),
                             (bqr, "bQR")):
                    sp.dma_start(t[:, :], dram["l1a_" + n]).then_inc(loaded, 16)
                sm.load_mask(sp)
                sp.dma_start(wo[:, :, :], dram["l1a_wO"].rearrange("(k p) n -> p k n", p=128)).then_inc(o_loaded, 16)
                sp.dma_start(bo[:, :], dram["l1a_bO"]).then_inc(o_loaded, 16)

            @block.tensor
            def _(pe):
                pe.wait_ge(loaded, 16 * 13)
                for i in range(3):
                    for c in range(3):
                        n = 3 * i + c
                        if n >= 8:
                            pe.wait_ge(latent_kept, n - 7)
                        for kk in range(KD):
                            mm = nc.tensor.matmul(m.ps[:DC, n % 8, :THIRD], wd[i][:, kk, :], m.xT[:, kk, third(c)],
                                                  start=(kk == 0), stop=(kk == KD - 1))
                        mm.then_inc(compressed, 1)
                
                def expand(g):
                    t0, n = GROUPS[g]
                    cols = slice(t0 * ROWS, (t0 + n) * ROWS)
                    for h in range(H):
                        for j, (w, src, M) in enumerate(((wuq, 0, DK), (wuk, 1, DK), (wqr, 0, DC))):
                            i = g * EXP + 3 * h + j
                            if i >= 2:
                                pe.wait_ge(kept, i - 1)
                            nc.tensor.matmul(m.ps[:M, 4 + i % 2, :n * ROWS], w[:, h * M:(h + 1) * M],
                                             latent[src][:DC, cols], start=True, stop=True).then_inc(expanded, 1)

                def values(t):
                    for j in range(2):
                        n = 2 * t + j
                        if n >= 4:
                            pe.wait_ge(v_kept, n - 3)
                        nc.tensor.matmul(m.ps[:ROWS, n % 4, :], latent[1][:, tile_cols(t)],
                                         wuv[:, j * 512:(j + 1) * 512], start=True, stop=True).then_inc(v_made, 1)

                def scores(i):
                    t, half = i // 2, i % 2
                    g, r = t // 4, t % 4
                    if i >= 2:
                        pe.wait_ge(sm.masked, i - 1)
                    pe.wait_ge(kept, (g + 1) * EXP)
                    own = slice(r * ROWS, (r + 1) * ROWS)
                    for j in range(4):
                        h = half * 4 + j
                        out = m.ps[:ROWS, i % 2, j * ROWS:(j + 1) * ROWS]
                        nc.tensor.matmul(out, q[:, h, g % 2, own], k[:, h, g % 2, own], start=True, stop=False)
                        mm = nc.tensor.matmul(out, qr[:, h, g % 2, own], latent[2][:, tile_cols(t)],
                                              start=False, stop=True)
                    mm.then_inc(sm.scored, 1)

                def mix(i):
                    t, half = i // 2, i % 2
                    pe.wait_ge(sm.kept, i + 1)
                    if t >= 1:
                        pe.wait_ge(mix_kept, i - 1)
                    for j in range(4):
                        h = half * 4 + j
                        mm = nc.tensor.matmul(m.ps[:, 6 + half, j * ROWS:(j + 1) * ROWS],
                                              v[:, t, h * DK:(h + 1) * DK], sm.turnedP[:, i % 2, j * ROWS:(j + 1) * ROWS],
                                              start=True, stop=True)
                    mm.then_inc(mixed, 1)

                def output(t, expanded_groups):
                    pe.wait_ge(mix_kept, 2 * t + 2)
                    if t == 0:
                        pe.wait_ge(o_loaded, 32)
                    pe.wait_ge(kept, expanded_groups * EXP)
                    if t >= 2:
                        pe.wait_ge(added, t - 1)
                    for h in range(H):
                        nc.tensor.matmul(m.ps[:ROWS, 4 + t % 2, :D], oT[:, t % 2, h, :], wo[:, h, :], start=(h == 0), stop=False)
                    nc.tensor.matmul(m.ps[:ROWS, 4 + t % 2, :D], m.ones[:, :ROWS], bo[:, :], start=False,
                                     stop=True).then_inc(out_done, 1)

                pe.wait_ge(latent_kept, 9)
                pe.wait_ge(ones_row_set, 1)
                for t in range(TILES):
                    values(t)
                expand(0)
                pe.wait_ge(v_kept, 2 * TILES)
                groups = 1
                for i in range(ITEMS + 3):
                    if i < ITEMS:
                        if i % 8 == 2 and i // 8 + 1 < len(GROUPS):
                            if i >= 5:
                                pe.wait_ge(added, (i - 5) // 2 + 1)
                            expand(i // 8 + 1)
                            groups += 1
                        scores(i)
                    if 2 <= i < ITEMS + 2:
                        sm.tensor_turn(pe, i - 2, sm.normed)
                    if i >= 3:
                        mix(i - 3)
                        if i % 2 == 0:
                            output((i - 4) // 2, groups)

            @block.scalar
            def _(act):
                for i in range(3):
                    for c in range(3):
                        n = 3 * i + c
                        act.wait_ge(compressed, n + 1)
                        nc.scalar.activation(latent[i][:DC, third(c)], m.ps[:DC, n % 8, :THIRD], ACT.Identity,
                                             bias=bd[i][:, 0:1]).then_inc(latent_kept, 1)

                def keep(g):
                    t0, n = GROUPS[g]
                    if g >= 2:
                        act.wait_ge(sm.scored, 2 * 4 * (g - 1))
                    for h in range(H):
                        for j, (dst, b, M) in enumerate(((q, buq, DK), (k, buk, DK), (qr, bqr, DC))):
                            i = g * EXP + 3 * h + j
                            act.wait_ge(expanded, i + 1)
                            nc.scalar.activation(dst[:, h, g % 2, :n * ROWS], m.ps[:M, 4 + i % 2, :n * ROWS],
                                                 ACT.Identity, bias=b[:, h:h + 1]).then_inc(kept, 1)

                for n in range(2 * TILES):
                    act.wait_ge(v_made, n + 1)
                    nc.scalar.activation(v[:, n // 2, (n % 2) * 512:(n % 2 + 1) * 512], m.ps[:ROWS, n % 4, :],
                                         ACT.Copy).then_inc(v_kept, 1)
                keep(0)
                for i in range(ITEMS + 3):
                    if i < ITEMS:
                        if i % 8 == 2 and i // 8 + 1 < len(GROUPS):
                            keep(i // 8 + 1)
                        sm.scalar_exp(act, i)
                    if 2 <= i < ITEMS + 2:
                        sm.scalar_keep(act, i - 2, mixed)
                    if i >= 3:
                        t, half = (i - 3) // 2, (i - 3) % 2
                        act.wait_ge(mixed, i - 2)
                        if t >= 2:
                            act.wait_ge(out_done, t - 1)
                        nc.scalar.activation(oT[:, t % 2, 4 * half:4 * half + 4, :],
                                             m.ps[:, 6 + half, :4 * ROWS].rearrange("p (g n) -> p g n", g=4),
                                             ACT.Copy).then_inc(mix_kept, 1)

            @block.vector
            def _(dve):
                nc.vector.memset(latent[1][DC:DC + 1, :], 1.0).then_inc(ones_row_set, 1)
                dve.wait_ge(sm.mask_loaded, 16)
                for i in range(ITEMS + 3):
                    if i < ITEMS:
                        sm.vector_mask(dve, i)
                    if 1 <= i < ITEMS + 1:
                        sm.vector_norm(dve, i - 1)
                    if i >= 4 and i % 2 == 0:
                        t = (i - 4) // 2
                        dve.wait_ge(out_done, t + 1)
                        nc.vector.tensor_tensor(m.h[:, t, :], m.ps[:ROWS, 4 + t % 2, :D], m.h[:, t, :],
                                                ALU.add).then_inc(added, 1)


STAGE[3] = lambda nc, m, dram: (normalise(nc, m, "l1a_ln", m.h), latent_attention(nc, m, dram))
def state_space(nc, m, dram):
    H, NS, DI = 8, 64, 512
    KI = DI // 128
    TAPS = 4
    with ExitStack() as ctx:
        wz = m.sbuf(ctx, "l2a_wz", [128, KD, DI])
        wx = m.sbuf(ctx, "l2a_wx", [128, KD, DI])
        wdt = m.sbuf(ctx, "l2a_wdt", [128, KD, H])
        wB = m.sbuf(ctx, "l2a_wB", [128, KD, NS])
        wC = m.sbuf(ctx, "l2a_wC", [128, KD, NS])
        conv_w = m.sbuf(ctx, "l2a_conv_w", [128, KI, TAPS])
        conv_b = m.sbuf(ctx, "l2a_conv_b", [128, KI])
        a_log = m.sbuf(ctx, "l2a_A_log", [H, 1])
        dt_bias = m.sbuf(ctx, "l2a_dt_bias", [H, 1])
        skip = m.sbuf(ctx, "l2a_skip", [ROWS, DI])
        norm_w = m.sbuf(ctx, "l2a_norm_w", [128, KI])
        wo = m.sbuf(ctx, "l2a_wo", [128, KI, D])
        causal = m.sbuf(ctx, "l2a_causal", [ROWS, 4 * ROWS])
        rows8 = m.sbuf(ctx, "l2a_rows8", [8, 8, 128])
        xc = m.sbuf(ctx, "l2a_xc", [128, KI, COLS])
        conv = m.sbuf(ctx, "l2a_conv", [128, KI, COLS])
        BT = m.sbuf(ctx, "l2a_BT", [NS, COLS])
        CT = m.sbuf(ctx, "l2a_CT", [NS, COLS])
        dt = m.sbuf(ctx, "l2a_dt", [H, COLS])
        mag = m.sbuf(ctx, "l2a_mag", [H, COLS])
        ones = m.sbuf(ctx, "l2a_ones", [H, COLS])
        logs = m.sbuf(ctx, "l2a_logs", [H, COLS])
        negL = m.sbuf(ctx, "l2a_negL", [ROWS, TILES, H])
        x_tok = m.sbuf(ctx, "l2a_x_tok", [ROWS, 2, DI])
        z_tok = m.sbuf(ctx, "l2a_z_tok", [ROWS, TILES, DI])
        G = m.sbuf(ctx, "l2a_G", [ROWS, 2, ROWS])
        W = m.sbuf(ctx, "l2a_W", [ROWS, 2, H, ROWS])
        y = m.sbuf(ctx, "l2a_y", [ROWS, 2, DI])
        sq = m.sbuf(ctx, "l2a_sq", [ROWS, DI])
        ss = m.sbuf(ctx, "l2a_ss", [ROWS, TILES])
        rms = m.sbuf(ctx, "l2a_rms", [ROWS, TILES])
        half = m.sbuf(ctx, "l2a_half", [ROWS, 1])
        yT = m.sbuf(ctx, "l2a_yT", [128, 2, KI, ROWS])
        S = {n: m.sem("l2a_" + n) for n in (
            "loaded", "late_loaded", "ones_set", "made", "kept", "convolved", "x_ready", "exp_a", "mag_ready", "logs_ready",
            "sp1", "lturn", "l_kept", "z_made", "z_kept", "lt_made", "e_made", "g_made", "g_kept", "w_made", "x_turned",
            "x_kept", "y_made", "y_step", "y_ready", "rooted", "scaled", "y_turned", "yt_kept", "out_done", "added")}
        jobs = [(wx, 128 * k, 128, xc[:, k, :]) for k in range(KI)] + [(wB, 0, NS, BT), (wC, 0, NS, CT), (wdt, 0, H, dt)]
        with nc.Block() as block:
            @block.sync
            def _(sp):
                for t, n in ((wx, "wx"), (wB, "wB"), (wC, "wC"), (wdt, "wdt"), (wz, "wz")):
                    sp.dma_start(t[:, :, :], dram["l2a_" + n].rearrange("(k p) n -> p k n", p=128)).then_inc(S["loaded"], 16)
                sp.dma_start(conv_w[:, :, :], dram["l2a_conv_w"]).then_inc(S["loaded"], 16)
                sp.dma_start(conv_b[:, :], dram["l2a_conv_b"]).then_inc(S["loaded"], 16)
                sp.dma_start(a_log[:, :], dram["l2a_A_log"]).then_inc(S["loaded"], 16)
                sp.dma_start(dt_bias[:, :], dram["l2a_dt_bias"]).then_inc(S["loaded"], 16)
                sp.dma_start(skip[:, :], dram["l2a_D"]).then_inc(S["late_loaded"], 16)
                sp.dma_start(norm_w[:, :], dram["l2a_norm_w"]).then_inc(S["late_loaded"], 16)
                sp.dma_start(wo[:, :, :], dram["l2a_owT"].rearrange("(k p) n -> p k n", p=128)).then_inc(S["late_loaded"], 16)
                sp.dma_start(causal[:, :], dram["c_causal"]).then_inc(S["late_loaded"], 16)
                sp.dma_start(rows8[:, :, :], dram["c_rows8"]).then_inc(S["late_loaded"], 16)

            @block.tensor
            def _(pe):
                pe.wait_ge(S["loaded"], 16 * 9)
                for j, (w, col, M, _) in enumerate(jobs):
                    for c in range(3):
                        n = 3 * j + c
                        if n >= 8:
                            pe.wait_ge(S["kept"], n - 7)
                        for k in range(KD):
                            mm = nc.tensor.matmul(m.ps[:M, n % 8, :THIRD], w[:, k, col:col + M], m.xT[:, k, third(c)],
                                                  start=(k == 0), stop=(k == KD - 1))
                        mm.then_inc(S["made"], 1)
                for t in range(TILES):
                    if t == 0:
                        pe.wait_ge(S["kept"], 3 * len(jobs))
                    if t >= 4:
                        pe.wait_ge(S["z_kept"], t - 3)
                    for k in range(KD):
                        mm = nc.tensor.matmul(m.ps[:ROWS, t % 4, :], m.xT[:, k, tile_cols(t)], wz[:, k, :],
                                              start=(k == 0), stop=(k == KD - 1))
                    mm.then_inc(S["z_made"], 1)
                pe.wait_ge(S["logs_ready"], 1)
                for t in range(TILES):
                    mm = nc.tensor.transpose(m.ps[:ROWS, 4, t * H:(t + 1) * H], logs[:, tile_cols(t)], m.ident[:H, :H])
                mm.then_inc(S["lturn"], 1)
                pe.wait_ge(S["late_loaded"], 16 * 5)
                pe.wait_ge(S["z_kept"], TILES)
                pe.wait_ge(S["l_kept"], 1)

                def decays(t):
                    if t >= 1:
                        pe.wait_ge(S["e_made"], 8 * t)
                    for b in range(2):
                        nc.tensor.matmul(m.ps[:ROWS, b, :4 * ROWS], m.ident[:ROWS, :ROWS], causal[:, :],
                                         start=True, stop=False, skip_group_check=True)
                        for j in range(4):
                            mm = nc.tensor.matmul(m.ps[:ROWS, b, j * ROWS:(j + 1) * ROWS], rows8[:, 4 * b + j, :ROWS],
                                                  logs[:, tile_cols(t)], start=False, stop=(j == 3), skip_group_check=True)
                    mm.then_inc(S["lt_made"], 1)
                    if t >= 1:
                        pe.wait_ge(S["g_kept"], t)
                    nc.tensor.matmul(m.ps[:ROWS, 2, :ROWS], BT[:, tile_cols(t)], CT[:, tile_cols(t)],
                                     start=True, stop=True).then_inc(S["g_made"], 1)
                    if t >= 1:
                        pe.wait_ge(S["x_kept"], t)
                    for k in range(KI):
                        mm = nc.tensor.transpose(m.ps[:ROWS, 3, k * 128:(k + 1) * 128], xc[:, k, tile_cols(t)],
                                                 m.ident[:, :])
                    mm.then_inc(S["x_turned"], 1)

                def weigh(t):
                    pe.wait_ge(S["w_made"], 2 * t + 2)
                    pe.wait_ge(S["x_kept"], t + 1)
                    if t >= 2:
                        pe.wait_ge(S["y_step"], 2 * (t - 1) - 1)
                    for h in range(H):
                        mm = nc.tensor.matmul(m.ps[:ROWS, 4 + t % 2, h * 64:(h + 1) * 64], W[:, t % 2, h, :],
                                              x_tok[:, t % 2, h * 64:(h + 1) * 64], start=True, stop=True)
                    mm.then_inc(S["y_made"], 1)

                def output(t):
                    pe.wait_ge(S["scaled"], t + 1)
                    if t >= 1:
                        pe.wait_ge(S["yt_kept"], KI * t)
                    for k in range(KI):
                        mm = nc.tensor.transpose(m.ps[:, 6, k * ROWS:(k + 1) * ROWS], y[:, t % 2, k * 128:(k + 1) * 128],
                                                 m.ident[:ROWS, :ROWS])
                    mm.then_inc(S["y_turned"], 1)
                    pe.wait_ge(S["yt_kept"], KI * (t + 1))
                    if t >= 1:
                        pe.wait_ge(S["added"], t)
                    for k in range(KI):
                        mm = nc.tensor.matmul(m.ps[:ROWS, 7, :D], yT[:, t % 2, k, :], wo[:, k, :],
                                              start=(k == 0), stop=(k == KI - 1))
                    mm.then_inc(S["out_done"], 1)

                pe.wait_ge(S["x_ready"], KI)
                for t in range(TILES + 2):
                    if t < TILES:
                        decays(t)
                    if 1 <= t <= TILES:
                        weigh(t - 1)
                    if t >= 2:
                        output(t - 2)

            @block.scalar
            def _(act):
                act.wait_ge(S["loaded"], 16 * 9)
                nc.scalar.activation(a_log[:, :], a_log[:, :], ACT.Exp).then_inc(S["exp_a"], 1)
                for j, (_, _, M, dst) in enumerate(jobs):
                    for c in range(3):
                        n = 3 * j + c
                        act.wait_ge(S["made"], n + 1)
                        src = m.ps[:M, n % 8, :THIRD]
                        if dst is dt:
                            nc.scalar.activation(dst[:, third(c)], src, ACT.Identity, bias=dt_bias[:, 0:1]).then_inc(S["kept"], 1)
                        else:
                            nc.scalar.activation(dst[:, third(c)], src, ACT.Copy).then_inc(S["kept"], 1)
                act.wait_ge(S["kept"], 3 * len(jobs))
                nc.scalar.activation(mag[:, :], dt[:, :], ACT.Abs).then_inc(S["sp1"], 1)
                act.wait_ge(S["sp1"], 1)
                nc.scalar.activation(mag[:, :], mag[:, :], ACT.Exp, scale=-1.0).then_inc(S["sp1"], 1)
                act.wait_ge(S["sp1"], 2)
                nc.scalar.activation(mag[:, :], mag[:, :], ACT.Ln, bias=1.0).then_inc(S["mag_ready"], 1)
                for k in range(KI):
                    act.wait_ge(S["convolved"], TAPS * (k + 1))
                    nc.scalar.activation(xc[:, k, :], conv[:, k, :], ACT.Silu).then_inc(S["x_ready"], 1)
                for t in range(TILES):
                    act.wait_ge(S["z_made"], t + 1)
                    nc.scalar.activation(z_tok[:, t, :], m.ps[:ROWS, t % 4, :], ACT.Silu).then_inc(S["z_kept"], 1)

                def kept_out(act, t):
                    act.wait_ge(S["y_turned"], t + 1)
                    if t >= 2:
                        act.wait_ge(S["out_done"], t - 1)
                    for k in range(KI):
                        nc.scalar.activation(yT[:, t % 2, k, :], m.ps[:, 6, k * ROWS:(k + 1) * ROWS], ACT.Copy,
                                             scale=norm_w[:, k:k + 1]).then_inc(S["yt_kept"], 1)

                def copies(t):
                    act.wait_ge(S["g_made"], t + 1)
                    if t >= 2:
                        act.wait_ge(S["w_made"], 2 * (t - 1))
                    nc.scalar.activation(G[:, t % 2, :], m.ps[:ROWS, 2, :ROWS], ACT.Copy).then_inc(S["g_kept"], 1)
                    act.wait_ge(S["x_turned"], t + 1)
                    if t >= 2:
                        act.wait_ge(S["y_made"], t - 1)
                        act.wait_ge(S["y_step"], 2 * (t - 1) - 1)
                    nc.scalar.activation(x_tok[:, t % 2, :], m.ps[:ROWS, 3, :], ACT.Copy).then_inc(S["x_kept"], 1)

                act.wait_ge(S["l_kept"], 1)
                for t in range(TILES):
                    act.wait_ge(S["lt_made"], t + 1)
                    if t >= 2:
                        act.wait_ge(S["y_made"], t - 1)
                    for h in range(H):
                        nc.scalar.activation(W[:, t % 2, h, :], m.ps[:ROWS, h // 4, (h % 4) * ROWS:(h % 4 + 1) * ROWS],
                                             ACT.Exp, bias=negL[:, t, h:h + 1]).then_inc(S["e_made"], 1)
                    copies(t)
                    if t >= 1:
                        kept_out(act, t - 1)
                kept_out(act, TILES - 1)

            @block.vector
            def _(dve):
                def seqs(x, k):
                    return x[:, k, :].rearrange("p (s t) -> p s t", t=T)

                nc.vector.memset(ones[:, :], 1.0).then_inc(S["ones_set"], 1)
                dve.wait_ge(S["ones_set"], 1)
                nc.vector.memset(ones[:, 0:COLS:T], 0.0).then_inc(S["exp_a"], 1)
                for k in range(KI):
                    dve.wait_ge(S["kept"], 3 * (k + 1))
                    nc.vector.tensor_scalar(conv[:, k, :], xc[:, k, :], conv_w[:, k, 3:4], conv_b[:, k:k + 1], ALU.mult,
                                            ALU.add).then_inc(S["convolved"], 1)
                    for shift in range(1, TAPS):
                        dve.wait_ge(S["convolved"], TAPS * k + shift)
                        nc.vector.scalar_tensor_tensor(seqs(conv, k)[:, :, shift:], seqs(xc, k)[:, :, :T - shift],
                                                       conv_w[:, k, 3 - shift:4 - shift], seqs(conv, k)[:, :, shift:],
                                                       ALU.mult, ALU.add).then_inc(S["convolved"], 1)
                dve.wait_ge(S["mag_ready"], 1)
                dve.wait_ge(S["exp_a"], 2)
                step = S["y_ready"]
                nc.vector.scalar_tensor_tensor(dt[:, :], dt[:, :], 0.0, mag[:, :], ALU.max, ALU.add).then_inc(step, 1)
                dve.wait_ge(step, 1)
                nc.vector.tensor_scalar(dt[:, :], dt[:, :], a_log[:, 0:1], -1.0, ALU.mult, ALU.mult).then_inc(step, 1)
                dve.wait_ge(step, 2)
                nc.vector.tensor_tensor_scan(logs[:, :], ones[:, :], dt[:, :], 0.0, ALU.mult,
                                             ALU.add).then_inc(S["logs_ready"], 1)
                dve.wait_ge(S["lturn"], 1)
                nc.vector.tensor_scalar(negL[:, :, :], m.ps[:ROWS, 4, :TILES * H].rearrange("p (t h) -> p t h", h=H),
                                        -1.0, None, ALU.mult).then_inc(S["l_kept"], 1)
                dve.wait_ge(S["late_loaded"], 16 * 5)

                def finish(t):
                    yy = y[:, t % 2, :]
                    dve.wait_ge(S["y_made"], t + 1)
                    if t >= 2:
                        dve.wait_ge(S["y_turned"], t - 1)
                    n = 2 + 4 * t
                    nc.vector.tensor_tensor(sq[:, :], x_tok[:, t % 2, :], skip[:, :], ALU.mult).then_inc(step, 1)
                    dve.wait_ge(step, n + 1)
                    nc.vector.tensor_tensor(yy, m.ps[:ROWS, 4 + t % 2, :], sq[:, :], ALU.add).then_inc(S["y_step"], 1)
                    dve.wait_ge(S["y_step"], 2 * t + 1)
                    nc.vector.tensor_tensor(yy, yy, z_tok[:, t, :], ALU.mult).then_inc(S["y_step"], 1)
                    dve.wait_ge(S["y_step"], 2 * t + 2)
                    nc.vector.tensor_tensor(sq[:, :], yy, yy, ALU.mult).then_inc(step, 1)
                    dve.wait_ge(step, n + 2)
                    nc.vector.tensor_reduce(ss[:, t:t + 1], sq[:, :], AX.X, ALU.add).then_inc(step, 1)
                    dve.wait_ge(step, n + 3)
                    nc.vector.tensor_scalar(ss[:, t:t + 1], ss[:, t:t + 1], 1.0 / DI, 1e-6, ALU.mult,
                                            ALU.add).then_inc(step, 1)
                    dve.wait_ge(S["rooted"], t + 2)
                    nc.vector.tensor_scalar(yy, yy, rms[:, t:t + 1], None, ALU.mult).then_inc(S["scaled"], 1)

                for t in range(TILES + 2):
                    if t < TILES:
                        dve.wait_ge(S["g_kept"], t + 1)
                        for b in range(2):
                            dve.wait_ge(S["e_made"], 8 * t + 4 * b + 4)
                            w4 = W[:, t % 2, 4 * b:4 * b + 4, :]
                            g4 = G[:, t % 2, :].rearrange("p (o n) -> p o n", o=1).broadcast_to([ROWS, 4, ROWS])
                            nc.vector.tensor_tensor(w4, w4, g4, ALU.mult).then_inc(S["w_made"], 1)
                    if 1 <= t <= TILES:
                        finish(t - 1)
                    if t >= 2:
                        dve.wait_ge(S["out_done"], t - 1)
                        nc.vector.tensor_tensor(m.h[:, t - 2, :], m.ps[:ROWS, 7, :D], m.h[:, t - 2, :],
                                                ALU.add).then_inc(S["added"], 1)

            @block.gpsimd
            def _(pool):
                nc.gpsimd.memset(half[:, :], -0.5).then_inc(S["rooted"], 1)
                pool.wait_ge(S["rooted"], 1)
                for t in range(TILES):
                    pool.wait_ge(S["y_ready"], 2 + 4 * t + 4)
                    nc.gpsimd.tensor_tensor(rms[:, t:t + 1], ss[:, t:t + 1], half[:, :], ALU.pow).then_inc(S["rooted"], 1)


STAGE[5] = lambda nc, m, dram: (normalise(nc, m, "l2a_ln", m.h), state_space(nc, m, dram))


def small_head_attention(nc, m, dram):
    H, DH = 16, 16
    HALF = H // KD
    ITEMS = TILES * 4
    scale = float(DH ** -0.5)
    with ExitStack() as ctx:
        wq = m.sbuf(ctx, "l2f_wq", [128, KD, D])
        wk = m.sbuf(ctx, "l2f_wk", [128, KD, D])
        wv = m.sbuf(ctx, "l2f_wv", [128, KD, D])
        wo = m.sbuf(ctx, "l2f_wo", [128, KD, D])
        heads = m.sbuf(ctx, "l2f_heads", [128, HALF])
        qT = m.sbuf(ctx, "l2f_qT", [128, KD, COLS])
        kT = m.sbuf(ctx, "l2f_kT", [128, KD, COLS])
        own = m.sbuf(ctx, "l2f_own", [128, 2, HALF, ROWS])
        v = m.sbuf(ctx, "l2f_v", [ROWS, TILES, D])
        mix = m.sbuf(ctx, "l2f_mix", [ROWS, 2, D])
        mixT = m.sbuf(ctx, "l2f_mixT", [128, 2, KD, ROWS])
        sm = MaskedSoftmax(nc, m, "l2f_sm", ctx, dram["c_mask"], scale, ITEMS)
        S = {n: m.sem("l2f_" + n) for n in (
            "loaded", "made", "kept", "v_made", "v_kept", "owned", "mixed", "mix_kept", "mix_turned", "mixT_kept",
            "out_done", "added")}
        jobs = [(wq, k, qT) for k in range(KD)] + [(wk, k, kT) for k in range(KD)]
        with nc.Block() as block:
            @block.sync
            def _(sp):
                for t, n in ((wq, "Wq"), (wk, "Wk"), (wv, "Wv"), (wo, "Wo")):
                    sp.dma_start(t[:, :, :], dram["l2f_" + n].rearrange("(k p) n -> p k n", p=128)).then_inc(S["loaded"], 16)
                sp.dma_start(heads[:, :], dram["c_heads"]).then_inc(S["loaded"], 16)
                sm.load_mask(sp)

            @block.tensor
            def _(pe):
                pe.wait_ge(S["loaded"], 16 * 5)
                for j, (w, mk, _) in enumerate(jobs):
                    for c in range(3):
                        n = 3 * j + c
                        if n >= 4:
                            pe.wait_ge(S["kept"], n - 3)
                        for k in range(KD):
                            mm = nc.tensor.matmul(m.ps[:, n % 4, :THIRD], w[:, k, mk * 128:(mk + 1) * 128],
                                                  m.xT[:, k, third(c)], start=(k == 0), stop=(k == KD - 1))
                        mm.then_inc(S["made"], 1)
                for t in range(TILES):
                    if t >= 4:
                        pe.wait_ge(S["v_kept"], t - 3)
                    for k in range(KD):
                        mm = nc.tensor.matmul(m.ps[:ROWS, 4 + t % 4, :D], m.xT[:, k, tile_cols(t)], wv[:, k, :],
                                              start=(k == 0), stop=(k == KD - 1))
                    mm.then_inc(S["v_made"], 1)
                pe.wait_ge(S["kept"], 3 * len(jobs))
                pe.wait_ge(S["v_kept"], TILES)

                def scores(i):
                    t, q4 = i // 4, i % 4
                    u = i // 2
                    pe.wait_ge(S["owned"], u + 1)
                    if i >= 2:
                        pe.wait_ge(sm.masked, i - 1)
                    nc.tensor.matmul(m.ps[:ROWS, i % 2, :4 * ROWS], qT[:, q4 // 2, tile_cols(t)],
                                     own[:, u % 2, 4 * (q4 % 2):4 * (q4 % 2) + 4, :], start=True,
                                     stop=True).then_inc(sm.scored, 1)

                def weigh(i):
                    t, q4 = i // 4, i % 4
                    pe.wait_ge(sm.kept, i + 1)
                    if q4 == 0 and t >= 2:
                        pe.wait_ge(S["mix_kept"], t - 1)
                    for j in range(4):
                        h = 4 * q4 + j
                        mm = nc.tensor.matmul(m.ps[:ROWS, 4 + t % 2, h * DH:(h + 1) * DH],
                                              sm.turnedP[:, i % 2, j * ROWS:(j + 1) * ROWS],
                                              v[:, t, h * DH:(h + 1) * DH], start=True, stop=True)
                    mm.then_inc(sm.used, 1)

                def turn_mix(t):
                    pe.wait_ge(S["mix_kept"], t + 1)
                    if t >= 1:
                        pe.wait_ge(S["mixT_kept"], t)
                    for k in range(KD):
                        mm = nc.tensor.transpose(m.ps[:, 6, k * ROWS:(k + 1) * ROWS], mix[:, t % 2, k * 128:(k + 1) * 128],
                                                 m.ident[:ROWS, :ROWS])
                    mm.then_inc(S["mix_turned"], 1)

                def output(t):
                    pe.wait_ge(S["mixT_kept"], t + 1)
                    if t >= 1:
                        pe.wait_ge(S["added"], t)
                    for k in range(KD):
                        mm = nc.tensor.matmul(m.ps[:ROWS, 7, :D], mixT[:, t % 2, k, :], wo[:, k, :],
                                              start=(k == 0), stop=(k == KD - 1))
                    mm.then_inc(S["out_done"], 1)

                for i in range(ITEMS + 5):
                    if i < ITEMS:
                        scores(i)
                    if 2 <= i < ITEMS + 2:
                        sm.tensor_turn(pe, i - 2, sm.expd)
                    if 3 <= i < ITEMS + 3:
                        weigh(i - 3)
                    if i >= 7 and (i - 7) % 4 == 0:
                        turn_mix((i - 7) // 4)
                    if i >= 8 and (i - 8) % 4 == 0:
                        output((i - 8) // 4)

            @block.scalar
            def _(act):
                for j, (_, mk, dst) in enumerate(jobs):
                    for c in range(3):
                        n = 3 * j + c
                        act.wait_ge(S["made"], n + 1)
                        nc.scalar.activation(dst[:, mk, third(c)], m.ps[:, n % 4, :THIRD], ACT.Copy).then_inc(S["kept"], 1)
                for t in range(TILES):
                    act.wait_ge(S["v_made"], t + 1)
                    nc.scalar.activation(v[:, t, :], m.ps[:ROWS, 4 + t % 4, :D], ACT.Copy).then_inc(S["v_kept"], 1)

                def keep_mixT(t):
                    act.wait_ge(S["mix_turned"], t + 1)
                    if t >= 2:
                        act.wait_ge(S["out_done"], t - 1)
                    nc.scalar.activation(mixT[:, t % 2, :, :].rearrange("p k n -> p (k n)"), m.ps[:, 6, :KD * ROWS],
                                         ACT.Copy).then_inc(S["mixT_kept"], 1)

                for i in range(ITEMS + 5):
                    if i < ITEMS:
                        sm.scalar_exp(act, i)
                    if 2 <= i < ITEMS + 2:
                        sm.scalar_keep(act, i - 2, sm.used)
                    if i >= 8 and (i - 8) % 4 == 0:
                        keep_mixT((i - 8) // 4)

            @block.vector
            def _(dve):
                dve.wait_ge(sm.mask_loaded, 16)

                def add(t):
                    dve.wait_ge(S["out_done"], t + 1)
                    nc.vector.tensor_tensor(m.xn[:, t, :], m.ps[:ROWS, 7, :D], m.xn[:, t, :],
                                            ALU.add).then_inc(S["added"], 1)

                def keep_mix(t):
                    den = sm.den[:, 4 * t:4 * t + 4, :].rearrange("p i (j o) -> p (i j) o", o=1)
                    dve.wait_ge(sm.expd, 4 * (t + 1))
                    nc.vector.reciprocal(sm.den[:, 4 * t:4 * t + 4, :], sm.den[:, 4 * t:4 * t + 4, :]).then_inc(sm.inverted, 1)
                    dve.wait_ge(sm.inverted, t + 1)
                    dve.wait_ge(sm.used, 4 * (t + 1))
                    if t >= 2:
                        dve.wait_ge(S["mix_turned"], t - 1)
                    nc.vector.tensor_tensor(mix[:, t % 2, :].rearrange("p (h d) -> p h d", h=H),
                                            m.ps[:ROWS, 4 + t % 2, :D].rearrange("p (h d) -> p h d", h=H),
                                            den.broadcast_to([ROWS, H, DH]), ALU.mult).then_inc(S["mix_kept"], 1)

                for i in range(ITEMS + 5):
                    if i < ITEMS:
                        sm.vector_mask(dve, i)
                    if i >= 6 and (i - 6) % 4 == 0:
                        keep_mix((i - 6) // 4)
                    if i >= 8 and (i - 8) % 4 == 0:
                        add((i - 8) // 4)

            @block.gpsimd
            def _(pool):
                pool.wait_ge(S["loaded"], 16 * 5)
                pool.wait_ge(S["kept"], 3 * len(jobs))

                def own_keys(u):
                    t, k = u // 2, u % 2
                    if u >= 2:
                        pool.wait_ge(sm.scored, 2 * (u - 1))
                    keys = kT[:, k, tile_cols(t)].rearrange("p (o n) -> p o n", o=1).broadcast_to([128, HALF, ROWS])
                    mine = heads[:, :].rearrange("p (h o) -> p h o", o=1).broadcast_to([128, HALF, ROWS])
                    nc.gpsimd.tensor_tensor(own[:, u % 2, :, :], keys, mine, ALU.mult).then_inc(S["owned"], 1)

                own_keys(0)
                own_keys(1)
                for i in range(ITEMS):
                    if i % 2 == 0 and 2 <= i and i // 2 + 1 < 2 * TILES:
                        own_keys(i // 2 + 1)


def ds(i):
    return bass.ds(i, 1)


def experts_mlp(nc, m, dram, wts, wtsT):
    E, F = 8, 1024
    KF = F // 128
    NG = len(GROUPS)
    with ExitStack() as ctx:
        w1_raw = m.sbuf(ctx, "l2m_w1_raw", [128, KD, F])
        w2_raw = m.sbuf(ctx, "l2m_w2_raw", [128, KF, D])
        w1 = [m.pair(ctx, f"l2m_w1_{p}", [128, KD, F]) for p in range(2)]
        w2 = [m.pair(ctx, f"l2m_w2_{p}", [128, KF, D]) for p in range(2)]
        b1 = [m.sbuf(ctx, f"l2m_b1_{p}", [128, KF]) for p in range(2)]
        b2 = m.sbuf(ctx, "l2m_b2", [E, D])
        x = m.pair(ctx, "l2m_x", [128, KD, COLS + 1])
        whole = m.sbuf(ctx, "l2m_whole", [128, 3, 4 * ROWS])
        hid = m.pair(ctx, "l2m_hid", [128, 2, KF, 4 * ROWS])
        w1_loaded = m.sem("l2m_w1_loaded")
        w2_loaded = m.sem("l2m_w2_loaded")
        b1_loaded = [m.sem(f"l2m_b1_loaded{p}") for p in range(2)]
        b2_loaded = m.sem("l2m_b2_loaded")
        x_high = m.sem("l2m_x_high")
        x_padded = m.sem("l2m_x_padded")
        x_low = m.sem("l2m_x_low")
        w_high = m.sem("l2m_w_high")
        w_low = m.sem("l2m_w_low")
        raised = m.sem("l2m_raised")
        gelued = m.sem("l2m_gelued")
        split = m.sem("l2m_split")
        lowered = m.sem("l2m_lowered")
        summed = m.sem("l2m_summed")
        biased = m.sem("l2m_biased")
        bias_added = m.sem("l2m_bias_added")
        UP, DOWN = 2 * NG * KF, 2 * TILES

        def steps(p):
            return [(g, p * NG + g, t0, n, p * TILES + t0) for g, (t0, n) in enumerate(GROUPS)]

        def turns(eng, turn):
            with eng.Fori(0, E // 2 - 1) as i:
                turn(i, False)
            turn(E // 2 - 1, True)

        with nc.Block() as block:
            @block.sync
            def _(sp):
                sp.dma_start(b2[:, :], dram["l2m_b2"]).then_inc(b2_loaded, 16)
                with sp.Fori(0, E // 2) as i:
                    for p in range(2):
                        sp.wait_ge(w_low, i * 4 + 2 * p + 1)
                        sp.dma_start(w1_raw[:, :, :], dram["l2m_w1"][ds(2 * i + p)].rearrange("o (k p) n -> p (o k) n", p=128)).then_inc(w1_loaded, 16)
                        sp.wait_ge(w_low, i * 4 + 2 * p + 2)
                        sp.dma_start(w2_raw[:, :, :], dram["l2m_w2"][ds(2 * i + p)].rearrange("o (k p) n -> p (o k) n", p=128)).then_inc(w2_loaded, 16)
                        sp.wait_ge(lowered, i * DOWN + (p + 1) * TILES)
                        sp.dma_start(b1[p][:, :], dram["l2m_b1"][ds(2 * i + p)].rearrange("o p f -> (o p) f")).then_inc(b1_loaded[p], 16)

            @block.tensor
            def _(pe):
                pe.sem_inc(lowered, DOWN)
                pe.wait_ge(b2_loaded, 16)
                for t in range(TILES):
                    if t >= 4:
                        pe.wait_ge(bias_added, t - 3)
                    nc.tensor.matmul(m.ps[:ROWS, t % 4, :D], wtsT[:, tile_cols(t)], b2[:, :], start=True,
                                     stop=True).then_inc(biased, 1)
                pe.wait_ge(bias_added, TILES)
                pe.wait_ge(x_low, 1)

                def turn(i, last):
                    def lower(p, u, t0, n, before):
                        pe.wait_ge(split, i * UP + (u + 1) * KF + UP)
                        pe.wait_ge(w_low, i * 4 + 2 * p + 4)
                        for r in range(n):
                            c = before + r
                            pe.wait_ge(summed, i * DOWN + DOWN + c - 1)
                            for f in range(KF):
                                for a, b in PASSES:
                                    mm = nc.tensor.matmul(m.ps[:ROWS, 6 + c % 2, :D], hid[a][:, u % 2, f, r * ROWS:(r + 1) * ROWS],
                                                          w2[p][b][:, f, :], start=(f == 0 and a + b == 0),
                                                          stop=(f == KF - 1 and a == 1))
                            mm.then_inc(lowered, 1)

                    waiting = None
                    for p in range(2):
                        pe.wait_ge(w_low, i * 4 + 2 * p + 3)
                        for g, u, t0, n, before in steps(p):
                            wide = n * ROWS + n * ROWS % 2
                            cols = slice(t0 * ROWS, t0 * ROWS + wide)
                            for f in range(KF):
                                c = u * KF + f
                                pe.wait_ge(gelued, i * UP + UP + c - 5)
                                for k in range(KD):
                                    for a, b in PASSES:
                                        mm = nc.tensor.matmul(m.ps[:, c % 6, :wide], w1[p][a][:, k, f * 128:(f + 1) * 128],
                                                              x[b][:, k, cols], start=(k == 0 and a + b == 0),
                                                              stop=(k == KD - 1 and a == 1))
                                mm.then_inc(raised, 1)
                            if waiting is not None:
                                lower(*waiting)
                            waiting = (p, u, t0, n, before)
                    lower(*waiting)

                turns(pe, turn)

            @block.scalar
            def _(act):
                nc.scalar.activation(x[0][:, :, :COLS], m.xT[:, :, :], ACT.Copy).then_inc(x_high, 1)
                act.sem_inc(gelued, UP)
                act.wait_ge(w1_loaded, 16)
                nc.scalar.activation(w1[0][0][:, :, :], w1_raw[:, :, :], ACT.Copy).then_inc(w_high, 1)
                act.wait_ge(w2_loaded, 16)
                nc.scalar.activation(w2[0][0][:, :, :], w2_raw[:, :, :], ACT.Copy).then_inc(w_high, 1)

                def turn(i, last):
                    for p in range(2):
                        act.wait_ge(b1_loaded[p], i * 16 + 16)
                        for g, u, t0, n, before in steps(p):
                            act.wait_ge(lowered, i * DOWN + DOWN + before - (GROUPS[g - 1][1]))
                            for f in range(KF):
                                c = u * KF + f
                                act.wait_ge(raised, i * UP + c + 1)
                                act.wait_ge(split, i * UP + UP + c - 2)
                                nc.scalar.activation(whole[:, c % 3, :n * ROWS], m.ps[:, c % 6, :n * ROWS],
                                                     ACT.Gelu_apprx_tanh, bias=b1[p][:, f:f + 1])
                                nc.scalar.activation(hid[0][:, u % 2, f, :n * ROWS], m.ps[:, c % 6, :n * ROWS],
                                                     ACT.Gelu_apprx_tanh,
                                                     bias=b1[p][:, f:f + 1]).then_inc(gelued, 1)
                            if g >= 1 and not (last and p == 1):
                                raw, halves, w_loaded = ((w1_raw, w1, w1_loaded), (w2_raw, w2, w2_loaded))[g - 1]
                                act.wait_ge(w_loaded, i * 32 + 16 * (p + 2))
                                act.wait_ge(lowered, i * DOWN + DOWN + p * TILES)
                                nc.scalar.activation(halves[1 - p][0][:, :, :], raw[:, :, :], ACT.Copy).then_inc(w_high, 1)

                turns(act, turn)

            @block.vector
            def _(dve):
                dve.sem_inc(summed, DOWN)
                dve.sem_inc(split, UP)
                dve.sem_inc(w_low, 2)
                for half in x:
                    nc.vector.tensor_copy(half[:, :, COLS:].rearrange("p k o -> p (k o)"), m.ident[:, :KD]).then_inc(x_padded, 1)
                dve.wait_ge(x_high, 1)
                dve.wait_ge(x_padded, 2)
                nc.vector.tensor_tensor(x[1][:, :, :COLS], m.xT[:, :, :], x[0][:, :, :COLS], ALU.subtract).then_inc(x_low, 1)
                for t in range(TILES):
                    dve.wait_ge(biased, t + 1)
                    nc.vector.tensor_tensor(m.xn[:, t, :], m.ps[:ROWS, t % 4, :D], m.xn[:, t, :],
                                            ALU.add).then_inc(bias_added, 1)
                dve.wait_ge(w_high, 1)
                nc.vector.tensor_tensor(w1[0][1][:, :, :], w1_raw[:, :, :], w1[0][0][:, :, :], ALU.subtract).then_inc(w_low, 1)
                dve.wait_ge(w_high, 2)
                nc.vector.tensor_tensor(w2[0][1][:, :, :], w2_raw[:, :, :], w2[0][0][:, :, :], ALU.subtract).then_inc(w_low, 1)

                def turn(i, last):
                    def add(p, u, t0, n, before):
                        for r in range(n):
                            c, t = before + r, t0 + r
                            dve.wait_ge(lowered, i * DOWN + DOWN + c + 1)
                            dve.wait_ge(summed, i * DOWN + DOWN + c - TILES + 1)
                            nc.vector.scalar_tensor_tensor(m.xn[:, t, :], m.ps[:ROWS, 6 + c % 2, :D],
                                                           wts[:, t, ds(2 * i + p)], m.xn[:, t, :], ALU.mult,
                                                           ALU.add).then_inc(summed, 1)

                    waiting = None
                    for p in range(2):
                        for g, u, t0, n, before in steps(p):
                            for f in range(KF):
                                c = u * KF + f
                                dve.wait_ge(gelued, i * UP + UP + c + 1)
                                nc.vector.tensor_tensor(hid[1][:, u % 2, f, :n * ROWS], whole[:, c % 3, :n * ROWS],
                                                        hid[0][:, u % 2, f, :n * ROWS], ALU.subtract).then_inc(split, 1)
                            if waiting is not None:
                                add(*waiting)
                            waiting = (p, u, t0, n, before)
                            if g >= 1 and not (last and p == 1):
                                raw, halves = ((w1_raw, w1), (w2_raw, w2))[g - 1]
                                dve.wait_ge(w_high, i * 4 + 2 * (p + 1) + g)
                                nc.vector.tensor_tensor(halves[1 - p][1][:, :, :], raw[:, :, :], halves[1 - p][0][:, :, :],
                                                        ALU.subtract).then_inc(w_low, 1)
                    add(*waiting)

                turns(dve, turn)
                dve.wait_ge(summed, DOWN * (E // 2 + 1))
                nc.vector.tensor_tensor(m.h[:, :, :], m.h[:, :, :], m.xn[:, :, :], ALU.add).then_inc(bias_added, 1)
                dve.wait_ge(bias_added, TILES + 1)


def layer2_ffn(nc, m, dram):
    normalise(nc, m, "l2f_ln", m.h, turn=False)
    with ExitStack() as ctx:
        scratch = m.sbuf(ctx, "l2f_scratch", [ROWS, TILES, D])
        normalise(nc, m, "l2f_ln1", m.xn, tok=scratch, affine=dram["l2f_ln1"])
    small_head_attention(nc, m, dram)
    with ExitStack() as ctx:
        scratch = m.sbuf(ctx, "l2f_scratch2", [ROWS, TILES, D])
        normalise(nc, m, "l2f_ln2", m.xn, tok=scratch, affine=dram["l2f_ln2"])
    with ExitStack() as ctx:
        wts = m.sbuf(ctx, "l2m_wts", [ROWS, TILES, 8])
        wtsT = m.sbuf(ctx, "l2m_wtsT", [8, COLS])
        gate(nc, m, "l2g", dram["l2g_gw"], dram["l2g_gb"], 8, wts, wtsT, True)
        experts_mlp(nc, m, dram, wts, wtsT)


STAGE[6] = layer2_ffn


def gated_sums(nc, m, dram, gT):
    H, DH, RANK = 16, 16, 16
    with ExitStack() as ctx:
        w = {n: m.sbuf(ctx, "l3a_" + n, [128, KD, D]) for n in ("Wq", "Wk", "Wv", "Wg")}
        w1 = m.sbuf(ctx, "l3a_Wgk1", [128, KD, RANK])
        w2 = m.sbuf(ctx, "l3a_Wgk2", [RANK, D])
        b2 = m.sbuf(ctx, "l3a_bgk2", [128, KD])
        spread_raw = m.sbuf(ctx, "l3a_spread_raw", [128, DH, 128])
        spread = m.sbuf(ctx, "l3a_spread", [128, DH, 128], F32R)
        low = m.sbuf(ctx, "l3a_low", [RANK, COLS])
        kT = m.pair(ctx, "l3a_kT", [128, KD, COLS + 1])
        vT = m.sbuf(ctx, "l3a_vT", [128, KD, COLS])
        qT = m.pair(ctx, "l3a_qT", [128, KD, COLS + 1])
        gates = m.sbuf(ctx, "l3a_gates", [128, KD, COLS])
        mag = m.sbuf(ctx, "l3a_mag", [128, KD, COLS])
        upd = m.sbuf(ctx, "l3a_upd", [128, 2, COLS])
        state = m.sbuf(ctx, "l3a_state", [128, 2, COLS])
        qs = m.sbuf(ctx, "l3a_qs", [128, 2, COLS])
        read = m.sbuf(ctx, "l3a_read", [128, 2, COLS])
        S = {n: m.sem("l3a_" + n) for n in (
            "loaded", "c_loaded", "low_made", "low_kept", "made", "kept", "soft", "log_ready", "gated", "cut", "k_spread",
            "q_spread", "padded", "low_part", "spread_rounded", "updated", "q_kept", "scanned", "was_read", "gathered", "o_kept", "turned", "stored")}
        jobs = [(w["Wk"], k, kT[0]) for k in range(KD)] + [(w["Wv"], k, vT) for k in range(KD)]
        jobs += [(w["Wq"], k, qT[0]) for k in range(KD)] + [(w["Wg"], k, gT) for k in range(KD)]
        split = [(3 * (j + KD) + c, jobs[j][1], pair, c) for j, pair in ((0, kT), (1, kT), (4, qT), (5, qT))
                 for c in range(3)]
        STEPS = KD * DH
        with nc.Block() as block:
            @block.sync
            def _(sp):
                sp.dma_start(w1[:, :, :], dram["l3a_Wgk1"].rearrange("(k p) n -> p k n", p=128)).then_inc(S["loaded"], 16)
                sp.dma_start(w2[:, :], dram["l3a_Wgk2"]).then_inc(S["loaded"], 16)
                sp.dma_start(b2[:, :], dram["l3a_bgk2"]).then_inc(S["loaded"], 16)
                for n in ("Wk", "Wv", "Wq", "Wg"):
                    sp.dma_start(w[n][:, :, :], dram["l3a_" + n].rearrange("(k p) n -> p k n", p=128)).then_inc(S["loaded"], 16)
                sp.dma_start(spread_raw[:, :, :], dram["c_spread"]).then_inc(S["c_loaded"], 16)

            @block.tensor
            def _(pe):
                pe.wait_ge(S["loaded"], 16 * 7)
                for c in range(3):
                    for k in range(KD):
                        mm = nc.tensor.matmul(m.ps[:RANK, 6, :THIRD] if c == 0 else m.ps[:RANK, 6 + (c % 2), :THIRD],
                                              w1[:, k, :], m.xT[:, k, third(c)], start=(k == 0), stop=(k == KD - 1))
                    mm.then_inc(S["low_made"], 1)
                    pe.wait_ge(S["low_kept"], c + 1)
                for j in range(KD + len(jobs)):
                    for c in range(3):
                        n = 3 * j + c
                        if n >= 6:
                            pe.wait_ge(S["kept"], n - 5)
                            lows = len([s for s in split if s[0] <= n - 6])
                            if lows > 0:
                                pe.wait_ge(S["low_part"], lows)
                        out = m.ps[:, n % 6, :THIRD]
                        if j < KD:
                            mm = nc.tensor.matmul(out, w2[:, j * 128:(j + 1) * 128], low[:, third(c)], start=True, stop=True)
                        else:
                            ww, mk, _ = jobs[j - KD]
                            for k in range(KD):
                                mm = nc.tensor.matmul(out, ww[:, k, mk * 128:(mk + 1) * 128], m.xT[:, k, third(c)],
                                                      start=(k == 0), stop=(k == KD - 1))
                        mm.then_inc(S["made"], 1)
                pe.wait_ge(S["kept"], 3 * (KD + len(jobs)))
                pe.wait_ge(S["low_part"], len(split))
                pe.wait_ge(S["spread_rounded"], 1)

                def spread_out(b, i, c, src):
                    for high_low in range(2):
                        mm = nc.tensor.matmul(m.ps[:, b, :width(even_part(c))], spread[:, i % DH, :],
                                              src[high_low][:, i // DH, even_part(c)], start=(high_low == 0),
                                              stop=(high_low == 1))
                    return mm

                def sum_up(i):
                    pe.wait_ge(S["was_read"], i + 1)
                    if i == DH:
                        pe.wait_ge(S["o_kept"], 3)
                    for c in range(3):
                        mm = nc.tensor.matmul(m.ps[:, 5 + c, :THIRD], m.ident[:, :], read[:, i % 2, third(c)],
                                              start=(i % DH == 0), stop=(i % DH == DH - 1), skip_group_check=True)
                    mm.then_inc(S["gathered"], 1)

                for i in range(STEPS):
                    for c in range(3):
                        n = 3 * i + c
                        if n >= 3:
                            pe.wait_ge(S["updated"], n - 2)
                        spread_out(n % 3, i, c, kT).then_inc(S["k_spread"], 1)
                        if n >= 2:
                            pe.wait_ge(S["q_kept"], n - 1)
                        spread_out(3 + n % 2, i, c, qT).then_inc(S["q_spread"], 1)
                    if i >= 1:
                        sum_up(i - 1)
                sum_up(STEPS - 1)
                pe.wait_ge(S["o_kept"], 6)
                for t in range(TILES):
                    if t >= 4:
                        pe.wait_ge(S["stored"], t - 3)
                    for k in range(KD):
                        mm = nc.tensor.transpose(m.ps[:ROWS, t % 4, k * 128:(k + 1) * 128], mag[:, k, tile_cols(t)],
                                                 m.ident[:, :])
                    mm.then_inc(S["turned"], 1)

            @block.scalar
            def _(act):
                for c in range(3):
                    act.wait_ge(S["low_made"], c + 1)
                    nc.scalar.activation(low[:, third(c)], m.ps[:RANK, 6 + (c % 2), :THIRD], ACT.Copy).then_inc(S["low_kept"], 1)
                for j in range(KD):
                    for c in range(3):
                        n = 3 * j + c
                        act.wait_ge(S["made"], n + 1)
                        nc.scalar.activation(gates[:, j, third(c)], m.ps[:, n % 6, :THIRD], ACT.Identity,
                                             bias=b2[:, j:j + 1]).then_inc(S["kept"], 1)
                for j, (_, mk, dst) in enumerate(jobs[:6]):
                    for c in range(3):
                        n = 3 * (j + KD) + c
                        act.wait_ge(S["made"], n + 1)
                        nc.scalar.activation(dst[:, mk, third(c)], m.ps[:, n % 6, :THIRD], ACT.Copy).then_inc(S["kept"], 1)
                act.wait_ge(S["c_loaded"], 16)
                nc.scalar.activation(spread[:, :, :], spread_raw[:, :, :], ACT.Copy).then_inc(S["spread_rounded"], 1)
                nc.scalar.activation(mag[:, :, :], gates[:, :, :], ACT.Abs).then_inc(S["soft"], 1)
                act.wait_ge(S["soft"], 1)
                nc.scalar.activation(mag[:, :, :], mag[:, :, :], ACT.Exp, scale=-1.0).then_inc(S["soft"], 1)
                act.wait_ge(S["soft"], 2)
                nc.scalar.activation(mag[:, :, :], mag[:, :, :], ACT.Ln, bias=1.0).then_inc(S["soft"], 1)
                act.wait_ge(S["log_ready"], 1)
                nc.scalar.activation(gates[:, :, :], gates[:, :, :], ACT.Exp, scale=1.0 / 16.0).then_inc(S["gated"], 1)
                for j, (_, mk, dst) in enumerate(jobs[6:]):
                    for c in range(3):
                        n = 3 * (j + 6 + KD) + c
                        act.wait_ge(S["made"], n + 1)
                        nc.scalar.activation(dst[:, mk, third(c)], m.ps[:, n % 6, :THIRD], ACT.Silu).then_inc(S["kept"], 1)
                def sums(act, k):
                    act.wait_ge(S["gathered"], DH * (k + 1))
                    for c in range(3):
                        nc.scalar.activation(mag[:, k, third(c)], m.ps[:, 5 + c, :THIRD], ACT.Copy).then_inc(S["o_kept"], 1)

                for i in range(STEPS):
                    if i >= 2:
                        act.wait_ge(S["was_read"], i - 1)
                    for c in range(3):
                        n = 3 * i + c
                        act.wait_ge(S["q_spread"], n + 1)
                        nc.scalar.activation(qs[:, i % 2, part(c)], m.ps[:, 3 + n % 2, :width(part(c))], ACT.Copy).then_inc(S["q_kept"], 1)
                    if i == DH + 1:
                        sums(act, 0)
                sums(act, 1)

            @block.vector
            def _(dve):
                for half in kT + qT:
                    nc.vector.tensor_copy(half[:, :, COLS:].rearrange("p k o -> p (k o)"), m.ident[:, :KD]).then_inc(S["padded"], 1)
                dve.wait_ge(S["padded"], 4)
                for n, k, (high, low), c in split:
                    dve.wait_ge(S["kept"], n + 1)
                    nc.vector.tensor_tensor(low[:, k, third(c)], m.ps[:, n % 6, :THIRD], high[:, k, third(c)],
                                            ALU.subtract).then_inc(S["low_part"], 1)
                dve.wait_ge(S["soft"], 3)
                nc.vector.scalar_tensor_tensor(gates[:, :, :], gates[:, :, :], 0.0, mag[:, :, :], ALU.min,
                                               ALU.subtract).then_inc(S["log_ready"], 1)
                dve.wait_ge(S["gated"], 1)
                nc.vector.memset(gates[:, 0, 0:COLS:T], 0.0).then_inc(S["cut"], 1)
                nc.vector.memset(gates[:, 1, 0:COLS:T], 0.0).then_inc(S["cut"], 1)
                dve.wait_ge(S["cut"], 2)
                dve.wait_ge(S["kept"], 3 * (KD + len(jobs)))
                for i in range(STEPS):
                    if i >= 2:
                        dve.wait_ge(S["scanned"], i - 1)
                    for c in range(3):
                        dve.wait_ge(S["k_spread"], 3 * i + c + 1)
                        nc.vector.tensor_tensor(upd[:, i % 2, part(c)], m.ps[:, (3 * i + c) % 3, :width(part(c))],
                                                vT[:, i // DH, part(c)], ALU.mult).then_inc(S["updated"], 1)
                    dve.wait_ge(S["updated"], 3 * i + 3)
                    if i >= 2:
                        dve.wait_ge(S["was_read"], i - 1)
                    nc.vector.tensor_tensor_scan(state[:, i % 2, :], gates[:, i // DH, :], upd[:, i % 2, :], 0.0,
                                                 ALU.mult, ALU.add).then_inc(S["scanned"], 1)
                for t in range(TILES):
                    dve.wait_ge(S["turned"], t + 1)
                    nc.vector.tensor_copy(m.xn[:, t, :], m.ps[:ROWS, t % 4, :D]).then_inc(S["stored"], 1)

            @block.gpsimd
            def _(pool):
                for i in range(STEPS):
                    pool.wait_ge(S["scanned"], i + 1)
                    pool.wait_ge(S["q_kept"], 3 * i + 3)
                    if i >= 2:
                        pool.wait_ge(S["gathered"], i - 1)
                    nc.gpsimd.tensor_tensor(read[:, i % 2, :], state[:, i % 2, :], qs[:, i % 2, :],
                                            ALU.mult).then_inc(S["was_read"], 1)


def gated_output(nc, m, dram, gT):
    with ExitStack() as ctx:
        wo = m.sbuf(ctx, "l3o_Wout", [128, KD, D])
        loaded = m.sem("l3o_loaded")
        gated = m.sem("l3o_gated")
        out_done = m.sem("l3o_out_done")
        added = m.sem("l3o_added")
        with nc.Block() as block:
            @block.sync
            def _(sp):
                sp.dma_start(wo[:, :, :], dram["l3a_Wout"].rearrange("(k p) n -> p k n", p=128)).then_inc(loaded, 16)

            @block.tensor
            def _(pe):
                pe.wait_ge(loaded, 16)
                for t in range(TILES):
                    pe.wait_ge(gated, t + 1)
                    if t >= 4:
                        pe.wait_ge(added, t - 3)
                    for k in range(KD):
                        mm = nc.tensor.matmul(m.ps[:ROWS, t % 4, :D], m.xT[:, k, tile_cols(t)], wo[:, k, :],
                                              start=(k == 0), stop=(k == KD - 1))
                    mm.then_inc(out_done, 1)

            @block.gpsimd
            def _(pool):
                for t in range(TILES):
                    x = m.xT[:, :, tile_cols(t)]
                    nc.gpsimd.tensor_tensor(x, x, gT[:, :, tile_cols(t)], ALU.mult).then_inc(gated, 1)

            @block.vector
            def _(dve):
                for t in range(TILES):
                    dve.wait_ge(out_done, t + 1)
                    nc.vector.tensor_tensor(m.h[:, t, :], m.ps[:ROWS, t % 4, :D], m.h[:, t, :],
                                            ALU.add).then_inc(added, 1)


def layer3_attention(nc, m, dram):
    normalise(nc, m, "l3a_ln", m.h)
    with ExitStack() as ctx:
        gT = m.sbuf(ctx, "l3a_gT", [128, KD, COLS])
        gated_sums(nc, m, dram, gT)
        scratch = m.sbuf(ctx, "l3a_scratch", [ROWS, TILES, D])
        normalise(nc, m, "l3a_on", m.xn, tok=scratch, affine=dram["l3a_norm"])
        gated_output(nc, m, dram, gT)


STAGE[7] = layer3_attention


def rms_turned(nc, m, name, src, rows, tiles, gamma, dstT, scratch):
    per = 512 // rows if rows < 128 else 4
    groups = [(g, min(per, tiles - g)) for g in range(0, tiles, per)]
    with ExitStack() as ctx:
        g = m.sbuf(ctx, name + "_gamma", [128, KD])
        ss = m.sbuf(ctx, name + "_ss", [rows, tiles])
        S = {n: m.sem(f"{name}_{n}") for n in ("loaded", "squared", "summed", "rooted", "step", "scaled", "turned", "kept")}
        with nc.Block() as block:
            @block.sync
            def _(sp):
                sp.dma_start(g[:, :], gamma).then_inc(S["loaded"], 16)

            @block.vector
            def _(dve):
                nc.vector.tensor_tensor(scratch[:, :, :], src[:, :, :], src[:, :, :], ALU.mult).then_inc(S["squared"], 1)
                dve.wait_ge(S["squared"], 1)
                nc.vector.tensor_reduce(ss[:, :], scratch[:, :, :], AX.X, ALU.add).then_inc(S["summed"], 1)
                dve.wait_ge(S["rooted"], 1)
                nc.vector.tensor_scalar(ss[:, :], ss[:, :], 1e-12, None, ALU.max).then_inc(S["step"], 1)
                dve.wait_ge(S["step"], 1)
                nc.vector.reciprocal(ss[:, :], ss[:, :]).then_inc(S["step"], 1)
                dve.wait_ge(S["step"], 2)
                for t in range(tiles):
                    nc.vector.tensor_scalar(scratch[:, t, :], src[:, t, :], ss[:, t:t + 1], float(D) ** 0.5, ALU.mult,
                                            ALU.mult).then_inc(S["scaled"], 1)

            @block.scalar
            def _(act):
                act.wait_ge(S["summed"], 1)
                nc.scalar.activation(ss[:, :], ss[:, :], ACT.Sqrt).then_inc(S["rooted"], 1)
                act.wait_ge(S["loaded"], 16)
                for i, (t0, n) in enumerate(groups):
                    for k in range(KD):
                        act.wait_ge(S["turned"], KD * i + k + 1)
                        nc.scalar.activation(dstT[:, k, t0 * rows:(t0 + n) * rows], m.ps[:, (KD * i + k) % 8, :n * rows],
                                             ACT.Copy, scale=g[:, k:k + 1]).then_inc(S["kept"], 1)

            @block.tensor
            def _(pe):
                for i, (t0, n) in enumerate(groups):
                    pe.wait_ge(S["scaled"], t0 + n)
                    for k in range(KD):
                        b = KD * i + k
                        if b >= 8:
                            pe.wait_ge(S["kept"], b - 7)
                        for j in range(n):
                            mm = nc.tensor.transpose(m.ps[:, b % 8, j * rows:(j + 1) * rows],
                                                     scratch[:, t0 + j, k * 128:(k + 1) * 128], m.ident[:rows, :rows])
                        mm.then_inc(S["turned"], 1)


def combine_weights(nc, m, dram, slotsT, combT, csumT):
    E, SL = 8, 128
    with ExitStack() as ctx:
        b2 = m.sbuf(ctx, "l3c_b2", [E, D])
        p = m.sbuf(ctx, "l3c_p", [ROWS, 2, E, SL])
        mx = m.sbuf(ctx, "l3c_mx", [ROWS, TILES])
        den = m.sbuf(ctx, "l3c_den", [ROWS, TILES])
        csum = m.sbuf(ctx, "l3c_csum", [ROWS, TILES, E])
        S = {n: m.sem("l3c_" + n) for n in ("loaded", "scored", "max_found", "expd", "inverted", "normed", "csummed",
                                            "turned", "kept", "c_turned", "c_kept", "biased", "added")}
        with nc.Block() as block:
            @block.sync
            def _(sp):
                sp.dma_start(b2[:, :], dram["l3f_b2"]).then_inc(S["loaded"], 16)

            @block.tensor
            def _(pe):
                def score(t):
                    if t >= 2:
                        pe.wait_ge(S["expd"], t - 1)
                    for j in range(2):
                        for k in range(KD):
                            mm = nc.tensor.matmul(m.ps[:ROWS, 2 * (t % 2) + j, :], m.xT[:, k, tile_cols(t)],
                                                  slotsT[:, k, j * 512:(j + 1) * 512], start=(k == 0), stop=(k == KD - 1))
                    mm.then_inc(S["scored"], 1)

                def turn(t):
                    pe.wait_ge(S["normed"], t + 1)
                    if t >= 1:
                        pe.wait_ge(S["kept"], 2 * t)
                    for j in range(2):
                        for e in range(4):
                            mm = nc.tensor.transpose(m.ps[:, 4 + j, e * ROWS:(e + 1) * ROWS], p[:, t % 2, 4 * j + e, :],
                                                     m.ident[:ROWS, :ROWS])
                        mm.then_inc(S["turned"], 1)

                for t in range(TILES + 1):
                    if t < TILES:
                        score(t)
                    if t >= 1:
                        turn(t - 1)
                pe.wait_ge(S["csummed"], TILES)
                for g, (t0, n) in enumerate(GROUPS):
                    for j in range(n):
                        mm = nc.tensor.transpose(m.ps[:E, 6, j * ROWS:(j + 1) * ROWS], csum[:, t0 + j, :],
                                                 m.ident[:ROWS, :ROWS])
                    mm.then_inc(S["c_turned"], 1)
                    pe.wait_ge(S["c_kept"], g + 1)
                pe.wait_ge(S["loaded"], 16)
                for t in range(TILES):
                    if t >= 4:
                        pe.wait_ge(S["added"], t - 3)
                    nc.tensor.matmul(m.ps[:ROWS, t % 4, :D], csumT[:, tile_cols(t)], b2[:, :], start=True,
                                     stop=True).then_inc(S["biased"], 1)

            @block.scalar
            def _(act):
                def keep(t):
                    for j in range(2):
                        act.wait_ge(S["turned"], 2 * t + j + 1)
                        nc.scalar.activation(combT[:, 4 * j:4 * j + 4, tile_cols(t)],
                                             m.ps[:, 4 + j, :4 * ROWS].rearrange("p (e n) -> p e n", e=4),
                                             ACT.Copy).then_inc(S["kept"], 1)

                for t in range(TILES + 1):
                    if t < TILES:
                        act.wait_ge(S["max_found"], t + 1)
                        if t >= 2:
                            act.wait_ge(S["turned"], 2 * (t - 1))
                            act.wait_ge(S["csummed"], t - 1)
                        nc.scalar.activation(p[:, t % 2, :, :].rearrange("p e s -> p (e s)"),
                                             m.ps[:ROWS, 2 * (t % 2):2 * (t % 2) + 2, :].rearrange("p b s -> p (b s)"),
                                             ACT.Exp, bias=mx[:, t:t + 1],
                                             accum_out=den[:, t:t + 1]).then_inc(S["expd"], 1)
                    if t >= 1:
                        keep(t - 1)
                for g, (t0, n) in enumerate(GROUPS):
                    act.wait_ge(S["c_turned"], g + 1)
                    nc.scalar.activation(csumT[:, t0 * ROWS:(t0 + n) * ROWS], m.ps[:E, 6, :n * ROWS],
                                         ACT.Copy).then_inc(S["c_kept"], 1)

            @block.vector
            def _(dve):
                def norm(t):
                    dve.wait_ge(S["expd"], t + 1)
                    nc.vector.reciprocal(den[:, t:t + 1], den[:, t:t + 1]).then_inc(S["inverted"], 1)
                    dve.wait_ge(S["inverted"], t + 1)
                    nc.vector.tensor_scalar(p[:, t % 2, :, :], p[:, t % 2, :, :], den[:, t:t + 1], None,
                                            ALU.mult).then_inc(S["normed"], 1)
                    dve.wait_ge(S["normed"], t + 1)
                    nc.vector.tensor_reduce(csum[:, t, :], p[:, t % 2, :, :], AX.X, ALU.add).then_inc(S["csummed"], 1)

                for t in range(TILES + 1):
                    if t < TILES:
                        dve.wait_ge(S["scored"], t + 1)
                        nc.vector.tensor_reduce(mx[:, t:t + 1], m.ps[:ROWS, 2 * (t % 2):2 * (t % 2) + 2, :], AX.XY, ALU.max,
                                                negate=True).then_inc(S["max_found"], 1)
                    if t >= 1:
                        norm(t - 1)
                for t in range(TILES):
                    dve.wait_ge(S["biased"], t + 1)
                    nc.vector.tensor_tensor(m.h[:, t, :], m.ps[:ROWS, t % 4, :D], m.h[:, t, :],
                                            ALU.add).then_inc(S["added"], 1)


def dispatch_weights(nc, m, slotsT, disp, combT, disp_store, comb_store):
    E = 8
    SEQS3 = NSEQ // 3
    with ExitStack() as ctx:
        mx = m.sbuf(ctx, "l3d_mx", [128, 3, NSEQ])
        den = m.sbuf(ctx, "l3d_den", [128, 3, NSEQ])
        S = {n: m.sem("l3d_" + n) for n in ("scored", "max_found", "shifted", "expd", "summed", "inverted", "normed",
                                            "stored")}

        def bank(x, c):
            return x[:, c * THIRD:(c + 1) * THIRD].rearrange("p (s t) -> p s t", t=T)

        def over_t(x, c=None):
            n = NSEQ if c is None else SEQS3
            x = x if c is None else x[:, c * SEQS3:(c + 1) * SEQS3]
            return x.rearrange("p (s o) -> p s o", o=1).broadcast_to([128, n, T])

        with nc.Block() as block:
            @block.sync
            def _(sp):
                for e in range(E):
                    sp.dma_start(comb_store[e], combT[:, e, :]).then_inc(S["stored"], 16)
                for e in range(E):
                    sp.wait_ge(S["normed"], e + 1)
                    sp.dma_start(disp_store[e], disp[:, e, :]).then_inc(S["stored"], 16)
                sp.wait_ge(S["stored"], 2 * E * 16)

            @block.tensor
            def _(pe):
                for e in range(E):
                    if e >= 2:
                        pe.wait_ge(S["shifted"], 3 * (e - 1))
                    for c in range(3):
                        for k in range(KD):
                            mm = nc.tensor.matmul(m.ps[:, 3 * (e % 2) + c, :THIRD], slotsT[:, k, e * 128:(e + 1) * 128],
                                                  m.xT[:, k, third(c)], start=(k == 0), stop=(k == KD - 1))
                    mm.then_inc(S["scored"], 1)

            @block.scalar
            def _(act):
                for e in range(E):
                    act.wait_ge(S["shifted"], 3 * (e + 1))
                    nc.scalar.activation(disp[:, e, :], disp[:, e, :], ACT.Exp).then_inc(S["expd"], 1)

            @block.vector
            def _(dve):
                def finish(e):
                    dve.wait_ge(S["expd"], e + 1)
                    nc.vector.tensor_reduce(den[:, e % 3, :], disp[:, e, :].rearrange("p (s t) -> p s t", t=T), AX.X,
                                            ALU.add).then_inc(S["summed"], 1)
                    dve.wait_ge(S["summed"], e + 1)
                    nc.vector.reciprocal(den[:, e % 3, :], den[:, e % 3, :]).then_inc(S["inverted"], 1)

                for e in range(E + 1):
                    if e < E:
                        dve.wait_ge(S["scored"], e + 1)
                        logits = m.ps[:, 3 * (e % 2):3 * (e % 2) + 3, :THIRD]
                        nc.vector.tensor_reduce(mx[:, e % 3, :], logits.rearrange("p c (s t) -> p c s t", t=T), AX.X,
                                                ALU.max).then_inc(S["max_found"], 1)
                        dve.wait_ge(S["max_found"], e + 1)
                        for c in range(3):
                            nc.vector.tensor_tensor(bank(disp[:, e, :], c),
                                                    m.ps[:, 3 * (e % 2) + c, :THIRD].rearrange("p (s t) -> p s t", t=T),
                                                    over_t(mx[:, e % 3, :], c), ALU.subtract).then_inc(S["shifted"], 1)
                    if e >= 1:
                        if e - 1 >= 3:
                            dve.wait_ge(S["normed"], e - 3)
                        finish(e - 1)

            @block.gpsimd
            def _(pool):
                for e in range(E):
                    pool.wait_ge(S["inverted"], e + 1)
                    x = disp[:, e, :].rearrange("p (s t) -> p s t", t=T)
                    nc.gpsimd.tensor_tensor(x, x, over_t(den[:, e % 3, :]), ALU.mult).then_inc(S["normed"], 1)


def soft_experts(nc, m, dram, comb_store, disp_store):
    E, F, SL = 8, 1024, 128
    KF = F // 128
    HALF = 512
    PAIR = 2 * TILES
    PIECES = 4
    FIRST_SPLIT = 3
    with ExitStack() as ctx:
        w1_raw = m.sbuf(ctx, "l3f_w1_raw", [128, KD, F])
        w2_raw = m.sbuf(ctx, "l3f_w2_raw", [128, KF, D])
        w1 = [m.pair(ctx, f"l3f_w1_{p}", [128, KD, F]) for p in range(2)]
        w2 = [m.pair(ctx, f"l3f_w2_{p}", [128, KF, D]) for p in range(2)]
        comb = [m.sbuf(ctx, f"l3f_comb_{p}", [128, COLS]) for p in range(2)]
        disp = [m.sbuf(ctx, f"l3f_disp_{p}", [128, COLS]) for p in range(2)]
        x = m.pair(ctx, "l3f_x", [128, KD, COLS])
        room = m.xn[:, :, :].rearrange("p t d -> p (t d)")
        b1 = [room[:, p * F:(p + 1) * F] for p in range(2)]
        whole = room[:, 2 * F:2 * F + HALF]
        up = m.pair(ctx, "l3f_up", [ROWS, 2, F])
        diag = m.sbuf(ctx, "l3f_diag", [128, 2, SEQ * ROWS])
        to_slots = m.pair(ctx, "l3f_to_slots", [ROWS, 2, SEQ * SL])
        hid = m.sbuf(ctx, "l3f_hid", [128, 2, F])
        backT = m.pair(ctx, "l3f_backT", [128, 2, KF, ROWS])
        w1_loaded = m.sem("l3f_w1_loaded")
        w2_loaded = m.sem("l3f_w2_loaded")
        rest_loaded = [m.sem(f"l3f_rest_loaded{p}") for p in range(2)]
        w_high = m.sem("l3f_w_high")
        w_low = m.sem("l3f_w_low")
        x_high = m.sem("l3f_x_high")
        x_low = m.sem("l3f_x_low")
        cleared = m.sem("l3f_cleared")
        counts = {"up_made": 2 * PAIR, "up_kept": 2 * PAIR, "up_high": 2 * PAIR, "up_split": 2 * PAIR, "diag_set": PAIR,
                  "d_turned": PAIR, "d_high": PAIR, "d_kept": PAIR, "raised": 3 * PAIR, "gelued": 3 * PAIR,
                  "drawn": 3 * PAIR, "back_high": PAIR, "back_split": PAIR, "lowered": PAIR, "added": PAIR}
        S = {n: m.sem("l3f_" + n) for n in counts}

        def wait(eng, i, name, n):
            eng.wait_ge(S[name], i * counts[name] + counts[name] + n)

        def start(eng, *names):
            for n in names:
                eng.sem_inc(S[n], counts[n])

        def turns(eng, turn):
            with eng.Fori(0, E // 2 - 1) as i:
                turn(i, False)
            turn(E // 2 - 1, True)

        def piece(q, p, part):
            j = q % 2
            if q < 2:
                return w1_raw[:, j, :], w1[p][part][:, j, :]
            half = slice(j * KF // 2, (j + 1) * KF // 2)
            return w2_raw[:, half, :], w2[p][part][:, half, :]

        with nc.Block() as block:
            @block.sync
            def _(sp):
                with sp.Fori(0, E // 2) as i:
                    for p in range(2):
                        e = ds(2 * i + p)
                        sp.wait_ge(w_low, i * 2 * PIECES + p * PIECES + 2)
                        sp.dma_start(w1_raw[:, :, :], dram["l3f_w1"][e].rearrange("o (k p) n -> p (o k) n", p=128)).then_inc(w1_loaded, 16)
                        sp.wait_ge(w_low, i * 2 * PIECES + p * PIECES + 4)
                        sp.dma_start(w2_raw[:, :, :], dram["l3f_w2"][e].rearrange("o (k p) n -> p (o k) n", p=128)).then_inc(w2_loaded, 16)
                        wait(sp, i, "added", (p + 1) * TILES - PAIR)
                        sp.dma_start(disp[p][:, :], disp_store[e].rearrange("o s n -> (o s) n")).then_inc(rest_loaded[p], 16)
                        sp.dma_start(b1[p], dram["l3f_b1"][e].broadcast_to([ROWS, F])).then_inc(rest_loaded[p], 16)
                        sp.dma_start(comb[p][:, :], comb_store[e].rearrange("o s n -> (o s) n")).then_inc(rest_loaded[p], 16)

            @block.tensor
            def _(pe):
                start(pe, "up_made", "d_turned", "raised", "drawn", "lowered")
                pe.wait_ge(x_low, 1)

                def turn(i, last):
                    def raise_tokens(c, half):
                        p, t = divmod(c, TILES)
                        if t == 0 and half == 0:
                            pe.wait_ge(w_low, i * 2 * PIECES + p * PIECES + PIECES + 2)
                        wait(pe, i, "up_kept", 2 * c + half)
                        for k in range(KD):
                            for a, b in PASSES:
                                mm = nc.tensor.matmul(m.ps[:ROWS, 6, :], x[a][:, k, tile_cols(t)],
                                                      w1[p][b][:, k, half * HALF:(half + 1) * HALF],
                                                      start=(k == 0 and a + b == 0), stop=(k == KD - 1 and a == 1))
                        mm.then_inc(S["up_made"], 1)

                    def turn_disp(c):
                        wait(pe, i, "diag_set", c + 1)
                        wait(pe, i, "d_kept", c)
                        wait(pe, i, "added", max(c - 2, 0))
                        for b in range(SEQ):
                            mm = nc.tensor.transpose(m.ps[:ROWS, 7, b * SL:(b + 1) * SL],
                                                     diag[:, c % 2, b * ROWS:(b + 1) * ROWS], m.ident[:, :])
                        mm.then_inc(S["d_turned"], 1)

                    def raise_slots(n):
                        c, b = divmod(n, SEQ)
                        if b == 0:
                            wait(pe, i, "d_kept", c + 1)
                        wait(pe, i, "gelued", n - 1)
                        for half in range(2):
                            if b == 0:
                                wait(pe, i, "up_split", 2 * c + half + 1)
                            for high_low, part in PASSES:
                                mm = nc.tensor.matmul(m.ps[:, 2 * (n % 2) + half, :],
                                                      to_slots[high_low][:, c % 2, b * SL:(b + 1) * SL],
                                                      up[part][:, c % 2, half * HALF:(half + 1) * HALF],
                                                      start=(high_low + part == 0), stop=(high_low == 1))
                        mm.then_inc(S["raised"], 1)

                    def draw(n):
                        c, b = divmod(n, SEQ)
                        p, t = divmod(c, TILES)
                        if t == 0 and b == 0:
                            pe.wait_ge(rest_loaded[p], i * 48 + 48)
                        wait(pe, i, "gelued", n + 1)
                        if b == 0:
                            wait(pe, i, "back_split", c)
                        own = slice(t * ROWS + b * T, t * ROWS + (b + 1) * T)
                        for f in range(KF):
                            col = (f % 4) * ROWS + b * T
                            mm = nc.tensor.matmul(m.ps[:, 4 + f // 4, col:col + T], hid[:, n % 2, f * 128:(f + 1) * 128],
                                                  comb[p][:, own], start=True, stop=True)
                        mm.then_inc(S["drawn"], 1)

                    def lower(c):
                        p, t = divmod(c, TILES)
                        if t == 0:
                            pe.wait_ge(w_low, i * 2 * PIECES + (p + 2) * PIECES)
                        wait(pe, i, "back_split", c + 1)
                        if c + 2 < PAIR:
                            wait(pe, i, "d_kept", c + 3)
                        else:
                            wait(pe, i, "added", c)
                        for f in range(KF):
                            for a, b in PASSES:
                                mm = nc.tensor.matmul(m.ps[:ROWS, 7, :D], backT[a][:, c % 2, f, :], w2[p][b][:, f, :],
                                                      start=(f == 0 and a + b == 0), stop=(f == KF - 1 and a == 1))
                        mm.then_inc(S["lowered"], 1)

                    turn_disp(0)
                    raise_tokens(0, 0)
                    raise_tokens(0, 1)
                    for c in range(PAIR):
                        more = c + 1 < PAIR
                        raise_slots(SEQ * c)
                        if more:
                            turn_disp(c + 1)
                        if c >= 1:
                            draw(SEQ * c - 1)
                        raise_slots(SEQ * c + 1)
                        if more:
                            raise_tokens(c + 1, 0)
                        draw(SEQ * c)
                        raise_slots(SEQ * c + 2)
                        if more:
                            raise_tokens(c + 1, 1)
                        if c >= 1:
                            lower(c - 1)
                        draw(SEQ * c + 1)
                    draw(SEQ * PAIR - 1)
                    lower(PAIR - 1)

                turns(pe, turn)

            @block.scalar
            def _(act):
                nc.scalar.activation(x[0][:, :, :], m.xT[:, :, :], ACT.Copy).then_inc(x_high, 1)
                start(act, "gelued", "back_high")
                for q in range(PIECES):
                    act.wait_ge((w1_loaded, w2_loaded)[q // 2], 16)
                    raw, high = piece(q, 0, 0)
                    nc.scalar.activation(high, raw, ACT.Copy).then_inc(w_high, 1)

                def turn(i, last):
                    def keep_back(c):
                        wait(act, i, "drawn", SEQ * (c + 1))
                        wait(act, i, "lowered", c - 1)
                        nc.scalar.activation(backT[0][:, c % 2, :, :].rearrange("p (b f) n -> p b (f n)", b=2),
                                             m.ps[:, 4:6, :4 * ROWS], ACT.Copy).then_inc(S["back_high"], 1)

                    def split_weights(p, q):
                        act.wait_ge((w1_loaded, w2_loaded)[q // 2], i * 32 + 16 * (p + 2))
                        wait(act, i, "lowered", p * TILES)
                        raw, high = piece(q, 1 - p, 0)
                        nc.scalar.activation(high, raw, ACT.Copy).then_inc(w_high, 1)

                    for n in range(SEQ * PAIR):
                        c, b = divmod(n, SEQ)
                        p, t = divmod(c, TILES)
                        wait(act, i, "raised", n + 1)
                        wait(act, i, "drawn", n - 1)
                        nc.scalar.activation(hid[:, n % 2, :],
                                             m.ps[:, 2 * (n % 2):2 * (n % 2) + 2, :].rearrange("p b s -> p (b s)"),
                                             ACT.Gelu).then_inc(S["gelued"], 1)
                        if b == 0 and c >= 1:
                            keep_back(c - 1)
                        q = t - FIRST_SPLIT
                        if b == 1 and 0 <= q < PIECES and not (last and p == 1):
                            split_weights(p, q)
                    keep_back(PAIR - 1)

                turns(act, turn)

            @block.vector
            def _(dve):
                start(dve, "up_kept", "up_high", "up_split", "diag_set", "d_high", "d_kept", "back_split", "added")
                dve.sem_inc(w_low, PIECES)
                nc.vector.memset(diag[:, :, :], 0.0).then_inc(cleared, 1)
                dve.wait_ge(cleared, 1)
                dve.wait_ge(x_high, 1)
                nc.vector.tensor_tensor(x[1][:, :, :], m.xT[:, :, :], x[0][:, :, :], ALU.subtract).then_inc(x_low, 1)

                def low_weights(p, q, seen):
                    raw, high = piece(q, p, 0)
                    dve.wait_ge(w_high, seen)
                    nc.vector.tensor_tensor(piece(q, p, 1)[1], raw, high, ALU.subtract).then_inc(w_low, 1)

                for q in range(PIECES):
                    low_weights(0, q, q + 1)

                def turn(i, last):
                    def set_diag(c):
                        p, t = divmod(c, TILES)
                        if t == 0:
                            dve.wait_ge(rest_loaded[p], i * 48 + 48)
                        wait(dve, i, "d_turned", c - 1)
                        out = diag[:, c % 2, :].rearrange("p (b s t) -> p b s t", b=SEQ, s=SEQ)
                        for b in range(SEQ):
                            own = slice(t * ROWS + b * T, t * ROWS + (b + 1) * T)
                            ins = nc.vector.tensor_scalar(out[:, b, b, :], disp[p][:, own], 1.0, None, ALU.mult)
                        ins.then_inc(S["diag_set"], 1)

                    def keep_up(c, half):
                        p = c // TILES
                        if half == 0:
                            wait(dve, i, "raised", SEQ * (c - 1))
                        cols = slice(half * HALF, (half + 1) * HALF)
                        wait(dve, i, "up_made", 2 * c + half + 1)
                        wait(dve, i, "up_split", 2 * c + half)
                        nc.vector.tensor_tensor(whole, m.ps[:ROWS, 6, :], b1[p][:, cols], ALU.add).then_inc(S["up_kept"], 1)
                        wait(dve, i, "up_kept", 2 * c + half + 1)
                        nc.vector.tensor_copy(up[0][:, c % 2, cols], whole).then_inc(S["up_high"], 1)
                        wait(dve, i, "up_high", 2 * c + half + 1)
                        nc.vector.tensor_tensor(up[1][:, c % 2, cols], whole, up[0][:, c % 2, cols],
                                                ALU.subtract).then_inc(S["up_split"], 1)

                    def keep_disp(c):
                        wait(dve, i, "d_turned", c + 1)
                        wait(dve, i, "raised", SEQ * (c - 1))
                        turned = m.ps[:ROWS, 7, :SEQ * SL]
                        nc.vector.tensor_copy(to_slots[0][:, c % 2, :], turned).then_inc(S["d_high"], 1)
                        wait(dve, i, "d_high", c + 1)
                        nc.vector.tensor_tensor(to_slots[1][:, c % 2, :], turned, to_slots[0][:, c % 2, :],
                                                ALU.subtract).then_inc(S["d_kept"], 1)

                    def split_back(c):
                        wait(dve, i, "back_high", c + 1)
                        high, low = (half[:, c % 2, :, :].rearrange("p (b f) n -> p b (f n)", b=2) for half in backT)
                        nc.vector.tensor_tensor(low, m.ps[:, 4:6, :4 * ROWS], high, ALU.subtract).then_inc(S["back_split"], 1)

                    def add(c):
                        t = c % TILES
                        wait(dve, i, "lowered", c + 1)
                        wait(dve, i, "added", c)
                        nc.vector.tensor_tensor(m.h[:, t, :], m.ps[:ROWS, 7, :D], m.h[:, t, :],
                                                ALU.add).then_inc(S["added"], 1)

                    set_diag(0)
                    keep_disp(0)
                    set_diag(1)
                    keep_up(0, 0)
                    keep_up(0, 1)
                    for c in range(PAIR):
                        more = c + 1 < PAIR
                        if more:
                            keep_disp(c + 1)
                        if c >= 1:
                            split_back(c - 1)
                        if more:
                            keep_up(c + 1, 0)
                            keep_up(c + 1, 1)
                        p, t = divmod(c, TILES)
                        q = t - FIRST_SPLIT
                        if 0 <= q < PIECES and not (last and p == 1):
                            low_weights(1 - p, q, i * 2 * PIECES + (p + 1) * PIECES + q + 1)
                        if c >= 1:
                            add(c - 1)
                        if c + 2 < PAIR:
                            set_diag(c + 2)
                    split_back(PAIR - 1)
                    add(PAIR - 1)

                turns(dve, turn)


def layer3_ffn(nc, m, dram):
    normalise(nc, m, "l3f_ln", m.h, turn=False)
    comb_store = nc.dram_tensor("l3f_comb_store", [8, 128, COLS], F32, kind="Internal").ap()
    disp_store = nc.dram_tensor("l3f_disp_store", [8, 128, COLS], F32, kind="Internal").ap()
    with ExitStack() as ctx:
        combT = m.sbuf(ctx, "l3f_combT", [128, 8, COLS])
        disp = m.sbuf(ctx, "l3f_disp", [128, 8, COLS])
        slots = m.sbuf(ctx, "l3f_slots", [128, 8, D])
        slotsT = m.sbuf(ctx, "l3f_slotsT", [128, KD, 8 * 128])
        csumT = m.sbuf(ctx, "l3f_csumT", [8, COLS])
        scratch = m.sbuf(ctx, "l3f_scratch", [ROWS, TILES, D])
        slot_scratch = m.sbuf(ctx, "l3f_slot_scratch", [128, 8, D])
        loaded = m.sem("l3f_slots_loaded")
        with nc.Block() as block:
            @block.sync
            def _(sp):
                sp.dma_start(slots[:, :, :], dram["l3f_slots"].rearrange("e s d -> s e d")).then_inc(loaded, 16)
                sp.wait_ge(loaded, 16)
        rms_turned(nc, m, "l3r", m.xn, ROWS, TILES, dram["l3f_gamma"], m.xT, scratch)
        rms_turned(nc, m, "l3s", slots, 128, 8, dram["l3f_slot_gamma"], slotsT, slot_scratch)
        combine_weights(nc, m, dram, slotsT, combT, csumT)
        dispatch_weights(nc, m, slotsT, disp, combT, disp_store, comb_store)
    soft_experts(nc, m, dram, comb_store, disp_store)


STAGE[8] = layer3_ffn


def arranged(x):
    import numpy as np
    C = np.ascontiguousarray
    a = {k: np.asarray(v) for k, v in x.items()}
    out = {}
    B = a["x"].shape[0]
    p = a["x"].reshape(B, 3, 6, 16, 6, 16).transpose(1, 3, 5, 0, 2, 4).reshape(768, B, T - 1)
    patches = np.zeros((768, NSEQ, T), np.float32)
    patches[:, :B, 1:] = p
    out["patchesT"] = patches.reshape(768, COLS)
    out["tok_wT"] = C(a["L0_tok_W"].T)
    one = np.concatenate([a["L0_tok_cls_token"].reshape(1, D), np.repeat(a["L0_tok_b"].reshape(1, D), T - 1, axis=0)])
    out["tok_base"] = np.concatenate([one] * SEQ)
    out["tok_pos"] = np.concatenate([a["L0_tok_pos_embed"].reshape(T, D)] * SEQ)
    cols = lambda v: C(v.reshape(-1, 128).T)
    row = lambda v: v.reshape(1, -1)
    out["c_ident"] = np.eye(128, dtype=np.float32)
    DH = 16
    spread = np.zeros((128, DH, 128), np.float32)
    for j in range(128):
        for e in range(DH):
            spread[(j // DH) * DH + e, e, j] = 1.0
    out["c_spread"] = spread
    out["c_gather"] = C(spread.transpose(2, 1, 0))
    seq = np.arange(ROWS) // T
    out["c_mask"] = np.tile(np.where(seq[:, None] == seq[None, :], 0.0, -1e30).astype(np.float32), (1, 4))
    late = (seq[:, None] == seq[None, :]) & (np.arange(ROWS)[:, None] <= np.arange(ROWS)[None, :])
    out["c_causal"] = np.tile(np.where(late, 0.0, -1e30).astype(np.float32), (1, 4))
    rows8 = np.zeros((8, 8, 128), np.float32)
    for h in range(8):
        rows8[h, h, :] = 1.0
    out["c_rows8"] = rows8
    out["l0a_kwT"] = C(a["L0_attn_key_w"].T)
    out["l0a_vqT"] = C(a["L0_attn_vq_w"].T)
    out["l0a_owT"] = C(a["L0_attn_out_w"].T)
    out["l0a_kb"] = cols(a["L0_attn_key_b"])
    out["l0a_ob"] = row(a["L0_attn_out_b"])
    out["l0f_gwT"] = C(a["L0_ffn_router_weight"].T)
    out["l0f_gb"] = row(a["L0_ffn_router_bias"])
    out["l0f_ew"] = a["L0_ffn_weight"]
    out["l0f_eb"] = a["L0_ffn_bias"]
    for n in ("DQ", "DKV", "KR"):
        out["l1a_w" + n] = a["L1_attn_W_" + n]
        out["l1a_b" + n] = C(a["L1_attn_b_" + n].reshape(-1, 1))
    out["l1a_wUQ"] = a["L1_attn_W_UQ"]
    out["l1a_wUK"] = a["L1_attn_W_UK"]
    out["l1a_wUV"] = np.concatenate([a["L1_attn_W_UV"], a["L1_attn_b_UV"].reshape(1, -1)])
    out["l1a_wQR"] = a["L1_attn_W_QR"]
    out["l1a_bUQ"] = cols(a["L1_attn_b_UQ"])
    out["l1a_bUK"] = cols(a["L1_attn_b_UK"])
    out["l1a_bQR"] = C(a["L1_attn_b_QR"].reshape(8, 32).T)
    out["l1a_wO"] = a["L1_attn_W_O"]
    out["l1a_bO"] = row(a["L1_attn_b_O"])
    out["l1f_gwT"] = C(a["L1_ffn_gate_w"].T)
    out["l1f_gb"] = row(a["L1_ffn_gate_b"])
    out["l1f_ew"] = a["L1_ffn_expert_w"]
    out["l1f_eb"] = a["L1_ffn_expert_b"]
    w = C(a["L2_attn_in_proj_w"].T)
    out["l2a_wz"], out["l2a_wx"] = C(w[:, :512]), C(w[:, 512:1024])
    out["l2a_wdt"], out["l2a_wB"], out["l2a_wC"] = C(w[:, 1024:1032]), C(w[:, 1032:1096]), C(w[:, 1096:1160])
    out["l2a_conv_w"] = C(a["L2_attn_conv_w"].reshape(4, 128, 4).transpose(1, 0, 2))
    out["l2a_conv_b"] = cols(a["L2_attn_conv_b"])
    out["l2a_A_log"] = C(a["L2_attn_A_log"].reshape(8, 1))
    out["l2a_dt_bias"] = C(a["L2_attn_dt_bias"].reshape(8, 1))
    out["l2a_D"] = C(np.broadcast_to(a["L2_attn_D_param"].reshape(1, 8, 1), (ROWS, 8, 64)).reshape(ROWS, 512))
    out["l2a_norm_w"] = cols(a["L2_attn_norm_w"])
    out["l2a_owT"] = C(a["L2_attn_out_proj_w"].T)
    for i in "12":
        out["l2f_ln" + i] = C(np.stack([a[f"L2_ffn_ln{i}_g"].reshape(2, 128), a[f"L2_ffn_ln{i}_b"].reshape(2, 128)]).transpose(2, 0, 1))
    for n in ("Wq", "Wk", "Wv", "Wo"):
        out["l2f_" + n] = a["L2_ffn_" + n]
    out["c_heads"] = np.repeat(np.eye(8, dtype=np.float32), 16, axis=0)
    out["l2g_gw"], out["l2g_gb"] = a["L2_ffn_Wg"], np.zeros((1, 8), np.float32)
    out["l2m_w1"], out["l2m_w2"] = a["L2_ffn_W1"], a["L2_ffn_W2"]
    out["l2m_b1"] = C(a["L2_ffn_b1"].reshape(8, 8, 128).transpose(0, 2, 1))
    out["l2m_b2"] = a["L2_ffn_b2"]
    for n in ("Wq", "Wk", "Wv", "Wg", "Wgk1", "Wgk2", "Wout"):
        out["l3a_" + n] = a["L3_attn_" + n]
    out["l3a_bgk2"] = cols(a["L3_attn_bgk2"])
    out["l3a_norm"] = C(np.stack([a["L3_attn_gamma"].reshape(2, 128), a["L3_attn_beta"].reshape(2, 128)]).transpose(2, 0, 1))
    out["l3f_gamma"] = cols(a["L3_ffn_norm_gamma"])
    out["l3f_slot_gamma"] = cols(a["L3_ffn_slot_norm_gamma"])
    out["l3f_slots"] = a["L3_ffn_slot_embeds"]
    out["l3f_w1"], out["l3f_w2"] = a["L3_ffn_w1"], a["L3_ffn_w2"]
    out["l3f_b1"] = a["L3_ffn_b1"]
    out["l3f_b2"] = a["L3_ffn_b2"]
    return {k: C(v) for k, v in out.items()}


def store(nc, m, out):
    whole = TILES - 1
    rows = out.rearrange("b t d -> (b t) d")
    left = rows.shape[0] - whole * ROWS
    stored = m.sem("stored")
    with nc.Block() as block:
        @block.sync
        def _(sp):
            sp.dma_start(rows[:whole * ROWS, :].rearrange("(t p) d -> p t d", p=ROWS), m.h[:, :whole, :]).then_inc(stored, 16)
            sp.dma_start(rows[whole * ROWS:, :], m.h[:left, whole, :]).then_inc(stored, 16)
            sp.wait_ge(stored, 32)


def vit_tower(nc, dram, out):
    with ExitStack() as ctx:
        m = Memory(nc, ctx)
        constants(nc, m, dram)
        for stage in sorted(STAGE):
            STAGE[stage](nc, m, dram)
            m.end_stage()
        store(nc, m, out)


def kernel(**inputs):
    import numpy as _np
    import concourse.bacc as _bacc
    from concourse import mybir as _mybir
    from concourse.bass_utils import run_bass_kernel_spmd as _run

    nc = _bacc.Bacc("TRN2", target_bir_lowering=False, num_devices=1)
    arrays, dram = {}, {}
    for name, a in arranged(inputs).items():
        arrays[f"in_{name}_dram"] = a
        dram[name] = nc.dram_tensor(f"in_{name}_dram", a.shape, _mybir.dt.from_np(a.dtype), kind="ExternalInput").ap()
    shape = (inputs["x"].shape[0], T, D)
    out = nc.dram_tensor("out_0_dram", shape, F32, kind="ExternalOutput").ap()
    vit_tower(nc, dram, out)
    r = _run(nc, [arrays], core_ids=[0])
    return r.results[0]["out_0_dram"]
```

```python
from contextlib import ExitStack

import concourse.bass as bass
from concourse import mybir

F32 = mybir.dt.float32
F32R = mybir.dt.float32r
PASSES = ((0, 0), (0, 1), (1, 0))
ACT = mybir.ActivationFunctionType
ALU = mybir.AluOpType
AX = mybir.AxisListType

T = 37
SEQ = 3
ROWS = SEQ * T
TILES = 11
COLS = ROWS * TILES
NSEQ = COLS // T
THIRD = COLS // 3
D = 256
KD = D // 128
GROUPS = [(0, 4), (4, 4), (8, 3)]
LN_EPS = 1e-5


class Memory:

    def __init__(self, nc, ctx):
        self.nc, self.ctx, self.sems = nc, ctx, []
        self.h = self.sbuf(ctx, "h", [ROWS, TILES, D])
        self.xn = self.sbuf(ctx, "xn", [ROWS, TILES, D])
        self.xT = self.sbuf(ctx, "xT", [128, KD, COLS])
        self.ident = self.sbuf(ctx, "ident", [128, 128])
        self.ones = self.sbuf(ctx, "ones", [1, 128])
        self.ps = ctx.enter_context(nc.psum_tensor("ps", [128, 8, 512], F32))

    def sbuf(self, ctx, name, shape, dtype=F32):
        return ctx.enter_context(self.nc.sbuf_tensor(name, shape, dtype))

    def pair(self, ctx, name, shape):
        return [self.sbuf(ctx, name + part, shape, F32R) for part in ("_hi", "_lo")]

    def sem(self, name):
        self.sems.append(self.nc.alloc_semaphore(name))
        return self.sems[-1]

    def end_stage(self):
        self.nc.clear_and_free_semaphores(self.sems)
        self.nc.all_engine_barrier()
        self.sems = []


def tile_cols(t):
    return slice(t * ROWS, (t + 1) * ROWS)


def third(c):
    return slice(c * THIRD, (c + 1) * THIRD)


EVEN = 2 * -(-COLS // 6)


def part(c):
    return slice(c * EVEN, min((c + 1) * EVEN, COLS))


def even_part(c):
    return slice(c * EVEN, min((c + 1) * EVEN, COLS + 1))


def width(cols):
    return cols.stop - cols.start


def constants(nc, m, dram):
    loaded = m.sem("const_loaded")
    ones_set = m.sem("const_ones")
    with nc.Block() as block:
        @block.sync
        def _(sp):
            sp.dma_start(m.ident[:, :], dram["c_ident"]).then_inc(loaded, 16)
            sp.wait_ge(loaded, 16)

        @block.vector
        def _(dve):
            nc.vector.memset(m.ones[:, :], 1.0).then_inc(ones_set, 1)
            dve.wait_ge(ones_set, 1)


def tokens(nc, m, dram):
    K = 6
    with ExitStack() as ctx:
        patches_raw = m.sbuf(ctx, "tok_patches_raw", [128, K, COLS])
        w_raw = m.sbuf(ctx, "tok_w_raw", [128, K, D])
        patches = m.pair(ctx, "tok_patches", [128, K, COLS])
        w = m.pair(ctx, "tok_w", [128, K, D])
        base = m.sbuf(ctx, "tok_base", [ROWS, D])
        pos = m.sbuf(ctx, "tok_pos", [ROWS, D])
        zeros_raw = m.sbuf(ctx, "tok_zeros_raw", [1, 2 * D])
        zeros = m.sbuf(ctx, "tok_zeros", [1, 2 * D], F32R)
        zeros_set = m.sem("tok_zeros_set")
        loaded = [m.sem(f"tok_loaded{k}") for k in range(K)]
        base_loaded = m.sem("tok_base_loaded")
        base_summed = m.sem("tok_base_summed")
        high = m.sem("tok_high")
        low = m.sem("tok_low")
        projected = m.sem("tok_projected")
        stored = m.sem("tok_stored")

        def sums(t):
            return m.ps[:ROWS, t // 2, (t % 2) * D:(t % 2 + 1) * D]

        with nc.Block() as block:
            @block.sync
            def _(sp):
                for k in range(K):
                    sp.dma_start(patches_raw[:, k, :], dram["patchesT"][k * 128:(k + 1) * 128, :]).then_inc(loaded[k], 16)
                    sp.dma_start(w_raw[:, k, :], dram["tok_wT"][k * 128:(k + 1) * 128, :]).then_inc(loaded[k], 16)
                sp.dma_start(base[:, :], dram["tok_base"]).then_inc(base_loaded, 16)
                sp.dma_start(pos[:, :], dram["tok_pos"]).then_inc(base_loaded, 16)

            @block.scalar
            def _(act):
                for k in range(K):
                    act.wait_ge(loaded[k], 32)
                    nc.scalar.activation(w[0][:, k, :], w_raw[:, k, :], ACT.Copy).then_inc(high, 1)
                    nc.scalar.activation(patches[0][:, k, :], patches_raw[:, k, :], ACT.Copy).then_inc(high, 1)

            @block.tensor
            def _(pe):
                pe.wait_ge(zeros_set, 2)
                for bank in range(-(-TILES // 2)):
                    nc.tensor.matmul(m.ps[:ROWS, bank, :], zeros[:, :ROWS], zeros[:, :], start=True, stop=False,
                                     skip_group_check=True)
                for k in range(K):
                    pe.wait_ge(low, 2 * k + 2)
                    for t in range(TILES):
                        for a, b in PASSES:
                            mm = nc.tensor.matmul(sums(t), patches[a][:, k, tile_cols(t)], w[b][:, k, :],
                                                  start=False, stop=(k == K - 1 and a == 1),
                                                  skip_group_check=True)
                        if k == K - 1:
                            mm.then_inc(projected, 1)

            @block.vector
            def _(dve):
                nc.vector.memset(zeros_raw[:, :], 0.0).then_inc(zeros_set, 1)
                dve.wait_ge(zeros_set, 1)
                nc.vector.tensor_copy(zeros[:, :], zeros_raw[:, :]).then_inc(zeros_set, 1)
                for k in range(K):
                    dve.wait_ge(high, 2 * k + 1)
                    nc.vector.tensor_tensor(w[1][:, k, :], w_raw[:, k, :], w[0][:, k, :], ALU.subtract).then_inc(low, 1)
                    dve.wait_ge(high, 2 * k + 2)
                    nc.vector.tensor_tensor(patches[1][:, k, :], patches_raw[:, k, :], patches[0][:, k, :],
                                            ALU.subtract).then_inc(low, 1)
                dve.wait_ge(base_loaded, 32)
                nc.vector.tensor_tensor(base[:, :], base[:, :], pos[:, :], ALU.add).then_inc(base_summed, 1)
                dve.wait_ge(base_summed, 1)
                for t in range(TILES):
                    dve.wait_ge(projected, min(t - t % 2 + 2, TILES))
                    nc.vector.tensor_tensor(m.h[:, t, :], sums(t), base[:, :], ALU.add).then_inc(stored, 1)


def normalise(nc, m, name, src, tok=None, dstT=None, eps=LN_EPS, affine=None, turn=True):
    tok = m.xn if tok is None else tok
    dstT = m.xT if dstT is None else dstT
    with ExitStack() as ctx:
        stats = m.sbuf(ctx, name + "_stats", [ROWS, TILES, 6])
        mv = m.sbuf(ctx, name + "_mv", [ROWS, TILES, 2])
        std = m.sbuf(ctx, name + "_std", [ROWS, TILES])
        rstd = m.sbuf(ctx, name + "_rstd", [ROWS, TILES])
        gb = m.sbuf(ctx, name + "_gb", [128, 2, KD])
        counted = m.sem(name + "_counted")
        varred = m.sem(name + "_var")
        rooted = m.sem(name + "_rooted")
        inverted = m.sem(name + "_inverted")
        centred = m.sem(name + "_centred")
        turned = m.sem(name + "_turned")
        kept = m.sem(name + "_kept")
        gb_loaded = m.sem(name + "_gb_loaded")
        with nc.Block() as block:
            @block.sync
            def _(sp):
                if affine is not None:
                    sp.dma_start(gb[:, :, :], affine).then_inc(gb_loaded, 16)

            @block.vector
            def _(dve):
                for t in range(TILES):
                    nc.vector.bn_stats(stats[:, t, :], src[:, t, :]).then_inc(counted, 1)
                for t in range(TILES):
                    dve.wait_ge(counted, t + 1)
                    nc.vector.bn_aggr(mv[:, t, :], stats[:, t, :]).then_inc(varred, 1)
                dve.wait_ge(varred, TILES)
                nc.vector.tensor_scalar(std[:, :], mv[:, :, 1], eps, None, ALU.add).then_inc(varred, 1)
                dve.wait_ge(rooted, 1)
                nc.vector.reciprocal(rstd[:, :], std[:, :]).then_inc(inverted, 1)
                dve.wait_ge(inverted, 1)
                for t in range(TILES):
                    nc.vector.tensor_scalar(tok[:, t, :], src[:, t, :], mv[:, t, 0:1], rstd[:, t:t + 1],
                                            ALU.subtract, ALU.mult).then_inc(centred, 1)

            @block.scalar
            def _(act):
                act.wait_ge(varred, TILES + 1)
                nc.scalar.activation(std[:, :], std[:, :], ACT.Sqrt).then_inc(rooted, 1)
                if affine is not None:
                    act.wait_ge(gb_loaded, 16)
                for g, (t0, n) in enumerate(GROUPS if turn else []):
                    for k in range(KD):
                        i = g * KD + k
                        act.wait_ge(turned, i + 1)
                        out = dstT[:, k, t0 * ROWS:(t0 + n) * ROWS]
                        if affine is None:
                            nc.scalar.activation(out, m.ps[:, i, :n * ROWS], ACT.Copy).then_inc(kept, 1)
                        else:
                            nc.scalar.activation(out, m.ps[:, i, :n * ROWS], ACT.Identity, scale=gb[:, 0, k:k + 1],
                                                 bias=gb[:, 1, k:k + 1]).then_inc(kept, 1)

            @block.tensor
            def _(pe):
                for g, (t0, n) in enumerate(GROUPS if turn else []):
                    pe.wait_ge(centred, t0 + n)
                    for k in range(KD):
                        for j in range(n):
                            mm = nc.tensor.transpose(m.ps[:, g * KD + k, j * ROWS:(j + 1) * ROWS],
                                                     tok[:, t0 + j, k * 128:(k + 1) * 128], m.ident[:ROWS, :ROWS])
                        mm.then_inc(turned, 1)


def decayed_sums(nc, m, dram):
    H, DH = 16, 16
    with ExitStack() as ctx:
        wk = m.sbuf(ctx, "l0a_wk", [128, KD, D])
        wv = m.sbuf(ctx, "l0a_wv", [128, KD, 2 * D])
        wo = m.sbuf(ctx, "l0a_wo", [128, KD, D])
        kb = m.sbuf(ctx, "l0a_kb", [128, KD])
        ob = m.sbuf(ctx, "l0a_ob", [1, D])
        spread_raw = m.sbuf(ctx, "l0a_spread_raw", [128, DH, 128])
        spread = m.sbuf(ctx, "l0a_spread", [128, DH, 128], F32R)
        gather = m.sbuf(ctx, "l0a_gather", [128, DH, 128])
        kT = m.sbuf(ctx, "l0a_kT", [128, KD, COLS])
        omk = m.sbuf(ctx, "l0a_omk", [128, KD, COLS])
        vT = m.pair(ctx, "l0a_vT", [128, KD, COLS + 1])
        qT = m.sbuf(ctx, "l0a_qT", [128, KD, COLS])
        upd = m.sbuf(ctx, "l0a_upd", [128, 2, COLS])
        state = m.sbuf(ctx, "l0a_state", [128, 3, COLS])
        read = m.sbuf(ctx, "l0a_read", [128, 3, COLS])
        oT = m.sbuf(ctx, "l0a_oT", [128, KD, COLS])
        w_loaded = m.sem("l0a_w_loaded")
        c_loaded = m.sem("l0a_c_loaded")
        projected = m.sem("l0a_projected")
        kept = m.sem("l0a_kept")
        padded = m.sem("l0a_padded")
        v_low = m.sem("l0a_v_low")
        spread_rounded = m.sem("l0a_spread_rounded")
        complemented = m.sem("l0a_complemented")
        cut = m.sem("l0a_cut")
        spread_done = m.sem("l0a_spread_done")
        updated = m.sem("l0a_updated")
        scanned = m.sem("l0a_scanned")
        was_read = m.sem("l0a_was_read")
        gathered = m.sem("l0a_gathered")
        o_kept = m.sem("l0a_o_kept")
        out_done = m.sem("l0a_out_done")
        added = m.sem("l0a_added")
        jobs = [(wk, 0, kT, 0), (wk, 128, kT, 1), (wv, 0, vT[0], 0), (wv, 128, vT[0], 1), (wv, 256, qT, 0), (wv, 384, qT, 1)]
        STEPS = KD * DH
        with nc.Block() as block:
            @block.sync
            def _(sp):
                sp.dma_start(wk[:, :, :], dram["l0a_kwT"].rearrange("(k p) n -> p k n", p=128)).then_inc(w_loaded, 16)
                sp.dma_start(wv[:, :, :], dram["l0a_vqT"].rearrange("(k p) n -> p k n", p=128)).then_inc(w_loaded, 16)
                sp.dma_start(kb[:, :], dram["l0a_kb"]).then_inc(w_loaded, 16)
                sp.dma_start(spread_raw[:, :, :], dram["c_spread"]).then_inc(c_loaded, 16)
                sp.dma_start(gather[:, :, :], dram["c_gather"]).then_inc(c_loaded, 16)
                sp.dma_start(wo[:, :, :], dram["l0a_owT"].rearrange("(k p) n -> p k n", p=128)).then_inc(c_loaded, 16)
                sp.dma_start(ob[:, :], dram["l0a_ob"]).then_inc(c_loaded, 16)

            @block.tensor
            def _(pe):
                pe.wait_ge(w_loaded, 48)
                for j, (w, col, _, _) in enumerate(jobs):
                    if j >= 2:
                        pe.wait_ge(kept, j - 1)
                    if j >= 4:
                        pe.wait_ge(v_low, j - 3)
                    for c in range(3):
                        for k in range(KD):
                            mm = nc.tensor.matmul(m.ps[:, 3 * (j % 2) + c, :THIRD], w[:, k, col:col + 128],
                                                  m.xT[:, k, third(c)], start=(k == 0), stop=(k == KD - 1))
                    mm.then_inc(projected, 1)
                pe.wait_ge(kept, len(jobs))
                pe.wait_ge(v_low, 2)
                pe.wait_ge(spread_rounded, 1)

                def sum_up(i):
                    pe.wait_ge(was_read, i + 1)
                    if i == DH:
                        pe.wait_ge(o_kept, 3)
                    for c in range(3):
                        mm = nc.tensor.matmul(m.ps[:, 5 + c, :THIRD], gather[:, i % DH, :], read[:, i % 3, third(c)],
                                              start=(i % DH == 0), stop=(i % DH == DH - 1), skip_group_check=True)
                    mm.then_inc(gathered, 1)

                for i in range(STEPS):
                    for c in range(3):
                        n = 3 * i + c
                        if n >= 5:
                            pe.wait_ge(updated, n - 4)
                        for high_low in range(2):
                            mm = nc.tensor.matmul(m.ps[:, n % 5, :width(even_part(c))], spread[:, i % DH, :],
                                                  vT[high_low][:, i // DH, even_part(c)], start=(high_low == 0),
                                                  stop=(high_low == 1))
                        mm.then_inc(spread_done, 1)
                    if i >= 2:
                        sum_up(i - 2)
                sum_up(STEPS - 2)
                sum_up(STEPS - 1)
                pe.wait_ge(o_kept, 6)
                for t in range(TILES):
                    if t >= 4:
                        pe.wait_ge(added, t - 3)
                    for k in range(KD):
                        nc.tensor.matmul(m.ps[:ROWS, t % 4, :D], oT[:, k, tile_cols(t)], wo[:, k, :],
                                         start=(k == 0), stop=False)
                    nc.tensor.matmul(m.ps[:ROWS, t % 4, :D], m.ones[:, :ROWS], ob[:, :],
                                     start=False, stop=True).then_inc(out_done, 1)

            @block.scalar
            def _(act):
                for j, (_, _, dst, k) in enumerate(jobs):
                    act.wait_ge(projected, j + 1)
                    src = m.ps[:, 3 * (j % 2):3 * (j % 2) + 3, :THIRD]
                    out = dst[:, k, :COLS].rearrange("p (c n) -> p c n", c=3)
                    if dst is kT:
                        nc.scalar.activation(out, src, ACT.Sigmoid, bias=kb[:, k:k + 1]).then_inc(kept, 1)
                    else:
                        nc.scalar.activation(out, src, ACT.Copy).then_inc(kept, 1)
                act.wait_ge(c_loaded, 64)
                nc.scalar.activation(spread[:, :, :], spread_raw[:, :, :], ACT.Copy).then_inc(spread_rounded, 1)
                for k in range(KD):
                    act.wait_ge(gathered, DH * (k + 1))
                    for c in range(3):
                        nc.scalar.activation(oT[:, k, third(c)], m.ps[:, 5 + c, :THIRD], ACT.Copy).then_inc(o_kept, 1)

            @block.vector
            def _(dve):
                for half in vT:
                    nc.vector.tensor_copy(half[:, :, COLS:].rearrange("p k o -> p (k o)"), m.ident[:, :KD]).then_inc(padded, 1)
                dve.wait_ge(padded, 2)
                for k in range(KD):
                    dve.wait_ge(kept, k + 1)
                    nc.vector.tensor_scalar(omk[:, k, :], kT[:, k, :], -1.0, 1.0, ALU.mult,
                                            ALU.add).then_inc(complemented, 1)
                    dve.wait_ge(complemented, k + 1)
                    nc.vector.memset(kT[:, k, 0:COLS:T], 0.0).then_inc(cut, 1)
                for k in range(KD):
                    dve.wait_ge(kept, k + 3)
                    high, low = (half[:, k, :COLS].rearrange("p (c n) -> p c n", c=3) for half in vT)
                    nc.vector.tensor_tensor(low, m.ps[:, 3 * k:3 * k + 3, :THIRD], high, ALU.subtract).then_inc(v_low, 1)
                dve.wait_ge(cut, 2)
                for i in range(STEPS):
                    if i >= 2:
                        dve.wait_ge(scanned, i - 1)
                    for c in range(3):
                        dve.wait_ge(spread_done, 3 * i + c + 1)
                        nc.vector.tensor_tensor(upd[:, i % 2, part(c)], m.ps[:, (3 * i + c) % 5, :width(part(c))],
                                                omk[:, i // DH, part(c)], ALU.mult).then_inc(updated, 1)
                    dve.wait_ge(updated, 3 * i + 3)
                    if i >= 3:
                        dve.wait_ge(was_read, i - 2)
                    nc.vector.tensor_tensor_scan(state[:, i % 3, :], kT[:, i // DH, :], upd[:, i % 2, :], 0.0,
                                                 ALU.mult, ALU.add).then_inc(scanned, 1)
                for t in range(TILES):
                    dve.wait_ge(out_done, t + 1)
                    nc.vector.tensor_tensor(m.h[:, t, :], m.ps[:ROWS, t % 4, :D], m.h[:, t, :],
                                            ALU.add).then_inc(added, 1)

            @block.gpsimd
            def _(pool):
                pool.wait_ge(kept, 6)
                for i in range(STEPS):
                    pool.wait_ge(scanned, i + 1)
                    if i >= 3:
                        pool.wait_ge(gathered, i - 2)
                    nc.gpsimd.tensor_tensor(read[:, i % 3, :], state[:, i % 3, :], qT[:, i // DH, :],
                                            ALU.mult).then_inc(was_read, 1)


def gate(nc, m, name, gw, gb, E, wts, wtsT, weighted, ahead=None):
    PAD = 6
    with ExitStack() as ctx:
        w = m.sbuf(ctx, name + "_gw", [128, KD, E])
        b = m.sbuf(ctx, name + "_gb", [ROWS, E])
        mx = m.sbuf(ctx, name + "_mx", [ROWS, TILES])
        ex = m.sbuf(ctx, name + "_ex", [ROWS, TILES, E])
        den = m.sbuf(ctx, name + "_den", [ROWS, TILES])
        pr = m.sbuf(ctx, name + "_pr", [ROWS, TILES, E + PAD])
        rest = m.sbuf(ctx, name + "_rest", [ROWS, TILES, E + PAD])
        top = m.sbuf(ctx, name + "_top", [ROWS, TILES, 8])
        loaded = m.sem(name + "_loaded")
        scored = m.sem(name + "_scored")
        step = m.sem(name + "_dve_step")
        shifted = m.sem(name + "_shifted")
        expd = m.sem(name + "_expd")
        weighed = m.sem(name + "_weighed")
        turned = m.sem(name + "_turned")
        kept = m.sem(name + "_kept")
        logits = m.ps[:ROWS, 0, :TILES * E].rearrange("p (t e) -> p t e", e=E)

        def over_e(x, n):
            return x[:, :].rearrange("p (t o) -> p t o", o=1).broadcast_to([ROWS, TILES, n])

        with nc.Block() as block:
            @block.sync
            def _(sp):
                sp.dma_start(w[:, :, :], gw.rearrange("(k p) n -> p k n", p=128)).then_inc(loaded, 16)
                sp.dma_start(b[:, :], gb.broadcast_to([ROWS, E])).then_inc(loaded, 16)
                if ahead is not None:
                    ahead.load(sp)

            @block.tensor
            def _(pe):
                pe.wait_ge(loaded, 32)
                for t in range(TILES):
                    for k in range(KD):
                        mm = nc.tensor.matmul(logits[:, t, :], m.xT[:, k, tile_cols(t)], w[:, k, :],
                                              start=(k == 0), stop=(k == KD - 1))
                mm.then_inc(scored, 1)
                pe.wait_ge(weighed, 1)
                for g, (t0, n) in enumerate(GROUPS):
                    for j in range(n):
                        mm = nc.tensor.transpose(m.ps[:8, 1 + g, j * ROWS:(j + 1) * ROWS], wts[:, t0 + j, :],
                                                 m.ident[:ROWS, :ROWS])
                    mm.then_inc(turned, 1)

            @block.scalar
            def _(act):
                if ahead is not None:
                    ahead.scalar_high(act)
                act.wait_ge(shifted, 1)
                nc.scalar.activation(ex[:, :, :], ex[:, :, :], ACT.Exp).then_inc(expd, 1)
                for g, (t0, n) in enumerate(GROUPS):
                    act.wait_ge(turned, g + 1)
                    nc.scalar.activation(wtsT[:, t0 * ROWS:(t0 + n) * ROWS], m.ps[:8, 1 + g, :n * ROWS],
                                         ACT.Copy).then_inc(kept, 1)

            @block.vector
            def _(dve):
                done = [0]

                def link(ins):
                    done[0] += 1
                    ins.then_inc(step, 1)
                    dve.wait_ge(step, done[0])

                if ahead is not None:
                    ahead.vector_low(dve)
                dve.wait_ge(loaded, 32)
                dve.wait_ge(scored, 1)
                link(nc.vector.memset(pr[:, :, E:], -1.0))
                bias = b[:, :].rearrange("p (o e) -> p o e", o=1).broadcast_to([ROWS, TILES, E])
                link(nc.vector.tensor_tensor(ex[:, :, :], logits, bias, ALU.add))
                link(nc.vector.tensor_reduce(mx[:, :], ex[:, :, :], AX.X, ALU.max))
                nc.vector.tensor_tensor(ex[:, :, :], ex[:, :, :], over_e(mx, E), ALU.subtract).then_inc(shifted, 1)
                dve.wait_ge(expd, 1)
                link(nc.vector.tensor_reduce(den[:, :], ex[:, :, :], AX.X, ALU.add))
                link(nc.vector.reciprocal(den[:, :], den[:, :]))
                link(nc.vector.tensor_tensor(pr[:, :, :E], ex[:, :, :], over_e(den, E), ALU.mult))
                for t in range(TILES):
                    ins = nc.vector.max(top[:, t, :], pr[:, t, :E])
                link(ins)
                link(nc.vector.memset(top[:, :, 2:], -1.0))
                for t in range(TILES):
                    ins = nc.vector.match_replace(rest[:, t, :], top[:, t, :], pr[:, t, :], -2.0)
                link(ins)
                if not weighted:
                    nc.vector.tensor_tensor(wts[:, :, :], pr[:, :, :8], rest[:, :, :8], ALU.is_gt).then_inc(weighed, 1)
                    return
                link(nc.vector.tensor_tensor(ex[:, :, :8], pr[:, :, :8], rest[:, :, :8], ALU.is_gt))
                link(nc.vector.tensor_tensor(ex[:, :, :8], ex[:, :, :8], pr[:, :, :8], ALU.mult))
                link(nc.vector.tensor_reduce(den[:, :], ex[:, :, :8], AX.X, ALU.add))
                link(nc.vector.scalar_tensor_tensor(mx[:, :], den[:, :], 0.0, den[:, :], ALU.is_le, ALU.add))
                link(nc.vector.reciprocal(den[:, :], mx[:, :]))
                nc.vector.tensor_tensor(wts[:, :, :], ex[:, :, :8], over_e(den, 8), ALU.mult).then_inc(weighed, 1)


class SmallExperts:

    E = 8

    def __init__(self, nc, m, ctx, name, ew):
        self.nc, self.m, self.ew = nc, m, ew
        self.raw = m.sbuf(ctx, name + "_w_raw", [128, KD, self.E, D])
        self.w = m.pair(ctx, name + "_w", [128, KD, self.E, D])
        self.x = m.pair(ctx, name + "_x", [128, KD, COLS])
        self.loaded = [m.sem(f"{name}_w_loaded{k}") for k in range(KD)]
        self.high = m.sem(name + "_high")
        self.low = m.sem(name + "_low")

    def load(self, sp):
        for k in range(KD):
            rows = slice(k * 128, (k + 1) * 128)
            sp.dma_start(self.raw[:, k, :, :], self.ew[:, rows, :].rearrange("e p n -> p e n")).then_inc(self.loaded[k], 16)

    def scalar_high(self, act):
        self.nc.scalar.activation(self.x[0][:, :, :], self.m.xT[:, :, :], ACT.Copy).then_inc(self.high, 1)
        for k in range(KD):
            act.wait_ge(self.loaded[k], 16)
            self.nc.scalar.activation(self.w[0][:, k, :, :], self.raw[:, k, :, :], ACT.Copy).then_inc(self.high, 1)

    def vector_low(self, dve):
        dve.wait_ge(self.high, 1)
        self.nc.vector.tensor_tensor(self.x[1][:, :, :], self.m.xT[:, :, :], self.x[0][:, :, :],
                                     ALU.subtract).then_inc(self.low, 1)
        for k in range(KD):
            dve.wait_ge(self.high, k + 2)
            self.nc.vector.tensor_tensor(self.w[1][:, k, :, :], self.raw[:, k, :, :], self.w[0][:, k, :, :],
                                         ALU.subtract).then_inc(self.low, 1)


def small_experts(nc, m, name, ready, eb, wts, wtsT):
    E = ready.E
    with ExitStack() as ctx:
        b = m.sbuf(ctx, name + "_b", [E, D])
        loaded = m.sem(name + "_loaded")
        multiplied = m.sem(name + "_multiplied")
        biased = m.sem(name + "_biased")
        added = m.sem(name + "_added")
        with nc.Block() as block:
            @block.sync
            def _(sp):
                sp.dma_start(b[:, :], eb).then_inc(loaded, 16)

            @block.tensor
            def _(pe):
                pe.wait_ge(ready.low, 1 + KD)
                pe.wait_ge(loaded, 16)
                for t in range(TILES):
                    if t >= 2:
                        pe.wait_ge(added, 9 * (t - 1) - 8)
                    nc.tensor.matmul(m.ps[:ROWS, 6 + t % 2, :D], wtsT[:, tile_cols(t)], b[:, :],
                                     start=True, stop=True).then_inc(biased, 1)
                    for p in range(E // 2):
                        i = t * (E // 2) + p
                        if i >= 6:
                            j = i - 6
                            pe.wait_ge(added, 9 * (j // 4) + 1 + 2 * (j % 4 + 1))
                        for k in range(KD):
                            for high_low, part_w in PASSES:
                                mm = nc.tensor.matmul(m.ps[:ROWS, i % 6, :], ready.x[high_low][:, k, tile_cols(t)],
                                                      ready.w[part_w][:, k, 2 * p:2 * p + 2, :],
                                                      start=(k == 0 and high_low + part_w == 0),
                                                      stop=(k == KD - 1 and high_low == 1))
                        mm.then_inc(multiplied, 1)

            @block.vector
            def _(dve):
                for t in range(TILES):
                    dve.wait_ge(biased, t + 1)
                    nc.vector.tensor_tensor(m.h[:, t, :], m.ps[:ROWS, 6 + t % 2, :D], m.h[:, t, :],
                                            ALU.add).then_inc(added, 1)
                    for e in range(E):
                        i = t * (E // 2) + e // 2
                        if e % 2 == 0:
                            dve.wait_ge(multiplied, i + 1)
                        dve.wait_ge(added, 9 * t + e + 1)
                        nc.vector.scalar_tensor_tensor(m.h[:, t, :], m.ps[:ROWS, i % 6, (e % 2) * D:(e % 2 + 1) * D],
                                                       wts[:, t, e:e + 1], m.h[:, t, :], ALU.mult,
                                                       ALU.add).then_inc(added, 1)


def selecting_experts(nc, m, dram, name, E, weighted):
    with ExitStack() as ctx:
        wts = m.sbuf(ctx, name + "_wts", [ROWS, TILES, 8])
        wtsT = m.sbuf(ctx, name + "_wtsT", [8, COLS])
        ready = SmallExperts(nc, m, ctx, name + "e", dram[name + "_ew"])
        gate(nc, m, name + "g", dram[name + "_gwT"], dram[name + "_gb"], E, wts, wtsT, weighted, ready)
        small_experts(nc, m, name + "e", ready, dram[name + "_eb"], wts, wtsT)


STAGE = {
    0: tokens,
    1: lambda nc, m, dram: (normalise(nc, m, "l0a_ln", m.h), decayed_sums(nc, m, dram)),
    2: lambda nc, m, dram: (normalise(nc, m, "l0f_ln", m.h), selecting_experts(nc, m, dram, "l0f", 8, False)),
    4: lambda nc, m, dram: (normalise(nc, m, "l1f_ln", m.h), selecting_experts(nc, m, dram, "l1f", 10, True)),
}
class MaskedSoftmax:

    N = 4 * ROWS

    def __init__(self, nc, m, name, ctx, mask_dram, scale, items, room=None):
        self.nc, self.m, self.scale, self.mask_dram = nc, m, scale, mask_dram
        self.mask = m.sbuf(ctx, name + "_mask", [ROWS, self.N])
        if room is None:
            room = m.sbuf(ctx, name + "_room", [ROWS, 6 * self.N])
        self.scores = room[:, :4 * self.N].rearrange("p (i n) -> p i n", i=4)
        self.turnedP = room[:, 4 * self.N:6 * self.N].rearrange("p (i n) -> p i n", i=2)
        self.mx = m.sbuf(ctx, name + "_mx", [ROWS, 4, 4])
        self.den = m.sbuf(ctx, name + "_den", [ROWS, items, 4])
        self.mask_loaded = m.sem(name + "_mask_loaded")
        self.scored = m.sem(name + "_scored")
        self.masked = m.sem(name + "_masked")
        self.max_found = m.sem(name + "_max_found")
        self.expd = m.sem(name + "_expd")
        self.inverted = m.sem(name + "_inverted")
        self.normed = m.sem(name + "_normed")
        self.turned = m.sem(name + "_turned")
        self.kept = m.sem(name + "_kept")
        self.used = m.sem(name + "_used")

    def by_head(self, x):
        return x.rearrange("p (g n) -> p g n", g=4)

    def spread(self, x):
        return x.rearrange("p (g o) -> p g o", o=1).broadcast_to([ROWS, 4, ROWS])

    def load_mask(self, sp):
        sp.dma_start(self.mask[:, :], self.mask_dram).then_inc(self.mask_loaded, 16)

    def vector_mask(self, dve, i):
        dve.wait_ge(self.scored, i + 1)
        if i >= 4:
            dve.wait_ge(self.turned, i - 3)
        self.nc.vector.scalar_tensor_tensor(self.scores[:, i % 4, :], self.m.ps[:ROWS, i % 2, :self.N], self.scale,
                                            self.mask[:, :], ALU.mult, ALU.add).then_inc(self.masked, 1)
        dve.wait_ge(self.masked, i + 1)
        if i >= 4:
            dve.wait_ge(self.expd, i - 3)
        self.nc.vector.tensor_reduce(self.mx[:, i % 4, :], self.by_head(self.scores[:, i % 4, :]), AX.X,
                                     ALU.max, negate=True).then_inc(self.max_found, 1)

    def vector_norm(self, dve, i):
        x = self.by_head(self.scores[:, i % 4, :])
        dve.wait_ge(self.expd, i + 1)
        self.nc.vector.reciprocal(self.den[:, i, :], self.den[:, i, :]).then_inc(self.inverted, 1)
        dve.wait_ge(self.inverted, i + 1)
        self.nc.vector.tensor_tensor(x, x, self.spread(self.den[:, i, :]), ALU.mult).then_inc(self.normed, 1)

    def scalar_exp(self, act, i):
        act.wait_ge(self.max_found, i + 1)
        for j in range(4):
            x = self.scores[:, i % 4, j * ROWS:(j + 1) * ROWS]
            ins = self.nc.scalar.activation(x, x, ACT.Exp, bias=self.mx[:, i % 4, j:j + 1],
                                            accum_out=self.den[:, i, j:j + 1])
        ins.then_inc(self.expd, 1)

    def scalar_keep(self, act, i, used):
        act.wait_ge(self.turned, i + 1)
        if i >= 2:
            act.wait_ge(used, i - 1)
        self.nc.scalar.activation(self.turnedP[:, i % 2, :], self.m.ps[:ROWS, 2 + i % 2, :self.N],
                                  ACT.Copy).then_inc(self.kept, 1)

    def tensor_turn(self, pe, i, ready):
        pe.wait_ge(ready, i + 1)
        if i >= 2:
            pe.wait_ge(self.kept, i - 1)
        for j in range(4):
            own = slice(j * ROWS, (j + 1) * ROWS)
            mm = self.nc.tensor.transpose(self.m.ps[:ROWS, 2 + i % 2, own], self.scores[:, i % 4, own],
                                          self.m.ident[:ROWS, :ROWS])
        mm.then_inc(self.turned, 1)


def latent_attention(nc, m, dram):
    H, DK, DC = 8, 128, 32
    KV = 2 * DC + 1
    scale = float((DK + DC) ** -0.5)
    with ExitStack() as ctx:
        wq = m.sbuf(ctx, "l1a_wq", [128, KD, DC])
        bq = m.sbuf(ctx, "l1a_bq", [DC, 1])
        wkv = m.sbuf(ctx, "l1a_wkv", [128, KD, 2 * DC])
        bkv = m.sbuf(ctx, "l1a_bkv", [2 * DC, 1])
        wuqT = m.sbuf(ctx, "l1a_wuqT", [128, H, DC + 1])
        wukT = m.sbuf(ctx, "l1a_wukT", [128, H, KV])
        wuvT = m.sbuf(ctx, "l1a_wuvT", [128, H, DC + 1])
        wo = m.sbuf(ctx, "l1a_wo", [128, H, D])
        bo = m.sbuf(ctx, "l1a_bo", [1, D])
        lq = m.sbuf(ctx, "l1a_lq", [DC + 1, COLS])
        kv = m.sbuf(ctx, "l1a_kv", [KV, COLS])
        kv_rows = m.sbuf(ctx, "l1a_kv_rows", [ROWS, TILES, DC])
        join = m.sbuf(ctx, "l1a_join", [KV, H, DC + 1])
        keys = m.sbuf(ctx, "l1a_keys", [DC + 1, H, COLS])
        out_w = m.sbuf(ctx, "l1a_out_w", [128, 2, D])
        out_b = m.sbuf(ctx, "l1a_out_b", [1, D])
        mixT = m.sbuf(ctx, "l1a_mixT", [128, 2, 2, ROWS])
        sm = MaskedSoftmax(nc, m, "l1a_sm", ctx, dram["c_mask"], scale, TILES * 2)
        loaded = m.sem("l1a_loaded")
        up_loaded = m.sem("l1a_up_loaded")
        compressed = m.sem("l1a_compressed")
        latent_kept = m.sem("l1a_latent_kept")
        ones_set = m.sem("l1a_ones_set")
        joined = m.sem("l1a_joined")
        join_kept = m.sem("l1a_join_kept")
        out_w_made = m.sem("l1a_out_w_made")
        out_w_kept = m.sem("l1a_out_w_kept")
        kv_turned = m.sem("l1a_kv_turned")
        kv_rows_kept = m.sem("l1a_kv_rows_kept")
        keys_made = m.sem("l1a_keys_made")
        keys_kept = [m.sem("l1a_keys_kept_vector"), m.sem("l1a_keys_kept_scalar")]
        mixed = m.sem("l1a_mixed")
        mix_kept = m.sem("l1a_mix_kept")
        out_done = m.sem("l1a_out_done")
        added = m.sem("l1a_added")
        ITEMS = TILES * 2
        KEYS = 3 * H

        def keep_keys(engine, copy, n):
            engine.wait_ge(keys_made, n + 1)
            copy(keys[:, n // 3, third(n % 3)], m.ps[:DC + 1, 2 + n % 4, :THIRD]).then_inc(keys_kept[n % 2], 1)

        with nc.Block() as block:
            @block.sync
            def _(sp):
                sp.dma_start(wq[:, :, :], dram["l1a_wq"].rearrange("(k p) n -> p k n", p=128)).then_inc(loaded, 16)
                sp.dma_start(bq[:, :], dram["l1a_bq"]).then_inc(loaded, 16)
                sp.dma_start(wkv[:, :, :], dram["l1a_wkv"].rearrange("(k p) n -> p k n", p=128)).then_inc(loaded, 16)
                sp.dma_start(bkv[:, :], dram["l1a_bkv"]).then_inc(loaded, 16)
                sp.dma_start(wuqT[:, :, :], dram["l1a_wUQT"]).then_inc(up_loaded, 16)
                sp.dma_start(wukT[:, :, :], dram["l1a_wUKT"]).then_inc(up_loaded, 16)
                sp.dma_start(join[DC:2 * DC, :, :], dram["l1a_wQRT"]).then_inc(up_loaded, 16)
                sp.dma_start(wuvT[:, :, :], dram["l1a_wUVT"]).then_inc(up_loaded, 16)
                sp.dma_start(wo[:, :, :], dram["l1a_wO"].rearrange("(k p) n -> p k n", p=128)).then_inc(up_loaded, 16)
                sp.dma_start(bo[:, :], dram["l1a_bO"]).then_inc(up_loaded, 16)
                sm.load_mask(sp)

            @block.tensor
            def _(pe):
                pe.wait_ge(loaded, 16 * 4)
                for j, (w, M) in enumerate(((wq, DC), (wkv, 2 * DC))):
                    for c in range(3):
                        for kk in range(KD):
                            mm = nc.tensor.matmul(m.ps[:M, 3 * j + c, :THIRD], w[:, kk, :], m.xT[:, kk, third(c)],
                                                  start=(kk == 0), stop=(kk == KD - 1))
                        mm.then_inc(compressed, 1)
                pe.wait_ge(up_loaded, 16 * 6)
                for h in range(H):
                    mm = nc.tensor.matmul(m.ps[:KV, 6, h * (DC + 1):(h + 1) * (DC + 1)], wukT[:, h, :], wuqT[:, h, :],
                                          start=True, stop=True)
                mm.then_inc(joined, 1)
                for h in range(H):
                    half, j = divmod(h, 4)
                    mm = nc.tensor.matmul(m.ps[j * DC:(j + 1) * DC, 7, half * D:(half + 1) * D], wuvT[:, h, :DC],
                                          wo[:, h, :], start=True, stop=True, tile_position=(0, j * DC))
                pe.wait_ge(latent_kept, 1)
                for h in range(H):
                    nc.tensor.matmul(m.ps[:1, 0, :D], wuvT[:, h, DC:DC + 1], wo[:, h, :], start=(h == 0), stop=False)
                nc.tensor.matmul(m.ps[:1, 0, :D], m.ones[:, :1], bo[:, :], start=False, stop=True).then_inc(out_w_made, 1)
                pe.wait_ge(latent_kept, 6)
                for t in range(TILES):
                    mm = nc.tensor.transpose(m.ps[:ROWS, 1, t * DC:(t + 1) * DC], kv[:DC, tile_cols(t)],
                                             m.ident[:DC, :DC])
                mm.then_inc(kv_turned, 1)
                pe.wait_ge(join_kept, 2)
                pe.wait_ge(ones_set, 2)
                for n in range(KEYS):
                    if n >= 4:
                        pe.wait_ge(keys_kept[n % 2], (n - 4) // 2 + 1)
                    nc.tensor.matmul(m.ps[:DC + 1, 2 + n % 4, :THIRD], join[:, n // 3, :], kv[:, third(n % 3)],
                                     start=True, stop=True).then_inc(keys_made, 1)
                pe.wait_ge(kv_rows_kept, 1)
                pe.wait_ge(out_w_kept, 2)
                for kept in keys_kept:
                    pe.wait_ge(kept, KEYS // 2)

                def scores(i):
                    t, half = i // 2, i % 2
                    if i >= 2:
                        pe.wait_ge(sm.masked, i - 1)
                    nc.tensor.matmul(m.ps[:ROWS, i % 2, :4 * ROWS], lq[:, tile_cols(t)],
                                     keys[:, 4 * half:4 * half + 4, tile_cols(t)], start=True,
                                     stop=True).then_inc(sm.scored, 1)

                def mix(i):
                    t, half = i // 2, i % 2
                    pe.wait_ge(sm.kept, i + 1)
                    if t >= 1:
                        pe.wait_ge(mix_kept, i - 1)
                    for j in range(4):
                        mm = nc.tensor.matmul(m.ps[j * DC:(j + 1) * DC, 6 + half, :ROWS], kv_rows[:, t, :],
                                              sm.turnedP[:, i % 2, j * ROWS:(j + 1) * ROWS], start=True, stop=True,
                                              tile_position=(0, j * DC))
                    mm.then_inc(mixed, 1)

                def output(t):
                    pe.wait_ge(mix_kept, 2 * t + 2)
                    if t >= 2:
                        pe.wait_ge(added, t - 1)
                    for half in range(2):
                        nc.tensor.matmul(m.ps[:ROWS, 4 + t % 2, :D], mixT[:, t % 2, half, :], out_w[:, half, :],
                                         start=(half == 0), stop=False)
                    nc.tensor.matmul(m.ps[:ROWS, 4 + t % 2, :D], m.ones[:, :ROWS], out_b[:, :], start=False,
                                     stop=True).then_inc(out_done, 1)

                for i in range(ITEMS + 4):
                    if i < ITEMS:
                        scores(i)
                    if 2 <= i < ITEMS + 2:
                        sm.tensor_turn(pe, i - 2, sm.normed)
                    if 3 <= i < ITEMS + 3:
                        mix(i - 3)
                    if i >= 5 and i % 2 == 1:
                        output((i - 5) // 2)

            @block.scalar
            def _(act):
                for j, (dst, b, M) in enumerate(((lq, bq, DC), (kv, bkv, 2 * DC))):
                    for c in range(3):
                        act.wait_ge(compressed, 3 * j + c + 1)
                        nc.scalar.activation(dst[:M, third(c)], m.ps[:M, 3 * j + c, :THIRD], ACT.Identity,
                                             bias=b[:, 0:1]).then_inc(latent_kept, 1)
                act.wait_ge(joined, 1)
                for rows in (slice(0, DC), slice(2 * DC, KV)):
                    nc.scalar.activation(join[rows, :, :], m.ps[rows, 6, :H * (DC + 1)].rearrange("p (h n) -> p h n", h=H),
                                         ACT.Copy).then_inc(join_kept, 1)
                act.wait_ge(out_w_made, 1)
                nc.scalar.activation(out_w[:, :, :], m.ps[:, 7, :].rearrange("p (h n) -> p h n", h=2),
                                     ACT.Copy).then_inc(out_w_kept, 1)
                nc.scalar.activation(out_b[:, :], m.ps[:1, 0, :D], ACT.Copy).then_inc(out_w_kept, 1)
                act.wait_ge(kv_turned, 1)
                nc.scalar.activation(kv_rows[:, :, :], m.ps[:ROWS, 1, :TILES * DC].rearrange("p (t n) -> p t n", t=TILES),
                                     ACT.Copy).then_inc(kv_rows_kept, 1)
                for n in range(1, KEYS, 2):
                    keep_keys(act, nc.scalar.copy, n)

                for i in range(ITEMS + 4):
                    if i < ITEMS:
                        sm.scalar_exp(act, i)
                    if 2 <= i < ITEMS + 2:
                        sm.scalar_keep(act, i - 2, mixed)
                    if 3 <= i < ITEMS + 3:
                        t, half = (i - 3) // 2, (i - 3) % 2
                        act.wait_ge(mixed, i - 2)
                        if t >= 2:
                            act.wait_ge(out_done, t - 1)
                        nc.scalar.activation(mixT[:, t % 2, half, :], m.ps[:, 6 + half, :ROWS],
                                             ACT.Copy).then_inc(mix_kept, 1)

            @block.vector
            def _(dve):
                nc.vector.memset(lq[DC:, :], 1.0).then_inc(ones_set, 1)
                nc.vector.memset(kv[2 * DC:, :], 1.0).then_inc(ones_set, 1)
                for n in range(0, KEYS, 2):
                    keep_keys(dve, nc.vector.tensor_copy, n)
                dve.wait_ge(sm.mask_loaded, 16)
                for i in range(ITEMS + 4):
                    if i < ITEMS:
                        sm.vector_mask(dve, i)
                    if 1 <= i < ITEMS + 1:
                        sm.vector_norm(dve, i - 1)
                    if i >= 5 and i % 2 == 1:
                        t = (i - 5) // 2
                        dve.wait_ge(out_done, t + 1)
                        nc.vector.tensor_tensor(m.h[:, t, :], m.ps[:ROWS, 4 + t % 2, :D], m.h[:, t, :],
                                                ALU.add).then_inc(added, 1)


STAGE[3] = lambda nc, m, dram: (normalise(nc, m, "l1a_ln", m.h), latent_attention(nc, m, dram))
def state_space(nc, m, dram):
    H, NS, DI = 8, 64, 512
    KI = DI // 128
    TAPS = 4
    with ExitStack() as ctx:
        wz = m.sbuf(ctx, "l2a_wz", [128, KD, DI])
        wx = m.sbuf(ctx, "l2a_wx", [128, KD, DI])
        wdt = m.sbuf(ctx, "l2a_wdt", [128, KD, H])
        wB = m.sbuf(ctx, "l2a_wB", [128, KD, NS])
        wC = m.sbuf(ctx, "l2a_wC", [128, KD, NS])
        conv_w = m.sbuf(ctx, "l2a_conv_w", [128, KI, TAPS])
        conv_b = m.sbuf(ctx, "l2a_conv_b", [128, KI])
        a_log = m.sbuf(ctx, "l2a_A_log", [H, 1])
        dt_bias = m.sbuf(ctx, "l2a_dt_bias", [H, 1])
        skip = m.sbuf(ctx, "l2a_skip", [ROWS, DI])
        norm_w = m.sbuf(ctx, "l2a_norm_w", [128, KI])
        wo = m.sbuf(ctx, "l2a_wo", [128, KI, D])
        causal_raw = m.sbuf(ctx, "l2a_causal_raw", [ROWS, 4 * ROWS])
        causal = m.sbuf(ctx, "l2a_causal", [ROWS, 4 * ROWS], F32R)
        ident = m.sbuf(ctx, "l2a_ident", [ROWS, ROWS], F32R)
        rows8 = m.sbuf(ctx, "l2a_rows8", [8, 8, 128])
        xc = m.sbuf(ctx, "l2a_xc", [128, KI, COLS])
        conv = m.sbuf(ctx, "l2a_conv", [128, KI, COLS])
        BT = m.sbuf(ctx, "l2a_BT", [NS, COLS])
        CT = m.sbuf(ctx, "l2a_CT", [NS, COLS])
        dt = m.sbuf(ctx, "l2a_dt", [H, COLS])
        mag = m.sbuf(ctx, "l2a_mag", [H, COLS])
        ones = m.sbuf(ctx, "l2a_ones", [H, COLS])
        logs = m.sbuf(ctx, "l2a_logs", [H, COLS])
        negL = m.sbuf(ctx, "l2a_negL", [ROWS, TILES, H])
        x_tok = m.sbuf(ctx, "l2a_x_tok", [ROWS, 2, DI])
        z_tok = m.sbuf(ctx, "l2a_z_tok", [ROWS, TILES, DI])
        G = m.sbuf(ctx, "l2a_G", [ROWS, 2, ROWS])
        W = m.sbuf(ctx, "l2a_W", [ROWS, 2, H, ROWS])
        y = m.sbuf(ctx, "l2a_y", [ROWS, 2, DI])
        sq = m.sbuf(ctx, "l2a_sq", [ROWS, DI])
        ss = m.sbuf(ctx, "l2a_ss", [ROWS, TILES])
        rms = m.sbuf(ctx, "l2a_rms", [ROWS, TILES])
        half = m.sbuf(ctx, "l2a_half", [ROWS, 1])
        yT = m.sbuf(ctx, "l2a_yT", [128, 2, KI, ROWS])
        S = {n: m.sem("l2a_" + n) for n in (
            "loaded", "late_loaded", "rounded", "ones_set", "made", "kept", "convolved", "x_ready", "exp_a", "mag_ready", "logs_ready",
            "sp1", "lturn", "l_kept", "z_made", "z_kept", "lt_made", "e_made", "g_made", "g_kept", "w_made", "x_turned",
            "x_kept", "y_made", "y_step", "y_ready", "rooted", "scaled", "y_turned", "yt_kept", "out_done", "added")}
        jobs = [(wx, 128 * k, 128, xc[:, k, :]) for k in range(KI)] + [(wB, 0, NS, BT), (wC, 0, NS, CT), (wdt, 0, H, dt)]
        with nc.Block() as block:
            @block.sync
            def _(sp):
                for t, n in ((wx, "wx"), (wB, "wB"), (wC, "wC"), (wdt, "wdt"), (wz, "wz")):
                    sp.dma_start(t[:, :, :], dram["l2a_" + n].rearrange("(k p) n -> p k n", p=128)).then_inc(S["loaded"], 16)
                sp.dma_start(conv_w[:, :, :], dram["l2a_conv_w"]).then_inc(S["loaded"], 16)
                sp.dma_start(conv_b[:, :], dram["l2a_conv_b"]).then_inc(S["loaded"], 16)
                sp.dma_start(a_log[:, :], dram["l2a_A_log"]).then_inc(S["loaded"], 16)
                sp.dma_start(dt_bias[:, :], dram["l2a_dt_bias"]).then_inc(S["loaded"], 16)
                sp.dma_start(skip[:, :], dram["l2a_D"]).then_inc(S["late_loaded"], 16)
                sp.dma_start(norm_w[:, :], dram["l2a_norm_w"]).then_inc(S["late_loaded"], 16)
                sp.dma_start(wo[:, :, :], dram["l2a_owT"].rearrange("(k p) n -> p k n", p=128)).then_inc(S["late_loaded"], 16)
                sp.dma_start(causal_raw[:, :], dram["c_causal"]).then_inc(S["late_loaded"], 16)
                sp.dma_start(rows8[:, :, :], dram["c_rows8"]).then_inc(S["late_loaded"], 16)

            @block.tensor
            def _(pe):
                pe.wait_ge(S["loaded"], 16 * 9)
                for j, (w, col, M, _) in enumerate(jobs):
                    for c in range(3):
                        n = 3 * j + c
                        if n >= 8:
                            pe.wait_ge(S["kept"], n - 7)
                        for k in range(KD):
                            mm = nc.tensor.matmul(m.ps[:M, n % 8, :THIRD], w[:, k, col:col + M], m.xT[:, k, third(c)],
                                                  start=(k == 0), stop=(k == KD - 1))
                        mm.then_inc(S["made"], 1)
                for t in range(TILES):
                    if t == 0:
                        pe.wait_ge(S["kept"], 3 * len(jobs))
                    if t >= 4:
                        pe.wait_ge(S["z_kept"], t - 3)
                    for k in range(KD):
                        mm = nc.tensor.matmul(m.ps[:ROWS, t % 4, :], m.xT[:, k, tile_cols(t)], wz[:, k, :],
                                              start=(k == 0), stop=(k == KD - 1))
                    mm.then_inc(S["z_made"], 1)
                pe.wait_ge(S["logs_ready"], 1)
                for t in range(TILES):
                    mm = nc.tensor.transpose(m.ps[:ROWS, 4, t * H:(t + 1) * H], logs[:, tile_cols(t)], m.ident[:H, :H])
                mm.then_inc(S["lturn"], 1)
                pe.wait_ge(S["late_loaded"], 16 * 5)
                pe.wait_ge(S["rounded"], 2)
                pe.wait_ge(S["z_kept"], TILES)
                pe.wait_ge(S["l_kept"], 1)

                def decays(t):
                    if t >= 1:
                        pe.wait_ge(S["e_made"], 8 * t)
                    for b in range(2):
                        nc.tensor.matmul(m.ps[:ROWS, b, :4 * ROWS], ident[:, :], causal[:, :],
                                         start=True, stop=False, skip_group_check=True)
                        for j in range(4):
                            mm = nc.tensor.matmul(m.ps[:ROWS, b, j * ROWS:(j + 1) * ROWS], rows8[:, 4 * b + j, :ROWS],
                                                  logs[:, tile_cols(t)], start=False, stop=(j == 3), skip_group_check=True)
                    mm.then_inc(S["lt_made"], 1)
                    if t >= 1:
                        pe.wait_ge(S["g_kept"], t)
                    nc.tensor.matmul(m.ps[:ROWS, 2, :ROWS], BT[:, tile_cols(t)], CT[:, tile_cols(t)],
                                     start=True, stop=True).then_inc(S["g_made"], 1)
                    if t >= 1:
                        pe.wait_ge(S["x_kept"], t)
                    for k in range(KI):
                        mm = nc.tensor.transpose(m.ps[:ROWS, 3, k * 128:(k + 1) * 128], xc[:, k, tile_cols(t)],
                                                 m.ident[:, :])
                    mm.then_inc(S["x_turned"], 1)

                def weigh(t):
                    pe.wait_ge(S["w_made"], 2 * t + 2)
                    pe.wait_ge(S["x_kept"], t + 1)
                    if t >= 2:
                        pe.wait_ge(S["y_step"], 2 * (t - 1) - 1)
                    for h in range(H):
                        mm = nc.tensor.matmul(m.ps[:ROWS, 4 + t % 2, h * 64:(h + 1) * 64], W[:, t % 2, h, :],
                                              x_tok[:, t % 2, h * 64:(h + 1) * 64], start=True, stop=True)
                    mm.then_inc(S["y_made"], 1)

                def turn_y(t):
                    pe.wait_ge(S["scaled"], t + 1)
                    if t >= 1:
                        pe.wait_ge(S["yt_kept"], KI * t)
                    for k in range(KI):
                        mm = nc.tensor.transpose(m.ps[:, 6, k * ROWS:(k + 1) * ROWS], y[:, t % 2, k * 128:(k + 1) * 128],
                                                 m.ident[:ROWS, :ROWS])
                    mm.then_inc(S["y_turned"], 1)

                def output(t):
                    pe.wait_ge(S["yt_kept"], KI * (t + 1))
                    if t >= 1:
                        pe.wait_ge(S["added"], t)
                    for k in range(KI):
                        mm = nc.tensor.matmul(m.ps[:ROWS, 7, :D], yT[:, t % 2, k, :], wo[:, k, :],
                                              start=(k == 0), stop=(k == KI - 1))
                    mm.then_inc(S["out_done"], 1)

                pe.wait_ge(S["x_ready"], KI)
                for t in range(TILES + 2):
                    if t < TILES:
                        decays(t)
                    if t >= 2:
                        turn_y(t - 2)
                    if 1 <= t <= TILES:
                        weigh(t - 1)
                    if t >= 2:
                        output(t - 2)

            @block.scalar
            def _(act):
                act.wait_ge(S["loaded"], 16 * 9)
                nc.scalar.activation(a_log[:, :], a_log[:, :], ACT.Exp).then_inc(S["exp_a"], 1)
                for j, (_, _, M, dst) in enumerate(jobs):
                    for c in range(3):
                        n = 3 * j + c
                        act.wait_ge(S["made"], n + 1)
                        src = m.ps[:M, n % 8, :THIRD]
                        if dst is dt:
                            nc.scalar.activation(dst[:, third(c)], src, ACT.Identity, bias=dt_bias[:, 0:1]).then_inc(S["kept"], 1)
                        else:
                            nc.scalar.activation(dst[:, third(c)], src, ACT.Copy).then_inc(S["kept"], 1)
                nc.scalar.activation(ident[:, :], m.ident[:ROWS, :ROWS], ACT.Copy).then_inc(S["rounded"], 1)
                act.wait_ge(S["late_loaded"], 16 * 5)
                nc.scalar.activation(causal[:, :], causal_raw[:, :], ACT.Copy).then_inc(S["rounded"], 1)
                act.wait_ge(S["kept"], 3 * len(jobs))
                nc.scalar.activation(mag[:, :], dt[:, :], ACT.Abs).then_inc(S["sp1"], 1)
                act.wait_ge(S["sp1"], 1)
                nc.scalar.activation(mag[:, :], mag[:, :], ACT.Exp, scale=-1.0).then_inc(S["sp1"], 1)
                act.wait_ge(S["sp1"], 2)
                nc.scalar.activation(mag[:, :], mag[:, :], ACT.Ln, bias=1.0).then_inc(S["mag_ready"], 1)
                for k in range(KI):
                    act.wait_ge(S["convolved"], TAPS * (k + 1))
                    nc.scalar.activation(xc[:, k, :], conv[:, k, :], ACT.Silu).then_inc(S["x_ready"], 1)
                for t in range(TILES):
                    act.wait_ge(S["z_made"], t + 1)
                    nc.scalar.activation(z_tok[:, t, :], m.ps[:ROWS, t % 4, :], ACT.Silu).then_inc(S["z_kept"], 1)

                def kept_out(act, t):
                    act.wait_ge(S["y_turned"], t + 1)
                    if t >= 2:
                        act.wait_ge(S["out_done"], t - 1)
                    for k in range(KI):
                        nc.scalar.activation(yT[:, t % 2, k, :], m.ps[:, 6, k * ROWS:(k + 1) * ROWS], ACT.Copy,
                                             scale=norm_w[:, k:k + 1]).then_inc(S["yt_kept"], 1)

                def copies(t):
                    act.wait_ge(S["g_made"], t + 1)
                    if t >= 2:
                        act.wait_ge(S["w_made"], 2 * (t - 1))
                    nc.scalar.activation(G[:, t % 2, :], m.ps[:ROWS, 2, :ROWS], ACT.Copy).then_inc(S["g_kept"], 1)
                    act.wait_ge(S["x_turned"], t + 1)
                    if t >= 2:
                        act.wait_ge(S["y_made"], t - 1)
                        act.wait_ge(S["y_step"], 2 * (t - 1) - 1)
                    nc.scalar.activation(x_tok[:, t % 2, :], m.ps[:ROWS, 3, :], ACT.Copy).then_inc(S["x_kept"], 1)

                def exponentials(t):
                    act.wait_ge(S["lt_made"], t + 1)
                    if t >= 2:
                        act.wait_ge(S["y_made"], t - 1)
                    for h in range(H):
                        nc.scalar.activation(W[:, t % 2, h, :], m.ps[:ROWS, h // 4, (h % 4) * ROWS:(h % 4 + 1) * ROWS],
                                             ACT.Exp, bias=negL[:, t, h:h + 1]).then_inc(S["e_made"], 1)

                act.wait_ge(S["l_kept"], 1)
                for t in range(TILES + 2):
                    if t < TILES:
                        exponentials(t)
                        copies(t)
                    if t >= 2:
                        kept_out(act, t - 2)

            @block.vector
            def _(dve):
                def seqs(x, k):
                    return x[:, k, :].rearrange("p (s t) -> p s t", t=T)

                nc.vector.memset(ones[:, :], 1.0).then_inc(S["ones_set"], 1)
                dve.wait_ge(S["ones_set"], 1)
                nc.vector.memset(ones[:, 0:COLS:T], 0.0).then_inc(S["exp_a"], 1)
                for k in range(KI):
                    dve.wait_ge(S["kept"], 3 * (k + 1))
                    nc.vector.tensor_scalar(conv[:, k, :], xc[:, k, :], conv_w[:, k, 3:4], conv_b[:, k:k + 1], ALU.mult,
                                            ALU.add).then_inc(S["convolved"], 1)
                    for shift in range(1, TAPS):
                        dve.wait_ge(S["convolved"], TAPS * k + shift)
                        nc.vector.scalar_tensor_tensor(seqs(conv, k)[:, :, shift:], seqs(xc, k)[:, :, :T - shift],
                                                       conv_w[:, k, 3 - shift:4 - shift], seqs(conv, k)[:, :, shift:],
                                                       ALU.mult, ALU.add).then_inc(S["convolved"], 1)
                dve.wait_ge(S["mag_ready"], 1)
                dve.wait_ge(S["exp_a"], 2)
                step = S["y_ready"]
                nc.vector.scalar_tensor_tensor(dt[:, :], dt[:, :], 0.0, mag[:, :], ALU.max, ALU.add).then_inc(step, 1)
                dve.wait_ge(step, 1)
                nc.vector.tensor_scalar(dt[:, :], dt[:, :], a_log[:, 0:1], -1.0, ALU.mult, ALU.mult).then_inc(step, 1)
                dve.wait_ge(step, 2)
                nc.vector.tensor_tensor_scan(logs[:, :], ones[:, :], dt[:, :], 0.0, ALU.mult,
                                             ALU.add).then_inc(S["logs_ready"], 1)
                dve.wait_ge(S["lturn"], 1)
                nc.vector.tensor_scalar(negL[:, :, :], m.ps[:ROWS, 4, :TILES * H].rearrange("p (t h) -> p t h", h=H),
                                        -1.0, None, ALU.mult).then_inc(S["l_kept"], 1)
                dve.wait_ge(S["late_loaded"], 16 * 5)

                def finish(t):
                    yy = y[:, t % 2, :]
                    dve.wait_ge(S["y_made"], t + 1)
                    if t >= 2:
                        dve.wait_ge(S["y_turned"], t - 1)
                    n = 2 + 4 * t
                    nc.vector.tensor_tensor(sq[:, :], x_tok[:, t % 2, :], skip[:, :], ALU.mult).then_inc(step, 1)
                    dve.wait_ge(step, n + 1)
                    nc.vector.tensor_tensor(yy, m.ps[:ROWS, 4 + t % 2, :], sq[:, :], ALU.add).then_inc(S["y_step"], 1)
                    dve.wait_ge(S["y_step"], 2 * t + 1)
                    nc.vector.tensor_tensor(yy, yy, z_tok[:, t, :], ALU.mult).then_inc(S["y_step"], 1)
                    dve.wait_ge(S["y_step"], 2 * t + 2)
                    nc.vector.tensor_tensor(sq[:, :], yy, yy, ALU.mult).then_inc(step, 1)
                    dve.wait_ge(step, n + 2)
                    nc.vector.tensor_reduce(ss[:, t:t + 1], sq[:, :], AX.X, ALU.add).then_inc(step, 1)
                    dve.wait_ge(step, n + 3)
                    nc.vector.tensor_scalar(ss[:, t:t + 1], ss[:, t:t + 1], 1.0 / DI, 1e-6, ALU.mult,
                                            ALU.add).then_inc(step, 1)
                    dve.wait_ge(S["rooted"], t + 2)
                    nc.vector.tensor_scalar(yy, yy, rms[:, t:t + 1], None, ALU.mult).then_inc(S["scaled"], 1)

                for t in range(TILES + 2):
                    if t < TILES:
                        dve.wait_ge(S["g_kept"], t + 1)
                        for b in range(2):
                            dve.wait_ge(S["e_made"], 8 * t + 4 * b + 4)
                            w4 = W[:, t % 2, 4 * b:4 * b + 4, :]
                            g4 = G[:, t % 2, :].rearrange("p (o n) -> p o n", o=1).broadcast_to([ROWS, 4, ROWS])
                            nc.vector.tensor_tensor(w4, w4, g4, ALU.mult).then_inc(S["w_made"], 1)
                    if 1 <= t <= TILES:
                        finish(t - 1)
                    if t >= 2:
                        dve.wait_ge(S["out_done"], t - 1)
                        nc.vector.tensor_tensor(m.h[:, t - 2, :], m.ps[:ROWS, 7, :D], m.h[:, t - 2, :],
                                                ALU.add).then_inc(S["added"], 1)

            @block.gpsimd
            def _(pool):
                nc.gpsimd.memset(half[:, :], -0.5).then_inc(S["rooted"], 1)
                pool.wait_ge(S["rooted"], 1)
                for t in range(TILES):
                    pool.wait_ge(S["y_ready"], 2 + 4 * t + 4)
                    nc.gpsimd.tensor_tensor(rms[:, t:t + 1], ss[:, t:t + 1], half[:, :], ALU.pow).then_inc(S["rooted"], 1)


STAGE[5] = lambda nc, m, dram: (normalise(nc, m, "l2a_ln", m.h), state_space(nc, m, dram))


def small_head_attention(nc, m, dram):
    H, DH = 16, 16
    HALF = H // KD
    ITEMS = TILES * 4
    scale = float(DH ** -0.5)
    with ExitStack() as ctx:
        wq = m.sbuf(ctx, "l2f_wq", [128, KD, D])
        wk = m.sbuf(ctx, "l2f_wk", [128, KD, D])
        wv = m.sbuf(ctx, "l2f_wv", [128, KD, D])
        wo = m.sbuf(ctx, "l2f_wo", [128, KD, D])
        heads = m.sbuf(ctx, "l2f_heads", [128, HALF])
        qT = m.sbuf(ctx, "l2f_qT", [128, KD, COLS])
        kT = m.sbuf(ctx, "l2f_kT", [128, KD, COLS])
        own = m.sbuf(ctx, "l2f_own", [128, 2, HALF, ROWS])
        v = m.sbuf(ctx, "l2f_v", [ROWS, TILES, D])
        wide_v = m.sbuf(ctx, "l2f_wide_v", [ROWS, 2, H, 2 * 128 - DH])
        mixT = m.sbuf(ctx, "l2f_mixT", [128, 2, KD, ROWS])
        sm = MaskedSoftmax(nc, m, "l2f_sm", ctx, dram["c_mask"], scale, ITEMS)
        S = {n: m.sem("l2f_" + n) for n in (
            "loaded", "made", "kept", "v_made", "v_kept", "owned", "cleared", "placed", "mixT_kept",
            "out_done", "added")}
        jobs = [(wq, k, qT) for k in range(KD)] + [(wk, k, kT) for k in range(KD)]
        with nc.Block() as block:
            @block.sync
            def _(sp):
                for t, n in ((wq, "Wq"), (wk, "Wk"), (wv, "Wv"), (wo, "Wo")):
                    sp.dma_start(t[:, :, :], dram["l2f_" + n].rearrange("(k p) n -> p k n", p=128)).then_inc(S["loaded"], 16)
                sp.dma_start(heads[:, :], dram["c_heads"]).then_inc(S["loaded"], 16)
                sm.load_mask(sp)

            @block.tensor
            def _(pe):
                pe.wait_ge(S["loaded"], 16 * 5)
                for j, (w, mk, _) in enumerate(jobs):
                    for c in range(3):
                        n = 3 * j + c
                        if n >= 4:
                            pe.wait_ge(S["kept"], n - 3)
                        for k in range(KD):
                            mm = nc.tensor.matmul(m.ps[:, n % 4, :THIRD], w[:, k, mk * 128:(mk + 1) * 128],
                                                  m.xT[:, k, third(c)], start=(k == 0), stop=(k == KD - 1))
                        mm.then_inc(S["made"], 1)
                for t in range(TILES):
                    if t >= 4:
                        pe.wait_ge(S["v_kept"], t - 3)
                    for k in range(KD):
                        mm = nc.tensor.matmul(m.ps[:ROWS, 4 + t % 4, :D], m.xT[:, k, tile_cols(t)], wv[:, k, :],
                                              start=(k == 0), stop=(k == KD - 1))
                    mm.then_inc(S["v_made"], 1)
                pe.wait_ge(S["kept"], 3 * len(jobs))
                pe.wait_ge(S["v_kept"], TILES)

                def scores(i):
                    t, q4 = i // 4, i % 4
                    u = i // 2
                    pe.wait_ge(S["owned"], u + 1)
                    if i >= 2:
                        pe.wait_ge(sm.masked, i - 1)
                    nc.tensor.matmul(m.ps[:ROWS, i % 2, :4 * ROWS], qT[:, q4 // 2, tile_cols(t)],
                                     own[:, u % 2, 4 * (q4 % 2):4 * (q4 % 2) + 4, :], start=True,
                                     stop=True).then_inc(sm.scored, 1)

                def weigh(i):
                    t, q4 = i // 4, i % 4
                    u = i // 2
                    pe.wait_ge(sm.kept, i + 1)
                    pe.wait_ge(S["placed"], t + 1)
                    if q4 % 2 == 0 and u >= 2:
                        pe.wait_ge(S["mixT_kept"], u - 1)
                    for j in range(4):
                        h = 4 * q4 + j
                        before = 128 - DH - (h % HALF) * DH
                        mm = nc.tensor.matmul(m.ps[:, 4 + u % 2, :ROWS], wide_v[:, t % 2, h, before:before + 128],
                                              sm.turnedP[:, i % 2, j * ROWS:(j + 1) * ROWS],
                                              start=(h % HALF == 0), stop=(h % HALF == HALF - 1))
                    mm.then_inc(sm.used, 1)

                def output(t):
                    pe.wait_ge(S["mixT_kept"], 2 * t + 2)
                    if t >= 2:
                        pe.wait_ge(S["added"], t - 1)
                    for k in range(KD):
                        mm = nc.tensor.matmul(m.ps[:ROWS, 6 + t % 2, :D], mixT[:, t % 2, k, :], wo[:, k, :],
                                              start=(k == 0), stop=(k == KD - 1))
                    mm.then_inc(S["out_done"], 1)

                for i in range(ITEMS + 5):
                    if i < ITEMS:
                        scores(i)
                    if 2 <= i < ITEMS + 2:
                        sm.tensor_turn(pe, i - 2, sm.normed)
                    if 3 <= i < ITEMS + 3:
                        weigh(i - 3)
                    if i >= 8 and (i - 8) % 4 == 0:
                        output((i - 8) // 4)

            @block.scalar
            def _(act):
                for j, (_, mk, dst) in enumerate(jobs):
                    for c in range(3):
                        n = 3 * j + c
                        act.wait_ge(S["made"], n + 1)
                        nc.scalar.activation(dst[:, mk, third(c)], m.ps[:, n % 4, :THIRD], ACT.Copy).then_inc(S["kept"], 1)
                for t in range(TILES):
                    act.wait_ge(S["v_made"], t + 1)
                    nc.scalar.activation(v[:, t, :], m.ps[:ROWS, 4 + t % 4, :D], ACT.Copy).then_inc(S["v_kept"], 1)

                for i in range(ITEMS + 5):
                    if i < ITEMS:
                        sm.scalar_exp(act, i)
                    if 2 <= i < ITEMS + 2:
                        sm.scalar_keep(act, i - 2, sm.used)

            @block.vector
            def _(dve):
                dve.wait_ge(sm.mask_loaded, 16)

                def add(t):
                    dve.wait_ge(S["out_done"], t + 1)
                    nc.vector.tensor_tensor(m.xn[:, t, :], m.ps[:ROWS, 6 + t % 2, :D], m.xn[:, t, :],
                                            ALU.add).then_inc(S["added"], 1)

                def keep_mixT(u):
                    t = u // 2
                    dve.wait_ge(sm.used, 2 * (u + 1))
                    if t >= 2:
                        dve.wait_ge(S["out_done"], t - 1)
                    nc.vector.tensor_copy(mixT[:, t % 2, u % 2, :], m.ps[:, 4 + u % 2, :ROWS]).then_inc(S["mixT_kept"], 1)

                for i in range(ITEMS + 6):
                    if i < ITEMS:
                        sm.vector_mask(dve, i)
                    if 1 <= i < ITEMS + 1:
                        sm.vector_norm(dve, i - 1)
                    if i >= 5 and (i - 5) % 2 == 0 and (i - 5) // 2 < 2 * TILES:
                        keep_mixT((i - 5) // 2)
                    if i >= 9 and (i - 9) % 4 == 0:
                        add((i - 9) // 4)

            @block.gpsimd
            def _(pool):
                nc.gpsimd.memset(wide_v[:, :, :, :], 0.0).then_inc(S["cleared"], 1)
                pool.wait_ge(S["loaded"], 16 * 5)
                pool.wait_ge(S["kept"], 3 * len(jobs))

                def place(t):
                    if t >= 2:
                        pool.wait_ge(sm.used, 4 * (t - 1))
                    nc.gpsimd.tensor_copy(wide_v[:, t % 2, :, 128 - DH:128],
                                          v[:, t, :].rearrange("p (h d) -> p h d", h=H)).then_inc(S["placed"], 1)

                def own_keys(u):
                    t, k = u // 2, u % 2
                    if u >= 2:
                        pool.wait_ge(sm.scored, 2 * (u - 1))
                    keys = kT[:, k, tile_cols(t)].rearrange("p (o n) -> p o n", o=1).broadcast_to([128, HALF, ROWS])
                    mine = heads[:, :].rearrange("p (h o) -> p h o", o=1).broadcast_to([128, HALF, ROWS])
                    nc.gpsimd.tensor_tensor(own[:, u % 2, :, :], keys, mine, ALU.mult).then_inc(S["owned"], 1)

                own_keys(0)
                own_keys(1)
                pool.wait_ge(S["cleared"], 1)
                pool.wait_ge(S["v_kept"], TILES)
                place(0)
                place(1)
                for i in range(ITEMS):
                    if i >= 6 and (i - 6) % 4 == 0 and (i - 6) // 4 + 2 < TILES:
                        place((i - 6) // 4 + 2)
                    if i % 2 == 0 and 2 <= i and i // 2 + 1 < 2 * TILES:
                        own_keys(i // 2 + 1)


def ds(i):
    return bass.ds(i, 1)


def experts_mlp(nc, m, dram, wts, wtsT):
    E, F = 8, 1024
    KF = F // 128
    NG = len(GROUPS)
    with ExitStack() as ctx:
        w1_raw = m.sbuf(ctx, "l2m_w1_raw", [128, KD, F])
        w2_raw = m.sbuf(ctx, "l2m_w2_raw", [128, KF, D])
        w1 = [m.pair(ctx, f"l2m_w1_{p}", [128, KD, F]) for p in range(2)]
        w2 = [m.pair(ctx, f"l2m_w2_{p}", [128, KF, D]) for p in range(2)]
        b1 = [m.sbuf(ctx, f"l2m_b1_{p}", [128, KF]) for p in range(2)]
        b2 = m.sbuf(ctx, "l2m_b2", [E, D])
        x = m.pair(ctx, "l2m_x", [128, KD, COLS + 1])
        whole = m.sbuf(ctx, "l2m_whole", [128, 3, 4 * ROWS])
        hid = m.pair(ctx, "l2m_hid", [128, 2, KF, 4 * ROWS])
        w1_loaded = m.sem("l2m_w1_loaded")
        w2_loaded = m.sem("l2m_w2_loaded")
        b1_loaded = [m.sem(f"l2m_b1_loaded{p}") for p in range(2)]
        b2_loaded = m.sem("l2m_b2_loaded")
        x_high = m.sem("l2m_x_high")
        x_padded = m.sem("l2m_x_padded")
        x_low = m.sem("l2m_x_low")
        w_high = m.sem("l2m_w_high")
        w_low = m.sem("l2m_w_low")
        raised = m.sem("l2m_raised")
        gelued = m.sem("l2m_gelued")
        split = m.sem("l2m_split")
        lowered = m.sem("l2m_lowered")
        summed = m.sem("l2m_summed")
        biased = m.sem("l2m_biased")
        bias_added = m.sem("l2m_bias_added")
        UP, DOWN = 2 * NG * KF, 2 * TILES

        def steps(p):
            return [(g, p * NG + g, t0, n, p * TILES + t0) for g, (t0, n) in enumerate(GROUPS)]

        def turns(eng, turn):
            with eng.Fori(0, E // 2 - 1) as i:
                turn(i, False)
            turn(E // 2 - 1, True)

        with nc.Block() as block:
            @block.sync
            def _(sp):
                sp.dma_start(b2[:, :], dram["l2m_b2"]).then_inc(b2_loaded, 16)
                with sp.Fori(0, E // 2) as i:
                    for p in range(2):
                        sp.wait_ge(w_low, i * 4 + 2 * p + 1)
                        sp.dma_start(w1_raw[:, :, :], dram["l2m_w1"][ds(2 * i + p)].rearrange("o (k p) n -> p (o k) n", p=128)).then_inc(w1_loaded, 16)
                        sp.wait_ge(w_low, i * 4 + 2 * p + 2)
                        sp.dma_start(w2_raw[:, :, :], dram["l2m_w2"][ds(2 * i + p)].rearrange("o (k p) n -> p (o k) n", p=128)).then_inc(w2_loaded, 16)
                        sp.wait_ge(lowered, i * DOWN + (p + 1) * TILES)
                        sp.dma_start(b1[p][:, :], dram["l2m_b1"][ds(2 * i + p)].rearrange("o p f -> (o p) f")).then_inc(b1_loaded[p], 16)

            @block.tensor
            def _(pe):
                pe.sem_inc(lowered, DOWN)
                pe.wait_ge(b2_loaded, 16)
                for t in range(TILES):
                    if t >= 4:
                        pe.wait_ge(bias_added, t - 3)
                    nc.tensor.matmul(m.ps[:ROWS, t % 4, :D], wtsT[:, tile_cols(t)], b2[:, :], start=True,
                                     stop=True).then_inc(biased, 1)
                pe.wait_ge(bias_added, TILES)
                pe.wait_ge(x_low, 1)

                def turn(i, last):
                    def lower(p, u, t0, n, before):
                        pe.wait_ge(split, i * UP + (u + 1) * KF + UP)
                        pe.wait_ge(w_low, i * 4 + 2 * p + 4)
                        for r in range(n):
                            c = before + r
                            pe.wait_ge(summed, i * DOWN + DOWN + c - 1)
                            for f in range(KF):
                                for a, b in PASSES:
                                    mm = nc.tensor.matmul(m.ps[:ROWS, 6 + c % 2, :D], hid[a][:, u % 2, f, r * ROWS:(r + 1) * ROWS],
                                                          w2[p][b][:, f, :], start=(f == 0 and a + b == 0),
                                                          stop=(f == KF - 1 and a == 1))
                            mm.then_inc(lowered, 1)

                    waiting = None
                    for p in range(2):
                        pe.wait_ge(w_low, i * 4 + 2 * p + 3)
                        for g, u, t0, n, before in steps(p):
                            wide = n * ROWS + n * ROWS % 2
                            cols = slice(t0 * ROWS, t0 * ROWS + wide)
                            for f in range(KF):
                                c = u * KF + f
                                pe.wait_ge(gelued, i * UP + UP + c - 5)
                                for k in range(KD):
                                    for a, b in PASSES:
                                        mm = nc.tensor.matmul(m.ps[:, c % 6, :wide], w1[p][a][:, k, f * 128:(f + 1) * 128],
                                                              x[b][:, k, cols], start=(k == 0 and a + b == 0),
                                                              stop=(k == KD - 1 and a == 1))
                                mm.then_inc(raised, 1)
                            if waiting is not None:
                                lower(*waiting)
                            waiting = (p, u, t0, n, before)
                    lower(*waiting)

                turns(pe, turn)

            @block.scalar
            def _(act):
                nc.scalar.activation(x[0][:, :, :COLS], m.xT[:, :, :], ACT.Copy).then_inc(x_high, 1)
                act.sem_inc(gelued, UP)
                act.wait_ge(w1_loaded, 16)
                nc.scalar.activation(w1[0][0][:, :, :], w1_raw[:, :, :], ACT.Copy).then_inc(w_high, 1)
                act.wait_ge(w2_loaded, 16)
                nc.scalar.activation(w2[0][0][:, :, :], w2_raw[:, :, :], ACT.Copy).then_inc(w_high, 1)

                def turn(i, last):
                    for p in range(2):
                        act.wait_ge(b1_loaded[p], i * 16 + 16)
                        for g, u, t0, n, before in steps(p):
                            act.wait_ge(lowered, i * DOWN + DOWN + before - (GROUPS[g - 1][1]))
                            for f in range(KF):
                                c = u * KF + f
                                act.wait_ge(raised, i * UP + c + 1)
                                act.wait_ge(split, i * UP + UP + c - 2)
                                nc.scalar.activation(whole[:, c % 3, :n * ROWS], m.ps[:, c % 6, :n * ROWS],
                                                     ACT.Gelu_apprx_tanh, bias=b1[p][:, f:f + 1])
                                nc.scalar.activation(hid[0][:, u % 2, f, :n * ROWS], m.ps[:, c % 6, :n * ROWS],
                                                     ACT.Gelu_apprx_tanh,
                                                     bias=b1[p][:, f:f + 1]).then_inc(gelued, 1)
                            if g >= 1 and not (last and p == 1):
                                raw, halves, w_loaded = ((w1_raw, w1, w1_loaded), (w2_raw, w2, w2_loaded))[g - 1]
                                act.wait_ge(w_loaded, i * 32 + 16 * (p + 2))
                                act.wait_ge(lowered, i * DOWN + DOWN + p * TILES)
                                nc.scalar.activation(halves[1 - p][0][:, :, :], raw[:, :, :], ACT.Copy).then_inc(w_high, 1)

                turns(act, turn)

            @block.vector
            def _(dve):
                dve.sem_inc(summed, DOWN)
                dve.sem_inc(split, UP)
                dve.sem_inc(w_low, 2)
                for half in x:
                    nc.vector.tensor_copy(half[:, :, COLS:].rearrange("p k o -> p (k o)"), m.ident[:, :KD]).then_inc(x_padded, 1)
                dve.wait_ge(x_high, 1)
                dve.wait_ge(x_padded, 2)
                nc.vector.tensor_tensor(x[1][:, :, :COLS], m.xT[:, :, :], x[0][:, :, :COLS], ALU.subtract).then_inc(x_low, 1)
                for t in range(TILES):
                    dve.wait_ge(biased, t + 1)
                    nc.vector.tensor_tensor(m.xn[:, t, :], m.ps[:ROWS, t % 4, :D], m.xn[:, t, :],
                                            ALU.add).then_inc(bias_added, 1)
                dve.wait_ge(w_high, 1)
                nc.vector.tensor_tensor(w1[0][1][:, :, :], w1_raw[:, :, :], w1[0][0][:, :, :], ALU.subtract).then_inc(w_low, 1)
                dve.wait_ge(w_high, 2)
                nc.vector.tensor_tensor(w2[0][1][:, :, :], w2_raw[:, :, :], w2[0][0][:, :, :], ALU.subtract).then_inc(w_low, 1)

                def turn(i, last):
                    def add(p, u, t0, n, before):
                        for r in range(n):
                            c, t = before + r, t0 + r
                            dve.wait_ge(lowered, i * DOWN + DOWN + c + 1)
                            dve.wait_ge(summed, i * DOWN + DOWN + c - TILES + 1)
                            nc.vector.scalar_tensor_tensor(m.xn[:, t, :], m.ps[:ROWS, 6 + c % 2, :D],
                                                           wts[:, t, ds(2 * i + p)], m.xn[:, t, :], ALU.mult,
                                                           ALU.add).then_inc(summed, 1)

                    waiting = None
                    for p in range(2):
                        for g, u, t0, n, before in steps(p):
                            for f in range(KF):
                                c = u * KF + f
                                dve.wait_ge(gelued, i * UP + UP + c + 1)
                                nc.vector.tensor_tensor(hid[1][:, u % 2, f, :n * ROWS], whole[:, c % 3, :n * ROWS],
                                                        hid[0][:, u % 2, f, :n * ROWS], ALU.subtract).then_inc(split, 1)
                            if waiting is not None:
                                add(*waiting)
                            waiting = (p, u, t0, n, before)
                            if g >= 1 and not (last and p == 1):
                                raw, halves = ((w1_raw, w1), (w2_raw, w2))[g - 1]
                                dve.wait_ge(w_high, i * 4 + 2 * (p + 1) + g)
                                nc.vector.tensor_tensor(halves[1 - p][1][:, :, :], raw[:, :, :], halves[1 - p][0][:, :, :],
                                                        ALU.subtract).then_inc(w_low, 1)
                    add(*waiting)

                turns(dve, turn)
                dve.wait_ge(summed, DOWN * (E // 2 + 1))
                nc.vector.tensor_tensor(m.h[:, :, :], m.h[:, :, :], m.xn[:, :, :], ALU.add).then_inc(bias_added, 1)
                dve.wait_ge(bias_added, TILES + 1)


def layer2_ffn(nc, m, dram):
    normalise(nc, m, "l2f_ln", m.h, turn=False)
    with ExitStack() as ctx:
        scratch = m.sbuf(ctx, "l2f_scratch", [ROWS, TILES, D])
        normalise(nc, m, "l2f_ln1", m.xn, tok=scratch, affine=dram["l2f_ln1"])
    small_head_attention(nc, m, dram)
    with ExitStack() as ctx:
        scratch = m.sbuf(ctx, "l2f_scratch2", [ROWS, TILES, D])
        normalise(nc, m, "l2f_ln2", m.xn, tok=scratch, affine=dram["l2f_ln2"])
    with ExitStack() as ctx:
        wts = m.sbuf(ctx, "l2m_wts", [ROWS, TILES, 8])
        wtsT = m.sbuf(ctx, "l2m_wtsT", [8, COLS])
        gate(nc, m, "l2g", dram["l2g_gw"], dram["l2g_gb"], 8, wts, wtsT, True)
        experts_mlp(nc, m, dram, wts, wtsT)


STAGE[6] = layer2_ffn


def gated_sums(nc, m, dram, gT):
    H, DH, RANK = 16, 16, 16
    with ExitStack() as ctx:
        w = {n: m.sbuf(ctx, "l3a_" + n, [128, KD, D]) for n in ("Wq", "Wk", "Wv", "Wg")}
        w1 = m.sbuf(ctx, "l3a_Wgk1", [128, KD, RANK])
        w2 = m.sbuf(ctx, "l3a_Wgk2", [RANK, D])
        b2 = m.sbuf(ctx, "l3a_bgk2", [128, KD])
        spread_raw = m.sbuf(ctx, "l3a_spread_raw", [128, DH, 128])
        spread = m.sbuf(ctx, "l3a_spread", [128, DH, 128], F32R)
        low = m.sbuf(ctx, "l3a_low", [RANK, COLS])
        kT = m.pair(ctx, "l3a_kT", [128, KD, COLS + 1])
        vT = m.sbuf(ctx, "l3a_vT", [128, KD, COLS])
        qT = m.pair(ctx, "l3a_qT", [128, KD, COLS + 1])
        gates = m.sbuf(ctx, "l3a_gates", [128, KD, COLS])
        mag = m.sbuf(ctx, "l3a_mag", [128, KD, COLS])
        upd = m.sbuf(ctx, "l3a_upd", [128, 2, COLS])
        state = m.sbuf(ctx, "l3a_state", [128, 2, COLS])
        qs = m.sbuf(ctx, "l3a_qs", [128, 2, COLS])
        read = m.sbuf(ctx, "l3a_read", [128, 2, COLS])
        S = {n: m.sem("l3a_" + n) for n in (
            "loaded", "c_loaded", "low_made", "low_kept", "made", "kept", "soft", "log_ready", "gated", "cut", "k_spread",
            "q_spread", "padded", "low_part", "spread_rounded", "updated", "q_kept", "scanned", "was_read", "gathered", "o_kept", "turned", "stored")}
        jobs = [(w["Wk"], k, kT[0]) for k in range(KD)] + [(w["Wv"], k, vT) for k in range(KD)]
        jobs += [(w["Wq"], k, qT[0]) for k in range(KD)] + [(w["Wg"], k, gT) for k in range(KD)]
        split = [(3 * (j + KD) + c, jobs[j][1], pair, c) for j, pair in ((0, kT), (1, kT), (4, qT), (5, qT))
                 for c in range(3)]
        STEPS = KD * DH
        with nc.Block() as block:
            @block.sync
            def _(sp):
                sp.dma_start(w1[:, :, :], dram["l3a_Wgk1"].rearrange("(k p) n -> p k n", p=128)).then_inc(S["loaded"], 16)
                sp.dma_start(w2[:, :], dram["l3a_Wgk2"]).then_inc(S["loaded"], 16)
                sp.dma_start(b2[:, :], dram["l3a_bgk2"]).then_inc(S["loaded"], 16)
                for n in ("Wk", "Wv", "Wq", "Wg"):
                    sp.dma_start(w[n][:, :, :], dram["l3a_" + n].rearrange("(k p) n -> p k n", p=128)).then_inc(S["loaded"], 16)
                sp.dma_start(spread_raw[:, :, :], dram["c_spread"]).then_inc(S["c_loaded"], 16)

            @block.tensor
            def _(pe):
                pe.wait_ge(S["loaded"], 16 * 7)
                for c in range(3):
                    for k in range(KD):
                        mm = nc.tensor.matmul(m.ps[:RANK, 6, :THIRD] if c == 0 else m.ps[:RANK, 6 + (c % 2), :THIRD],
                                              w1[:, k, :], m.xT[:, k, third(c)], start=(k == 0), stop=(k == KD - 1))
                    mm.then_inc(S["low_made"], 1)
                    pe.wait_ge(S["low_kept"], c + 1)
                for j in range(KD + len(jobs)):
                    for c in range(3):
                        n = 3 * j + c
                        if n >= 6:
                            pe.wait_ge(S["kept"], n - 5)
                            lows = len([s for s in split if s[0] <= n - 6])
                            if lows > 0:
                                pe.wait_ge(S["low_part"], lows)
                        out = m.ps[:, n % 6, :THIRD]
                        if j < KD:
                            mm = nc.tensor.matmul(out, w2[:, j * 128:(j + 1) * 128], low[:, third(c)], start=True, stop=True)
                        else:
                            ww, mk, _ = jobs[j - KD]
                            for k in range(KD):
                                mm = nc.tensor.matmul(out, ww[:, k, mk * 128:(mk + 1) * 128], m.xT[:, k, third(c)],
                                                      start=(k == 0), stop=(k == KD - 1))
                        mm.then_inc(S["made"], 1)
                pe.wait_ge(S["kept"], 3 * (KD + len(jobs)))
                pe.wait_ge(S["low_part"], len(split))
                pe.wait_ge(S["spread_rounded"], 1)

                def spread_out(b, i, c, src):
                    for high_low in range(2):
                        mm = nc.tensor.matmul(m.ps[:, b, :width(even_part(c))], spread[:, i % DH, :],
                                              src[high_low][:, i // DH, even_part(c)], start=(high_low == 0),
                                              stop=(high_low == 1))
                    return mm

                def sum_up(i):
                    pe.wait_ge(S["was_read"], i + 1)
                    if i == DH:
                        pe.wait_ge(S["o_kept"], 3)
                    for c in range(3):
                        mm = nc.tensor.matmul(m.ps[:, 5 + c, :THIRD], m.ident[:, :], read[:, i % 2, third(c)],
                                              start=(i % DH == 0), stop=(i % DH == DH - 1), skip_group_check=True)
                    mm.then_inc(S["gathered"], 1)

                for i in range(STEPS):
                    for c in range(3):
                        n = 3 * i + c
                        if n >= 3:
                            pe.wait_ge(S["updated"], n - 2)
                        spread_out(n % 3, i, c, kT).then_inc(S["k_spread"], 1)
                        if n >= 2:
                            pe.wait_ge(S["q_kept"], n - 1)
                        spread_out(3 + n % 2, i, c, qT).then_inc(S["q_spread"], 1)
                    if i >= 1:
                        sum_up(i - 1)
                sum_up(STEPS - 1)
                pe.wait_ge(S["o_kept"], 6)
                for t in range(TILES):
                    if t >= 4:
                        pe.wait_ge(S["stored"], t - 3)
                    for k in range(KD):
                        mm = nc.tensor.transpose(m.ps[:ROWS, t % 4, k * 128:(k + 1) * 128], mag[:, k, tile_cols(t)],
                                                 m.ident[:, :])
                    mm.then_inc(S["turned"], 1)

            @block.scalar
            def _(act):
                for c in range(3):
                    act.wait_ge(S["low_made"], c + 1)
                    nc.scalar.activation(low[:, third(c)], m.ps[:RANK, 6 + (c % 2), :THIRD], ACT.Copy).then_inc(S["low_kept"], 1)
                for j in range(KD):
                    for c in range(3):
                        n = 3 * j + c
                        act.wait_ge(S["made"], n + 1)
                        nc.scalar.activation(gates[:, j, third(c)], m.ps[:, n % 6, :THIRD], ACT.Identity,
                                             bias=b2[:, j:j + 1]).then_inc(S["kept"], 1)
                for j, (_, mk, dst) in enumerate(jobs[:6]):
                    for c in range(3):
                        n = 3 * (j + KD) + c
                        act.wait_ge(S["made"], n + 1)
                        nc.scalar.activation(dst[:, mk, third(c)], m.ps[:, n % 6, :THIRD], ACT.Copy).then_inc(S["kept"], 1)
                act.wait_ge(S["c_loaded"], 16)
                nc.scalar.activation(spread[:, :, :], spread_raw[:, :, :], ACT.Copy).then_inc(S["spread_rounded"], 1)
                nc.scalar.activation(mag[:, :, :], gates[:, :, :], ACT.Abs).then_inc(S["soft"], 1)
                act.wait_ge(S["soft"], 1)
                nc.scalar.activation(mag[:, :, :], mag[:, :, :], ACT.Exp, scale=-1.0).then_inc(S["soft"], 1)
                act.wait_ge(S["soft"], 2)
                nc.scalar.activation(mag[:, :, :], mag[:, :, :], ACT.Ln, bias=1.0).then_inc(S["soft"], 1)
                act.wait_ge(S["log_ready"], 1)
                nc.scalar.activation(gates[:, :, :], gates[:, :, :], ACT.Exp, scale=1.0 / 16.0).then_inc(S["gated"], 1)
                for j, (_, mk, dst) in enumerate(jobs[6:]):
                    for c in range(3):
                        n = 3 * (j + 6 + KD) + c
                        act.wait_ge(S["made"], n + 1)
                        nc.scalar.activation(dst[:, mk, third(c)], m.ps[:, n % 6, :THIRD], ACT.Silu).then_inc(S["kept"], 1)
                def sums(act, k):
                    act.wait_ge(S["gathered"], DH * (k + 1))
                    for c in range(3):
                        nc.scalar.activation(mag[:, k, third(c)], m.ps[:, 5 + c, :THIRD], ACT.Copy).then_inc(S["o_kept"], 1)

                for i in range(STEPS):
                    if i >= 2:
                        act.wait_ge(S["was_read"], i - 1)
                    for c in range(3):
                        n = 3 * i + c
                        act.wait_ge(S["q_spread"], n + 1)
                        nc.scalar.activation(qs[:, i % 2, part(c)], m.ps[:, 3 + n % 2, :width(part(c))], ACT.Copy).then_inc(S["q_kept"], 1)
                    if i == DH + 1:
                        sums(act, 0)
                sums(act, 1)

            @block.vector
            def _(dve):
                for half in kT + qT:
                    nc.vector.tensor_copy(half[:, :, COLS:].rearrange("p k o -> p (k o)"), m.ident[:, :KD]).then_inc(S["padded"], 1)
                dve.wait_ge(S["padded"], 4)
                for n, k, (high, low), c in split:
                    dve.wait_ge(S["kept"], n + 1)
                    nc.vector.tensor_tensor(low[:, k, third(c)], m.ps[:, n % 6, :THIRD], high[:, k, third(c)],
                                            ALU.subtract).then_inc(S["low_part"], 1)
                dve.wait_ge(S["soft"], 3)
                nc.vector.scalar_tensor_tensor(gates[:, :, :], gates[:, :, :], 0.0, mag[:, :, :], ALU.min,
                                               ALU.subtract).then_inc(S["log_ready"], 1)
                dve.wait_ge(S["gated"], 1)
                nc.vector.memset(gates[:, 0, 0:COLS:T], 0.0).then_inc(S["cut"], 1)
                nc.vector.memset(gates[:, 1, 0:COLS:T], 0.0).then_inc(S["cut"], 1)
                dve.wait_ge(S["cut"], 2)
                dve.wait_ge(S["kept"], 3 * (KD + len(jobs)))
                for i in range(STEPS):
                    if i >= 2:
                        dve.wait_ge(S["scanned"], i - 1)
                    for c in range(3):
                        dve.wait_ge(S["k_spread"], 3 * i + c + 1)
                        nc.vector.tensor_tensor(upd[:, i % 2, part(c)], m.ps[:, (3 * i + c) % 3, :width(part(c))],
                                                vT[:, i // DH, part(c)], ALU.mult).then_inc(S["updated"], 1)
                    dve.wait_ge(S["updated"], 3 * i + 3)
                    if i >= 2:
                        dve.wait_ge(S["was_read"], i - 1)
                    nc.vector.tensor_tensor_scan(state[:, i % 2, :], gates[:, i // DH, :], upd[:, i % 2, :], 0.0,
                                                 ALU.mult, ALU.add).then_inc(S["scanned"], 1)
                for t in range(TILES):
                    dve.wait_ge(S["turned"], t + 1)
                    nc.vector.tensor_copy(m.xn[:, t, :], m.ps[:ROWS, t % 4, :D]).then_inc(S["stored"], 1)

            @block.gpsimd
            def _(pool):
                for i in range(STEPS):
                    pool.wait_ge(S["scanned"], i + 1)
                    pool.wait_ge(S["q_kept"], 3 * i + 3)
                    if i >= 2:
                        pool.wait_ge(S["gathered"], i - 1)
                    nc.gpsimd.tensor_tensor(read[:, i % 2, :], state[:, i % 2, :], qs[:, i % 2, :],
                                            ALU.mult).then_inc(S["was_read"], 1)


def gated_output(nc, m, dram, gT):
    with ExitStack() as ctx:
        wo = m.sbuf(ctx, "l3o_Wout", [128, KD, D])
        loaded = m.sem("l3o_loaded")
        gated = m.sem("l3o_gated")
        out_done = m.sem("l3o_out_done")
        added = m.sem("l3o_added")
        with nc.Block() as block:
            @block.sync
            def _(sp):
                sp.dma_start(wo[:, :, :], dram["l3a_Wout"].rearrange("(k p) n -> p k n", p=128)).then_inc(loaded, 16)

            @block.tensor
            def _(pe):
                pe.wait_ge(loaded, 16)
                for t in range(TILES):
                    pe.wait_ge(gated, t + 1)
                    if t >= 4:
                        pe.wait_ge(added, t - 3)
                    for k in range(KD):
                        mm = nc.tensor.matmul(m.ps[:ROWS, t % 4, :D], m.xT[:, k, tile_cols(t)], wo[:, k, :],
                                              start=(k == 0), stop=(k == KD - 1))
                    mm.then_inc(out_done, 1)

            @block.gpsimd
            def _(pool):
                for t in range(TILES):
                    x = m.xT[:, :, tile_cols(t)]
                    nc.gpsimd.tensor_tensor(x, x, gT[:, :, tile_cols(t)], ALU.mult).then_inc(gated, 1)

            @block.vector
            def _(dve):
                for t in range(TILES):
                    dve.wait_ge(out_done, t + 1)
                    nc.vector.tensor_tensor(m.h[:, t, :], m.ps[:ROWS, t % 4, :D], m.h[:, t, :],
                                            ALU.add).then_inc(added, 1)


def layer3_attention(nc, m, dram):
    normalise(nc, m, "l3a_ln", m.h)
    with ExitStack() as ctx:
        gT = m.sbuf(ctx, "l3a_gT", [128, KD, COLS])
        gated_sums(nc, m, dram, gT)
        scratch = m.sbuf(ctx, "l3a_scratch", [ROWS, TILES, D])
        normalise(nc, m, "l3a_on", m.xn, tok=scratch, affine=dram["l3a_norm"])
        gated_output(nc, m, dram, gT)


STAGE[7] = layer3_attention


def rms_turned(nc, m, name, src, rows, tiles, gamma, dstT, scratch):
    per = 512 // rows if rows < 128 else 4
    groups = [(g, min(per, tiles - g)) for g in range(0, tiles, per)]
    with ExitStack() as ctx:
        g = m.sbuf(ctx, name + "_gamma", [128, KD])
        ss = m.sbuf(ctx, name + "_ss", [rows, tiles])
        S = {n: m.sem(f"{name}_{n}") for n in ("loaded", "squared", "summed", "rooted", "step", "scaled", "turned", "kept")}
        with nc.Block() as block:
            @block.sync
            def _(sp):
                sp.dma_start(g[:, :], gamma).then_inc(S["loaded"], 16)

            @block.vector
            def _(dve):
                nc.vector.tensor_tensor(scratch[:, :, :], src[:, :, :], src[:, :, :], ALU.mult).then_inc(S["squared"], 1)
                dve.wait_ge(S["squared"], 1)
                nc.vector.tensor_reduce(ss[:, :], scratch[:, :, :], AX.X, ALU.add).then_inc(S["summed"], 1)
                dve.wait_ge(S["rooted"], 1)
                nc.vector.tensor_scalar(ss[:, :], ss[:, :], 1e-12, None, ALU.max).then_inc(S["step"], 1)
                dve.wait_ge(S["step"], 1)
                nc.vector.reciprocal(ss[:, :], ss[:, :]).then_inc(S["step"], 1)
                dve.wait_ge(S["step"], 2)
                for t in range(tiles):
                    nc.vector.tensor_scalar(scratch[:, t, :], src[:, t, :], ss[:, t:t + 1], float(D) ** 0.5, ALU.mult,
                                            ALU.mult).then_inc(S["scaled"], 1)

            @block.scalar
            def _(act):
                act.wait_ge(S["summed"], 1)
                nc.scalar.activation(ss[:, :], ss[:, :], ACT.Sqrt).then_inc(S["rooted"], 1)
                act.wait_ge(S["loaded"], 16)
                for i, (t0, n) in enumerate(groups):
                    for k in range(KD):
                        act.wait_ge(S["turned"], KD * i + k + 1)
                        nc.scalar.activation(dstT[:, k, t0 * rows:(t0 + n) * rows], m.ps[:, (KD * i + k) % 8, :n * rows],
                                             ACT.Copy, scale=g[:, k:k + 1]).then_inc(S["kept"], 1)

            @block.tensor
            def _(pe):
                for i, (t0, n) in enumerate(groups):
                    pe.wait_ge(S["scaled"], t0 + n)
                    for k in range(KD):
                        b = KD * i + k
                        if b >= 8:
                            pe.wait_ge(S["kept"], b - 7)
                        for j in range(n):
                            mm = nc.tensor.transpose(m.ps[:, b % 8, j * rows:(j + 1) * rows],
                                                     scratch[:, t0 + j, k * 128:(k + 1) * 128], m.ident[:rows, :rows])
                        mm.then_inc(S["turned"], 1)


def combine_weights(nc, m, dram, slotsT, combT, csumT):
    E, SL = 8, 128
    with ExitStack() as ctx:
        b2 = m.sbuf(ctx, "l3c_b2", [E, D])
        p = m.sbuf(ctx, "l3c_p", [ROWS, 3, E, SL])
        mx = m.sbuf(ctx, "l3c_mx", [ROWS, TILES])
        den = m.sbuf(ctx, "l3c_den", [ROWS, TILES])
        csum = m.sbuf(ctx, "l3c_csum", [ROWS, TILES, E])
        S = {n: m.sem("l3c_" + n) for n in ("loaded", "scored", "max_found", "expd", "inverted", "normed", "csummed",
                                            "turned", "kept", "c_turned", "c_kept", "biased", "added")}
        with nc.Block() as block:
            @block.sync
            def _(sp):
                sp.dma_start(b2[:, :], dram["l3f_b2"]).then_inc(S["loaded"], 16)

            @block.tensor
            def _(pe):
                def score(t):
                    if t >= 2:
                        pe.wait_ge(S["expd"], t - 1)
                    for j in range(2):
                        for k in range(KD):
                            mm = nc.tensor.matmul(m.ps[:ROWS, 2 * (t % 2) + j, :], m.xT[:, k, tile_cols(t)],
                                                  slotsT[:, k, j * 512:(j + 1) * 512], start=(k == 0), stop=(k == KD - 1))
                    mm.then_inc(S["scored"], 1)

                def turn(t):
                    pe.wait_ge(S["normed"], t + 1)
                    if t >= 1:
                        pe.wait_ge(S["kept"], 2 * t)
                    for j in range(2):
                        for e in range(4):
                            mm = nc.tensor.transpose(m.ps[:, 4 + j, e * ROWS:(e + 1) * ROWS], p[:, t % 3, 4 * j + e, :],
                                                     m.ident[:ROWS, :ROWS])
                        mm.then_inc(S["turned"], 1)

                for t in range(TILES + 2):
                    if t < TILES:
                        score(t)
                    if t >= 2:
                        turn(t - 2)
                pe.wait_ge(S["csummed"], TILES)
                for g, (t0, n) in enumerate(GROUPS):
                    for j in range(n):
                        mm = nc.tensor.transpose(m.ps[:E, 6, j * ROWS:(j + 1) * ROWS], csum[:, t0 + j, :],
                                                 m.ident[:ROWS, :ROWS])
                    mm.then_inc(S["c_turned"], 1)
                    pe.wait_ge(S["c_kept"], g + 1)
                pe.wait_ge(S["loaded"], 16)
                for t in range(TILES):
                    if t >= 4:
                        pe.wait_ge(S["added"], t - 3)
                    nc.tensor.matmul(m.ps[:ROWS, t % 4, :D], csumT[:, tile_cols(t)], b2[:, :], start=True,
                                     stop=True).then_inc(S["biased"], 1)

            @block.scalar
            def _(act):
                def keep(t):
                    for j in range(2):
                        act.wait_ge(S["turned"], 2 * t + j + 1)
                        nc.scalar.activation(combT[:, 4 * j:4 * j + 4, tile_cols(t)],
                                             m.ps[:, 4 + j, :4 * ROWS].rearrange("p (e n) -> p e n", e=4),
                                             ACT.Copy).then_inc(S["kept"], 1)

                for t in range(TILES + 2):
                    if t < TILES:
                        act.wait_ge(S["max_found"], t + 1)
                        if t >= 3:
                            act.wait_ge(S["turned"], 2 * (t - 2))
                            act.wait_ge(S["csummed"], t - 2)
                        nc.scalar.activation(p[:, t % 3, :, :].rearrange("p e s -> p (e s)"),
                                             m.ps[:ROWS, 2 * (t % 2):2 * (t % 2) + 2, :].rearrange("p b s -> p (b s)"),
                                             ACT.Exp, bias=mx[:, t:t + 1],
                                             accum_out=den[:, t:t + 1]).then_inc(S["expd"], 1)
                    if t >= 2:
                        keep(t - 2)
                for g, (t0, n) in enumerate(GROUPS):
                    act.wait_ge(S["c_turned"], g + 1)
                    nc.scalar.activation(csumT[:, t0 * ROWS:(t0 + n) * ROWS], m.ps[:E, 6, :n * ROWS],
                                         ACT.Copy).then_inc(S["c_kept"], 1)

            @block.vector
            def _(dve):
                def norm(t):
                    dve.wait_ge(S["expd"], t + 1)
                    nc.vector.reciprocal(den[:, t:t + 1], den[:, t:t + 1]).then_inc(S["inverted"], 1)
                    dve.wait_ge(S["inverted"], t + 1)
                    nc.vector.tensor_scalar(p[:, t % 3, :, :], p[:, t % 3, :, :], den[:, t:t + 1], None,
                                            ALU.mult).then_inc(S["normed"], 1)
                    dve.wait_ge(S["normed"], t + 1)
                    nc.vector.tensor_reduce(csum[:, t, :], p[:, t % 3, :, :], AX.X, ALU.add).then_inc(S["csummed"], 1)

                for t in range(TILES + 1):
                    if t < TILES:
                        dve.wait_ge(S["scored"], t + 1)
                        nc.vector.tensor_reduce(mx[:, t:t + 1], m.ps[:ROWS, 2 * (t % 2):2 * (t % 2) + 2, :], AX.XY, ALU.max,
                                                negate=True).then_inc(S["max_found"], 1)
                    if t >= 1:
                        norm(t - 1)
                for t in range(TILES):
                    dve.wait_ge(S["biased"], t + 1)
                    nc.vector.tensor_tensor(m.h[:, t, :], m.ps[:ROWS, t % 4, :D], m.h[:, t, :],
                                            ALU.add).then_inc(S["added"], 1)


def dispatch_weights(nc, m, slotsT, disp, combT, disp_store, comb_store):
    E = 8
    SEQS3 = NSEQ // 3
    with ExitStack() as ctx:
        mx = m.sbuf(ctx, "l3d_mx", [128, 3, NSEQ])
        den = m.sbuf(ctx, "l3d_den", [128, 3, NSEQ])
        S = {n: m.sem("l3d_" + n) for n in ("scored", "max_found", "shifted", "expd", "summed", "inverted", "normed",
                                            "stored")}

        def bank(x, c):
            return x[:, c * THIRD:(c + 1) * THIRD].rearrange("p (s t) -> p s t", t=T)

        def over_t(x, c=None):
            n = NSEQ if c is None else SEQS3
            x = x if c is None else x[:, c * SEQS3:(c + 1) * SEQS3]
            return x.rearrange("p (s o) -> p s o", o=1).broadcast_to([128, n, T])

        with nc.Block() as block:
            @block.sync
            def _(sp):
                for e in range(E):
                    sp.dma_start(comb_store[e], combT[:, e, :]).then_inc(S["stored"], 16)
                for e in range(E):
                    sp.wait_ge(S["normed"], e + 1)
                    sp.dma_start(disp_store[e], disp[:, e, :]).then_inc(S["stored"], 16)
                sp.wait_ge(S["stored"], 2 * E * 16)

            @block.tensor
            def _(pe):
                for e in range(E):
                    if e >= 2:
                        pe.wait_ge(S["shifted"], 3 * (e - 1))
                    for c in range(3):
                        for k in range(KD):
                            mm = nc.tensor.matmul(m.ps[:, 3 * (e % 2) + c, :THIRD], slotsT[:, k, e * 128:(e + 1) * 128],
                                                  m.xT[:, k, third(c)], start=(k == 0), stop=(k == KD - 1))
                    mm.then_inc(S["scored"], 1)

            @block.scalar
            def _(act):
                for e in range(E):
                    act.wait_ge(S["shifted"], 3 * (e + 1))
                    nc.scalar.activation(disp[:, e, :], disp[:, e, :], ACT.Exp).then_inc(S["expd"], 1)

            @block.vector
            def _(dve):
                def finish(e):
                    dve.wait_ge(S["expd"], e + 1)
                    nc.vector.tensor_reduce(den[:, e % 3, :], disp[:, e, :].rearrange("p (s t) -> p s t", t=T), AX.X,
                                            ALU.add).then_inc(S["summed"], 1)
                    dve.wait_ge(S["summed"], e + 1)
                    nc.vector.reciprocal(den[:, e % 3, :], den[:, e % 3, :]).then_inc(S["inverted"], 1)

                for e in range(E + 1):
                    if e < E:
                        dve.wait_ge(S["scored"], e + 1)
                        logits = m.ps[:, 3 * (e % 2):3 * (e % 2) + 3, :THIRD]
                        nc.vector.tensor_reduce(mx[:, e % 3, :], logits.rearrange("p c (s t) -> p c s t", t=T), AX.X,
                                                ALU.max).then_inc(S["max_found"], 1)
                        dve.wait_ge(S["max_found"], e + 1)
                        for c in range(3):
                            nc.vector.tensor_tensor(bank(disp[:, e, :], c),
                                                    m.ps[:, 3 * (e % 2) + c, :THIRD].rearrange("p (s t) -> p s t", t=T),
                                                    over_t(mx[:, e % 3, :], c), ALU.subtract).then_inc(S["shifted"], 1)
                    if e >= 1:
                        if e - 1 >= 3:
                            dve.wait_ge(S["normed"], e - 3)
                        finish(e - 1)

            @block.gpsimd
            def _(pool):
                for e in range(E):
                    pool.wait_ge(S["inverted"], e + 1)
                    x = disp[:, e, :].rearrange("p (s t) -> p s t", t=T)
                    nc.gpsimd.tensor_tensor(x, x, over_t(den[:, e % 3, :]), ALU.mult).then_inc(S["normed"], 1)


def soft_experts(nc, m, dram, comb_store, disp_store):
    E, F, SL = 8, 1024, 128
    KF = F // 128
    HALF = 512
    PAIR = 2 * TILES
    PIECES = 4
    FIRST_SPLIT = 3
    with ExitStack() as ctx:
        w1_raw = m.sbuf(ctx, "l3f_w1_raw", [128, KD, F])
        w2_raw = m.sbuf(ctx, "l3f_w2_raw", [128, KF, D])
        w1 = [m.pair(ctx, f"l3f_w1_{p}", [128, KD, F]) for p in range(2)]
        w2 = [m.pair(ctx, f"l3f_w2_{p}", [128, KF, D]) for p in range(2)]
        comb = [m.sbuf(ctx, f"l3f_comb_{p}", [128, COLS]) for p in range(2)]
        disp = [m.sbuf(ctx, f"l3f_disp_{p}", [128, COLS]) for p in range(2)]
        x = m.pair(ctx, "l3f_x", [128, KD, COLS])
        room = m.xn[:, :, :].rearrange("p t d -> p (t d)")
        b1 = [room[:, p * F:(p + 1) * F] for p in range(2)]
        whole = room[:, 2 * F:2 * F + HALF]
        up = m.pair(ctx, "l3f_up", [ROWS, 2, F])
        diag = m.sbuf(ctx, "l3f_diag", [128, 2, SEQ * ROWS])
        to_slots = m.pair(ctx, "l3f_to_slots", [ROWS, 2, SEQ * SL])
        hid = m.sbuf(ctx, "l3f_hid", [128, 2, F])
        backT = m.pair(ctx, "l3f_backT", [128, 2, KF, ROWS])
        w1_loaded = m.sem("l3f_w1_loaded")
        w2_loaded = m.sem("l3f_w2_loaded")
        rest_loaded = [m.sem(f"l3f_rest_loaded{p}") for p in range(2)]
        w_high = m.sem("l3f_w_high")
        w_low = m.sem("l3f_w_low")
        x_high = m.sem("l3f_x_high")
        x_low = m.sem("l3f_x_low")
        cleared = m.sem("l3f_cleared")
        counts = {"up_made": 2 * PAIR, "up_kept": 2 * PAIR, "up_high": 2 * PAIR, "up_split": 2 * PAIR, "diag_set": PAIR,
                  "d_turned": PAIR, "d_high": PAIR, "d_kept": PAIR, "raised": 3 * PAIR, "gelued": 3 * PAIR,
                  "drawn": 3 * PAIR, "back_high": PAIR, "back_split": PAIR, "lowered": PAIR, "added": PAIR}
        S = {n: m.sem("l3f_" + n) for n in counts}

        def wait(eng, i, name, n):
            eng.wait_ge(S[name], i * counts[name] + counts[name] + n)

        def start(eng, *names):
            for n in names:
                eng.sem_inc(S[n], counts[n])

        def turns(eng, turn):
            with eng.Fori(0, E // 2 - 1) as i:
                turn(i, False)
            turn(E // 2 - 1, True)

        def piece(q, p, part):
            j = q % 2
            if q < 2:
                return w1_raw[:, j, :], w1[p][part][:, j, :]
            half = slice(j * KF // 2, (j + 1) * KF // 2)
            return w2_raw[:, half, :], w2[p][part][:, half, :]

        with nc.Block() as block:
            @block.sync
            def _(sp):
                with sp.Fori(0, E // 2) as i:
                    for p in range(2):
                        e = ds(2 * i + p)
                        sp.wait_ge(w_low, i * 2 * PIECES + p * PIECES + 2)
                        sp.dma_start(w1_raw[:, :, :], dram["l3f_w1"][e].rearrange("o (k p) n -> p (o k) n", p=128)).then_inc(w1_loaded, 16)
                        sp.wait_ge(w_low, i * 2 * PIECES + p * PIECES + 4)
                        sp.dma_start(w2_raw[:, :, :], dram["l3f_w2"][e].rearrange("o (k p) n -> p (o k) n", p=128)).then_inc(w2_loaded, 16)
                        wait(sp, i, "added", (p + 1) * TILES - PAIR)
                        sp.dma_start(disp[p][:, :], disp_store[e].rearrange("o s n -> (o s) n")).then_inc(rest_loaded[p], 16)
                        sp.dma_start(b1[p], dram["l3f_b1"][e].broadcast_to([ROWS, F])).then_inc(rest_loaded[p], 16)
                        sp.dma_start(comb[p][:, :], comb_store[e].rearrange("o s n -> (o s) n")).then_inc(rest_loaded[p], 16)

            @block.tensor
            def _(pe):
                start(pe, "up_made", "d_turned", "raised", "drawn", "lowered")
                pe.wait_ge(x_low, 1)

                def turn(i, last):
                    def raise_tokens(c, half):
                        p, t = divmod(c, TILES)
                        if t == 0 and half == 0:
                            pe.wait_ge(w_low, i * 2 * PIECES + p * PIECES + PIECES + 2)
                        wait(pe, i, "up_kept", 2 * c + half)
                        for k in range(KD):
                            for a, b in PASSES:
                                mm = nc.tensor.matmul(m.ps[:ROWS, 6, :], x[a][:, k, tile_cols(t)],
                                                      w1[p][b][:, k, half * HALF:(half + 1) * HALF],
                                                      start=(k == 0 and a + b == 0), stop=(k == KD - 1 and a == 1))
                        mm.then_inc(S["up_made"], 1)

                    def turn_disp(c):
                        wait(pe, i, "diag_set", c + 1)
                        wait(pe, i, "d_kept", c)
                        wait(pe, i, "added", max(c - 2, 0))
                        for b in range(SEQ):
                            mm = nc.tensor.transpose(m.ps[:ROWS, 7, b * SL:(b + 1) * SL],
                                                     diag[:, c % 2, b * ROWS:(b + 1) * ROWS], m.ident[:, :])
                        mm.then_inc(S["d_turned"], 1)

                    def raise_slots(n):
                        c, b = divmod(n, SEQ)
                        if b == 0:
                            wait(pe, i, "d_kept", c + 1)
                        wait(pe, i, "gelued", n - 1)
                        for half in range(2):
                            if b == 0:
                                wait(pe, i, "up_split", 2 * c + half + 1)
                            for high_low, part in PASSES:
                                mm = nc.tensor.matmul(m.ps[:, 2 * (n % 2) + half, :],
                                                      to_slots[high_low][:, c % 2, b * SL:(b + 1) * SL],
                                                      up[part][:, c % 2, half * HALF:(half + 1) * HALF],
                                                      start=(high_low + part == 0), stop=(high_low == 1))
                        mm.then_inc(S["raised"], 1)

                    def draw(n):
                        c, b = divmod(n, SEQ)
                        p, t = divmod(c, TILES)
                        if t == 0 and b == 0:
                            pe.wait_ge(rest_loaded[p], i * 48 + 48)
                        wait(pe, i, "gelued", n + 1)
                        if b == 0:
                            wait(pe, i, "back_split", c)
                        own = slice(t * ROWS + b * T, t * ROWS + (b + 1) * T)
                        for f in range(KF):
                            col = (f % 4) * ROWS + b * T
                            mm = nc.tensor.matmul(m.ps[:, 4 + f // 4, col:col + T], hid[:, n % 2, f * 128:(f + 1) * 128],
                                                  comb[p][:, own], start=True, stop=True)
                        mm.then_inc(S["drawn"], 1)

                    def lower(c):
                        p, t = divmod(c, TILES)
                        if t == 0:
                            pe.wait_ge(w_low, i * 2 * PIECES + (p + 2) * PIECES)
                        wait(pe, i, "back_split", c + 1)
                        if c + 2 < PAIR:
                            wait(pe, i, "d_kept", c + 3)
                        else:
                            wait(pe, i, "added", c)
                        for f in range(KF):
                            for a, b in PASSES:
                                mm = nc.tensor.matmul(m.ps[:ROWS, 7, :D], backT[a][:, c % 2, f, :], w2[p][b][:, f, :],
                                                      start=(f == 0 and a + b == 0), stop=(f == KF - 1 and a == 1))
                        mm.then_inc(S["lowered"], 1)

                    turn_disp(0)
                    raise_tokens(0, 0)
                    raise_tokens(0, 1)
                    for c in range(PAIR):
                        more = c + 1 < PAIR
                        raise_slots(SEQ * c)
                        if more:
                            turn_disp(c + 1)
                        if c >= 1:
                            draw(SEQ * c - 1)
                        raise_slots(SEQ * c + 1)
                        if more:
                            raise_tokens(c + 1, 0)
                        draw(SEQ * c)
                        raise_slots(SEQ * c + 2)
                        if more:
                            raise_tokens(c + 1, 1)
                        if c >= 1:
                            lower(c - 1)
                        draw(SEQ * c + 1)
                    draw(SEQ * PAIR - 1)
                    lower(PAIR - 1)

                turns(pe, turn)

            @block.scalar
            def _(act):
                nc.scalar.activation(x[0][:, :, :], m.xT[:, :, :], ACT.Copy).then_inc(x_high, 1)
                start(act, "gelued", "back_high")
                for q in range(PIECES):
                    act.wait_ge((w1_loaded, w2_loaded)[q // 2], 16)
                    raw, high = piece(q, 0, 0)
                    nc.scalar.activation(high, raw, ACT.Copy).then_inc(w_high, 1)

                def turn(i, last):
                    def keep_back(c):
                        wait(act, i, "drawn", SEQ * (c + 1))
                        wait(act, i, "lowered", c - 1)
                        nc.scalar.activation(backT[0][:, c % 2, :, :].rearrange("p (b f) n -> p b (f n)", b=2),
                                             m.ps[:, 4:6, :4 * ROWS], ACT.Copy).then_inc(S["back_high"], 1)

                    def split_weights(p, q):
                        act.wait_ge((w1_loaded, w2_loaded)[q // 2], i * 32 + 16 * (p + 2))
                        wait(act, i, "lowered", p * TILES)
                        raw, high = piece(q, 1 - p, 0)
                        nc.scalar.activation(high, raw, ACT.Copy).then_inc(w_high, 1)

                    for n in range(SEQ * PAIR):
                        c, b = divmod(n, SEQ)
                        p, t = divmod(c, TILES)
                        wait(act, i, "raised", n + 1)
                        wait(act, i, "drawn", n - 1)
                        nc.scalar.activation(hid[:, n % 2, :],
                                             m.ps[:, 2 * (n % 2):2 * (n % 2) + 2, :].rearrange("p b s -> p (b s)"),
                                             ACT.Gelu).then_inc(S["gelued"], 1)
                        if b == 0 and c >= 1:
                            keep_back(c - 1)
                        q = t - FIRST_SPLIT
                        if b == 1 and 0 <= q < PIECES and not (last and p == 1):
                            split_weights(p, q)
                    keep_back(PAIR - 1)

                turns(act, turn)

            @block.vector
            def _(dve):
                start(dve, "up_kept", "up_high", "up_split", "diag_set", "d_high", "d_kept", "back_split", "added")
                dve.sem_inc(w_low, PIECES)
                nc.vector.memset(diag[:, :, :], 0.0).then_inc(cleared, 1)
                dve.wait_ge(cleared, 1)
                dve.wait_ge(x_high, 1)
                nc.vector.tensor_tensor(x[1][:, :, :], m.xT[:, :, :], x[0][:, :, :], ALU.subtract).then_inc(x_low, 1)

                def low_weights(p, q, seen):
                    raw, high = piece(q, p, 0)
                    dve.wait_ge(w_high, seen)
                    nc.vector.tensor_tensor(piece(q, p, 1)[1], raw, high, ALU.subtract).then_inc(w_low, 1)

                for q in range(PIECES):
                    low_weights(0, q, q + 1)

                def turn(i, last):
                    def set_diag(c):
                        p, t = divmod(c, TILES)
                        if t == 0:
                            dve.wait_ge(rest_loaded[p], i * 48 + 48)
                        wait(dve, i, "d_turned", c - 1)
                        out = diag[:, c % 2, :].rearrange("p (b s t) -> p b s t", b=SEQ, s=SEQ)
                        for b in range(SEQ):
                            own = slice(t * ROWS + b * T, t * ROWS + (b + 1) * T)
                            ins = nc.vector.tensor_scalar(out[:, b, b, :], disp[p][:, own], 1.0, None, ALU.mult)
                        ins.then_inc(S["diag_set"], 1)

                    def keep_up(c, half):
                        p = c // TILES
                        if half == 0:
                            wait(dve, i, "raised", SEQ * (c - 1))
                        cols = slice(half * HALF, (half + 1) * HALF)
                        wait(dve, i, "up_made", 2 * c + half + 1)
                        wait(dve, i, "up_split", 2 * c + half)
                        nc.vector.tensor_tensor(whole, m.ps[:ROWS, 6, :], b1[p][:, cols], ALU.add).then_inc(S["up_kept"], 1)
                        wait(dve, i, "up_kept", 2 * c + half + 1)
                        nc.vector.tensor_copy(up[0][:, c % 2, cols], whole).then_inc(S["up_high"], 1)
                        wait(dve, i, "up_high", 2 * c + half + 1)
                        nc.vector.tensor_tensor(up[1][:, c % 2, cols], whole, up[0][:, c % 2, cols],
                                                ALU.subtract).then_inc(S["up_split"], 1)

                    def keep_disp(c):
                        wait(dve, i, "d_turned", c + 1)
                        wait(dve, i, "raised", SEQ * (c - 1))
                        turned = m.ps[:ROWS, 7, :SEQ * SL]
                        nc.vector.tensor_copy(to_slots[0][:, c % 2, :], turned).then_inc(S["d_high"], 1)
                        wait(dve, i, "d_high", c + 1)
                        nc.vector.tensor_tensor(to_slots[1][:, c % 2, :], turned, to_slots[0][:, c % 2, :],
                                                ALU.subtract).then_inc(S["d_kept"], 1)

                    def split_back(c):
                        wait(dve, i, "back_high", c + 1)
                        high, low = (half[:, c % 2, :, :].rearrange("p (b f) n -> p b (f n)", b=2) for half in backT)
                        nc.vector.tensor_tensor(low, m.ps[:, 4:6, :4 * ROWS], high, ALU.subtract).then_inc(S["back_split"], 1)

                    def add(c):
                        t = c % TILES
                        wait(dve, i, "lowered", c + 1)
                        wait(dve, i, "added", c)
                        nc.vector.tensor_tensor(m.h[:, t, :], m.ps[:ROWS, 7, :D], m.h[:, t, :],
                                                ALU.add).then_inc(S["added"], 1)

                    set_diag(0)
                    keep_disp(0)
                    set_diag(1)
                    keep_up(0, 0)
                    keep_up(0, 1)
                    for c in range(PAIR):
                        more = c + 1 < PAIR
                        if more:
                            keep_disp(c + 1)
                        if c >= 1:
                            split_back(c - 1)
                        if more:
                            keep_up(c + 1, 0)
                            keep_up(c + 1, 1)
                        p, t = divmod(c, TILES)
                        q = t - FIRST_SPLIT
                        if 0 <= q < PIECES and not (last and p == 1):
                            low_weights(1 - p, q, i * 2 * PIECES + (p + 1) * PIECES + q + 1)
                        if c >= 1:
                            add(c - 1)
                        if c + 2 < PAIR:
                            set_diag(c + 2)
                    split_back(PAIR - 1)
                    add(PAIR - 1)

                turns(dve, turn)


def layer3_ffn(nc, m, dram):
    normalise(nc, m, "l3f_ln", m.h, turn=False)
    comb_store = nc.dram_tensor("l3f_comb_store", [8, 128, COLS], F32, kind="Internal").ap()
    disp_store = nc.dram_tensor("l3f_disp_store", [8, 128, COLS], F32, kind="Internal").ap()
    with ExitStack() as ctx:
        combT = m.sbuf(ctx, "l3f_combT", [128, 8, COLS])
        disp = m.sbuf(ctx, "l3f_disp", [128, 8, COLS])
        slots = m.sbuf(ctx, "l3f_slots", [128, 8, D])
        slotsT = m.sbuf(ctx, "l3f_slotsT", [128, KD, 8 * 128])
        csumT = m.sbuf(ctx, "l3f_csumT", [8, COLS])
        scratch = m.sbuf(ctx, "l3f_scratch", [ROWS, TILES, D])
        slot_scratch = m.sbuf(ctx, "l3f_slot_scratch", [128, 8, D])
        loaded = m.sem("l3f_slots_loaded")
        with nc.Block() as block:
            @block.sync
            def _(sp):
                sp.dma_start(slots[:, :, :], dram["l3f_slots"].rearrange("e s d -> s e d")).then_inc(loaded, 16)
                sp.wait_ge(loaded, 16)
        rms_turned(nc, m, "l3r", m.xn, ROWS, TILES, dram["l3f_gamma"], m.xT, scratch)
        rms_turned(nc, m, "l3s", slots, 128, 8, dram["l3f_slot_gamma"], slotsT, slot_scratch)
        combine_weights(nc, m, dram, slotsT, combT, csumT)
        dispatch_weights(nc, m, slotsT, disp, combT, disp_store, comb_store)
    soft_experts(nc, m, dram, comb_store, disp_store)


STAGE[8] = layer3_ffn


def arranged(x):
    import numpy as np
    C = np.ascontiguousarray
    a = {k: np.asarray(v) for k, v in x.items()}
    out = {}
    B = a["x"].shape[0]
    p = a["x"].reshape(B, 3, 6, 16, 6, 16).transpose(1, 3, 5, 0, 2, 4).reshape(768, B, T - 1)
    patches = np.zeros((768, NSEQ, T), np.float32)
    patches[:, :B, 1:] = p
    out["patchesT"] = patches.reshape(768, COLS)
    out["tok_wT"] = C(a["L0_tok_W"].T)
    one = np.concatenate([a["L0_tok_cls_token"].reshape(1, D), np.repeat(a["L0_tok_b"].reshape(1, D), T - 1, axis=0)])
    out["tok_base"] = np.concatenate([one] * SEQ)
    out["tok_pos"] = np.concatenate([a["L0_tok_pos_embed"].reshape(T, D)] * SEQ)
    cols = lambda v: C(v.reshape(-1, 128).T)
    row = lambda v: v.reshape(1, -1)
    out["c_ident"] = np.eye(128, dtype=np.float32)
    DH = 16
    spread = np.zeros((128, DH, 128), np.float32)
    for j in range(128):
        for e in range(DH):
            spread[(j // DH) * DH + e, e, j] = 1.0
    out["c_spread"] = spread
    out["c_gather"] = C(spread.transpose(2, 1, 0))
    seq = np.arange(ROWS) // T
    out["c_mask"] = np.tile(np.where(seq[:, None] == seq[None, :], 0.0, -1e30).astype(np.float32), (1, 4))
    late = (seq[:, None] == seq[None, :]) & (np.arange(ROWS)[:, None] <= np.arange(ROWS)[None, :])
    out["c_causal"] = np.tile(np.where(late, 0.0, -1e30).astype(np.float32), (1, 4))
    rows8 = np.zeros((8, 8, 128), np.float32)
    for h in range(8):
        rows8[h, h, :] = 1.0
    out["c_rows8"] = rows8
    out["l0a_kwT"] = C(a["L0_attn_key_w"].T)
    out["l0a_vqT"] = C(a["L0_attn_vq_w"].T)
    out["l0a_owT"] = C(a["L0_attn_out_w"].T)
    out["l0a_kb"] = cols(a["L0_attn_key_b"])
    out["l0a_ob"] = row(a["L0_attn_out_b"])
    out["l0f_gwT"] = C(a["L0_ffn_router_weight"].T)
    out["l0f_gb"] = row(a["L0_ffn_router_bias"])
    out["l0f_ew"] = a["L0_ffn_weight"]
    out["l0f_eb"] = a["L0_ffn_bias"]
    out["l1a_wq"], out["l1a_bq"] = a["L1_attn_W_DQ"], C(a["L1_attn_b_DQ"].reshape(-1, 1))
    out["l1a_wkv"] = np.concatenate([a["L1_attn_W_DKV"], a["L1_attn_W_KR"]], axis=1)
    out["l1a_bkv"] = np.concatenate([a["L1_attn_b_DKV"], a["L1_attn_b_KR"]]).reshape(-1, 1)

    def up_turned(w, b, at=32, rows=33):
        turned = np.zeros((w.shape[1] // 8, 8, rows), np.float32)
        turned[:, :, :32] = w.reshape(32, 8, -1).transpose(2, 1, 0)
        turned[:, :, at] = b.reshape(8, -1).T
        return turned

    out["l1a_wUQT"] = up_turned(a["L1_attn_W_UQ"], a["L1_attn_b_UQ"])
    out["l1a_wUKT"] = up_turned(a["L1_attn_W_UK"], a["L1_attn_b_UK"], 64, 65)
    out["l1a_wUVT"] = up_turned(a["L1_attn_W_UV"], a["L1_attn_b_UV"])
    out["l1a_wQRT"] = up_turned(a["L1_attn_W_QR"], a["L1_attn_b_QR"])
    out["l1a_wO"] = a["L1_attn_W_O"]
    out["l1a_bO"] = row(a["L1_attn_b_O"])
    out["l1f_gwT"] = C(a["L1_ffn_gate_w"].T)
    out["l1f_gb"] = row(a["L1_ffn_gate_b"])
    out["l1f_ew"] = a["L1_ffn_expert_w"]
    out["l1f_eb"] = a["L1_ffn_expert_b"]
    w = C(a["L2_attn_in_proj_w"].T)
    out["l2a_wz"], out["l2a_wx"] = C(w[:, :512]), C(w[:, 512:1024])
    out["l2a_wdt"], out["l2a_wB"], out["l2a_wC"] = C(w[:, 1024:1032]), C(w[:, 1032:1096]), C(w[:, 1096:1160])
    out["l2a_conv_w"] = C(a["L2_attn_conv_w"].reshape(4, 128, 4).transpose(1, 0, 2))
    out["l2a_conv_b"] = cols(a["L2_attn_conv_b"])
    out["l2a_A_log"] = C(a["L2_attn_A_log"].reshape(8, 1))
    out["l2a_dt_bias"] = C(a["L2_attn_dt_bias"].reshape(8, 1))
    out["l2a_D"] = C(np.broadcast_to(a["L2_attn_D_param"].reshape(1, 8, 1), (ROWS, 8, 64)).reshape(ROWS, 512))
    out["l2a_norm_w"] = cols(a["L2_attn_norm_w"])
    out["l2a_owT"] = C(a["L2_attn_out_proj_w"].T)
    for i in "12":
        out["l2f_ln" + i] = C(np.stack([a[f"L2_ffn_ln{i}_g"].reshape(2, 128), a[f"L2_ffn_ln{i}_b"].reshape(2, 128)]).transpose(2, 0, 1))
    for n in ("Wq", "Wk", "Wv", "Wo"):
        out["l2f_" + n] = a["L2_ffn_" + n]
    out["c_heads"] = np.repeat(np.eye(8, dtype=np.float32), 16, axis=0)
    out["l2g_gw"], out["l2g_gb"] = a["L2_ffn_Wg"], np.zeros((1, 8), np.float32)
    out["l2m_w1"], out["l2m_w2"] = a["L2_ffn_W1"], a["L2_ffn_W2"]
    out["l2m_b1"] = C(a["L2_ffn_b1"].reshape(8, 8, 128).transpose(0, 2, 1))
    out["l2m_b2"] = a["L2_ffn_b2"]
    for n in ("Wq", "Wk", "Wv", "Wg", "Wgk1", "Wgk2", "Wout"):
        out["l3a_" + n] = a["L3_attn_" + n]
    out["l3a_bgk2"] = cols(a["L3_attn_bgk2"])
    out["l3a_norm"] = C(np.stack([a["L3_attn_gamma"].reshape(2, 128), a["L3_attn_beta"].reshape(2, 128)]).transpose(2, 0, 1))
    out["l3f_gamma"] = cols(a["L3_ffn_norm_gamma"])
    out["l3f_slot_gamma"] = cols(a["L3_ffn_slot_norm_gamma"])
    out["l3f_slots"] = a["L3_ffn_slot_embeds"]
    out["l3f_w1"], out["l3f_w2"] = a["L3_ffn_w1"], a["L3_ffn_w2"]
    out["l3f_b1"] = a["L3_ffn_b1"]
    out["l3f_b2"] = a["L3_ffn_b2"]
    return {k: C(v) for k, v in out.items()}


def store(nc, m, out):
    whole = TILES - 1
    rows = out.rearrange("b t d -> (b t) d")
    left = rows.shape[0] - whole * ROWS
    stored = m.sem("stored")
    with nc.Block() as block:
        @block.sync
        def _(sp):
            sp.dma_start(rows[:whole * ROWS, :].rearrange("(t p) d -> p t d", p=ROWS), m.h[:, :whole, :]).then_inc(stored, 16)
            sp.dma_start(rows[whole * ROWS:, :], m.h[:left, whole, :]).then_inc(stored, 16)
            sp.wait_ge(stored, 32)


def vit_tower(nc, dram, out):
    with ExitStack() as ctx:
        m = Memory(nc, ctx)
        constants(nc, m, dram)
        for stage in sorted(STAGE):
            STAGE[stage](nc, m, dram)
            m.end_stage()
        store(nc, m, out)


def kernel(**inputs):
    import numpy as _np
    import concourse.bacc as _bacc
    from concourse import mybir as _mybir
    from concourse.bass_utils import run_bass_kernel_spmd as _run

    nc = _bacc.Bacc("TRN2", target_bir_lowering=False, num_devices=1)
    arrays, dram = {}, {}
    for name, a in arranged(inputs).items():
        arrays[f"in_{name}_dram"] = a
        dram[name] = nc.dram_tensor(f"in_{name}_dram", a.shape, _mybir.dt.from_np(a.dtype), kind="ExternalInput").ap()
    shape = (inputs["x"].shape[0], T, D)
    out = nc.dram_tensor("out_0_dram", shape, F32, kind="ExternalOutput").ap()
    vit_tower(nc, dram, out)
    r = _run(nc, [arrays], core_ids=[0])
    return r.results[0]["out_0_dram"]
```
